# Optimizing a Trainium2 kernel written in Bass

```python
import numpy as np
import jax
import jax.numpy as jnp

def _softmax(x, axis=-1):
    return jax.nn.softmax(x, axis=axis)

def _gelu(x):
    return jax.nn.gelu(x, approximate=True)

def _silu(x):
    return jax.nn.silu(x)

def _sigmoid(x):
    return jax.nn.sigmoid(x)

def _layernorm(x, axis=-1, eps=1e-05):
    m = jnp.mean(x, axis=axis, keepdims=True)
    v = jnp.var(x, axis=axis, keepdims=True)
    return (x - m) / jnp.sqrt(v + eps)

def _scatter_add(tgt, idx, src, axis=0):
    return tgt.at[idx].add(src)

def _segment_sum(src, seg, n):
    return jax.ops.segment_sum(src, seg, n)
kernel_name = 'mk_prb_d4_jaxref_r8_d512ef'

def setup_inputs(seed: int=0):
    np.random.seed(seed)
    _w = jnp.asarray

    def _L0_attn_setup():
        import jax, jax.numpy as jnp
        import numpy as np
        D = 128
        H = 16
        DH = D // H
        key = jax.random.key(seed)
        ks = jax.random.split(key, 7)
        s = 0.02
        return {'z': jax.random.normal(ks[0], (8, 128, D), dtype=jnp.float32), 'ln_w': jnp.ones((D,), dtype=jnp.float32), 'ln_b': jnp.zeros((D,), dtype=jnp.float32), 'W_qkv': jax.random.normal(ks[1], (D, 3 * D), dtype=jnp.float32) * s, 'b_qkv': jnp.zeros((3 * D,), dtype=jnp.float32), 'W_proj': jax.random.normal(ks[2], (D, D), dtype=jnp.float32) * s, 'b_proj': jnp.zeros((D,), dtype=jnp.float32)}
    _L0_attn_in = _L0_attn_setup()

    def _L0_ffn_setup():
        import jax, jax.numpy as jnp
        import numpy as np
        DIM = 128
        DEPTH = 2
        HEADS = 8
        DIM_HEAD = 64
        WINDOW = 64
        INNER = HEADS * DIM_HEAD
        HID = int(DIM * 4 * 2 / 3)
        B, N = (2, 1024)
        QK_SCALE = 8.0

        def shift_token(t):
            t1, t2 = jnp.split(t, 2, axis=-1)
            t2 = jnp.pad(t2, ((0, 0), (1, 0), (0, 0)))[:, :-1]
            return jnp.concatenate([t1, t2], axis=-1)

        def l2norm(t):
            return t / jnp.clip(jnp.linalg.norm(t, axis=-1, keepdims=True), 1e-12)

        def rotate_half(x):
            x1, x2 = jnp.split(x, 2, axis=-1)
            return jnp.concatenate([-x2, x1], axis=-1)

        def rotary_xpos(q, k):
            n = q.shape[-2]
            half_idx = jnp.arange(0, DIM_HEAD, 2, dtype=jnp.float32)
            inv_freq = 1.0 / 10000.0 ** (half_idx / DIM_HEAD)
            t = jnp.arange(n, dtype=jnp.float32)
            freqs = t[:, None] * inv_freq[None, :]
            freqs = jnp.concatenate([freqs, freqs], axis=-1)
            base = (half_idx + 0.4 * DIM_HEAD) / (1.4 * DIM_HEAD)
            power = (t - n // 2) / float(WINDOW // 2)
            scale = base[None, :] ** power[:, None]
            scale = jnp.concatenate([scale, scale], axis=-1)
            cos, sin = (jnp.cos(freqs), jnp.sin(freqs))
            q = q * cos * scale + rotate_half(q) * sin * scale
            k = k * cos / scale + rotate_half(k) * sin / scale
            return (q, k)

        def local_attention(q, k, v):
            b, h, n, d = q.shape
            w = n // WINDOW
            bq = q.reshape(b, h, w, WINDOW, d) * QK_SCALE
            bk = k.reshape(b, h, w, WINDOW, d)
            bv = v.reshape(b, h, w, WINDOW, d)

            def look_around(t):
                p = jnp.pad(t, ((0, 0), (0, 0), (1, 0), (0, 0), (0, 0)))
                return jnp.concatenate([p[:, :, :w], p[:, :, 1:]], axis=3)
            bk, bv = (look_around(bk), look_around(bv))
            bt = jnp.arange(n).reshape(w, WINDOW)
            btp = jnp.pad(bt, ((1, 0), (0, 0)), constant_values=-1)
            btk = jnp.concatenate([btp[:w], btp[1:]], axis=1)
            sim = jnp.einsum('bhwid,bhwjd->bhwij', bq, bk)
            i = bt[:, :, None]
            j = btk[:, None, :]
            mask = (i < j) | (i > j + WINDOW) | (j == -1)
            sim = jnp.where(mask, -jnp.finfo(sim.dtype).max, sim)
            attn = jax.nn.softmax(sim, axis=-1)
            out = jnp.einsum('bhwij,bhwjd->bhwid', attn, bv)
            return out.reshape(b, h, n, d)

        def _layer(x, wqkv, qs, ksc, wo, lg, lb, w1, b1, w2, b2):
            b, n, _ = x.shape
            h = shift_token(x)
            qkv = h @ wqkv
            q, k, v = jnp.split(qkv, 3, axis=-1)
            to_heads = lambda t: t.reshape(b, n, HEADS, DIM_HEAD).transpose(0, 2, 1, 3)
            q, k, v = (to_heads(q), to_heads(k), to_heads(v))
            q = l2norm(q) * qs
            k = l2norm(k) * ksc
            q, k = rotary_xpos(q, k)
            o = local_attention(q, k, v)
            o = o.transpose(0, 2, 1, 3).reshape(b, n, INNER)
            x = x + o @ wo
            h = shift_token(x)
            mu = h.mean(-1, keepdims=True)
            var = h.var(-1, keepdims=True)
            h = (h - mu) / jnp.sqrt(var + 1e-05) * lg + lb
            h = h @ w1 + b1
            a, g = jnp.split(h, 2, axis=-1)
            h = a * jax.nn.gelu(g, approximate=False)
            x = x + h @ w2 + b2
            return x
        key = jax.random.key(seed)
        ks = jax.random.split(key, 6)
        return {'x': jax.random.normal(ks[0], (B, N, DIM), jnp.float32), 'wqkv': jax.random.normal(ks[1], (DEPTH, DIM, 3 * INNER), jnp.float32) * 0.02, 'q_scale': jnp.ones((DEPTH, DIM_HEAD), jnp.float32), 'k_scale': jnp.ones((DEPTH, DIM_HEAD), jnp.float32), 'wo': jax.random.normal(ks[2], (DEPTH, INNER, DIM), jnp.float32) * 0.02, 'ln_g': jnp.ones((DEPTH, DIM), jnp.float32), 'ln_b': jnp.zeros((DEPTH, DIM), jnp.float32), 'w1': jax.random.normal(ks[3], (DEPTH, DIM, 2 * HID), jnp.float32) * 0.02, 'b1': jnp.zeros((DEPTH, 2 * HID), jnp.float32), 'w2': jax.random.normal(ks[4], (DEPTH, HID, DIM), jnp.float32) * 0.02, 'b2': jnp.zeros((DEPTH, DIM), jnp.float32)}
    _L0_ffn_in = _L0_ffn_setup()

    def _L1_attn_setup():
        import jax, jax.numpy as jnp
        import numpy as np
        D = 128
        H = 16
        KVH = 4
        HD = D // H
        LAT = 32
        WIN = 32
        B, S = (1, 256)
        BASE_G, BASE_L = (1000000.0, 10000.0)
        EPS = 1e-06

        def rmsnorm(x, w):
            return x * jax.lax.rsqrt(jnp.mean(x * x, axis=-1, keepdims=True) + EPS) * w

        def qk_norm(x):
            return x * jax.lax.rsqrt(jnp.mean(x * x, axis=-1, keepdims=True) + EPS)

        def rope(x, base):
            s, hd = (x.shape[-2], x.shape[-1])
            inv_freq = 1.0 / base ** (jnp.arange(0, hd, 2, dtype=jnp.float32) / hd)
            freqs = jnp.arange(s, dtype=jnp.float32)[:, None] * inv_freq[None, :]
            cos, sin = (jnp.cos(freqs), jnp.sin(freqs))
            xe, xo = (x[..., ::2], x[..., 1::2])
            out = jnp.stack([xe * cos - xo * sin, xe * sin + xo * cos], axis=-1)
            return out.reshape(x.shape)

        def split_heads(x, n_heads):
            b, s, _ = x.shape
            return x.reshape(b, s, n_heads, HD).transpose(0, 2, 1, 3)

        def repeat_kv(x):
            return jnp.repeat(x, H // KVH, axis=1)

        def sdpa(q, k, v, mask):
            scores = jnp.einsum('bhqd,bhkd->bhqk', q, k) / np.sqrt(HD).astype(np.float32)
            scores = jnp.where(mask, scores, jnp.float32(-1e+30))
            probs = jax.nn.softmax(scores, axis=-1)
            return jnp.einsum('bhqk,bhkd->bhqd', probs, v)

        def merge_heads(x):
            b, h, s, hd = x.shape
            return x.transpose(0, 2, 1, 3).reshape(b, s, h * hd)

        def global_latent_attn(x, wq, w_kv_down, w_k_up, w_v_up, wo):
            q = split_heads(x @ wq, H)
            latent = x @ w_kv_down
            k = split_heads(latent @ w_k_up, KVH)
            v = split_heads(latent @ w_v_up, KVH)
            q, k = (rope(q, BASE_G), rope(k, BASE_G))
            q, k = (qk_norm(q), qk_norm(k))
            k, v = (repeat_kv(k), repeat_kv(v))
            i = jnp.arange(x.shape[1])
            causal = i[:, None] >= i[None, :]
            return merge_heads(sdpa(q, k, v, causal)) @ wo

        def local_gqa_attn(x, wq, wk, wv, wo):
            q = split_heads(x @ wq, H)
            k = split_heads(x @ wk, KVH)
            v = split_heads(x @ wv, KVH)
            q, k = (rope(q, BASE_L), rope(k, BASE_L))
            q, k = (qk_norm(q), qk_norm(k))
            k, v = (repeat_kv(k), repeat_kv(v))
            i = jnp.arange(x.shape[1])
            diff = i[:, None] - i[None, :]
            mask = (diff >= 0) & (diff < WIN)
            return merge_heads(sdpa(q, k, v, mask)) @ wo
        key = jax.random.key(seed)
        ks = jax.random.split(key, 12)
        std = 0.02
        return {'hidden': jax.random.normal(ks[0], (B, S, D), dtype=jnp.float32), 'norm1_w': jnp.ones((D,), jnp.float32), 'norm2_w': jnp.ones((D,), jnp.float32), 'g_wq': jax.random.normal(ks[1], (D, H * HD), jnp.float32) * std, 'g_kv_down': jax.random.normal(ks[2], (D, LAT), jnp.float32) * std, 'g_k_up': jax.random.normal(ks[3], (LAT, KVH * HD), jnp.float32) * std, 'g_v_up': jax.random.normal(ks[4], (LAT, KVH * HD), jnp.float32) * std, 'g_wo': jax.random.normal(ks[5], (D, D), jnp.float32) * std, 'l_wq': jax.random.normal(ks[6], (D, H * HD), jnp.float32) * std, 'l_wk': jax.random.normal(ks[7], (D, KVH * HD), jnp.float32) * std, 'l_wv': jax.random.normal(ks[8], (D, KVH * HD), jnp.float32) * std, 'l_wo': jax.random.normal(ks[9], (D, D), jnp.float32) * std}
    _L1_attn_in = _L1_attn_setup()

    def _L1_ffn_setup():
        import jax, jax.numpy as jnp
        import numpy as np
        B, S, D = (2, 256, 128)
        H = 256
        E = 8
        K = 2
        HS = 256 * 1
        SCALE = 1.0 / float(np.sqrt(D))
        key = jax.random.key(seed)
        ks = jax.random.split(key, 9)
        init = 0.02
        return {'x': jax.random.normal(ks[0], (B, S, D), dtype=jnp.float32), 'Wr': jax.random.normal(ks[1], (D, E), dtype=jnp.float32) * init, 'rb': jnp.zeros((E,), dtype=jnp.float32), 'W1': jax.random.normal(ks[2], (E, D, H), dtype=jnp.float32) * init, 'W2': jax.random.normal(ks[3], (E, H, D), dtype=jnp.float32) * init, 'W3': jax.random.normal(ks[4], (E, D, H), dtype=jnp.float32) * init, 'Ws1': jax.random.normal(ks[5], (D, HS), dtype=jnp.float32) * init, 'Ws2': jax.random.normal(ks[6], (HS, D), dtype=jnp.float32) * init, 'Ws3': jax.random.normal(ks[7], (D, HS), dtype=jnp.float32) * init}
    _L1_ffn_in = _L1_ffn_setup()

    def _L2_attn_setup():
        import jax, jax.numpy as jnp
        import numpy as np
        D_MODEL = 128
        THRESH = 0.01
        key = jax.random.key(seed)
        kx, kw = jax.random.split(key)
        x = jax.random.normal(kx, (4, 256, D_MODEL), dtype=jnp.float32)
        W = jax.random.normal(kw, (D_MODEL, D_MODEL), dtype=jnp.float32) / np.sqrt(D_MODEL)
        return {'x': x, 'W': W}
    _L2_attn_in = _L2_attn_setup()

    def _L2_ffn_setup():
        import jax, jax.numpy as jnp
        import numpy as np
        BLOCK_SIZE = 32
        FP6_E2M3_MAX = 7.5

        def _build_fp6_e2m3_grid():
            vals = set()
            for bits in range(64):
                s = bits >> 5 & 1
                e = bits >> 3 & 3
                m = bits & 7
                v = m / 8.0 if e == 0 else (1.0 + m / 8.0) * 2.0 ** (e - 1)
                vals.add(-v if s else v)
            return np.array(sorted(vals), dtype=np.float32)
        _GRID = jnp.asarray(_build_fp6_e2m3_grid())

        def _nearest_on_grid(x, grid):
            idx = jnp.clip(jnp.searchsorted(grid, x), 0, grid.shape[0] - 1)
            idx_lo = jnp.maximum(idx - 1, 0)
            v_hi = grid[idx]
            v_lo = grid[idx_lo]
            return jnp.where(jnp.abs(x - v_lo) <= jnp.abs(x - v_hi), v_lo, v_hi)

        def _mx_quantize(t, eps=1e-30):
            rows, K = t.shape
            blocks = t.reshape(rows, K // BLOCK_SIZE, BLOCK_SIZE)
            scales = jnp.maximum(jnp.max(jnp.abs(blocks), axis=-1) / FP6_E2M3_MAX, eps)
            q = _nearest_on_grid(blocks / scales[..., None], _GRID)
            return (q, scales)
        key = jax.random.key(seed)
        k1, k2, k3 = jax.random.split(key, 3)
        x = jax.random.normal(k1, (8, 1024, 128), dtype=jnp.float32)
        weight = jax.random.normal(k2, (128, 128), dtype=jnp.float32) * 0.02
        bias = jax.random.normal(k3, (128,), dtype=jnp.float32) * 0.02
        return {'x': x, 'weight': weight, 'bias': bias}
    _L2_ffn_in = _L2_ffn_setup()

    def _L3_attn_setup():
        import jax, jax.numpy as jnp
        import numpy as np
        LAMBDA_0 = 1.0
        EPS = 1e-06
        key = jax.random.key(seed)
        ks = jax.random.split(key, 5)
        B, T, D, H = (4, 256, 128, 128)
        x = jax.random.normal(ks[0], (B, T, D), dtype=jnp.float32)
        Wq = jax.random.normal(ks[1], (H, D), dtype=jnp.float32) * D ** (-0.5)
        Wk = jax.random.normal(ks[2], (H, D), dtype=jnp.float32) * D ** (-0.5)
        Wv = jax.random.normal(ks[3], (H, D), dtype=jnp.float32) * D ** (-0.5)
        Wo = jax.random.normal(ks[4], (D, H), dtype=jnp.float32) * H ** (-0.5)
        bq = jnp.zeros((H,), jnp.float32)
        bk = jnp.zeros((H,), jnp.float32)
        bv = jnp.zeros((H,), jnp.float32)
        bo = jnp.zeros((D,), jnp.float32)
        return {'x': x, 'Wq': Wq, 'bq': bq, 'Wk': Wk, 'bk': bk, 'Wv': Wv, 'bv': bv, 'Wo': Wo, 'bo': bo}
    _L3_attn_in = _L3_attn_setup()

    def _L3_ffn_setup():
        import jax, jax.numpy as jnp
        import numpy as np
        E = 8
        K = 2
        C = 128
        F = 256
        EPS = 1e-05
        key = jax.random.key(seed)
        ks = jax.random.split(key, 6)
        x = jax.random.normal(ks[0], (2, 128, C), dtype=jnp.float32)
        ln_gamma = 1.0 + 0.02 * jax.random.normal(ks[1], (C,), dtype=jnp.float32)
        ln_beta = 0.02 * jax.random.normal(ks[2], (C,), dtype=jnp.float32)
        gate_w = jax.random.normal(ks[3], (E, C), dtype=jnp.float32) / np.sqrt(C)
        w1 = jax.random.normal(ks[4], (E, F, C), dtype=jnp.float32) / np.sqrt(C)
        w2 = jax.random.normal(ks[5], (E, C, F), dtype=jnp.float32) / np.sqrt(F)
        return {'x': x, 'ln_gamma': ln_gamma, 'ln_beta': ln_beta, 'gate_w': gate_w, 'w1': w1, 'w2': w2}
    _L3_ffn_in = _L3_ffn_setup()
    _d = {'L0_attn_z': _L0_attn_in['z'], 'L0_attn_ln_w': _L0_attn_in['ln_w'], 'L0_attn_ln_b': _L0_attn_in['ln_b'], 'L0_attn_W_qkv': _L0_attn_in['W_qkv'], 'L0_attn_b_qkv': _L0_attn_in['b_qkv'], 'L0_attn_W_proj': _L0_attn_in['W_proj'], 'L0_attn_b_proj': _L0_attn_in['b_proj'], 'L0_ffn_wqkv': _L0_ffn_in['wqkv'], 'L0_ffn_q_scale': _L0_ffn_in['q_scale'], 'L0_ffn_k_scale': _L0_ffn_in['k_scale'], 'L0_ffn_wo': _L0_ffn_in['wo'], 'L0_ffn_ln_g': _L0_ffn_in['ln_g'], 'L0_ffn_ln_b': _L0_ffn_in['ln_b'], 'L0_ffn_w1': _L0_ffn_in['w1'], 'L0_ffn_b1': _L0_ffn_in['b1'], 'L0_ffn_w2': _L0_ffn_in['w2'], 'L0_ffn_b2': _L0_ffn_in['b2'], 'L1_attn_norm1_w': _L1_attn_in['norm1_w'], 'L1_attn_norm2_w': _L1_attn_in['norm2_w'], 'L1_attn_g_wq': _L1_attn_in['g_wq'], 'L1_attn_g_kv_down': _L1_attn_in['g_kv_down'], 'L1_attn_g_k_up': _L1_attn_in['g_k_up'], 'L1_attn_g_v_up': _L1_attn_in['g_v_up'], 'L1_attn_g_wo': _L1_attn_in['g_wo'], 'L1_attn_l_wq': _L1_attn_in['l_wq'], 'L1_attn_l_wk': _L1_attn_in['l_wk'], 'L1_attn_l_wv': _L1_attn_in['l_wv'], 'L1_attn_l_wo': _L1_attn_in['l_wo'], 'L1_ffn_Wr': _L1_ffn_in['Wr'], 'L1_ffn_rb': _L1_ffn_in['rb'], 'L1_ffn_W1': _L1_ffn_in['W1'], 'L1_ffn_W2': _L1_ffn_in['W2'], 'L1_ffn_W3': _L1_ffn_in['W3'], 'L1_ffn_Ws1': _L1_ffn_in['Ws1'], 'L1_ffn_Ws2': _L1_ffn_in['Ws2'], 'L1_ffn_Ws3': _L1_ffn_in['Ws3'], 'L2_attn_W': _L2_attn_in['W'], 'L2_ffn_weight': _L2_ffn_in['weight'], 'L2_ffn_bias': _L2_ffn_in['bias'], 'L3_attn_Wq': _L3_attn_in['Wq'], 'L3_attn_bq': _L3_attn_in['bq'], 'L3_attn_Wk': _L3_attn_in['Wk'], 'L3_attn_bk': _L3_attn_in['bk'], 'L3_attn_Wv': _L3_attn_in['Wv'], 'L3_attn_bv': _L3_attn_in['bv'], 'L3_attn_Wo': _L3_attn_in['Wo'], 'L3_attn_bo': _L3_attn_in['bo'], 'L3_ffn_ln_gamma': _L3_ffn_in['ln_gamma'], 'L3_ffn_ln_beta': _L3_ffn_in['ln_beta'], 'L3_ffn_gate_w': _L3_ffn_in['gate_w'], 'L3_ffn_w1': _L3_ffn_in['w1'], 'L3_ffn_w2': _L3_ffn_in['w2']}
    _x0 = _d['L0_attn_z']
    _d['L0_attn_z'] = jax.random.normal(jax.random.fold_in(jax.random.key(seed), 1), (4, 1024, 128), dtype=_x0.dtype)
    del _x0
    return _d

def reference(L0_attn_z, L0_attn_ln_w, L0_attn_ln_b, L0_attn_W_qkv, L0_attn_b_qkv, L0_attn_W_proj, L0_attn_b_proj, L0_ffn_wqkv, L0_ffn_q_scale, L0_ffn_k_scale, L0_ffn_wo, L0_ffn_ln_g, L0_ffn_ln_b, L0_ffn_w1, L0_ffn_b1, L0_ffn_w2, L0_ffn_b2, L1_attn_norm1_w, L1_attn_norm2_w, L1_attn_g_wq, L1_attn_g_kv_down, L1_attn_g_k_up, L1_attn_g_v_up, L1_attn_g_wo, L1_attn_l_wq, L1_attn_l_wk, L1_attn_l_wv, L1_attn_l_wo, L1_ffn_Wr, L1_ffn_rb, L1_ffn_W1, L1_ffn_W2, L1_ffn_W3, L1_ffn_Ws1, L1_ffn_Ws2, L1_ffn_Ws3, L2_attn_W, L2_ffn_weight, L2_ffn_bias, L3_attn_Wq, L3_attn_bq, L3_attn_Wk, L3_attn_bk, L3_attn_Wv, L3_attn_bv, L3_attn_Wo, L3_attn_bo, L3_ffn_ln_gamma, L3_ffn_ln_beta, L3_ffn_gate_w, L3_ffn_w1, L3_ffn_w2):

    def _L0_attn_ref(z, ln_w, ln_b, W_qkv, b_qkv, W_proj, b_proj):
        import jax, jax.numpy as jnp
        import numpy as np
        D = 128
        H = 16
        DH = D // H
        b, n, d = z.shape
        mu = jnp.mean(z, axis=-1, keepdims=True)
        var = jnp.var(z, axis=-1, keepdims=True)
        zn = (z - mu) / jnp.sqrt(var + 1e-05) * ln_w + ln_b
        qkv = (zn @ W_qkv + b_qkv).reshape(b, n, 3, H, DH)
        q = qkv[:, :, 0].transpose(0, 2, 1, 3)
        k = qkv[:, :, 1].transpose(0, 2, 1, 3)
        v = qkv[:, :, 2].transpose(0, 2, 1, 3)
        scale = 1.0 / jnp.sqrt(jnp.asarray(DH, dtype=z.dtype))
        scores = jnp.einsum('bhqd,bhkd->bhqk', q, k) * scale
        attn = jax.nn.softmax(scores, axis=-1)
        msa = jnp.einsum('bhqk,bhkd->bhqd', attn, v)
        msa_cat = msa.transpose(0, 2, 1, 3).reshape(b, n, d)
        out = msa_cat @ W_proj + b_proj
        return z + out

    def _L0_ffn_ref(x, wqkv, q_scale, k_scale, wo, ln_g, ln_b, w1, b1, w2, b2):
        import jax, jax.numpy as jnp
        import numpy as np
        DIM = 128
        DEPTH = 2
        HEADS = 8
        DIM_HEAD = 64
        WINDOW = 64
        INNER = HEADS * DIM_HEAD
        HID = int(DIM * 4 * 2 / 3)
        B, N = (2, 1024)
        QK_SCALE = 8.0

        def shift_token(t):
            t1, t2 = jnp.split(t, 2, axis=-1)
            t2 = jnp.pad(t2, ((0, 0), (1, 0), (0, 0)))[:, :-1]
            return jnp.concatenate([t1, t2], axis=-1)

        def l2norm(t):
            return t / jnp.clip(jnp.linalg.norm(t, axis=-1, keepdims=True), 1e-12)

        def rotate_half(x):
            x1, x2 = jnp.split(x, 2, axis=-1)
            return jnp.concatenate([-x2, x1], axis=-1)

        def rotary_xpos(q, k):
            n = q.shape[-2]
            half_idx = jnp.arange(0, DIM_HEAD, 2, dtype=jnp.float32)
            inv_freq = 1.0 / 10000.0 ** (half_idx / DIM_HEAD)
            t = jnp.arange(n, dtype=jnp.float32)
            freqs = t[:, None] * inv_freq[None, :]
            freqs = jnp.concatenate([freqs, freqs], axis=-1)
            base = (half_idx + 0.4 * DIM_HEAD) / (1.4 * DIM_HEAD)
            power = (t - n // 2) / float(WINDOW // 2)
            scale = base[None, :] ** power[:, None]
            scale = jnp.concatenate([scale, scale], axis=-1)
            cos, sin = (jnp.cos(freqs), jnp.sin(freqs))
            q = q * cos * scale + rotate_half(q) * sin * scale
            k = k * cos / scale + rotate_half(k) * sin / scale
            return (q, k)

        def local_attention(q, k, v):
            b, h, n, d = q.shape
            w = n // WINDOW
            bq = q.reshape(b, h, w, WINDOW, d) * QK_SCALE
            bk = k.reshape(b, h, w, WINDOW, d)
            bv = v.reshape(b, h, w, WINDOW, d)

            def look_around(t):
                p = jnp.pad(t, ((0, 0), (0, 0), (1, 0), (0, 0), (0, 0)))
                return jnp.concatenate([p[:, :, :w], p[:, :, 1:]], axis=3)
            bk, bv = (look_around(bk), look_around(bv))
            bt = jnp.arange(n).reshape(w, WINDOW)
            btp = jnp.pad(bt, ((1, 0), (0, 0)), constant_values=-1)
            btk = jnp.concatenate([btp[:w], btp[1:]], axis=1)
            sim = jnp.einsum('bhwid,bhwjd->bhwij', bq, bk)
            i = bt[:, :, None]
            j = btk[:, None, :]
            mask = (i < j) | (i > j + WINDOW) | (j == -1)
            sim = jnp.where(mask, -jnp.finfo(sim.dtype).max, sim)
            attn = jax.nn.softmax(sim, axis=-1)
            out = jnp.einsum('bhwij,bhwjd->bhwid', attn, bv)
            return out.reshape(b, h, n, d)

        def _layer(x, wqkv, qs, ksc, wo, lg, lb, w1, b1, w2, b2):
            b, n, _ = x.shape
            h = shift_token(x)
            qkv = h @ wqkv
            q, k, v = jnp.split(qkv, 3, axis=-1)
            to_heads = lambda t: t.reshape(b, n, HEADS, DIM_HEAD).transpose(0, 2, 1, 3)
            q, k, v = (to_heads(q), to_heads(k), to_heads(v))
            q = l2norm(q) * qs
            k = l2norm(k) * ksc
            q, k = rotary_xpos(q, k)
            o = local_attention(q, k, v)
            o = o.transpose(0, 2, 1, 3).reshape(b, n, INNER)
            x = x + o @ wo
            h = shift_token(x)
            mu = h.mean(-1, keepdims=True)
            var = h.var(-1, keepdims=True)
            h = (h - mu) / jnp.sqrt(var + 1e-05) * lg + lb
            h = h @ w1 + b1
            a, g = jnp.split(h, 2, axis=-1)
            h = a * jax.nn.gelu(g, approximate=False)
            x = x + h @ w2 + b2
            return x
        for l in range(DEPTH):
            x = _layer(x, wqkv[l], q_scale[l], k_scale[l], wo[l], ln_g[l], ln_b[l], w1[l], b1[l], w2[l], b2[l])
        return x

    def _L1_attn_ref(hidden, norm1_w, norm2_w, g_wq, g_kv_down, g_k_up, g_v_up, g_wo, l_wq, l_wk, l_wv, l_wo):
        import jax, jax.numpy as jnp
        import numpy as np
        D = 128
        H = 16
        KVH = 4
        HD = D // H
        LAT = 32
        WIN = 32
        B, S = (1, 256)
        BASE_G, BASE_L = (1000000.0, 10000.0)
        EPS = 1e-06

        def rmsnorm(x, w):
            return x * jax.lax.rsqrt(jnp.mean(x * x, axis=-1, keepdims=True) + EPS) * w

        def qk_norm(x):
            return x * jax.lax.rsqrt(jnp.mean(x * x, axis=-1, keepdims=True) + EPS)

        def rope(x, base):
            s, hd = (x.shape[-2], x.shape[-1])
            inv_freq = 1.0 / base ** (jnp.arange(0, hd, 2, dtype=jnp.float32) / hd)
            freqs = jnp.arange(s, dtype=jnp.float32)[:, None] * inv_freq[None, :]
            cos, sin = (jnp.cos(freqs), jnp.sin(freqs))
            xe, xo = (x[..., ::2], x[..., 1::2])
            out = jnp.stack([xe * cos - xo * sin, xe * sin + xo * cos], axis=-1)
            return out.reshape(x.shape)

        def split_heads(x, n_heads):
            b, s, _ = x.shape
            return x.reshape(b, s, n_heads, HD).transpose(0, 2, 1, 3)

        def repeat_kv(x):
            return jnp.repeat(x, H // KVH, axis=1)

        def sdpa(q, k, v, mask):
            scores = jnp.einsum('bhqd,bhkd->bhqk', q, k) / np.sqrt(HD).astype(np.float32)
            scores = jnp.where(mask, scores, jnp.float32(-1e+30))
            probs = jax.nn.softmax(scores, axis=-1)
            return jnp.einsum('bhqk,bhkd->bhqd', probs, v)

        def merge_heads(x):
            b, h, s, hd = x.shape
            return x.transpose(0, 2, 1, 3).reshape(b, s, h * hd)

        def global_latent_attn(x, wq, w_kv_down, w_k_up, w_v_up, wo):
            q = split_heads(x @ wq, H)
            latent = x @ w_kv_down
            k = split_heads(latent @ w_k_up, KVH)
            v = split_heads(latent @ w_v_up, KVH)
            q, k = (rope(q, BASE_G), rope(k, BASE_G))
            q, k = (qk_norm(q), qk_norm(k))
            k, v = (repeat_kv(k), repeat_kv(v))
            i = jnp.arange(x.shape[1])
            causal = i[:, None] >= i[None, :]
            return merge_heads(sdpa(q, k, v, causal)) @ wo

        def local_gqa_attn(x, wq, wk, wv, wo):
            q = split_heads(x @ wq, H)
            k = split_heads(x @ wk, KVH)
            v = split_heads(x @ wv, KVH)
            q, k = (rope(q, BASE_L), rope(k, BASE_L))
            q, k = (qk_norm(q), qk_norm(k))
            k, v = (repeat_kv(k), repeat_kv(v))
            i = jnp.arange(x.shape[1])
            diff = i[:, None] - i[None, :]
            mask = (diff >= 0) & (diff < WIN)
            return merge_heads(sdpa(q, k, v, mask)) @ wo
        x = hidden
        x = x + global_latent_attn(rmsnorm(x, norm1_w), g_wq, g_kv_down, g_k_up, g_v_up, g_wo)
        x = x + local_gqa_attn(rmsnorm(x, norm2_w), l_wq, l_wk, l_wv, l_wo)
        return x

    def _L1_ffn_ref(x, Wr, rb, W1, W2, W3, Ws1, Ws2, Ws3):
        import jax, jax.numpy as jnp
        import numpy as np
        B, S, D = (2, 256, 128)
        H = 256
        E = 8
        K = 2
        HS = 256 * 1
        SCALE = 1.0 / float(np.sqrt(D))
        logits = jnp.einsum('bsd,de->bse', x, Wr) * SCALE
        _, idx = jax.lax.top_k(logits + rb, K)
        gathered = jnp.take_along_axis(logits, idx, axis=-1)
        w = jax.nn.softmax(gathered, axis=-1)
        w_full = jnp.sum(jax.nn.one_hot(idx, E, dtype=x.dtype) * w[..., None], axis=-2)
        h = jnp.einsum('bsd,edh->bseh', x, W1) * jax.nn.silu(jnp.einsum('bsd,edh->bseh', x, W3))
        expert_out = jnp.einsum('bseh,ehd->bsed', h, W2)
        out = jnp.einsum('bsed,bse->bsd', expert_out, w_full)
        hs = jnp.einsum('bsd,dh->bsh', x, Ws1) * jax.nn.silu(jnp.einsum('bsd,dh->bsh', x, Ws3))
        out = out + jnp.einsum('bsh,hd->bsd', hs, Ws2)
        return out

    def _L2_attn_ref(x, W):
        import jax, jax.numpy as jnp
        import numpy as np
        D_MODEL = 128
        THRESH = 0.01
        B, T, D = x.shape
        scale = 1.0 / jnp.sqrt(jnp.asarray(D, x.dtype))
        scores = jnp.einsum('btd,bsd->bts', x, x) * scale
        probs = jax.nn.softmax(scores, axis=-1)
        vacuum_mask = probs < THRESH
        vacuum_energy = jnp.where(vacuum_mask, probs, 0.0)
        vac_sum = vacuum_energy.sum(axis=-1, keepdims=True)
        vac_in = jnp.broadcast_to(vac_sum, (B, T, D))
        casimir = jnp.einsum('btd,od->bto', vac_in, W)
        sparse_probs = jnp.where(vacuum_mask, 0.0, probs)
        sparse_probs = sparse_probs / (sparse_probs.sum(axis=-1, keepdims=True) + 1e-09)
        attended = jnp.einsum('bts,bsd->btd', sparse_probs, x)
        return attended + casimir * 0.01

    def _L2_ffn_ref(x, weight, bias):
        import jax, jax.numpy as jnp
        import numpy as np
        BLOCK_SIZE = 32
        FP6_E2M3_MAX = 7.5

        def _build_fp6_e2m3_grid():
            vals = set()
            for bits in range(64):
                s = bits >> 5 & 1
                e = bits >> 3 & 3
                m = bits & 7
                v = m / 8.0 if e == 0 else (1.0 + m / 8.0) * 2.0 ** (e - 1)
                vals.add(-v if s else v)
            return np.array(sorted(vals), dtype=np.float32)
        _GRID = jnp.asarray(_build_fp6_e2m3_grid())

        def _nearest_on_grid(x, grid):
            idx = jnp.clip(jnp.searchsorted(grid, x), 0, grid.shape[0] - 1)
            idx_lo = jnp.maximum(idx - 1, 0)
            v_hi = grid[idx]
            v_lo = grid[idx_lo]
            return jnp.where(jnp.abs(x - v_lo) <= jnp.abs(x - v_hi), v_lo, v_hi)

        def _mx_quantize(t, eps=1e-30):
            rows, K = t.shape
            blocks = t.reshape(rows, K // BLOCK_SIZE, BLOCK_SIZE)
            scales = jnp.maximum(jnp.max(jnp.abs(blocks), axis=-1) / FP6_E2M3_MAX, eps)
            q = _nearest_on_grid(blocks / scales[..., None], _GRID)
            return (q, scales)
        batch_shape = x.shape[:-1]
        in_features = x.shape[-1]
        x2 = x.astype(jnp.float32).reshape(-1, in_features)
        w2 = weight.astype(jnp.float32)
        xq, xs = _mx_quantize(x2)
        wq, ws = _mx_quantize(w2)
        xd = (xq * xs[..., None]).reshape(x2.shape)
        wd = (wq * ws[..., None]).reshape(w2.shape)
        out = xd @ wd.T + bias
        return out.reshape(*batch_shape, -1)

    def _L3_attn_ref(x, Wq, bq, Wk, bk, Wv, bv, Wo, bo):
        import jax, jax.numpy as jnp
        import numpy as np
        LAMBDA_0 = 1.0
        EPS = 1e-06
        B, T, D = x.shape
        H = Wq.shape[0]
        Q = jnp.einsum('btd,hd->bth', x, Wq) + bq
        K = jnp.einsum('btd,hd->bth', x, Wk) + bk
        V = jnp.einsum('btd,hd->bth', x, Wv) + bv
        A0 = jnp.broadcast_to(jnp.eye(H, dtype=jnp.float32) / LAMBDA_0, (B, H, H))
        M0 = jnp.zeros((B, H, H), jnp.float32)

        def step(carry, qkv):
            A, M = carry
            q, k, v = qkv
            s_t = jnp.sum(k * q, axis=-1, keepdims=True)
            u = k / (jnp.linalg.norm(k, axis=-1, keepdims=True) + EPS)
            Au = jnp.einsum('bij,bj->bi', A, u)
            denom = 1.0 + jnp.sum(u * Au, axis=-1, keepdims=True)
            A = A - jnp.einsum('bi,bj->bij', Au, Au) / denom[..., None]
            z = Au / denom
            alpha = s_t * z
            M = M + jnp.einsum('bi,bj->bij', v, alpha)
            o = jnp.einsum('bij,bj->bi', M, q)
            return ((A, M), o)
        qkv = (jnp.swapaxes(Q, 0, 1), jnp.swapaxes(K, 0, 1), jnp.swapaxes(V, 0, 1))
        _, O = jax.lax.scan(step, (A0, M0), qkv)
        O = jnp.swapaxes(O, 0, 1)
        return jnp.einsum('bth,dh->btd', O, Wo) + bo

    def _L3_ffn_ref(x, ln_gamma, ln_beta, gate_w, w1, w2):
        import jax, jax.numpy as jnp
        import numpy as np
        E = 8
        K = 2
        C = 128
        F = 256
        EPS = 1e-05
        B, T, Cc = x.shape
        xf = x.reshape(-1, Cc)
        mu = jnp.mean(xf, axis=-1, keepdims=True)
        var = jnp.var(xf, axis=-1, keepdims=True)
        rn = (xf - mu) * jax.lax.rsqrt(var + EPS) * ln_gamma + ln_beta
        logits = rn @ gate_w.T
        probs = jax.nn.softmax(logits, axis=-1)
        rw, sel = jax.lax.top_k(probs, K)
        comb = jnp.sum(jax.nn.one_hot(sel, E, dtype=xf.dtype) * rw[..., None], axis=1)
        h = jax.nn.gelu(jnp.einsum('nc,efc->enf', xf, w1), approximate=False)
        y = jnp.einsum('enf,ecf->enc', h, w2)
        out = jnp.einsum('enc,ne->nc', y, comb)
        return out.reshape(B, T, Cc)
    x = L0_attn_z
    xn = _layernorm(x, axis=-1)
    x = x + _L0_attn_ref(xn, L0_attn_ln_w, L0_attn_ln_b, L0_attn_W_qkv, L0_attn_b_qkv, L0_attn_W_proj, L0_attn_b_proj) + _L0_ffn_ref(xn, L0_ffn_wqkv, L0_ffn_q_scale, L0_ffn_k_scale, L0_ffn_wo, L0_ffn_ln_g, L0_ffn_ln_b, L0_ffn_w1, L0_ffn_b1, L0_ffn_w2, L0_ffn_b2)
    xn = _layernorm(x, axis=-1)
    x = x + _L1_attn_ref(xn, L1_attn_norm1_w, L1_attn_norm2_w, L1_attn_g_wq, L1_attn_g_kv_down, L1_attn_g_k_up, L1_attn_g_v_up, L1_attn_g_wo, L1_attn_l_wq, L1_attn_l_wk, L1_attn_l_wv, L1_attn_l_wo) + _L1_ffn_ref(xn, L1_ffn_Wr, L1_ffn_rb, L1_ffn_W1, L1_ffn_W2, L1_ffn_W3, L1_ffn_Ws1, L1_ffn_Ws2, L1_ffn_Ws3)
    xn = _layernorm(x, axis=-1)
    x = x + _L2_attn_ref(xn, L2_attn_W) + _L2_ffn_ref(xn, L2_ffn_weight, L2_ffn_bias)
    xn = _layernorm(x, axis=-1)
    x = x + _L3_attn_ref(xn, L3_attn_Wq, L3_attn_bq, L3_attn_Wk, L3_attn_bk, L3_attn_Wv, L3_attn_bv, L3_attn_Wo, L3_attn_bo) + _L3_ffn_ref(xn, L3_ffn_ln_gamma, L3_ffn_ln_beta, L3_ffn_gate_w, L3_ffn_w1, L3_ffn_w2)
    return x

_drawn_inputs = setup_inputs


def setup_inputs(seed=0):
    import zlib

    import numpy as np

    out = dict(_drawn_inputs(seed))
    spreads = {'L0_attn_ln_w': (1.0, 0.6),
     'L0_attn_ln_b': (0.0, 0.8),
     'L0_attn_b_qkv': (0.0, 0.445),
     'L0_attn_b_proj': (0.0, 0.1),
     'L0_ffn_q_scale': (1.0, 0.6),
     'L0_ffn_k_scale': (1.0, 0.6),
     'L0_ffn_ln_g': (1.0, 0.6),
     'L0_ffn_ln_b': (0.0, 0.8),
     'L0_ffn_b1': (0.0, 0.8),
     'L0_ffn_b2': (0.0, 0.1),
     'L1_attn_norm1_w': (1.0, 0.6),
     'L1_attn_norm2_w': (1.0, 0.6),
     'L1_ffn_rb': (0.0, 0.8),
     'L3_attn_bq': (0.0, 0.1),
     'L3_attn_bk': (0.0, 0.1),
     'L3_attn_bv': (0.0, 0.1),
     'L3_attn_bo': (0.0, 2.0)}
    factors = {'L0_attn_W_qkv': 8.0,
     'L0_attn_W_proj': 2.963,
     'L0_ffn_w1': 4.359,
     'L0_ffn_w2': 4.293,
     'L1_attn_g_wq': 8.0,
     'L1_attn_g_kv_down': 8.0,
     'L1_attn_g_k_up': 8.0,
     'L1_attn_g_v_up': 8.0,
     'L1_attn_g_wo': 8.0,
     'L1_attn_l_wq': 8.0,
     'L1_attn_l_wk': 8.0,
     'L1_attn_l_wv': 6.263,
     'L1_attn_l_wo': 6.574,
     'L1_ffn_Wr': 8.0,
     'L1_ffn_W1': 8.0,
     'L1_ffn_W2': 8.0,
     'L1_ffn_W3': 8.0,
     'L1_ffn_Ws1': 8.0,
     'L1_ffn_Ws2': 8.0,
     'L1_ffn_Ws3': 8.0,
     'L2_attn_W': 64.0,
     'L2_ffn_bias': 6.424,
     'L3_ffn_ln_gamma': 23.087,
     'L3_ffn_ln_beta': 30.459,
     'L3_ffn_gate_w': 8.0,
     'L3_ffn_w1': 8.0,
     'L3_ffn_w2': 8.0}
    for name, (base, spread) in spreads.items():
        noise = np.random.default_rng([zlib.crc32(name.encode()), seed]).standard_normal(out[name].shape)
        drawn = base * np.exp(spread * noise) if base else spread * noise
        out[name] = jnp.asarray(drawn.astype(out[name].dtype))
    for name, factor in factors.items():
        out[name] = (out[name] * factor).astype(out[name].dtype)
    return out
```

```python
from contextlib import ExitStack

import concourse.bass as bass
from concourse import mybir

F32 = mybir.dt.float32
U32 = mybir.dt.uint32
ALU = mybir.AluOpType
ACT = mybir.ActivationFunctionType
AX = mybir.AxisListType.X

P = 128
B, T = 4, 1024
NTOK = B * T
BLK = 512
NB = NTOK // BLK
HALVES = T // BLK
TILES = T // P


class Core:

    def __init__(self, nc, ctx, d):
        self.nc, self.ctx, self.d = nc, ctx, d
        self.sem, self.per = {}, {}
        self.xt = self.sb(ctx, "xt", [P, NTOK])
        self.xnt = self.sb(ctx, "xnt", [P, NTOK])
        self.ps = ctx.enter_context(nc.psum_tensor("ps", [P, 8, BLK], F32))
        self.mean_w = self.sb(ctx, "mean_w", [P, P])
        self.ident = self.sb(ctx, "ident", [P, P])
        self.eps5 = self.sb(ctx, "eps5", [P, 1])
        self.eps6 = self.sb(ctx, "eps6", [P, 1])

    def sb(self, ctx, name, shape, dt=F32):
        return ctx.enter_context(self.nc.sbuf_tensor(name, shape, dt))

    def signals(self, **per):
        for name, n in per.items():
            if name not in self.sem:
                self.sem[name] = self.nc.alloc_semaphore(name)
                self.per[name] = n
        return self.sem

    def retire(self, *prefixes):
        names = [n for n in self.sem if n.startswith(prefixes)]
        with self.nc.Block() as block:
            @block.gpsimd
            def _(pool):
                for n in names:
                    pool.sem_clear(self.sem[n])
        for n in names:
            self.nc.release_semaphore(self.sem.pop(n))
            del self.per[n]

    def up(self, name, it, i=0):
        return it * self.per[name] + (i + 1)


class Chain:

    def __init__(self, core, eng, name, per):
        core.signals(**{name: per})
        self.core, self.eng, self.name, self.n = core, eng, name, 0
        self.it = 0

    def start(self, it):
        self.it, self.n = it, 0

    def __call__(self, ins):
        ins.then_inc(self.core.sem[self.name], 1)
        self.eng.wait_ge(self.core.sem[self.name], self.core.up(self.name, self.it, self.n))
        self.n += 1

    def close(self):
        assert self.n == self.core.per[self.name], (self.name, self.n)


def tokens(start, n):
    return bass.ds(start, n)


def load_phase(c):
    s = c.signals(load_in=1, load_const=1, load_set=1, load_ps=32, load_xt=32)
    nc, d = c.nc, c.d
    with ExitStack() as ctx:
        raw = c.sb(ctx, "load_raw", [P, NTOK // P, P])
        block = ctx.enter_context(nc.Block())

        @block.sync
        def _(sp):
            sp.dma_start(c.ident[:, :], d["c_ident"]).then_inc(s["load_const"], 16)
            z = d["z"].rearrange("b (n p) d -> p (b n) d", p=P)
            for i in range(4):
                sp.dma_start(raw[:, 8 * i:8 * i + 8, :], z[:, 8 * i:8 * i + 8, :]).then_inc(s["load_in"], 16)
            sp.wait_ge(s["load_const"], 16)
            sp.wait_ge(s["load_in"], 64)

        @block.vector
        def _(dve):
            nc.vector.memset(c.mean_w[:, :], 1.0 / P).then_inc(s["load_set"], 1)
            nc.vector.memset(c.eps5[:, :], 1e-5).then_inc(s["load_set"], 1)
            nc.vector.memset(c.eps6[:, :], 1e-6).then_inc(s["load_set"], 1)
            for n in range(8):
                dve.wait_ge(s["load_ps"], 4 * n + 4)
                nc.vector.tensor_copy(c.xt[:, n * BLK:(n + 1) * BLK], c.ps[:, n, :]).then_inc(s["load_xt"], 1)

        @block.tensor
        def _(pe):
            pe.wait_ge(s["load_const"], 16)
            pe.wait_ge(s["load_in"], 64)
            for n in range(32):
                nc.tensor.transpose(c.ps[:, n // 4, (n % 4) * P:(n % 4 + 1) * P], raw[:, n, :],
                                    c.ident[:, :]).then_inc(s["load_ps"], 1)


def norm_phase(c, run):
    s = c.signals(ln_mean=1, ln_xc=1, ln_sq=1, ln_var=1, ln_sd=1, ln_done=1)
    nc = c.nc
    with ExitStack() as ctx:
        xc = c.sb(ctx, f"ln{run}_xc", [P, BLK])
        sq = c.sb(ctx, f"ln{run}_sq", [P, BLK])
        sd = c.sb(ctx, f"ln{run}_sd", [P, BLK])
        block = ctx.enter_context(nc.Block())

        @block.tensor
        def _(pe):
            if run == 0:
                pe.sem_inc(s["ln_done"], 1)
            with pe.Fori(run * NB, (run + 1) * NB) as it:
                pe.wait_ge(s["ln_done"], it + 1)
                nc.tensor.matmul(c.ps[:, 0, :], c.mean_w[:, :], c.xt[:, tokens((it - run * NB) * BLK, BLK)],
                                 start=True, stop=True).then_inc(s["ln_mean"], 1)
                pe.wait_ge(s["ln_sq"], it + 1)
                nc.tensor.matmul(c.ps[:, 1, :], c.mean_w[:, :], sq[:, :],
                                 start=True, stop=True).then_inc(s["ln_var"], 1)

        @block.scalar
        def _(act):
            with act.Fori(run * NB, (run + 1) * NB) as it:
                act.wait_ge(s["ln_xc"], it + 1)
                nc.scalar.activation(sq[:, :], xc[:, :], ACT.Square).then_inc(s["ln_sq"], 1)
                act.wait_ge(s["ln_var"], it + 1)
                nc.scalar.activation(sd[:, :], c.ps[:, 1, :], ACT.Sqrt, bias=c.eps5[:, 0:1]).then_inc(s["ln_sd"], 1)

        @block.vector
        def _(dve):
            link = Chain(c, dve, "ln_dve", 1)
            with dve.Fori(run * NB, (run + 1) * NB) as it:
                link.start(it)
                here = tokens((it - run * NB) * BLK, BLK)
                dve.wait_ge(s["ln_mean"], it + 1)
                nc.vector.tensor_tensor(xc[:, :], c.xt[:, here], c.ps[:, 0, :], ALU.subtract).then_inc(s["ln_xc"], 1)
                dve.wait_ge(s["ln_sd"], it + 1)
                link(nc.vector.reciprocal(sd[:, :], sd[:, :]))
                nc.vector.tensor_tensor(c.xnt[:, here], xc[:, :], sd[:, :], ALU.mult).then_inc(s["ln_done"], 1)
            link.close()


def store_phase(c):
    s = c.signals(store_ps=8, store_sb=8, store_out=1)
    nc = c.nc
    with ExitStack() as ctx:
        rows = c.sb(ctx, "store_rows", [P, NTOK // P, P])
        block = ctx.enter_context(nc.Block())

        @block.tensor
        def _(pe):
            for n in range(8):
                for i in range(4):
                    t = 4 * n + i
                    last = nc.tensor.transpose(c.ps[:, n, i * P:(i + 1) * P], c.xt[:, t * P:(t + 1) * P],
                                               c.ident[:, :])
                last.then_inc(s["store_ps"], 1)

        @block.vector
        def _(dve):
            for n in range(8):
                dve.wait_ge(s["store_ps"], n + 1)
                nc.vector.tensor_copy(rows[:, 4 * n:4 * n + 4, :],
                                      c.ps[:, n, :].rearrange("p (i d) -> p i d", i=4)).then_inc(s["store_sb"], 1)

        @block.sync
        def _(sp):
            out = c.d["out"].rearrange("b (n p) d -> p (b n) d", p=P)
            for n in range(8):
                sp.wait_ge(s["store_sb"], n + 1)
                sp.dma_start(out[:, 4 * n:4 * n + 4, :], rows[:, 4 * n:4 * n + 4, :]).then_inc(s["store_out"], 16)
            sp.wait_ge(s["store_out"], 16 * 8)


G0, J0, HD0 = 4, 4, 8


def full_attention_phase(c):
    units = G0 * HALVES * J0 * TILES
    s = c.signals(fa_w=1, fa_set=1, fa_mean=2, fa_xc=2, fa_sq=2, fa_var=2, fa_sd=2, fa_zn=2,
                  fa_qk_ps=16, fa_qk=16, fa_v_ps=8, fa_v=8, fa_s_ps=128, fa_max=128, fa_m_ps=8, fa_q=8,
                  fa_st=units, fa_exp=units, fa_av=units, fa_o=8, fa_sum_ps=8, fa_ot=8, fa_y_ps=2, fa_done=1)
    nc, d, up = c.nc, c.d, c.up
    scale = float(HD0) ** -0.5
    with ExitStack() as ctx:
        wq = c.sb(ctx, "fa_wq", [P, G0, P])
        wk = c.sb(ctx, "fa_wk", [P, G0, P])
        wv = c.sb(ctx, "fa_wv", [P, P])
        wp = c.sb(ctx, "fa_wp", [P, G0, P])
        bq = c.sb(ctx, "fa_bq", [P, G0])
        bk = c.sb(ctx, "fa_bk", [P, G0])
        bv = c.sb(ctx, "fa_bv", [P, P])
        cols = c.sb(ctx, "fa_cols", [P, 3])
        row8 = c.sb(ctx, "fa_row8", [P, P])
        znt = c.sb(ctx, "fa_znt", [P, T])
        tmp = c.sb(ctx, "fa_tmp", [P, 3, BLK])
        qt = c.sb(ctx, "fa_qt", [P, G0, T])
        kt = c.sb(ctx, "fa_kt", [P, G0, T])
        mx = c.sb(ctx, "fa_mx", [P, TILES, G0, P])
        v = c.sb(ctx, "fa_vt", [P, TILES, 16, 32])
        pt = c.sb(ctx, "fa_pt", [P, 3, BLK])
        os = c.sb(ctx, "fa_os", [P, 2, BLK])
        rs = c.sb(ctx, "fa_rs", [P, 2, BLK])
        ot = c.sb(ctx, "fa_otb", [P, G0, T])
        block = ctx.enter_context(nc.Block())
        ps = c.ps

        @block.sync
        def _(sp):
            loads = [(wq[:, :, :], "fa_wq"), (wk[:, :, :], "fa_wk"), (wv[:, :], "fa_wv"), (wp[:, :, :], "fa_wp"),
                     (bq[:, :], "fa_bq"), (bk[:, :], "fa_bk"), (bv[:, :], "fa_bv"), (cols[:, :], "fa_cols"),
                     (row8[:, :], "c_row8")]
            for dst, name in loads:
                sp.dma_start(dst, d[name]).then_inc(s["fa_w"], 16)
            sp.wait_ge(s["fa_w"], 16 * 9)

        @block.gpsimd
        def _(pool):
            nc.gpsimd.memset(mx[:, :, :, :], 0.0).then_inc(s["fa_set"], 1)
            nc.gpsimd.memset(v[:, :, :, :], 0.0).then_inc(s["fa_set"], 1)
            pool.wait_ge(s["fa_set"], 2)
            nc.gpsimd.memset(v[:, :, :, 8:9], 1.0).then_inc(s["fa_set"], 1)

        @block.tensor
        def _(pe):
            pe.wait_ge(s["fa_w"], 16 * 9)
            pe.sem_inc(s["fa_done"], 1)
            with pe.Fori(0, B) as it:
                pe.wait_ge(s["fa_done"], it + 1)
                for i in range(HALVES):
                    if i:
                        pe.wait_ge(s["fa_zn"], up("fa_zn", it, i - 1))
                    nc.tensor.matmul(ps[:, 0, :], c.mean_w[:, :], c.xnt[:, tokens(it * T + i * BLK, BLK)],
                                     start=True, stop=True).then_inc(s["fa_mean"], 1)
                    pe.wait_ge(s["fa_sq"], up("fa_sq", it, i))
                    nc.tensor.matmul(ps[:, 1, :], c.mean_w[:, :], tmp[:, 1, :],
                                     start=True, stop=True).then_inc(s["fa_var"], 1)
                pe.wait_ge(s["fa_zn"], up("fa_zn", it, 1))
                for n in range(16):
                    w, g, i = (wq, wk)[n // 8], n % 8 // 2, n % 2
                    if n >= 2:
                        pe.wait_ge(s["fa_qk"], up("fa_qk", it, n - 2))
                    nc.tensor.matmul(ps[:, n % 2, :], w[:, g, :], znt[:, i * BLK:(i + 1) * BLK],
                                     start=True, stop=True).then_inc(s["fa_qk_ps"], 1)
                for t in range(TILES):
                    if t >= 2:
                        pe.wait_ge(s["fa_v"], up("fa_v", it, t - 2))
                    nc.tensor.matmul(ps[:, 2 + t % 2, 0:P], znt[:, t * P:(t + 1) * P], wv[:, :],
                                     start=True, stop=True).then_inc(s["fa_v_ps"], 1)
                pe.wait_ge(s["fa_qk"], up("fa_qk", it, 15))
                pe.wait_ge(s["fa_v"], up("fa_v", it, 7))
                for g in range(G0):
                    for u in range(J0 * TILES):
                        n, j, t = g * J0 * TILES + u, u // TILES, u % TILES
                        rows = slice(32 * j, 32 * j + HD0)
                        if n >= 3:
                            pe.wait_ge(s["fa_max"], up("fa_max", it, n - 3))
                        for i in range(HALVES):
                            last = nc.tensor.matmul(ps[:, 2 * (n % 3) + i, :], qt[rows, g, t * P:(t + 1) * P],
                                                    kt[rows, g, i * BLK:(i + 1) * BLK], start=True, stop=True,
                                                    tile_position=(32 * j, 0))
                        last.then_inc(s["fa_s_ps"], 1)
                    for i in range(HALVES):
                        n = g * HALVES + i
                        pe.wait_ge(s["fa_max"], up("fa_max", it, (g + 1) * J0 * TILES - 1))
                        if n >= 2:
                            pe.wait_ge(s["fa_q"], up("fa_q", it, n - 2))
                        for t in range(4):
                            last = nc.tensor.transpose(ps[:, 6 + i, t * P:(t + 1) * P], mx[:, 4 * i + t, g, :],
                                                       c.ident[:, :])
                        last.then_inc(s["fa_m_ps"], 1)
                pe.wait_ge(s["fa_q"], up("fa_q", it, 7))

                def scores(n):
                    g, i, j, t = n // 64, n // 32 % 2, n // 8 % 4, n % 8
                    rows = slice(32 * j, 32 * j + HD0 + 1)
                    if n >= 3:
                        pe.wait_ge(s["fa_exp"], up("fa_exp", it, n - 3))
                    nc.tensor.matmul(ps[:, n % 3, :], kt[rows, g, t * P:(t + 1) * P],
                                     qt[rows, g, i * BLK:(i + 1) * BLK], start=True, stop=True,
                                     tile_position=(32 * j, 0)).then_inc(s["fa_st"], 1)

                def values(n):
                    g, i, j, t = n // 64, n // 32 % 2, n // 8 % 4, n % 8
                    m = n // 32
                    if n % 32 == 0 and m >= 2:
                        pe.wait_ge(s["fa_o"], up("fa_o", it, m - 2))
                    pe.wait_ge(s["fa_exp"], up("fa_exp", it, n))
                    nc.tensor.matmul(ps[32 * j:32 * j + 32, 3 + m % 2, :], v[:, t, 4 * g + j, :], pt[:, n % 3, :],
                                     start=(t == 0), stop=(t == TILES - 1),
                                     tile_position=(0, 32 * j)).then_inc(s["fa_av"], 1)

                def sums(m):
                    pe.wait_ge(s["fa_o"], up("fa_o", it, m))
                    if m:
                        pe.wait_ge(s["fa_ot"], up("fa_ot", it, m - 1))
                    nc.tensor.matmul(ps[:, 5, :], row8[:, :], os[:, m % 2, :],
                                     start=True, stop=True).then_inc(s["fa_sum_ps"], 1)

                for n in range(units + 2):
                    if n < units:
                        scores(n)
                    if n >= 2:
                        values(n - 2)
                    if n >= 40 and n % 32 == 8:
                        sums(n // 32 - 1)
                sums(7)
                pe.wait_ge(s["fa_ot"], up("fa_ot", it, 7))
                for i in range(HALVES):
                    for g in range(G0):
                        last = nc.tensor.matmul(ps[:, 6 + i, :], wp[:, g, :], ot[:, g, i * BLK:(i + 1) * BLK],
                                                start=(g == 0), stop=(g == G0 - 1))
                    last.then_inc(s["fa_y_ps"], 1)

        @block.scalar
        def _(act):
            act.wait_ge(s["fa_w"], 16 * 9)
            with act.Fori(0, B) as it:
                for i in range(HALVES):
                    act.wait_ge(s["fa_xc"], up("fa_xc", it, i))
                    nc.scalar.activation(tmp[:, 1, :], tmp[:, 0, :], ACT.Square).then_inc(s["fa_sq"], 1)
                    act.wait_ge(s["fa_var"], up("fa_var", it, i))
                    nc.scalar.activation(tmp[:, 2, :], ps[:, 1, :], ACT.Sqrt,
                                         bias=c.eps5[:, 0:1]).then_inc(s["fa_sd"], 1)
                for n in range(16):
                    dst, bias, g, i = (qt, kt)[n // 8], (bq, bk)[n // 8], n % 8 // 2, n % 2
                    act.wait_ge(s["fa_qk_ps"], up("fa_qk_ps", it, n))
                    nc.scalar.activation(dst[:, g, i * BLK:(i + 1) * BLK], ps[:, n % 2, :], ACT.Identity,
                                         bias=bias[:, g:g + 1]).then_inc(s["fa_qk"], 1)
                for n in range(units + 3):
                    if n < units:
                        act.wait_ge(s["fa_st"], up("fa_st", it, n))
                        if n >= 3:
                            act.wait_ge(s["fa_av"], up("fa_av", it, n - 3))
                        nc.scalar.activation(pt[:, n % 3, :], ps[:, n % 3, :], ACT.Exp,
                                             scale=scale).then_inc(s["fa_exp"], 1)
                    if n >= 32 and n % 32 == 2 or n == units + 2:
                        m = (n - 2) // 32 - 1
                        act.wait_ge(s["fa_av"], up("fa_av", it, 32 * m + 31))
                        if m >= 2:
                            act.wait_ge(s["fa_ot"], up("fa_ot", it, m - 2))
                        nc.scalar.activation(os[:, m % 2, :], ps[:, 3 + m % 2, :], ACT.Copy).then_inc(s["fa_o"], 1)

        @block.vector
        def _(dve):
            link = Chain(c, dve, "fa_dve", 2 * 2 + 8 + 2)
            dve.wait_ge(s["fa_w"], 16 * 9)
            dve.wait_ge(s["fa_set"], 3)
            with dve.Fori(0, B) as it:
                link.start(it)
                for i in range(HALVES):
                    dve.wait_ge(s["fa_mean"], up("fa_mean", it, i))
                    nc.vector.tensor_tensor(tmp[:, 0, :], c.xnt[:, tokens(it * T + i * BLK, BLK)], ps[:, 0, :],
                                            ALU.subtract).then_inc(s["fa_xc"], 1)
                    dve.wait_ge(s["fa_sd"], up("fa_sd", it, i))
                    link(nc.vector.reciprocal(tmp[:, 2, :], tmp[:, 2, :]))
                    link(nc.vector.tensor_tensor(tmp[:, 1, :], tmp[:, 0, :], tmp[:, 2, :], ALU.mult))
                    nc.vector.tensor_scalar(znt[:, i * BLK:(i + 1) * BLK], tmp[:, 1, :], cols[:, 0:1], cols[:, 1:2],
                                            ALU.mult, ALU.add).then_inc(s["fa_zn"], 1)
                for t in range(TILES):
                    dve.wait_ge(s["fa_v_ps"], up("fa_v_ps", it, t))
                    nc.vector.tensor_tensor(v[:, t, :, 0:8],
                                            ps[:, 2 + t % 2, 0:P].rearrange("p (h e) -> p h e", e=8),
                                            bv[:, :].rearrange("p (h e) -> p h e", e=8),
                                            ALU.add).then_inc(s["fa_v"], 1)
                for g in range(G0):
                    for u in range(J0 * TILES):
                        n, j, t = g * J0 * TILES + u, u // TILES, u % TILES
                        dve.wait_ge(s["fa_s_ps"], up("fa_s_ps", it, n))
                        b0 = 2 * (n % 3)
                        nc.vector.tensor_reduce(mx[:, t, g, 32 * j + 8:32 * j + 9], ps[:, b0:b0 + 2, :],
                                                mybir.AxisListType.XY, ALU.max, negate=True).then_inc(s["fa_max"], 1)
                    for i in range(HALVES):
                        dve.wait_ge(s["fa_m_ps"], up("fa_m_ps", it, g * HALVES + i))
                        here = qt[:, g, i * BLK:(i + 1) * BLK]
                        nc.vector.tensor_tensor(here, here, ps[:, 6 + i, :], ALU.add).then_inc(s["fa_q"], 1)
                for m in range(8):
                    g, i = m // 2, m % 2
                    dve.wait_ge(s["fa_sum_ps"], up("fa_sum_ps", it, m))
                    link(nc.vector.reciprocal(rs[:, m % 2, :], ps[:, 5, :]))
                    nc.vector.tensor_tensor(ot[:, g, i * BLK:(i + 1) * BLK], os[:, m % 2, :], rs[:, m % 2, :],
                                            ALU.mult).then_inc(s["fa_ot"], 1)
                for i in range(HALVES):
                    here = tokens(it * T + i * BLK, BLK)
                    dve.wait_ge(s["fa_y_ps"], up("fa_y_ps", it, i))
                    link(nc.vector.scalar_tensor_tensor(tmp[:, i, :], ps[:, 6 + i, :], cols[:, 2:3],
                                                        c.xnt[:, here], ALU.add, ALU.add))
                    ins = nc.vector.tensor_tensor(c.xt[:, here], c.xt[:, here], tmp[:, i, :], ALU.add)
                    if i == HALVES - 1:
                        ins.then_inc(s["fa_done"], 1)
            link.close()


HD1, NPAIR = 64, 4
HID = 341
CHUNKS = [(0, 128), (128, 128), (256, HID - 256)]


def shifted_copy(nc, c, dst, start, link, last):
    link(nc.vector.tensor_scalar(dst[0:64, :], c.xnt[0:64, tokens(start, T)], 1.0, None, ALU.mult))
    nc.vector.tensor_scalar(dst[64:P, 1:T], c.xnt[64:P, tokens(start, T - 1)], 1.0, None, ALU.mult).then_inc(last, 1)


def window_phase(c, run):
    QK, U = 16, 2 * TILES
    s = c.signals(wa_w=1, wa_set=1, wa_h=1, wa_qk_ps=QK, wa_sq=QK, wa_ss=QK, wa_sd=QK, wa_rot=QK, wa_qk=QK,
                  wa_v_ps=TILES, wa_v=TILES, wa_s_ps=U, wa_sm=U, wa_nmx=U, wa_exp=U, wa_p=U, wa_t_ps=U, wa_t=U,
                  wa_o_ps=U, wa_o=U, wa_y_ps=TILES, wa_y=TILES,
                  wm_h=1, wm_mean=2, wm_xc=2, wm_sq=2, wm_var=2, wm_sd=2, wm_n=2, wm_ag=6, wm_gelu=6, wm_hg=6,
                  wm_y_ps=2, wm_y=2, wa_done=1)
    nc, d, up = c.nc, c.d, c.up
    ps = c.ps
    NW = 16
    with ExitStack() as ctx:
        name = lambda n: f"wa{run}_{n}"
        sb = lambda n, shape: c.sb(ctx, name(n), shape)
        wqk = sb("wqk", [P, 2, BLK])
        wsw = sb("wsw", [P, 2, BLK])
        wv = sb("wv", [P, BLK])
        wo = sb("wo", [P, NPAIR, P])
        w1 = sb("w1", [P, 2 * HID])
        w2 = sb("w2", [P, 3, P])
        qks = sb("qks", [P, 4])
        lnc = sb("lnc", [P, 3])
        b1 = sb("b1", [P, 3, 2])
        tab = sb("tab", [P, 4, T])
        band = sb("band", [P, 2, 2 * P])
        blk = sb("blk", [P, P])
        h = sb("h", [P, T])
        sq = sb("sq", [P, 2, BLK])
        sd = sb("sd", [P, 2, BLK])
        rot = sb("rot", [P, 2, BLK])
        qt = sb("qt", [P, NPAIR, P + T])
        kt = sb("kt", [P, NPAIR, P + T])
        v = sb("v", [P, 1 + TILES, BLK])
        sm = sb("sm", [P, 2, 4, 2 * P])
        nmx = sb("nmx", [P, 2, 4])
        tot = sb("tot", [P, 2, 4])
        pt = sb("pt", [P, 4, 2, P])
        ot = sb("ot", [P, 2, NPAIR, P])
        hg = sb("hg", [P, 3, BLK])
        block = ctx.enter_context(nc.Block())
        ITS = (run * B, (run + 1) * B)

        @block.sync
        def _(sp):
            loads = [(wqk[:, :, :], d["wa_wqk"][run]), (wsw[:, :, :], d["wa_wsw"][run]), (wv[:, :], d["wa_wv"][run]),
                     (wo[:, :, :], d["wa_wo"][run]), (w1[:, :], d["wa_w1"][run]), (w2[:, :, :], d["wa_w2"][run]),
                     (qks[:, :], d["wa_qks"][run]),
                     (lnc[:, :], d["wa_lnc"][run]), (b1[:, :, :], d["wa_b1"][run]),
                     (tab[:, :, :], d["c_tab"]),
                     (band[:, :, :], d["c_band"]), (blk[:, :], d["c_blk64"])]
            for dst, src in loads:
                sp.dma_start(dst, src).then_inc(s["wa_w"], 16)
            sp.wait_ge(s["wa_w"], 16 * 12 * (run + 1))

        @block.tensor
        def _(pe):
            pe.wait_ge(s["wa_w"], 16 * 12 * (run + 1))
            pe.wait_ge(s["wa_set"], 3 * (run + 1))
            with pe.Fori(*ITS) as it:
                pe.wait_ge(s["wa_h"], up("wa_h", it))

                def square_sums(n):
                    pe.wait_ge(s["wa_sq"], up("wa_sq", it, n))
                    nc.tensor.matmul(ps[:, 4 + n % 2, :], blk[:, :], sq[:, n % 2, :],
                                     start=True, stop=True).then_inc(s["wa_ss"], 1)

                for n in range(QK):
                    x, p, i = n // 8, n % 8 // 2, n % 2
                    if n >= 2:
                        pe.wait_ge(s["wa_rot"], up("wa_rot", it, n - 2))
                    nc.tensor.matmul(ps[:, n % 2, :], wqk[:, x, p * P:(p + 1) * P], h[:, i * BLK:(i + 1) * BLK],
                                     start=True, stop=True)
                    nc.tensor.matmul(ps[:, 2 + n % 2, :], wsw[:, x, p * P:(p + 1) * P], h[:, i * BLK:(i + 1) * BLK],
                                     start=True, stop=True).then_inc(s["wa_qk_ps"], 1)
                    if n:
                        square_sums(n - 1)
                square_sums(QK - 1)
                for t in range(TILES):
                    if t >= 2:
                        pe.wait_ge(s["wa_v"], up("wa_v", it, t - 2))
                    nc.tensor.matmul(ps[:, 6 + t % 2, :], h[:, t * P:(t + 1) * P], wv[:, :],
                                     start=True, stop=True).then_inc(s["wa_v_ps"], 1)
                pe.wait_ge(s["wa_qk"], up("wa_qk", it, QK - 1))
                pe.wait_ge(s["wa_v"], up("wa_v", it, TILES - 1))

                def scores(u):
                    t, hh = u // 2, u % 2
                    if u >= 2:
                        pe.wait_ge(s["wa_sm"], up("wa_sm", it, u - 2))
                    for k in range(4):
                        p, j = 2 * hh + k % 2, k // 2
                        rows = slice(64 * j, 64 * j + 64)
                        last = nc.tensor.matmul(ps[:, 2 * (u % 2) + k // 2, (k % 2) * 2 * P:(k % 2 + 1) * 2 * P],
                                                qt[rows, p, t * P:(t + 1) * P], kt[rows, p, t * P:(t + 2) * P],
                                                start=True, stop=True, tile_position=(64 * j, 0))
                    last.then_inc(s["wa_s_ps"], 1)

                def turn(u):
                    if u:
                        pe.wait_ge(s["wa_t"], up("wa_t", it, u - 1))
                    pe.wait_ge(s["wa_p"], up("wa_p", it, u))
                    for k in range(8):
                        last = nc.tensor.transpose(ps[:, 4 + k // 4, (k % 4) * P:(k % 4 + 1) * P],
                                                   sm[:, u % 2, k // 2, (k % 2) * P:(k % 2 + 1) * P], c.ident[:, :])
                    last.then_inc(s["wa_t_ps"], 1)

                def values(u):
                    t, hh = u // 2, u % 2
                    if u:
                        pe.wait_ge(s["wa_o"], up("wa_o", it, u - 1))
                    pe.wait_ge(s["wa_t"], up("wa_t", it, u))
                    for k in range(4):
                        p, j = 2 * hh + k % 2, k // 2
                        head = 2 * p + j
                        for e in range(2):
                            last = nc.tensor.matmul(ps[64 * j:64 * j + 64, 6, (k % 2) * P:(k % 2 + 1) * P],
                                                    v[:, t + e, head * 64:head * 64 + 64], pt[:, k, e, :],
                                                    start=(e == 0), stop=(e == 1), tile_position=(0, 64 * j))
                    last.then_inc(s["wa_o_ps"], 1)

                def project(t):
                    if t:
                        pe.wait_ge(s["wa_y"], up("wa_y", it, t - 1))
                    pe.wait_ge(s["wa_o"], up("wa_o", it, 2 * t + 1))
                    for p in range(NPAIR):
                        last = nc.tensor.matmul(ps[:, 7, 0:P], wo[:, p, :], ot[:, t % 2, p, :],
                                                start=(p == 0), stop=(p == NPAIR - 1))
                    last.then_inc(s["wa_y_ps"], 1)

                scores(0)
                for u in range(U):
                    if u + 1 < U:
                        scores(u + 1)
                    turn(u)
                    values(u)
                    if u % 2 == 0 and u >= 2:
                        project(u // 2 - 1)
                project(TILES - 1)
                pe.wait_ge(s["wm_h"], up("wm_h", it))
                for i in range(HALVES):
                    if i:
                        pe.wait_ge(s["wm_n"], up("wm_n", it, i - 1))
                    nc.tensor.matmul(ps[:, 0, :], c.mean_w[:, :], h[:, i * BLK:(i + 1) * BLK],
                                     start=True, stop=True).then_inc(s["wm_mean"], 1)
                    pe.wait_ge(s["wm_sq"], up("wm_sq", it, i))
                    nc.tensor.matmul(ps[:, 1, :], c.mean_w[:, :], sq[:, 0, :],
                                     start=True, stop=True).then_inc(s["wm_var"], 1)
                    pe.wait_ge(s["wm_n"], up("wm_n", it, i))
                    for k, (r0, r) in enumerate(CHUNKS):
                        n = 3 * i + k
                        if n >= 2:
                            pe.wait_ge(s["wm_hg"], up("wm_hg", it, n - 2))
                        nc.tensor.matmul(ps[0:r, 2 + n % 2, :], w1[:, r0:r0 + r], rot[:, i, :],
                                         start=True, stop=True)
                        nc.tensor.matmul(ps[0:r, 4 + n % 2, :], w1[:, HID + r0:HID + r0 + r], rot[:, i, :],
                                         start=True, stop=True).then_inc(s["wm_ag"], 1)
                    for k, (r0, r) in enumerate(CHUNKS):
                        pe.wait_ge(s["wm_hg"], up("wm_hg", it, 3 * i + k))
                        last = nc.tensor.matmul(ps[:, 6 + i, :], w2[0:r, k, :], hg[0:r, k, :],
                                                start=(k == 0), stop=(k == 2))
                    last.then_inc(s["wm_y_ps"], 1)

        @block.scalar
        def _(act):
            act.wait_ge(s["wa_w"], 16 * 12 * (run + 1))
            with act.Fori(*ITS) as it:

                def root(n):
                    act.wait_ge(s["wa_ss"], up("wa_ss", it, n))
                    if n >= 2:
                        act.wait_ge(s["wa_qk"], up("wa_qk", it, n - 2))
                    nc.scalar.activation(sd[:, n % 2, :], ps[:, 4 + n % 2, :], ACT.Sqrt).then_inc(s["wa_sd"], 1)

                for n in range(QK):
                    act.wait_ge(s["wa_qk_ps"], up("wa_qk_ps", it, n))
                    nc.scalar.activation(sq[:, n % 2, :], ps[:, n % 2, :], ACT.Square).then_inc(s["wa_sq"], 1)
                    if n:
                        root(n - 1)
                root(QK - 1)
                for t in range(TILES):
                    act.wait_ge(s["wa_v_ps"], up("wa_v_ps", it, t))
                    nc.scalar.activation(v[:, 1 + t, :], ps[:, 6 + t % 2, :], ACT.Copy).then_inc(s["wa_v"], 1)
                for u in range(U):
                    act.wait_ge(s["wa_nmx"], up("wa_nmx", it, u))
                    for k in range(4):
                        ins = nc.scalar.activation(sm[:, u % 2, k, :], sm[:, u % 2, k, :], ACT.Exp, scale=8.0,
                                                   bias=nmx[:, u % 2, k:k + 1], accum_out=tot[:, u % 2, k:k + 1])
                    ins.then_inc(s["wa_exp"], 1)
                    act.wait_ge(s["wa_t_ps"], up("wa_t_ps", it, u))
                    if u:
                        act.wait_ge(s["wa_o_ps"], up("wa_o_ps", it, u - 1))
                    nc.scalar.activation(pt[:, :, :, :].rearrange("p a b q -> p (a b q)"),
                                         ps[:, 4:6, :].rearrange("p a q -> p (a q)"),
                                         ACT.Copy).then_inc(s["wa_t"], 1)
                    act.wait_ge(s["wa_o_ps"], up("wa_o_ps", it, u))
                    t, hh = u // 2, u % 2
                    if t >= 2:
                        act.wait_ge(s["wa_y_ps"], up("wa_y_ps", it, t - 2))
                    nc.scalar.activation(ot[:, t % 2, 2 * hh:2 * hh + 2, :],
                                         ps[:, 6, 0:2 * P].rearrange("p (a q) -> p a q", a=2),
                                         ACT.Copy).then_inc(s["wa_o"], 1)
                for i in range(HALVES):
                    act.wait_ge(s["wm_xc"], up("wm_xc", it, i))
                    nc.scalar.activation(sq[:, 0, :], sd[:, 1, :], ACT.Square).then_inc(s["wm_sq"], 1)
                    act.wait_ge(s["wm_var"], up("wm_var", it, i))
                    nc.scalar.activation(sd[:, 0, :], ps[:, 1, :], ACT.Sqrt,
                                         bias=c.eps5[:, 0:1]).then_inc(s["wm_sd"], 1)
                    for k, (r0, r) in enumerate(CHUNKS):
                        n = 3 * i + k
                        act.wait_ge(s["wm_ag"], up("wm_ag", it, n))
                        if n >= 3:
                            act.wait_ge(s["wm_y_ps"], up("wm_y_ps", it, n // 3 - 1))
                        nc.scalar.activation(hg[0:r, k, :], ps[0:r, 4 + n % 2, :], ACT.Gelu,
                                             bias=b1[0:r, k, 1:2]).then_inc(s["wm_gelu"], 1)

        @block.vector
        def _(dve):
            link = Chain(c, dve, "wa_dve", 4 * QK + 2 * U + 2 + HALVES * 3)
            dve.wait_ge(s["wa_w"], 16 * 12 * (run + 1))
            nc.vector.memset(h[64:P, 0:1], 0.0).then_inc(s["wa_set"], 1)
            nc.vector.memset(kt[:, :, 0:P], 0.0).then_inc(s["wa_set"], 1)
            nc.vector.memset(v[:, 0, :], 0.0).then_inc(s["wa_set"], 1)
            if run == 0:
                dve.sem_inc(s["wa_done"], 1)
            with dve.Fori(*ITS) as it:
                link.start(it)
                base = (it - run * B) * T
                dve.wait_ge(s["wa_done"], it + 1)
                shifted_copy(nc, c, h, base, link, s["wa_h"])
                for n in range(QK):
                    x, p, i = n // 8, n % 8 // 2, n % 2
                    half = slice(i * BLK, (i + 1) * BLK)
                    dve.wait_ge(s["wa_sq"], up("wa_sq", it, n))
                    if n:
                        dve.wait_ge(s["wa_qk"], up("wa_qk", it, n - 1))
                    link(nc.vector.scalar_tensor_tensor(rot[:, 0, :], ps[:, n % 2, :], qks[:, 2 * x:2 * x + 1],
                                                        tab[:, 2 * x, half], ALU.mult, ALU.mult))
                    nc.vector.scalar_tensor_tensor(rot[:, 1, :], ps[:, 2 + n % 2, :], qks[:, 2 * x + 1:2 * x + 2],
                                                   tab[:, 2 * x + 1, half], ALU.mult, ALU.mult).then_inc(s["wa_rot"], 1)
                    dve.wait_ge(s["wa_rot"], up("wa_rot", it, n))
                    link(nc.vector.tensor_tensor(rot[:, 0, :], rot[:, 0, :], rot[:, 1, :], ALU.add))
                    dve.wait_ge(s["wa_sd"], up("wa_sd", it, n))
                    link(nc.vector.tensor_scalar(sd[:, n % 2, :], sd[:, n % 2, :], 1e-12, None, ALU.max))
                    link(nc.vector.reciprocal(sd[:, n % 2, :], sd[:, n % 2, :]))
                    off = 0 if x == 0 else P
                    nc.vector.tensor_tensor((qt, kt)[x][:, p, off + i * BLK:off + (i + 1) * BLK], rot[:, 0, :],
                                            sd[:, n % 2, :], ALU.mult).then_inc(s["wa_qk"], 1)

                def mask(u):
                    dve.wait_ge(s["wa_s_ps"], up("wa_s_ps", it, u))
                    if u >= 2:
                        dve.wait_ge(s["wa_t_ps"], up("wa_t_ps", it, u - 2))
                    first = 0 if u < 2 else 1
                    nc.vector.tensor_tensor(sm[:, u % 2, :, :],
                                            ps[:, 2 * (u % 2):2 * (u % 2) + 2, :].rearrange("p a (b k) -> p (a b) k", b=2),
                                            band[:, first:first + 1, :].to_broadcast([P, 4, 2 * P]),
                                            ALU.add).then_inc(s["wa_sm"], 1)
                    dve.wait_ge(s["wa_sm"], up("wa_sm", it, u))
                    link(nc.vector.tensor_reduce(nmx[:, u % 2, :], sm[:, u % 2, :, :], AX, ALU.max, negate=True))
                    nc.vector.tensor_scalar(nmx[:, u % 2, :], nmx[:, u % 2, :], 8.0, None,
                                            ALU.mult).then_inc(s["wa_nmx"], 1)

                def out_tile(t):
                    here = tokens(base + t * P, P)
                    dve.wait_ge(s["wa_y_ps"], up("wa_y_ps", it, t))
                    nc.vector.tensor_tensor(c.xnt[:, here], c.xnt[:, here], ps[:, 7, 0:P],
                                            ALU.add).then_inc(s["wa_y"], 1)

                mask(0)
                for u in range(U):
                    if u + 1 < U:
                        mask(u + 1)
                    dve.wait_ge(s["wa_exp"], up("wa_exp", it, u))
                    link(nc.vector.reciprocal(tot[:, u % 2, :], tot[:, u % 2, :]))
                    nc.vector.tensor_tensor(sm[:, u % 2, :, :], sm[:, u % 2, :, :],
                                            tot[:, u % 2, :].unsqueeze(2).to_broadcast([P, 4, 2 * P]),
                                            ALU.mult).then_inc(s["wa_p"], 1)
                    if u % 2 == 1 and u >= 3:
                        out_tile(u // 2 - 1)
                out_tile(TILES - 1)
                dve.wait_ge(s["wa_y"], up("wa_y", it, TILES - 1))
                shifted_copy(nc, c, h, base, link, s["wm_h"])
                for i in range(HALVES):
                    half = slice(i * BLK, (i + 1) * BLK)
                    here = tokens(base + i * BLK, BLK)
                    dve.wait_ge(s["wm_mean"], up("wm_mean", it, i))
                    nc.vector.tensor_tensor(sd[:, 1, :], h[:, half], ps[:, 0, :], ALU.subtract).then_inc(s["wm_xc"], 1)
                    dve.wait_ge(s["wm_sd"], up("wm_sd", it, i))
                    link(nc.vector.reciprocal(sd[:, 0, :], sd[:, 0, :]))
                    link(nc.vector.tensor_tensor(sq[:, 1, :], sd[:, 1, :], sd[:, 0, :], ALU.mult))
                    nc.vector.tensor_scalar(rot[:, i, :], sq[:, 1, :], lnc[:, 0:1], lnc[:, 1:2],
                                            ALU.mult, ALU.add).then_inc(s["wm_n"], 1)
                    for k, (r0, r) in enumerate(CHUNKS):
                        n = 3 * i + k
                        dve.wait_ge(s["wm_gelu"], up("wm_gelu", it, n))
                        nc.vector.scalar_tensor_tensor(hg[0:r, k, :], ps[0:r, 2 + n % 2, :], b1[0:r, k, 0:1],
                                                       hg[0:r, k, :], ALU.add, ALU.mult).then_inc(s["wm_hg"], 1)
                    dve.wait_ge(s["wm_y_ps"], up("wm_y_ps", it, i))
                    link(nc.vector.scalar_tensor_tensor(c.xnt[:, here], ps[:, 6 + i, :], lnc[:, 2:3],
                                                        c.xnt[:, here], ALU.add, ALU.add))
                    if run == 1:
                        last = nc.vector.tensor_tensor(c.xt[:, here], c.xt[:, here], c.xnt[:, here], ALU.add)
                if run == 1:
                    last.then_inc(s["wa_done"], 1)
                else:
                    dve.sem_inc(s["wa_done"], 1)
            link.close()


GQ, LAT = 4, 32


def grouped_attention_phase(c, run):
    units = []
    for t in range(TILES):
        for k in range(0 if run == 0 else max(t - 1, 0), t + 1):
            units += [(t, k, j, None if run == 0 and k < t else t - k) for j in range(4)]
    U = len(units)
    last_of = {t: max(n for n, x in enumerate(units) if x[0] == t) for t in range(TILES)}
    masked = [n for n, x in enumerate(units) if x[3] is not None]
    NQK = 10
    pre = f"ga{run}_"
    counts = dict(w=1, set=1, sq=2, ms=2, sd=2, h=2, lat_ps=2, lat=2, qk_ps=NQK, rot=NQK, qsq=NQK, qms=NQK, qsd=NQK,
                  qk=NQK, v_ps=TILES, v=TILES, st=U, exp=U, mask=len(masked), av=U, o=TILES, sum_ps=TILES, ot=TILES,
                  y_ps=2, done=1)
    c.signals(**{pre + k: n for k, n in counts.items()})
    s = {k: c.sem[pre + k] for k in counts}
    up = lambda name, it, i=0: c.up(pre + name, it, i)
    nc, d, ps = c.nc, c.d, c.ps
    R = LAT if run == 0 else P
    NW = 10 if run == 0 else 9
    with ExitStack() as ctx:
        sb = lambda n, shape: c.sb(ctx, pre + "b_" + n, shape)
        wq = sb("wq", [P, 2, GQ, P])
        wk = sb("wk", [P, 2, P])
        wv = sb("wv", [P, 32])
        wd = sb("wd", [P, LAT])
        wo = sb("wo", [P, GQ, P])
        nw = sb("nw", [P, 1])
        tab = sb("tab", [P, 2, T])
        msk = sb("msk", [P, 2, P])
        row8 = sb("row8", [P, P])
        m8 = sb("m8", [P, P])
        h = sb("h", [P, T])
        lat = sb("lat", [P, T])
        sq = sb("sq", [P, 2, BLK])
        sd = sb("sd", [P, 2, BLK])
        rot = sb("rot", [P, 2, 2, BLK])
        qt = sb("qt", [P, GQ, T])
        kt = sb("kt", [P, T])
        v = sb("v", [P, TILES, 4, 32])
        pt = sb("pt", [P, 3, BLK])
        os = sb("os", [P, 2, BLK])
        rs = sb("rs", [P, 2, BLK])
        ot = sb("ot", [P, GQ, T])
        src = lat if run == 0 else h
        block = ctx.enter_context(nc.Block())

        @block.sync
        def _(sp):
            loads = [(wq[:, :, :, :], d[pre + "wq"]), (wk[0:R, :, :], d[pre + "wk"]), (wv[0:R, :], d[pre + "wv"]),
                     (wo[:, :, :], d[pre + "wo"]), (nw[:, :], d[pre + "nw"]), (tab[:, :, :], d["c_" + pre + "tab"]),
                     (msk[:, :, :], d["c_" + pre + "mask"]), (row8[:, :], d["c_row8"]), (m8[:, :], d["c_mean8"])]
            if run == 0:
                loads.append((wd[:, :], d["ga0_wd"]))
            for dst, x in loads:
                sp.dma_start(dst, x).then_inc(s["w"], 16)
            sp.wait_ge(s["w"], 16 * NW)

        @block.tensor
        def _(pe):
            pe.wait_ge(s["w"], 16 * NW)
            pe.wait_ge(s["set"], 2)
            with pe.Fori(0, B) as it:
                for i in range(HALVES):
                    pe.wait_ge(s["sq"], up("sq", it, i))
                    nc.tensor.matmul(ps[:, i, :], c.mean_w[:, :], sq[:, i, :],
                                     start=True, stop=True).then_inc(s["ms"], 1)
                for i in range(HALVES):
                    pe.wait_ge(s["h"], up("h", it, i))
                    if run == 0:
                        nc.tensor.matmul(ps[0:LAT, 2 + i, :], wd[:, :], h[:, i * BLK:(i + 1) * BLK],
                                         start=True, stop=True).then_inc(s["lat_ps"], 1)
                if run == 0:
                    pe.wait_ge(s["lat"], up("lat", it, 1))

                def head_means(n):
                    pe.wait_ge(s["qsq"], up("qsq", it, n))
                    nc.tensor.matmul(ps[:, 4 + n % 2, :], m8[:, :], sq[:, n % 2, :],
                                     start=True, stop=True).then_inc(s["qms"], 1)

                for n in range(NQK):
                    g, i = n // 2, n % 2
                    half = slice(i * BLK, (i + 1) * BLK)
                    if n >= 2:
                        pe.wait_ge(s["rot"], up("rot", it, n - 2))
                    for x in range(2):
                        if g < GQ:
                            last = nc.tensor.matmul(ps[:, 2 * x + n % 2, :], wq[:, x, g, :], h[:, half],
                                                    start=True, stop=True)
                        else:
                            last = nc.tensor.matmul(ps[:, 2 * x + n % 2, :], wk[0:R, x, :], src[0:R, half],
                                                    start=True, stop=True)
                    last.then_inc(s["qk_ps"], 1)
                    if n:
                        head_means(n - 1)
                head_means(NQK - 1)
                for t in range(TILES):
                    if t >= 2:
                        pe.wait_ge(s["v"], up("v", it, t - 2))
                    nc.tensor.matmul(ps[:, 6 + t % 2, 0:32], src[0:R, t * P:(t + 1) * P], wv[0:R, :],
                                     start=True, stop=True).then_inc(s["v_ps"], 1)
                pe.wait_ge(s["qk"], up("qk", it, NQK - 1))
                pe.wait_ge(s["v"], up("v", it, TILES - 1))

                def scores(n):
                    t, k, j, m = units[n]
                    rows = slice(32 * j, 32 * j + 8)
                    if n >= 3:
                        pe.wait_ge(s["exp"], up("exp", it, n - 3))
                    nc.tensor.matmul(ps[:, n % 3, :].rearrange("p (g q) -> p g q", g=GQ),
                                     kt[rows, k * P:(k + 1) * P], qt[rows, :, t * P:(t + 1) * P],
                                     start=True, stop=True, tile_position=(32 * j, 0)).then_inc(s["st"], 1)

                def values(n):
                    t, k, j, m = units[n]
                    if (n == 0 or units[n - 1][0] != t) and t >= 2:
                        pe.wait_ge(s["o"], up("o", it, t - 2))
                    if m is None:
                        pe.wait_ge(s["exp"], up("exp", it, n))
                    else:
                        pe.wait_ge(s["mask"], up("mask", it, masked.index(n)))
                    first = units[n][1] == (0 if run == 0 else max(t - 1, 0))
                    nc.tensor.matmul(ps[32 * j:32 * j + 32, 3 + t % 2, :], v[:, k, j, :], pt[:, n % 3, :],
                                     start=first, stop=(k == t), tile_position=(0, 32 * j)).then_inc(s["av"], 1)

                def sums(t):
                    pe.wait_ge(s["o"], up("o", it, t))
                    if t:
                        pe.wait_ge(s["ot"], up("ot", it, t - 1))
                    nc.tensor.matmul(ps[:, 5, :], row8[:, :], os[:, t % 2, :],
                                     start=True, stop=True).then_inc(s["sum_ps"], 1)

                for n in range(U + 2):
                    if n < U:
                        scores(n)
                    if n >= 2:
                        values(n - 2)
                        t = units[n - 2][0]
                        if t and n - 2 == last_of[t - 1] + 4:
                            sums(t - 1)
                sums(TILES - 1)
                pe.wait_ge(s["ot"], up("ot", it, TILES - 1))
                for i in range(HALVES):
                    for g in range(GQ):
                        last = nc.tensor.matmul(ps[:, 6 + i, :], wo[:, g, :], ot[:, g, i * BLK:(i + 1) * BLK],
                                                start=(g == 0), stop=(g == GQ - 1))
                    last.then_inc(s["y_ps"], 1)

        @block.scalar
        def _(act):
            with act.Fori(0, B) as it:
                for i in range(HALVES):
                    act.wait_ge(s["ms"], up("ms", it, i))
                    nc.scalar.activation(sd[:, i, :], ps[:, i, :], ACT.Sqrt, bias=c.eps6[:, 0:1]).then_inc(s["sd"], 1)
                if run == 0:
                    for i in range(HALVES):
                        act.wait_ge(s["lat_ps"], up("lat_ps", it, i))
                        nc.scalar.activation(lat[0:LAT, i * BLK:(i + 1) * BLK], ps[0:LAT, 2 + i, :],
                                             ACT.Copy).then_inc(s["lat"], 1)

                def root(n):
                    act.wait_ge(s["qms"], up("qms", it, n))
                    if n >= 2:
                        act.wait_ge(s["qk"], up("qk", it, n - 2))
                    nc.scalar.activation(sd[:, n % 2, :], ps[:, 4 + n % 2, :], ACT.Sqrt,
                                         bias=c.eps6[:, 0:1]).then_inc(s["qsd"], 1)

                for n in range(NQK):
                    act.wait_ge(s["rot"], up("rot", it, n))
                    nc.scalar.activation(sq[:, n % 2, :], rot[:, n % 2, 0, :], ACT.Square).then_inc(s["qsq"], 1)
                    if n:
                        root(n - 1)
                root(NQK - 1)
                for t in range(TILES):
                    act.wait_ge(s["v_ps"], up("v_ps", it, t))
                    nc.scalar.activation(v[:, t, :, 0:8], ps[:, 6 + t % 2, 0:32].rearrange("p (j e) -> p j e", e=8),
                                         ACT.Copy).then_inc(s["v"], 1)

                def copy_out(t):
                    act.wait_ge(s["av"], up("av", it, last_of[t]))
                    if t >= 2:
                        act.wait_ge(s["ot"], up("ot", it, t - 2))
                    nc.scalar.activation(os[:, t % 2, :], ps[:, 3 + t % 2, :], ACT.Copy).then_inc(s["o"], 1)

                for n in range(U):
                    act.wait_ge(s["st"], up("st", it, n))
                    if n >= 3:
                        act.wait_ge(s["av"], up("av", it, n - 3))
                    nc.scalar.activation(pt[:, n % 3, :], ps[:, n % 3, :], ACT.Exp,
                                         scale=float(8) ** -0.5).then_inc(s["exp"], 1)
                    t = units[n][0]
                    if t and n == last_of[t - 1] + 3:
                        copy_out(t - 1)
                copy_out(TILES - 1)

        @block.vector
        def _(dve):
            link = Chain(c, dve, pre + "dve", 3 * NQK + TILES + 2 * HALVES)
            dve.wait_ge(s["w"], 16 * NW)
            nc.vector.memset(v[:, :, :, :], 0.0).then_inc(s["set"], 1)
            dve.wait_ge(s["set"], 1)
            nc.vector.memset(v[:, :, :, 8:9], 1.0).then_inc(s["set"], 1)
            dve.sem_inc(s["done"], 1)
            with dve.Fori(0, B) as it:
                link.start(it)
                dve.wait_ge(s["done"], it + 1)
                for i in range(HALVES):
                    here = tokens(it * T + i * BLK, BLK)
                    nc.vector.tensor_tensor(sq[:, i, :], c.xnt[:, here], c.xnt[:, here], ALU.mult).then_inc(s["sq"], 1)
                for i in range(HALVES):
                    here = tokens(it * T + i * BLK, BLK)
                    dve.wait_ge(s["sd"], up("sd", it, i))
                    link(nc.vector.reciprocal(sd[:, i, :], sd[:, i, :]))
                    nc.vector.scalar_tensor_tensor(h[:, i * BLK:(i + 1) * BLK], c.xnt[:, here], nw[:, 0:1],
                                                   sd[:, i, :], ALU.mult, ALU.mult).then_inc(s["h"], 1)
                def to_length(n):
                    g, half = n // 2, slice(n % 2 * BLK, (n % 2 + 1) * BLK)
                    dve.wait_ge(s["qsd"], up("qsd", it, n))
                    link(nc.vector.reciprocal(sd[:, n % 2, :], sd[:, n % 2, :]))
                    dst = qt[:, g, half] if g < GQ else kt[:, half]
                    nc.vector.tensor_tensor(dst, rot[:, n % 2, 0, :], sd[:, n % 2, :], ALU.mult).then_inc(s["qk"], 1)

                for n in range(NQK):
                    g, i = n // 2, n % 2
                    half = slice(i * BLK, (i + 1) * BLK)
                    dve.wait_ge(s["qk_ps"], up("qk_ps", it, n))
                    if n >= 2:
                        dve.wait_ge(s["qk"], up("qk", it, n - 2))
                    link(nc.vector.tensor_tensor(rot[:, n % 2, 0, :], tab[:, 0, half], ps[:, n % 2, :], ALU.mult))
                    link(nc.vector.tensor_tensor(rot[:, n % 2, 1, :], tab[:, 1, half], ps[:, 2 + n % 2, :], ALU.mult))
                    nc.vector.tensor_tensor(rot[:, n % 2, 0, :], rot[:, n % 2, 0, :], rot[:, n % 2, 1, :],
                                            ALU.add).then_inc(s["rot"], 1)
                    if n:
                        to_length(n - 1)
                to_length(NQK - 1)

                def normalise(t):
                    dve.wait_ge(s["sum_ps"], up("sum_ps", it, t))
                    link(nc.vector.reciprocal(rs[:, t % 2, :], ps[:, 5, :]))
                    nc.vector.tensor_tensor(ot[:, :, t * P:(t + 1) * P],
                                            os[:, t % 2, :].rearrange("p (g q) -> p g q", g=GQ),
                                            rs[:, t % 2, :].rearrange("p (g q) -> p g q", g=GQ),
                                            ALU.mult).then_inc(s["ot"], 1)

                for n in masked:
                    t, k, j, m = units[n]
                    dve.wait_ge(s["exp"], up("exp", it, n))
                    here = pt[:, n % 3, :].rearrange("p (g q) -> p g q", g=GQ)
                    nc.vector.tensor_tensor(here, here, msk[:, m:m + 1, :].to_broadcast([P, GQ, P]),
                                            ALU.mult).then_inc(s["mask"], 1)
                    if n == last_of[t] and t:
                        normalise(t - 1)
                normalise(TILES - 1)
                for i in range(HALVES):
                    here = tokens(it * T + i * BLK, BLK)
                    dve.wait_ge(s["y_ps"], up("y_ps", it, i))
                    link(nc.vector.tensor_tensor(c.xnt[:, here], c.xnt[:, here], ps[:, 6 + i, :], ALU.add))
                    if run == 1:
                        last = nc.vector.tensor_tensor(c.xt[:, here], c.xt[:, here], c.xnt[:, here], ALU.add)
                if run == 1:
                    last.then_inc(s["done"], 1)
                else:
                    dve.sem_inc(s["done"], 1)
            link.close()


NE, FF = 8, 256


def experts_phase(c, which):
    swiglu = which == 1
    E = NE + 1 if swiglu else NE
    U = 2 * E
    pre = f"moe{which}_"
    counts = dict(w=1, h=1, mean=1, xc=1, sq=1, var=1, sd=1, rn=1, lg_ps=1, lg=1, exp=1, wt_ps=1, gate=1, wt=1,
                  wb=NE, h_ps=U, act=U, hs=U, out=U, done=1)
    if swiglu:
        for k in ("mean", "xc", "sq", "var", "sd", "rn"):
            del counts[k]
    c.signals(**{pre + k: n for k, n in counts.items()})
    s = {k: c.sem[pre + k] for k in counts}
    up = lambda name, it, i=0: c.up(pre + name, it, i)
    nc, d, ps = c.nc, c.d, c.ps
    NW = 5 if not swiglu else 6
    with ExitStack() as ctx:
        sb = lambda n, shape, dt=F32: c.sb(ctx, pre + "b_" + n, shape, dt)
        w1 = sb("w1", [P, E, FF])
        w3 = sb("w3", [P, E, FF]) if swiglu else None
        w2 = sb("w2", [P, E, 2, P])
        wr = sb("wr", [P, NE])
        gcon = sb("gcon", [P, 2 + 4 * NE])
        sel = sb("sel", [NE, NE, P])
        order = sb("order", [P, 4, NE])
        h = sb("h", [P, BLK])
        rn = sb("rn", [P, BLK])
        tmp = sb("tmp", [P, 3, BLK])
        lg = sb("lg", [P, 4, NE])
        lr = sb("lr", [P, 4, NE])
        others = sb("others", [P, 4, NE])
        hot = sb("hot", [P, 4, NE])
        hot2 = sb("hot2", [P, 4, NE])
        g1 = sb("g1", [P, 4])
        wt = sb("wt", [NE, BLK])
        ga = sb("ga", [P, 2, BLK])
        hs = sb("hs", [P, 2, BLK])
        block = ctx.enter_context(nc.Block())

        @block.sync
        def _(sp):
            loads = [(w1[:, :, :], pre + "w1"), (w2[:, :, :, :], pre + "w2"), (wr[:, :], pre + "wr"),
                     (gcon[:, :], pre + "gcon"), (sel[:, :, :], "c_sel")]
            if swiglu:
                loads.append((w3[:, :, :], pre + "w3"))
            for dst, x in loads:
                sp.dma_start(dst, d[x]).then_inc(s["w"], 16)
            sp.dma_start(order[:, :, :], d["c_order"]).then_inc(s["w"], 16)
            sp.wait_ge(s["w"], 16 * (NW + 1))

        @block.tensor
        def _(pe):
            pe.wait_ge(s["w"], 16 * (NW + 1))
            with pe.Fori(0, NB) as it:
                pe.wait_ge(s["h"], up("h", it))
                if not swiglu:
                    nc.tensor.matmul(ps[:, 0, :], c.mean_w[:, :], h[:, :], start=True, stop=True).then_inc(s["mean"], 1)
                    pe.wait_ge(s["sq"], up("sq", it))
                    nc.tensor.matmul(ps[:, 1, :], c.mean_w[:, :], tmp[:, 1, :],
                                     start=True, stop=True).then_inc(s["var"], 1)
                    pe.wait_ge(s["rn"], up("rn", it))
                for t in range(4):
                    x = h if swiglu else rn
                    last = nc.tensor.matmul(ps[:, 0, t * NE:(t + 1) * NE], x[:, t * P:(t + 1) * P], wr[:, :],
                                            start=True, stop=True)
                last.then_inc(s["lg_ps"], 1)

                def first(n):
                    e, f = n // 2, slice(n % 2 * P, n % 2 * P + P)
                    if n >= 2:
                        pe.wait_ge(s["hs"], up("hs", it, n - 2))
                    last = nc.tensor.matmul(ps[:, 2 + n % 2, :], w1[:, e, f], h[:, :], start=True, stop=True)
                    if swiglu:
                        last = nc.tensor.matmul(ps[:, 4 + n % 2, :], w3[:, e, f], h[:, :], start=True, stop=True)
                    last.then_inc(s["h_ps"], 1)

                def spread(e):
                    if e >= 2:
                        pe.wait_ge(s["hs"], up("hs", it, 2 * e - 3))
                    nc.tensor.matmul(ps[:, e % 2, :], sel[:, e, :], wt[:, :],
                                     start=True, stop=True).then_inc(s["wb"], 1)

                def second(n):
                    pe.wait_ge(s["hs"], up("hs", it, n))
                    nc.tensor.matmul(ps[:, 6, :], w2[:, n // 2, n % 2, :], hs[:, n % 2, :],
                                     start=(n == 0), stop=(n == U - 1)).then_inc(s["out"], 1)

                first(0)
                first(1)
                pe.wait_ge(s["gate"], up("gate", it))
                for t in range(4):
                    last = nc.tensor.transpose(ps[0:NE, 7, t * P:(t + 1) * P], lr[:, t, :], c.ident[:, :])
                last.then_inc(s["wt_ps"], 1)
                pe.wait_ge(s["wt"], up("wt", it))
                spread(0)
                for n in range(U):
                    if n % 2 == 0 and n // 2 + 1 < NE:
                        spread(n // 2 + 1)
                    if n + 2 < U:
                        first(n + 2)
                    second(n)

        @block.scalar
        def _(act):
            with act.Fori(0, NB) as it:
                if not swiglu:
                    act.wait_ge(s["xc"], up("xc", it))
                    nc.scalar.activation(tmp[:, 1, :], tmp[:, 0, :], ACT.Square).then_inc(s["sq"], 1)
                    act.wait_ge(s["var"], up("var", it))
                    nc.scalar.activation(tmp[:, 2, :], ps[:, 1, :], ACT.Sqrt, bias=c.eps5[:, 0:1]).then_inc(s["sd"], 1)
                act.wait_ge(s["lg"], up("lg", it))
                nc.scalar.activation(lr[:, :, :], lr[:, :, :], ACT.Exp).then_inc(s["exp"], 1)
                act.wait_ge(s["wt_ps"], up("wt_ps", it))
                nc.scalar.activation(wt[:, :], ps[0:NE, 7, :], ACT.Copy).then_inc(s["wt"], 1)
                for n in range(U):
                    act.wait_ge(s["h_ps"], up("h_ps", it, n))
                    if n >= 2:
                        act.wait_ge(s["hs"], up("hs", it, n - 2))
                    if swiglu:
                        nc.scalar.activation(ga[:, n % 2, :], ps[:, 4 + n % 2, :], ACT.Silu).then_inc(s["act"], 1)
                    else:
                        nc.scalar.activation(ga[:, n % 2, :], ps[:, 2 + n % 2, :], ACT.Gelu).then_inc(s["act"], 1)

        @block.vector
        def _(dve):
            link = Chain(c, dve, pre + "dve", (20 + 2 * NE) if swiglu else 18)
            dve.wait_ge(s["w"], 16 * (NW + 1))
            dve.sem_inc(s["done"], 1)
            with dve.Fori(0, NB) as it:
                link.start(it)
                here = tokens(it * BLK, BLK)
                dve.wait_ge(s["done"], it + 1)
                nc.vector.tensor_scalar(h[:, :], c.xnt[:, here], 1.0, None, ALU.mult).then_inc(s["h"], 1)
                spread4 = lambda x: x.unsqueeze(2).to_broadcast([P, 4, NE])
                if not swiglu:
                    dve.wait_ge(s["mean"], up("mean", it))
                    nc.vector.tensor_tensor(tmp[:, 0, :], h[:, :], ps[:, 0, :], ALU.subtract).then_inc(s["xc"], 1)
                    dve.wait_ge(s["sd"], up("sd", it))
                    link(nc.vector.reciprocal(tmp[:, 2, :], tmp[:, 2, :]))
                    link(nc.vector.tensor_tensor(tmp[:, 1, :], tmp[:, 0, :], tmp[:, 2, :], ALU.mult))
                    nc.vector.tensor_scalar(rn[:, :], tmp[:, 1, :], gcon[:, 0:1], gcon[:, 1:2],
                                            ALU.mult, ALU.add).then_inc(s["rn"], 1)

                def best_two(x, others):
                    for k, dst in enumerate((hot, hot2)):
                        link(nc.vector.tensor_reduce(g1[:, :], x[:, :, :], AX, ALU.max))
                        link(nc.vector.tensor_tensor(dst[:, :, :], x[:, :, :], spread4(g1[:, :]), ALU.is_equal))
                        link(nc.vector.tensor_tensor(dst[:, :, :], dst[:, :, :], order[:, :, :], ALU.mult))
                        link(nc.vector.tensor_reduce(g1[:, :], dst[:, :, :], AX, ALU.max))
                        link(nc.vector.tensor_tensor(dst[:, :, :], dst[:, :, :], spread4(g1[:, :]), ALU.is_equal))
                        if k == 0:
                            link(nc.vector.scalar_tensor_tensor(others[:, :, :], hot[:, :, :], -1e30, x[:, :, :],
                                                                ALU.mult, ALU.add))
                            x = others
                    link(nc.vector.tensor_tensor(hot[:, :, :], hot[:, :, :], hot2[:, :, :], ALU.add))

                dve.wait_ge(s["lg_ps"], up("lg_ps", it))
                logits = ps[:, 0, 0:4 * NE].rearrange("p (t e) -> p t e", e=NE)
                if swiglu:
                    link(nc.vector.tensor_scalar(lg[:, :, :], logits, float(P) ** -0.5, None, ALU.mult))
                    link(nc.vector.tensor_tensor(lr[:, :, :], lg[:, :, :],
                                                 gcon[:, 2:].rearrange("p (t e) -> p t e", e=NE), ALU.add))
                    best_two(lr, others)
                    link(nc.vector.tensor_scalar(lr[:, :, :], hot[:, :, :], 1e30, -1e30, ALU.mult, ALU.add))
                    link(nc.vector.tensor_tensor(lg[:, :, :], lg[:, :, :], hot[:, :, :], ALU.mult))
                    link(nc.vector.tensor_tensor(lr[:, :, :], lr[:, :, :], lg[:, :, :], ALU.add))
                    src = lr
                else:
                    src = logits
                link(nc.vector.tensor_reduce(g1[:, :], src if src is logits else src[:, :, :], AX, ALU.max, negate=True))
                nc.vector.tensor_tensor(lr[:, :, :], src if src is logits else src[:, :, :], spread4(g1[:, :]),
                                        ALU.add).then_inc(s["lg"], 1)
                dve.wait_ge(s["exp"], up("exp", it))
                link(nc.vector.tensor_reduce(g1[:, :], lr[:, :, :], AX, ALU.add))
                link(nc.vector.reciprocal(g1[:, :], g1[:, :]))
                if swiglu:
                    nc.vector.tensor_tensor(lr[:, :, :], lr[:, :, :], spread4(g1[:, :]), ALU.mult).then_inc(s["gate"], 1)
                else:
                    link(nc.vector.tensor_tensor(lg[:, :, :], lr[:, :, :], spread4(g1[:, :]), ALU.mult))
                    best_two(lg, others)
                    nc.vector.tensor_tensor(lr[:, :, :], lg[:, :, :], hot[:, :, :], ALU.mult).then_inc(s["gate"], 1)

                for n in range(U):
                    e = n // 2
                    dve.wait_ge(s["act"], up("act", it, n))
                    if n >= 2:
                        dve.wait_ge(s["out"], up("out", it, n - 2))
                    if e < NE:
                        dve.wait_ge(s["wb"], up("wb", it, e))
                    if swiglu and e < NE:
                        link(nc.vector.tensor_tensor(ga[:, n % 2, :], ga[:, n % 2, :], ps[:, 2 + n % 2, :], ALU.mult))
                    other = ps[:, e % 2, :] if e < NE else ps[:, 2 + n % 2, :]
                    nc.vector.tensor_tensor(hs[:, n % 2, :], ga[:, n % 2, :], other, ALU.mult).then_inc(s["hs"], 1)
                dve.wait_ge(s["out"], up("out", it, U - 1))
                nc.vector.tensor_tensor(c.xt[:, here], c.xt[:, here], ps[:, 6, :], ALU.add).then_inc(s["done"], 1)
            link.close()


THRESH = 0.01


def threshold_attention_phase(c):
    s = c.signals(th_w=1, th_set=1, th_x=1, th_x_ps=1, th_v=1, th_s_ps=TILES, th_exp=TILES, th_p=TILES, th_t_ps=TILES,
                  th_t=TILES, th_y_ps=TILES, th_done=1)
    nc, d, up, ps = c.nc, c.d, c.up, c.ps
    with ExitStack() as ctx:
        w = c.sb(ctx, "th_wt", [P, P])
        ones = c.sb(ctx, "th_ones", [P, P])
        xb = c.sb(ctx, "th_xb", [P, T])
        v = c.sb(ctx, "th_vt", [P, TILES, P])
        e = c.sb(ctx, "th_e", [P, 2, T])
        keep = c.sb(ctx, "th_keep", [P, 2, T])
        low = c.sb(ctx, "th_low", [P, T])
        z = c.sb(ctx, "th_z", [P, 2, 4])
        vac = c.sb(ctx, "th_vac", [P, 2, P])
        pt = c.sb(ctx, "th_pt", [P, TILES + 1, P])
        block = ctx.enter_context(nc.Block())

        @block.sync
        def _(sp):
            sp.dma_start(w[:, :], d["th_w"]).then_inc(s["th_w"], 16)
            sp.wait_ge(s["th_w"], 16)

        @block.tensor
        def _(pe):
            pe.wait_ge(s["th_w"], 16)
            with pe.Fori(0, B) as it:
                pe.wait_ge(s["th_x"], up("th_x", it))
                for t in range(TILES):
                    last = nc.tensor.transpose(ps[:, 6 + t // 4, (t % 4) * P:(t % 4 + 1) * P],
                                               xb[:, t * P:(t + 1) * P], c.ident[:, :])
                last.then_inc(s["th_x_ps"], 1)
                pe.wait_ge(s["th_v"], up("th_v", it))

                def scores(t):
                    if t >= 2:
                        pe.wait_ge(s["th_exp"], up("th_exp", it, t - 2))
                    for i in range(HALVES):
                        last = nc.tensor.matmul(ps[:, 2 * (t % 2) + i, :], xb[:, t * P:(t + 1) * P],
                                                xb[:, i * BLK:(i + 1) * BLK], start=True, stop=True)
                    last.then_inc(s["th_s_ps"], 1)

                def turn(t):
                    if t:
                        pe.wait_ge(s["th_t"], up("th_t", it, t - 1))
                    pe.wait_ge(s["th_p"], up("th_p", it, t))
                    for k in range(TILES):
                        nc.tensor.transpose(ps[:, 4 + k // 4, (k % 4) * P:(k % 4 + 1) * P],
                                            keep[:, t % 2, k * P:(k + 1) * P], c.ident[:, :])
                    nc.tensor.transpose(ps[:, 6, 0:P], vac[:, t % 2, :], c.ident[:, :]).then_inc(s["th_t_ps"], 1)

                def values(t):
                    pe.wait_ge(s["th_t"], up("th_t", it, t))
                    if t:
                        pe.wait_ge(s["th_done"], it * TILES + t + 1)
                    for k in range(TILES):
                        nc.tensor.matmul(ps[:, 7, 0:P], v[:, k, :], pt[:, k, :], start=(k == 0), stop=False)
                    nc.tensor.matmul(ps[:, 7, 0:P], w[:, :], pt[:, TILES, :],
                                     start=False, stop=True).then_inc(s["th_y_ps"], 1)

                scores(0)
                for t in range(TILES):
                    if t + 1 < TILES:
                        scores(t + 1)
                    turn(t)
                    values(t)

        @block.scalar
        def _(act):
            with act.Fori(0, B) as it:
                act.wait_ge(s["th_x_ps"], up("th_x_ps", it))
                nc.scalar.activation(v[:, :, :].rearrange("p a q -> p (a q)"),
                                     ps[:, 6:8, :].rearrange("p a q -> p (a q)"), ACT.Copy).then_inc(s["th_v"], 1)
                for t in range(TILES):
                    act.wait_ge(s["th_s_ps"], up("th_s_ps", it, t))
                    if t >= 2:
                        act.wait_ge(s["th_p"], up("th_p", it, t - 2))
                    nc.scalar.activation(e[:, t % 2, :], ps[:, 2 * (t % 2):2 * (t % 2) + 2, :].rearrange("p a q -> p (a q)"),
                                         ACT.Exp, scale=float(P) ** -0.5,
                                         accum_out=z[:, t % 2, 0:1]).then_inc(s["th_exp"], 1)
                    act.wait_ge(s["th_t_ps"], up("th_t_ps", it, t))
                    if t:
                        act.wait_ge(s["th_y_ps"], up("th_y_ps", it, t - 1))
                    nc.scalar.activation(pt[:, 0:TILES, :].rearrange("p a q -> p (a q)"),
                                         ps[:, 4:6, :].rearrange("p a q -> p (a q)"), ACT.Copy)
                    nc.scalar.activation(pt[:, TILES, :], ps[:, 6, 0:P], ACT.Copy).then_inc(s["th_t"], 1)

        @block.vector
        def _(dve):
            link = Chain(c, dve, "th_dve", 7 * TILES)
            nc.vector.memset(ones[:, :], 1.0).then_inc(s["th_set"], 1)
            dve.wait_ge(s["th_set"], 1)
            dve.sem_inc(s["th_done"], 1)
            with dve.Fori(0, B) as it:
                link.start(it)
                dve.wait_ge(s["th_done"], it * TILES + 1)
                nc.vector.tensor_scalar(xb[:, :], c.xnt[:, tokens(it * T, T)], 1.0, None,
                                        ALU.mult).then_inc(s["th_x"], 1)
                for t in range(TILES):
                    m = t % 2
                    dve.wait_ge(s["th_exp"], up("th_exp", it, t))
                    if t >= 2:
                        dve.wait_ge(s["th_t_ps"], up("th_t_ps", it, t - 2))
                    link(nc.vector.reciprocal(z[:, m, 1:2], z[:, m, 0:1]))
                    link(nc.vector.tensor_scalar(e[:, m, :], e[:, m, :], z[:, m, 1:2], None, ALU.mult))
                    link(nc.vector.scalar_tensor_tensor(keep[:, m, :], e[:, m, :], THRESH, e[:, m, :],
                                                        ALU.is_ge, ALU.mult, accum_out=z[:, m, 2:3]))
                    link(nc.vector.scalar_tensor_tensor(low[:, :], e[:, m, :], THRESH, e[:, m, :],
                                                        ALU.is_lt, ALU.mult, accum_out=z[:, m, 3:4]))
                    link(nc.vector.tensor_scalar(z[:, m, 2:3], z[:, m, 2:3], 1e-9, None, ALU.add))
                    link(nc.vector.reciprocal(z[:, m, 2:3], z[:, m, 2:3]))
                    link(nc.vector.tensor_scalar(keep[:, m, :], keep[:, m, :], z[:, m, 2:3], None, ALU.mult))
                    nc.vector.tensor_scalar(vac[:, m, :], ones[:, :], z[:, m, 3:4], 0.01,
                                            ALU.mult, ALU.mult).then_inc(s["th_p"], 1)
                    here = tokens(it * T + t * P, P)
                    dve.wait_ge(s["th_y_ps"], up("th_y_ps", it, t))
                    nc.vector.tensor_tensor(c.xt[:, here], c.xt[:, here], ps[:, 7, 0:P], ALU.add).then_inc(s["th_done"], 1)
            link.close()


def quantise(c, link, x, q, sc, tmp, n):
    nc = c.nc
    g = 4 * n
    grp = lambda t: t.rearrange("p n (b e) -> p (n b) e", e=32)
    by = lambda t: t.unsqueeze(2).to_broadcast([P, g, 32])
    a, b, y = tmp[:, 0, 0:n, :], tmp[:, 1, 0:n, :], tmp[:, 2, 0:n, :]
    big = 1.5 * 2.0 ** 23
    link(nc.vector.tensor_reduce(sc[:, 0, 0:g], grp(x), AX, ALU.max, apply_absolute_value=True))
    link(nc.vector.tensor_scalar(sc[:, 0, 0:g], sc[:, 0, 0:g], 1 / 7.5, 1e-30, ALU.mult, ALU.max))
    link(nc.vector.reciprocal(sc[:, 1, 0:g], sc[:, 0, 0:g]))
    link(nc.vector.tensor_tensor(grp(y), grp(x), by(sc[:, 1, 0:g]), ALU.mult))
    link(nc.vector.scalar_tensor_tensor(a, y, -1.0, y, ALU.mult, ALU.max))
    link(nc.vector.tensor_scalar(b, a, 4.0, 2.0, ALU.is_lt, ALU.mult))
    link(nc.vector.tensor_scalar(a, a, 2.0, 4.0, ALU.is_lt, ALU.mult))
    link(nc.vector.scalar_tensor_tensor(q, b, 2.0, a, ALU.add, ALU.add))
    link(nc.vector.scalar_tensor_tensor(b, b, 4.0, a, ALU.mult, ALU.add))
    link(nc.vector.tensor_scalar(b, b, -1 / 32, 0.5, ALU.mult, ALU.add))
    link(nc.vector.tensor_tensor(y, y, q, ALU.mult))
    link(nc.vector.tensor_scalar(a, y, big, -big, ALU.add, ALU.add))
    link(nc.vector.tensor_tensor(y, a, y, ALU.subtract))
    link(nc.vector.scalar_tensor_tensor(a, y, 0.5, a, ALU.is_ge, ALU.subtract))
    link(nc.vector.scalar_tensor_tensor(a, a, -1.0, b, ALU.mult, ALU.mult))
    return nc.vector.tensor_tensor(grp(q), grp(a), by(sc[:, 0, 0:g]), ALU.mult)


def quantised_linear_phase(c):
    s = c.signals(ql_w=1, ql_wq=1, ql_w_ps=1, ql_x=1, ql_t_ps=1, ql_t=1, ql_q=1, ql_q_ps=1, ql_qt=1, ql_y_ps=1,
                  ql_done=1)
    nc, d, up, ps = c.nc, c.d, c.up, c.ps
    with ExitStack() as ctx:
        w = c.sb(ctx, "ql_wb", [P, 1, P])
        wt = c.sb(ctx, "ql_wt", [P, P])
        bias = c.sb(ctx, "ql_bias", [P, 1])
        xb = c.sb(ctx, "ql_xb", [P, BLK])
        x = c.sb(ctx, "ql_xr", [P, 4, P])
        q = c.sb(ctx, "ql_qb", [P, 4, P])
        qt = c.sb(ctx, "ql_qtb", [P, BLK])
        tmp = c.sb(ctx, "ql_tmp", [P, 3, 4, P])
        sc = c.sb(ctx, "ql_sc", [P, 2, 16])
        block = ctx.enter_context(nc.Block())

        @block.sync
        def _(sp):
            sp.dma_start(w[:, 0, :], d["ql_w"]).then_inc(s["ql_w"], 16)
            sp.dma_start(bias[:, :], d["ql_b"]).then_inc(s["ql_w"], 16)
            sp.wait_ge(s["ql_w"], 32)

        @block.tensor
        def _(pe):
            pe.wait_ge(s["ql_wq"], 1)
            nc.tensor.transpose(ps[:, 0, 0:P], q[:, 0, :], c.ident[:, :]).then_inc(s["ql_w_ps"], 1)
            with pe.Fori(0, NB) as it:
                pe.wait_ge(s["ql_x"], up("ql_x", it))
                for t in range(4):
                    last = nc.tensor.transpose(ps[:, 1, t * P:(t + 1) * P], xb[:, t * P:(t + 1) * P], c.ident[:, :])
                last.then_inc(s["ql_t_ps"], 1)
                pe.wait_ge(s["ql_q"], up("ql_q", it))
                for t in range(4):
                    last = nc.tensor.transpose(ps[:, 2, t * P:(t + 1) * P], q[:, t, :], c.ident[:, :])
                last.then_inc(s["ql_q_ps"], 1)
                pe.wait_ge(s["ql_qt"], up("ql_qt", it))
                nc.tensor.matmul(ps[:, 3, :], wt[:, :], qt[:, :], start=True, stop=True).then_inc(s["ql_y_ps"], 1)

        @block.scalar
        def _(act):
            with act.Fori(0, NB) as it:
                act.wait_ge(s["ql_t_ps"], up("ql_t_ps", it))
                nc.scalar.activation(x[:, :, :].rearrange("p a q -> p (a q)"), ps[:, 1, :], ACT.Copy).then_inc(s["ql_t"], 1)
                act.wait_ge(s["ql_q_ps"], up("ql_q_ps", it))
                nc.scalar.activation(qt[:, :], ps[:, 2, :], ACT.Copy).then_inc(s["ql_qt"], 1)

        @block.vector
        def _(dve):
            once = Chain(c, dve, "ql_once", 15)
            link = Chain(c, dve, "ql_dve", 15)
            dve.wait_ge(s["ql_w"], 32)
            once.start(0)
            quantise(c, once, w[:, :, :], q[:, 0:1, :], sc, tmp, 1).then_inc(s["ql_wq"], 1)
            once.close()
            dve.wait_ge(s["ql_w_ps"], 1)
            nc.vector.tensor_copy(wt[:, :], ps[:, 0, 0:P]).then_inc(s["ql_done"], 1)
            with dve.Fori(0, NB) as it:
                link.start(it)
                here = tokens(it * BLK, BLK)
                dve.wait_ge(s["ql_done"], it + 1)
                nc.vector.tensor_scalar(xb[:, :], c.xnt[:, here], 1.0, None, ALU.mult).then_inc(s["ql_x"], 1)
                dve.wait_ge(s["ql_t"], up("ql_t", it))
                quantise(c, link, x[:, :, :], q[:, :, :], sc, tmp, 4).then_inc(s["ql_q"], 1)
                dve.wait_ge(s["ql_y_ps"], up("ql_y_ps", it))
                nc.vector.scalar_tensor_tensor(c.xt[:, here], ps[:, 3, :], bias[:, 0:1], c.xt[:, here],
                                               ALU.add, ALU.add).then_inc(s["ql_done"], 1)
            link.close()


S = 16
NS = T // S


class LinearState:

    def __init__(self, c, ctx):
        self.u = c.sb(ctx, "li_u", [P, B, T])
        self.q = c.sb(ctx, "li_q", [P, B, T])
        self.z = c.sb(ctx, "li_z", [P, B, T])
        self.v = c.sb(ctx, "li_v", [P, B, TILES, P])
        self.wo = c.sb(ctx, "li_wo", [P, P])
        self.cols = c.sb(ctx, "li_cols", [P, 3])


def linear_project_phase(c, st):
    s = c.signals(lp_w=1, lp_x=1, lp_qk_ps=2, lp_k=2, lp_sq=2, lp_ms=2, lp_sd=2, lp_u=2, lp_s_ps=1, lp_s=1,
                  lp_v_ps=TILES, lp_v=TILES, lp_done=1)
    nc, d, up, ps = c.nc, c.d, c.up, c.ps
    with ExitStack() as ctx:
        w = c.sb(ctx, "lp_wb", [P, 3, P])
        bv = c.sb(ctx, "lp_bv", [P, P])
        ones = c.sb(ctx, "lp_ones", [P, 1])
        eps = c.eps6
        xb = c.sb(ctx, "lp_xb", [P, T])
        k = c.sb(ctx, "lp_kb", [P, T])
        kq = c.sb(ctx, "lp_kq", [P, T])
        sq = c.sb(ctx, "lp_sqb", [P, 2, BLK])
        sd = c.sb(ctx, "lp_sdb", [P, 2, BLK])
        sk = c.sb(ctx, "lp_sk", [P, TILES])
        vb = c.sb(ctx, "lp_vb", [P, P])
        block = ctx.enter_context(nc.Block())

        @block.sync
        def _(sp):
            for dst, x in [(w[:, :, :], "lp_w"), (bv[:, :], "lp_bv"), (st.wo[:, :], "li_wo"), (st.cols[:, :], "li_cols"),
                           (ones[:, :], "c_ones")]:
                sp.dma_start(dst, d[x]).then_inc(s["lp_w"], 16)
            sp.wait_ge(s["lp_w"], 80)

        @block.tensor
        def _(pe):
            pe.wait_ge(s["lp_w"], 80)
            with pe.Fori(0, B) as it:
                pe.wait_ge(s["lp_x"], up("lp_x", it))
                for i in range(HALVES):
                    for x in range(2):
                        last = nc.tensor.matmul(ps[:, 2 * x + i, :], w[:, x, :], xb[:, i * BLK:(i + 1) * BLK],
                                                start=True, stop=True)
                    last.then_inc(s["lp_qk_ps"], 1)
                for i in range(HALVES):
                    pe.wait_ge(s["lp_sq"], up("lp_sq", it, i))
                    nc.tensor.matmul(ps[:, 4 + i, :], c.mean_w[:, :], sq[:, i, :],
                                     start=True, stop=True).then_inc(s["lp_ms"], 1)
                pe.wait_ge(s["lp_u"], up("lp_u", it, 1))
                for t in range(TILES):
                    last = nc.tensor.matmul(ps[:, 0, t:t + 1], kq[:, t * P:(t + 1) * P], ones[:, :],
                                            start=True, stop=True)
                last.then_inc(s["lp_s_ps"], 1)
                for t in range(TILES):
                    if t >= 2:
                        pe.wait_ge(s["lp_v"], up("lp_v", it, t - 2))
                    nc.tensor.matmul(ps[:, 6 + t % 2, 0:P], xb[:, t * P:(t + 1) * P], w[:, 2, :],
                                     start=True, stop=True).then_inc(s["lp_v_ps"], 1)

        @block.scalar
        def _(act):
            with act.Fori(0, B) as it:
                for i in range(HALVES):
                    act.wait_ge(s["lp_k"], up("lp_k", it, i))
                    nc.scalar.activation(sq[:, i, :], k[:, i * BLK:(i + 1) * BLK], ACT.Square).then_inc(s["lp_sq"], 1)
                for i in range(HALVES):
                    act.wait_ge(s["lp_ms"], up("lp_ms", it, i))
                    nc.scalar.activation(sd[:, i, :], ps[:, 4 + i, :], ACT.Sqrt, scale=float(P)).then_inc(s["lp_sd"], 1)

        @block.vector
        def _(dve):
            link = Chain(c, dve, "lp_dve", 1 + HALVES + 3 * HALVES + TILES)
            dve.wait_ge(s["lp_w"], 80)
            dve.sem_inc(s["lp_done"], 1)
            with dve.Fori(0, B) as it:
                link.start(it)
                dve.wait_ge(s["lp_done"], it + 1)
                nc.vector.tensor_scalar(xb[:, :], c.xnt[:, tokens(it * T, T)], 1.0, None, ALU.mult).then_inc(s["lp_x"], 1)
                uu = st.u[:, :, :].rearrange("p b t -> p (b t)")
                qq = st.q[:, :, :].rearrange("p b t -> p (b t)")
                vv = st.v[:, :, :, :].rearrange("p b t e -> p (b t e)")
                for i in range(HALVES):
                    half = slice(i * BLK, (i + 1) * BLK)
                    here = tokens(it * T + i * BLK, BLK)
                    dve.wait_ge(s["lp_qk_ps"], up("lp_qk_ps", it, i))
                    link(nc.vector.tensor_scalar(qq[:, here], ps[:, i, :], st.cols[:, 0:1], None, ALU.add))
                    nc.vector.tensor_scalar(k[:, half], ps[:, 2 + i, :], st.cols[:, 1:2], None,
                                            ALU.add).then_inc(s["lp_k"], 1)
                for i in range(HALVES):
                    half = slice(i * BLK, (i + 1) * BLK)
                    here = tokens(it * T + i * BLK, BLK)
                    dve.wait_ge(s["lp_sd"], up("lp_sd", it, i))
                    link(nc.vector.tensor_tensor(kq[:, half], k[:, half], qq[:, here], ALU.mult))
                    link(nc.vector.tensor_scalar(sd[:, i, :], sd[:, i, :], 1e-6, None, ALU.add))
                    link(nc.vector.reciprocal(sd[:, i, :], sd[:, i, :]))
                    nc.vector.tensor_tensor(uu[:, here], k[:, half], sd[:, i, :], ALU.mult).then_inc(s["lp_u"], 1)
                dve.wait_ge(s["lp_s_ps"], up("lp_s_ps", it))
                link(nc.vector.tensor_scalar(sk[:, :], ps[:, 0, 0:TILES], 1.0, None, ALU.mult))
                for t in range(TILES):
                    dve.wait_ge(s["lp_v_ps"], up("lp_v_ps", it, t))
                    link(nc.vector.tensor_tensor(vb[:, :], bv[:, :], ps[:, 6 + t % 2, 0:P], ALU.add))
                    last = nc.vector.tensor_scalar(vv[:, tokens(it * T + t * P, P)], vb[:, :], sk[:, t:t + 1], None,
                                                   ALU.mult).then_inc(s["lp_v"], 1)
                    dve.wait_ge(s["lp_v"], up("lp_v", it, t))
                dve.sem_inc(s["lp_done"], 1)
            link.close()


def linear_scan_phase(c, st):
    s = c.signals(ls_w=1, ls_u=1, ls_v_ps=1, ls_vk=1, ls_vt=1, ls_s_ps=1, ls_s=1, ls_s_in=64, ls_m=1, ls_m_in=64,
                  ls_z_ps=1, ls_wz=1, ls_z=1, ls_a_ps=1, ls_a=1)
    nc, d, up, ps = c.nc, c.d, c.up, c.ps
    with ExitStack() as ctx:
        eye = c.sb(ctx, "ls_eye", [S, S])
        low = c.sb(ctx, "ls_low", [B, 2, S, S])
        a = c.sb(ctx, "ls_ab", [P, B, P])
        ub = c.sb(ctx, "ls_ub", [P, B, S])
        vk = c.sb(ctx, "ls_vkb", [S, B, P])
        vt = c.sb(ctx, "ls_vtb", [P, B, S])
        sb = c.sb(ctx, "ls_sb", [S, B, S])
        f = c.sb(ctx, "ls_f", [B, S, S])
        g = c.sb(ctx, "ls_g", [B, S, S])
        dinv = c.sb(ctx, "ls_dinv", [B, S])
        m = c.sb(ctx, "ls_mb", [B, S, 2, S])
        mm = c.sb(ctx, "ls_mm", [S, B, 2, S])
        w = c.sb(ctx, "ls_wb", [S, B, P])
        z = c.sb(ctx, "ls_zb", [S, B, P])
        block = ctx.enter_context(nc.Block())

        @block.sync
        def _(sp):
            sp.dma_start(eye[:, :], c.ident[0:S, 0:S]).then_inc(s["ls_w"], 16)
            sp.dma_start(low[:, :, :, :], d["c_low"]).then_inc(s["ls_w"], 16)
            for b in range(B):
                sp.dma_start(a[:, b, :], c.ident[:, :]).then_inc(s["ls_w"], 16)
            sp.wait_ge(s["ls_w"], 96)
            with sp.Fori(0, NS) as it:
                sp.wait_ge(s["ls_s"], up("ls_s", it))
                for b in range(B):
                    sp.dma_start(f[b:b + 1, :, :], sb[:, b, :]).then_inc(s["ls_s_in"], 16)
                sp.wait_ge(s["ls_m"], up("ls_m", it))
                for b in range(B):
                    sp.dma_start(mm[:, b, :, :], m[b:b + 1, :, :, :]).then_inc(s["ls_m_in"], 16)
            sp.wait_ge(s["ls_m_in"], 64 * NS)

        @block.tensor
        def _(pe):
            pe.wait_ge(s["ls_w"], 96)
            with pe.Fori(0, NS) as it:
                pe.wait_ge(s["ls_u"], up("ls_u", it))
                for b in range(B):
                    nc.tensor.matmul(ps[:, 1, b * S:(b + 1) * S], a[:, b, :], ub[:, b, :], start=True, stop=True)
                for b in range(B):
                    last = nc.tensor.matmul(ps[0:S, 0, b * P:(b + 1) * P], ub[:, b, :], a[:, b, :],
                                            start=True, stop=True)
                last.then_inc(s["ls_v_ps"], 1)
                pe.wait_ge(s["ls_vt"], up("ls_vt", it))
                for b in range(B):
                    last = nc.tensor.matmul(ps[0:S, 2, b * S:(b + 1) * S], vt[:, b, :], ub[:, b, :],
                                            start=True, stop=True)
                last.then_inc(s["ls_s_ps"], 1)
                pe.wait_ge(s["ls_vk"], up("ls_vk", it))
                pe.wait_ge(s["ls_m_in"], (it + 1) * 64)
                for b in range(B):
                    nc.tensor.matmul(ps[:, 5, b * S:(b + 1) * S], vk[:, b, :], mm[:, b, 1, :], start=True, stop=True)
                for b in range(B):
                    nc.tensor.matmul(ps[0:S, 3, b * P:(b + 1) * P], mm[:, b, 0, :], vk[:, b, :], start=True, stop=True)
                    last = nc.tensor.matmul(ps[0:S, 4, b * P:(b + 1) * P], mm[:, b, 1, :], vk[:, b, :],
                                            start=True, stop=True)
                last.then_inc(s["ls_z_ps"], 1)
                pe.wait_ge(s["ls_wz"], up("ls_wz", it))
                for b in range(B):
                    last = nc.tensor.matmul(ps[:, 6, b * P:(b + 1) * P], w[:, b, :], z[:, b, :], start=True, stop=True)
                last.then_inc(s["ls_a_ps"], 1)

        @block.scalar
        def _(act):
            flat = lambda t: t.rearrange("p b e -> p (b e)")
            with act.Fori(0, NS) as it:
                act.wait_ge(s["ls_v_ps"], up("ls_v_ps", it))
                nc.scalar.activation(flat(vk[:, :, :]), ps[0:S, 0, :], ACT.Copy).then_inc(s["ls_vk"], 1)
                act.wait_ge(s["ls_z_ps"], up("ls_z_ps", it))
                nc.scalar.activation(flat(w[:, :, :]), ps[0:S, 3, :], ACT.Copy)
                nc.scalar.activation(flat(z[:, :, :]), ps[0:S, 4, :], ACT.Copy).then_inc(s["ls_wz"], 1)

        @block.vector
        def _(dve):
            link = Chain(c, dve, "ls_dve", 4 * (S - 1) + 1 + 2)
            uu = st.u[:, :, :].rearrange("p b t -> p b t")
            dve.wait_ge(s["ls_w"], 96)
            dve.sem_inc(s["ls_a"], 1)
            with dve.Fori(0, NS) as it:
                link.start(it)
                dve.wait_ge(s["ls_a"], it + 1)
                nc.vector.tensor_scalar(ub[:, :, :], uu[:, :, tokens(it * S, S)], 1.0, None, ALU.mult).then_inc(s["ls_u"], 1)
                dve.wait_ge(s["ls_v_ps"], up("ls_v_ps", it))
                nc.vector.tensor_scalar(vt[:, :, :], ps[:, 1, 0:B * S].rearrange("p (b e) -> p b e", e=S), 1.0, None,
                                        ALU.mult).then_inc(s["ls_vt"], 1)
                dve.wait_ge(s["ls_s_ps"], up("ls_s_ps", it))
                nc.vector.tensor_tensor(sb[:, :, :], ps[0:S, 2, 0:B * S].rearrange("p (b e) -> p b e", e=S),
                                        eye[:, :].unsqueeze(1).to_broadcast([S, B, S]), ALU.add).then_inc(s["ls_s"], 1)
                dve.wait_ge(s["ls_s_in"], (it + 1) * 64)
                for t in range(S):
                    link(nc.vector.reciprocal(dinv[:, t:t + 1], f[:, t, t:t + 1]))
                    if t == S - 1:
                        break
                    rest = S - 1 - t
                    link(nc.vector.tensor_scalar(f[:, t, t:t + 1], f[:, t, t:t + 1], 1.0, None, ALU.add))
                    link(nc.vector.scalar_tensor_tensor(g[:, :, 0:rest], f[:, :, t:t + 1].to_broadcast([B, S, rest]),
                                                        dinv[:, t:t + 1],
                                                        f[:, t:t + 1, t + 1:S].to_broadcast([B, S, rest]),
                                                        ALU.mult, ALU.mult))
                    link(nc.vector.tensor_tensor(f[:, :, t + 1:S], f[:, :, t + 1:S], g[:, :, 0:rest], ALU.subtract))
                link(nc.vector.tensor_tensor(f[:, :, :], f[:, :, :], low[:, 0, :, :], ALU.mult))
                link(nc.vector.tensor_tensor(m[:, :, 0, :], f[:, :, :], low[:, 1, :, :], ALU.add))
                nc.vector.tensor_tensor(m[:, :, 1, :], m[:, :, 0, :],
                                        dinv[:, :].unsqueeze(1).to_broadcast([B, S, S]), ALU.mult).then_inc(s["ls_m"], 1)
                dve.wait_ge(s["ls_z_ps"], up("ls_z_ps", it))
                nc.vector.tensor_scalar(st.z[:, :, tokens(it * S, S)],
                                        ps[:, 5, 0:B * S].rearrange("p (b e) -> p b e", e=S), 1.0, None,
                                        ALU.mult).then_inc(s["ls_z"], 1)
                dve.wait_ge(s["ls_a_ps"], up("ls_a_ps", it))
                nc.vector.tensor_tensor(a[:, :, :].rearrange("p b e -> p (b e)"), a[:, :, :].rearrange("p b e -> p (b e)"),
                                        ps[:, 6, :], ALU.subtract).then_inc(s["ls_a"], 1)
            link.close()


def linear_output_phase(c, st):
    units = [(i, k) for i in range(HALVES) for k in range(4 * i + 4)]
    U = len(units)
    s = c.signals(lo_w=1, lo_in=1, lo_s_ps=U, lo_p=U, lo_av=U, lo_o=2, lo_y_ps=2, lo_done=1)
    nc, d, up, ps = c.nc, c.d, c.up, c.ps
    with ExitStack() as ctx:
        causal = c.sb(ctx, "lo_causal", [P, P])
        z = c.sb(ctx, "lo_z", [P, T])
        q = c.sb(ctx, "lo_q", [P, T])
        v = c.sb(ctx, "lo_v", [P, T])
        pt = c.sb(ctx, "lo_pt", [P, 3, BLK])
        o = c.sb(ctx, "lo_ob", [P, 2, BLK])
        block = ctx.enter_context(nc.Block())
        start = lambda i, k: max(k * P, i * BLK)

        @block.sync
        def _(sp):
            sp.dma_start(causal[:, :], d["c_causal"]).then_inc(s["lo_w"], 16)
            sp.wait_ge(s["lo_w"], 16)

        @block.tensor
        def _(pe):
            with pe.Fori(0, B) as it:
                pe.wait_ge(s["lo_in"], up("lo_in", it))

                def scores(n):
                    i, k = units[n]
                    q0, q1 = start(i, k), (i + 1) * BLK
                    if n >= 3:
                        pe.wait_ge(s["lo_p"], up("lo_p", it, n - 3))
                    nc.tensor.matmul(ps[:, n % 3, 0:q1 - q0], z[:, k * P:(k + 1) * P], q[:, q0:q1],
                                     start=True, stop=True).then_inc(s["lo_s_ps"], 1)

                def values(n):
                    i, k = units[n]
                    q0, q1 = start(i, k), (i + 1) * BLK
                    pe.wait_ge(s["lo_p"], up("lo_p", it, n))
                    nc.tensor.matmul(ps[:, 4 + i, q0 - i * BLK:BLK], v[:, k * P:(k + 1) * P], pt[:, n % 3, 0:q1 - q0],
                                     start=(k == 0), stop=(k == 4 * i + 3)).then_inc(s["lo_av"], 1)

                for n in range(U + 2):
                    if n < U:
                        scores(n)
                    if n >= 2:
                        values(n - 2)
                for i in range(HALVES):
                    pe.wait_ge(s["lo_o"], up("lo_o", it, i))
                    nc.tensor.matmul(ps[:, 6 + i, :], st.wo[:, :], o[:, i, :], start=True, stop=True).then_inc(s["lo_y_ps"], 1)

        @block.scalar
        def _(act):
            with act.Fori(0, B) as it:
                for i in range(HALVES):
                    act.wait_ge(s["lo_av"], up("lo_av", it, (3, U - 1)[i]))
                    nc.scalar.activation(o[:, i, :], ps[:, 4 + i, :], ACT.Copy).then_inc(s["lo_o"], 1)

        @block.vector
        def _(dve):
            link = Chain(c, dve, "lo_dve", 1)
            dve.wait_ge(s["lo_w"], 16)
            dve.sem_inc(s["lo_done"], 1)
            with dve.Fori(0, B) as it:
                link.start(it)
                dve.wait_ge(s["lo_done"], it + 1)
                here = tokens(it * T, T)
                for dst, src in ((z, st.z[:, :, :].rearrange("p b t -> p (b t)")),
                                 (q, st.q[:, :, :].rearrange("p b t -> p (b t)")),
                                 (v, st.v[:, :, :, :].rearrange("p b t e -> p (b t e)"))):
                    last = nc.vector.tensor_scalar(dst[:, :], src[:, here], 1.0, None, ALU.mult)
                last.then_inc(s["lo_in"], 1)
                for n, (i, k) in enumerate(units):
                    q0, q1 = start(i, k), (i + 1) * BLK
                    dve.wait_ge(s["lo_s_ps"], up("lo_s_ps", it, n))
                    if n >= 3:
                        dve.wait_ge(s["lo_av"], up("lo_av", it, n - 3))
                    off = P if k >= 4 * i else 0
                    if off:
                        last = nc.vector.tensor_tensor(pt[:, n % 3, 0:P], ps[:, n % 3, 0:P], causal[:, :], ALU.mult)
                    if q1 - q0 > off:
                        last = nc.vector.tensor_scalar(pt[:, n % 3, off:q1 - q0], ps[:, n % 3, off:q1 - q0], 1.0, None,
                                                       ALU.mult)
                    last.then_inc(s["lo_p"], 1)
                for i in range(HALVES):
                    here = tokens(it * T + i * BLK, BLK)
                    dve.wait_ge(s["lo_y_ps"], up("lo_y_ps", it, i))
                    ins = nc.vector.scalar_tensor_tensor(c.xt[:, here], ps[:, 6 + i, :], st.cols[:, 2:3], c.xt[:, here],
                                                         ALU.add, ALU.add)
                    if i == 0:
                        link(ins)
                ins.then_inc(s["lo_done"], 1)
            link.close()


def linear_attention(c):
    with ExitStack() as ctx:
        st = LinearState(c, ctx)
        linear_project_phase(c, st)
        linear_scan_phase(c, st)
        linear_output_phase(c, st)


def more_constants(np):
    f = np.float32
    o = {}
    blk = np.zeros((P, P), f)
    blk[:64, :64] = blk[64:, 64:] = 1
    o["c_blk64"] = blk
    i, j = np.arange(P)[:, None], np.arange(2 * P)[None, :] - P
    ok = (i >= j) & (i <= j + 64)
    band = np.where(ok, 0, -1e30).astype(f)
    first = np.where(ok & (j >= 0), 0, -1e30).astype(f)
    o["c_band"] = np.stack([first, band], 1)
    half = np.arange(0, 64, 2, dtype=f)
    inv = (f(1.0) / f(10000.0) ** (half / f(64))).astype(f)
    t = np.arange(T, dtype=f)
    fr = (t[:, None] * inv[None, :]).astype(f)
    base = ((half + f(0.4 * 64)) / f(1.4 * 64)).astype(f)
    power = ((t - T // 2) / f(32)).astype(f)
    scale = (base[None, :] ** power[:, None]).astype(f)
    cos, sin = np.cos(fr), np.sin(fr)
    tabs = []
    for sc in (scale, 1 / scale):
        tabs.append(np.concatenate([cos * sc] * 4, 1).T)
        tabs.append(np.concatenate([-sin * sc, sin * sc] * 2, 1).T)
    o["c_tab"] = np.stack(tabs, 1).astype(f)
    m8 = np.zeros((P, P), f)
    for j in range(4):
        m8[32 * j:32 * j + 8, 32 * j:32 * j + 8] = 1 / 8
    o["c_mean8"] = m8
    k, q = np.arange(P)[:, None], np.arange(P)[None, :]
    causal = (k <= q).astype(f)
    o["c_causal"] = causal
    o["c_ga0_mask"] = np.stack([causal, causal], 1)
    o["c_ga1_mask"] = np.stack([((q - k >= 0) & (q - k < 32)), (q + P - k < 32)], 1).astype(f)
    for n, theta in enumerate((1000000.0, 10000.0)):
        inv = (f(1.0) / f(theta) ** (np.arange(0, 8, 2, dtype=f) / f(8))).astype(f)
        fr = (t[:, None] * inv[None, :]).astype(f)
        tab = np.zeros((P, 2, T), f)
        for j in range(4):
            for e in range(8):
                tab[32 * j + e, 0] = np.cos(fr[:, e // 2])
                tab[32 * j + e, 1] = np.sin(fr[:, e // 2]) * (1 if e % 2 else -1)
        o[f"c_ga{n}_tab"] = tab
    sel = np.zeros((8, 8, P), f)
    sel[np.arange(8), np.arange(8)] = 1
    o["c_sel"] = sel
    o["c_order"] = np.broadcast_to(np.arange(8, 0, -1, dtype=f), (P, 4, 8))
    low = np.zeros((4, 2, 16, 16), f)
    low[:, 0] = np.triu(np.ones((16, 16), f), 1)
    low[:, 1] = np.eye(16, dtype=f)
    o["c_low"] = low
    o["c_ones"] = np.ones((P, 1), f)
    return o


def halves_swapped(np, w):
    w = w.reshape(w.shape[:-1] + (w.shape[-1] // 64, 2, 32))
    return w[..., ::-1, :].reshape(w.shape[:-3] + (-1,))


def more_layout(np, x):
    o = {}
    w = x["L0_ffn_wqkv"]
    qk = w[:, :, 0:1024].reshape(2, P, 2, 512)
    o["wa_wqk"], o["wa_wsw"], o["wa_wv"] = qk, halves_swapped(np, qk), w[:, :, 1024:]
    o["wa_wo"] = x["L0_ffn_wo"].reshape(2, 4, P, P).transpose(0, 2, 1, 3)
    o["wa_w1"] = x["L0_ffn_w1"]
    w2 = np.zeros((2, 3 * P, P), w.dtype)
    w2[:, :HID] = x["L0_ffn_w2"]
    o["wa_w2"] = w2.reshape(2, 3, P, P).transpose(0, 2, 1, 3)
    qs, ks = x["L0_ffn_q_scale"], x["L0_ffn_k_scale"]
    four = np.stack([qs, halves_swapped(np, qs), ks, halves_swapped(np, ks)], 2)
    o["wa_qks"] = np.concatenate([four, four], 1)
    o["wa_lnc"] = np.stack([x["L0_ffn_ln_g"], x["L0_ffn_ln_b"], x["L0_ffn_b2"]], 2)
    b1 = np.zeros((2, 2, 3 * P), w.dtype)
    b1[:, :, :HID] = x["L0_ffn_b1"].reshape(2, 2, HID)
    o["wa_b1"] = b1.reshape(2, 2, 3, P).transpose(0, 3, 2, 1)
    for n, p in enumerate(("g", "l")):
        def padded(w):
            z = np.zeros(w.shape[:-1] + (32,), w.dtype)
            z[..., :8] = w
            return z
        wq = x[f"L1_attn_{p}_wq"].reshape(P, 4, 4, 8).transpose(0, 2, 1, 3)
        wk = x["L1_attn_g_k_up" if n == 0 else "L1_attn_l_wk"]
        wk = wk.reshape(wk.shape[0], 4, 8)
        both = lambda w: [padded(w), padded(w.reshape(w.shape[:-1] + (4, 2))[..., ::-1].reshape(w.shape))]
        o[f"ga{n}_wq"] = np.stack(both(wq), 1).reshape(P, 2, 4, P)
        o[f"ga{n}_wk"] = np.stack(both(wk), 1).reshape(wk.shape[0], 2, P)
        o[f"ga{n}_wv"] = x["L1_attn_g_v_up" if n == 0 else "L1_attn_l_wv"]
        wo = np.zeros((4, 32, 4, P), wq.dtype)
        wo[:, :8] = x[f"L1_attn_{p}_wo"].reshape(4, 4, 8, P).transpose(0, 2, 1, 3)
        o[f"ga{n}_wo"] = wo.reshape(P, 4, P)
        o[f"ga{n}_nw"] = x[f"L1_attn_norm{n + 1}_w"].reshape(P, 1)
    o["ga0_wd"] = x["L1_attn_g_kv_down"]
    o["moe1_w1"] = np.concatenate([x["L1_ffn_W1"], x["L1_ffn_Ws1"][None]]).transpose(1, 0, 2)
    o["moe1_w3"] = np.concatenate([x["L1_ffn_W3"], x["L1_ffn_Ws3"][None]]).transpose(1, 0, 2)
    o["moe1_w2"] = np.concatenate([x["L1_ffn_W2"], x["L1_ffn_Ws2"][None]]).reshape(9, 2, P, P).transpose(2, 0, 1, 3)
    o["moe1_wr"] = x["L1_ffn_Wr"]
    gcon = np.zeros((P, 2 + 32), wo.dtype)
    gcon[:, 2:] = np.tile(x["L1_ffn_rb"], 4)
    o["moe1_gcon"] = gcon
    o["moe3_w1"] = x["L3_ffn_w1"].transpose(2, 0, 1)
    o["moe3_w2"] = x["L3_ffn_w2"].reshape(8, P, 2, P).transpose(3, 0, 2, 1)
    o["moe3_wr"] = x["L3_ffn_gate_w"].T
    gcon = np.zeros((P, 2 + 32), wo.dtype)
    gcon[:, 0], gcon[:, 1] = x["L3_ffn_ln_gamma"], x["L3_ffn_ln_beta"]
    o["moe3_gcon"] = gcon
    o["th_w"] = x["L2_attn_W"].T
    o["ql_w"] = x["L2_ffn_weight"]
    o["ql_b"] = x["L2_ffn_bias"].reshape(P, 1)
    o["lp_w"] = np.stack([x["L3_attn_Wq"].T, x["L3_attn_Wk"].T, x["L3_attn_Wv"].T], 1)
    o["lp_bv"] = np.broadcast_to(x["L3_attn_bv"], (P, P))
    o["li_wo"] = x["L3_attn_Wo"].T
    o["li_cols"] = np.stack([x["L3_attn_bq"], x["L3_attn_bk"], x["L3_attn_bo"]], 1)
    return o



def build(nc, d):
    with ExitStack() as ctx:
        c = Core(nc, ctx, d)
        load_phase(c)
        norm_phase(c, 0)
        full_attention_phase(c)
        window_phase(c, 0)
        window_phase(c, 1)
        c.retire("load_", "fa_", "wa_", "wm_")
        norm_phase(c, 1)
        experts_phase(c, 1)
        grouped_attention_phase(c, 0)
        grouped_attention_phase(c, 1)
        c.retire("moe1_", "ga0_", "ga1_")
        norm_phase(c, 2)
        threshold_attention_phase(c)
        quantised_linear_phase(c)
        norm_phase(c, 3)
        experts_phase(c, 3)
        linear_attention(c)
        store_phase(c)


def constants():
    import numpy as np
    f = np.float32
    out = {"c_ident": np.eye(P, dtype=f)}
    row8 = np.zeros((P, P), f)
    for j in range(4):
        row8[32 * j + 8, 32 * j:32 * j + 32] = 1
    out["c_row8"] = row8
    out.update(more_constants(np))
    return out


def heads_padded(np, w):
    w = w.reshape(w.shape[:-1] + (4, 4, 8))
    out = np.zeros(w.shape[:-1] + (32,), w.dtype)
    out[..., :8] = w
    return out.reshape(w.shape[:-3] + (4, P))


def laid_out(np, x):
    o = {"z": x["L0_attn_z"]}
    wqkv, bqkv = x["L0_attn_W_qkv"], x["L0_attn_b_qkv"]
    o["fa_wq"] = heads_padded(np, wqkv[:, 0:P])
    o["fa_wk"] = heads_padded(np, wqkv[:, P:2 * P])
    o["fa_wv"] = wqkv[:, 2 * P:]
    o["fa_wp"] = heads_padded(np, x["L0_attn_W_proj"].T).transpose(2, 1, 0)
    o["fa_bq"] = heads_padded(np, bqkv[0:P]).T
    bk = heads_padded(np, bqkv[P:2 * P]).T.copy()
    bk[8::32] = 1
    o["fa_bk"] = bk
    o["fa_bv"] = np.broadcast_to(bqkv[2 * P:], (P, P))
    o["fa_cols"] = np.stack([x["L0_attn_ln_w"], x["L0_attn_ln_b"], x["L0_attn_b_proj"]], 1)
    o.update(more_layout(np, x))
    return o


def kernel(**inputs):
    import numpy as np
    import concourse.bacc as bacc
    from concourse.bass_utils import run_bass_kernel_spmd

    nc = bacc.Bacc("TRN2", target_bir_lowering=False, num_devices=1)
    host = constants()
    host.update(laid_out(np, {k: np.asarray(a) for k, a in inputs.items()}))
    arrays, d = {}, {}
    for name, a in host.items():
        arrays[f"in_{name}"] = np.ascontiguousarray(a)
        d[name] = nc.dram_tensor(f"in_{name}", a.shape, mybir.dt.from_np(a.dtype), kind="ExternalInput").ap()
    d["out"] = nc.dram_tensor("out_x", (B, T, P), F32, kind="ExternalOutput").ap()
    build(nc, d)
    r = run_bass_kernel_spmd(nc, [arrays], core_ids=[0])
    return r.results[0]["out_x"]
```

```python
from contextlib import ExitStack

import concourse.bass as bass
from concourse import mybir

F32 = mybir.dt.float32
BF16 = mybir.dt.bfloat16
U32 = mybir.dt.uint32
ALU = mybir.AluOpType
ACT = mybir.ActivationFunctionType
AX = mybir.AxisListType.X

P = 128
B, T = 4, 1024
NTOK = B * T
BLK = 512
NB = NTOK // BLK
HALVES = T // BLK
TILES = T // P


class Core:

    def __init__(self, nc, ctx, d):
        self.nc, self.ctx, self.d = nc, ctx, d
        self.sem, self.per = {}, {}
        self.xt = self.sb(ctx, "xt", [P, NTOK])
        self.xnt = self.sb(ctx, "xnt", [P, NTOK])
        self.ps = ctx.enter_context(nc.psum_tensor("ps", [P, 8, BLK], F32))
        self.mean_w = self.sb(ctx, "mean_w", [P, P])
        self.ident = self.sb(ctx, "ident", [P, P])
        self.eps5 = self.sb(ctx, "eps5", [P, 1])
        self.eps6 = self.sb(ctx, "eps6", [P, 1])

    def sb(self, ctx, name, shape, dt=F32):
        return ctx.enter_context(self.nc.sbuf_tensor(name, shape, dt))

    def signals(self, **per):
        for name, n in per.items():
            if name not in self.sem:
                self.sem[name] = self.nc.alloc_semaphore(name)
                self.per[name] = n
        return self.sem

    def retire(self, *prefixes):
        names = [n for n in self.sem if n.startswith(prefixes)]
        with self.nc.Block() as block:
            @block.gpsimd
            def _(pool):
                for n in names:
                    pool.sem_clear(self.sem[n])
        for n in names:
            self.nc.release_semaphore(self.sem.pop(n))
            del self.per[n]

    def up(self, name, it, i=0):
        return it * self.per[name] + (i + 1)


class Chain:

    def __init__(self, core, eng, name, per):
        core.signals(**{name: per})
        self.core, self.eng, self.name, self.n = core, eng, name, 0
        self.it = 0

    def start(self, it):
        self.it, self.n = it, 0

    def __call__(self, ins):
        ins.then_inc(self.core.sem[self.name], 1)
        self.eng.wait_ge(self.core.sem[self.name], self.core.up(self.name, self.it, self.n))
        self.n += 1

    def close(self):
        assert self.n == self.core.per[self.name], (self.name, self.n)


class LocalChain:

    def __init__(self, core, eng, name):
        core.signals(**{name: 1})
        self.sem, self.eng, self.n = core.sem[name], eng, 0

    def __call__(self, ins):
        self.n += 1
        ins.then_inc(self.sem, 1)
        self.eng.wait_ge(self.sem, self.n)

    def clear(self):
        self.n = 0
        self.eng.sem_clear(self.sem)


def tokens(start, n):
    return bass.ds(start, n)


def load_phase(c):
    s = c.signals(load_in=1, load_const=1, load_set=1, load_ps=32, load_xt=32)
    nc, d = c.nc, c.d
    with ExitStack() as ctx:
        raw = c.sb(ctx, "load_raw", [P, NTOK // P, P])
        block = ctx.enter_context(nc.Block())

        @block.sync
        def _(sp):
            sp.dma_start(c.ident[:, :], d["c_ident"]).then_inc(s["load_const"], 16)
            z = d["z"].rearrange("b (n p) d -> p (b n) d", p=P)
            for i in range(4):
                sp.dma_start(raw[:, 8 * i:8 * i + 8, :], z[:, 8 * i:8 * i + 8, :]).then_inc(s["load_in"], 16)
            sp.wait_ge(s["load_const"], 16)
            sp.wait_ge(s["load_in"], 64)

        @block.vector
        def _(dve):
            nc.vector.memset(c.mean_w[:, :], 1.0 / P).then_inc(s["load_set"], 1)
            nc.vector.memset(c.eps5[:, :], 1e-5).then_inc(s["load_set"], 1)
            nc.vector.memset(c.eps6[:, :], 1e-6).then_inc(s["load_set"], 1)
            for n in range(8):
                dve.wait_ge(s["load_ps"], 4 * n + 4)
                nc.vector.tensor_copy(c.xt[:, n * BLK:(n + 1) * BLK], c.ps[:, n, :]).then_inc(s["load_xt"], 1)

        @block.tensor
        def _(pe):
            pe.wait_ge(s["load_const"], 16)
            pe.wait_ge(s["load_in"], 64)
            for n in range(32):
                nc.tensor.transpose(c.ps[:, n // 4, (n % 4) * P:(n % 4 + 1) * P], raw[:, n, :],
                                    c.ident[:, :]).then_inc(s["load_ps"], 1)


def norm_phase(c, run):
    s = c.signals(ln_mean=1, ln_xc=1, ln_sq=1, ln_var=1, ln_sd=1, ln_done=1)
    nc = c.nc
    with ExitStack() as ctx:
        xc = c.sb(ctx, f"ln{run}_xc", [P, BLK])
        sq = c.sb(ctx, f"ln{run}_sq", [P, BLK])
        sd = c.sb(ctx, f"ln{run}_sd", [P, BLK])
        block = ctx.enter_context(nc.Block())

        @block.tensor
        def _(pe):
            if run == 0:
                pe.sem_inc(s["ln_done"], 1)
            with pe.Fori(run * NB, (run + 1) * NB) as it:
                pe.wait_ge(s["ln_done"], it + 1)
                nc.tensor.matmul(c.ps[:, 0, :], c.mean_w[:, :], c.xt[:, tokens((it - run * NB) * BLK, BLK)],
                                 start=True, stop=True).then_inc(s["ln_mean"], 1)
                pe.wait_ge(s["ln_sq"], it + 1)
                nc.tensor.matmul(c.ps[:, 1, :], c.mean_w[:, :], sq[:, :],
                                 start=True, stop=True).then_inc(s["ln_var"], 1)

        @block.scalar
        def _(act):
            with act.Fori(run * NB, (run + 1) * NB) as it:
                act.wait_ge(s["ln_xc"], it + 1)
                nc.scalar.activation(sq[:, :], xc[:, :], ACT.Square).then_inc(s["ln_sq"], 1)
                act.wait_ge(s["ln_var"], it + 1)
                nc.scalar.activation(sd[:, :], c.ps[:, 1, :], ACT.Sqrt, bias=c.eps5[:, 0:1]).then_inc(s["ln_sd"], 1)

        @block.vector
        def _(dve):
            link = Chain(c, dve, "ln_dve", 1)
            with dve.Fori(run * NB, (run + 1) * NB) as it:
                link.start(it)
                here = tokens((it - run * NB) * BLK, BLK)
                dve.wait_ge(s["ln_mean"], it + 1)
                nc.vector.tensor_tensor(xc[:, :], c.xt[:, here], c.ps[:, 0, :], ALU.subtract).then_inc(s["ln_xc"], 1)
                dve.wait_ge(s["ln_sd"], it + 1)
                link(nc.vector.reciprocal(sd[:, :], sd[:, :]))
                nc.vector.tensor_tensor(c.xnt[:, here], xc[:, :], sd[:, :], ALU.mult).then_inc(s["ln_done"], 1)
            link.close()


def store_phase(c):
    s = c.signals(store_ps=8, store_sb=8, store_out=1)
    nc = c.nc
    with ExitStack() as ctx:
        rows = c.sb(ctx, "store_rows", [P, NTOK // P, P])
        block = ctx.enter_context(nc.Block())

        @block.tensor
        def _(pe):
            for n in range(8):
                for i in range(4):
                    t = 4 * n + i
                    last = nc.tensor.transpose(c.ps[:, n, i * P:(i + 1) * P], c.xt[:, t * P:(t + 1) * P],
                                               c.ident[:, :])
                last.then_inc(s["store_ps"], 1)

        @block.vector
        def _(dve):
            for n in range(8):
                dve.wait_ge(s["store_ps"], n + 1)
                nc.vector.tensor_copy(rows[:, 4 * n:4 * n + 4, :],
                                      c.ps[:, n, :].rearrange("p (i d) -> p i d", i=4)).then_inc(s["store_sb"], 1)

        @block.sync
        def _(sp):
            out = c.d["out"].rearrange("b (n p) d -> p (b n) d", p=P)
            for n in range(8):
                sp.wait_ge(s["store_sb"], n + 1)
                sp.dma_start(out[:, 4 * n:4 * n + 4, :], rows[:, 4 * n:4 * n + 4, :]).then_inc(s["store_out"], 16)
            sp.wait_ge(s["store_out"], 16 * 8)


NH0, HD0, GRP, NG0 = 16, 8, 4, 4
PARTS = 3
MROW = 96
KROWS = MROW + PARTS


def split_parts(nc, link, x, rest, parts):
    for k in range(PARTS - 1):
        link(nc.vector.tensor_scalar(parts[k], x, 1.0, None, ALU.mult))
        link(nc.vector.tensor_tensor(rest, x, parts[k], ALU.subtract))
        x = rest
    return nc.vector.tensor_scalar(parts[PARTS - 1], x, 1.0, None, ALU.mult)


def full_attention_phase(c):
    MU, EU = GRP * TILES, GRP * HALVES * TILES
    s = c.signals(fa_w=1, fa_set=1, fa_kset=1, fa_mean=2, fa_xc=2, fa_sq=2, fa_var=2, fa_sd=2, fa_zn=2,
                  fa_qk_ps=4, fa_qk=4, fa_split=4, fa_out=96, fa_rows=288, fa_v_ps=8, fa_v=8,
                  fa_s_ps=NG0 * MU, fa_max=NG0 * MU, fa_m_ps=8, fa_m=8, fa_m_in=NG0 * PARTS * 16,
                  fa_st=NG0 * EU, fa_exp=NG0 * EU, fa_av=NG0 * EU, fa_o=8, fa_sum_ps=8, fa_ot=8,
                  fa_y_ps=2, fa_done=1)
    nc, d, up = c.nc, c.d, c.up
    scale = float(HD0) ** -0.5
    scratch = nc.dram_tensor("fa_scratch", [2, PARTS, P, T], BF16, kind="Internal").ap()
    with ExitStack() as ctx:
        wqk = c.sb(ctx, "fa_wqk", [P, 2, P])
        wv = c.sb(ctx, "fa_wv", [P, P])
        wp = c.sb(ctx, "fa_wp", [P, NG0, P])
        cols = c.sb(ctx, "fa_cols", [P, 5])
        bv = c.sb(ctx, "fa_bv", [P, P])
        row8 = c.sb(ctx, "fa_row8", [P, P])
        znt = c.sb(ctx, "fa_znt", [P, T])
        tmp = c.sb(ctx, "fa_tmp", [P, 3, BLK])
        qf = c.sb(ctx, "fa_qf", [P, 2, BLK])
        qp = c.sb(ctx, "fa_qp", [P, 2, PARTS, T], BF16)
        q = c.sb(ctx, "fa_q6", [P, NH0, T], BF16)
        k = c.sb(ctx, "fa_k6", [P, NH0, T], BF16)
        mx = c.sb(ctx, "fa_mx", [P, 2, TILES, GRP])
        mf = c.sb(ctx, "fa_mf", [GRP, BLK])
        mp = c.sb(ctx, "fa_mp", [GRP, PARTS, T], BF16)
        v = c.sb(ctx, "fa_vt", [P, TILES, NH0, 32])
        pt = c.sb(ctx, "fa_pt", [P, 3, BLK])
        os = c.sb(ctx, "fa_os", [P, BLK])
        rs = c.sb(ctx, "fa_rs", [P, BLK])
        ot = c.sb(ctx, "fa_otb", [P, NG0, T])
        block = ctx.enter_context(nc.Block())
        ps = c.ps

        @block.sync
        def _(sp):
            loads = [(wqk[:, :, :], "fa_wqk"), (wv[:, :], "fa_wv"), (wp[:, :, :], "fa_wp"), (bv[:, :], "fa_bv"),
                     (cols[:, :], "fa_cols"), (row8[:, :], "c_row8")]
            for dst, name in loads:
                sp.dma_start(dst, d[name]).then_inc(s["fa_w"], 16)
            sp.wait_ge(s["fa_w"], 16 * 6)
            sp.wait_ge(s["fa_set"], 3)
            sp.wait_ge(s["fa_kset"], 2)
            with sp.Fori(0, B) as it:
                sp.wait_ge(s["fa_split"], up("fa_split", it, 3))
                for x in range(2):
                    for p in range(PARTS):
                        sp.dma_start(scratch[x, p], qp[:, x, p, :]).then_inc(s["fa_out"], 16)
                sp.wait_ge(s["fa_out"], (it + 1) * 96)
                for x, dst in ((0, q), (1, k)):
                    for r in range(9):
                        part = r // 3 if x == 0 else r % 3
                        sp.dma_start(dst[8 * r:8 * r + 8, :, :],
                                     scratch[x, part].rearrange("(h e) t -> e h t", e=HD0)).then_inc(s["fa_rows"], 16)
                for g in range(NG0):
                    sp.wait_ge(s["fa_m"], up("fa_m", it, 2 * g + 1))
                    for p in range(PARTS):
                        sp.dma_start(q[MROW + p:MROW + p + 1, GRP * g:GRP * (g + 1), :],
                                     mp[:, p, :]).then_inc(s["fa_m_in"], 16)
            sp.wait_ge(s["fa_m_in"], B * NG0 * PARTS * 16)

        @block.gpsimd
        def _(pool):
            nc.gpsimd.memset(v[:, :, :, :], 0.0).then_inc(s["fa_set"], 1)
            pool.wait_ge(s["fa_set"], 1)
            nc.gpsimd.memset(v[:, :, :, 8:9], 1.0).then_inc(s["fa_set"], 1)
            pool.wait_ge(s["fa_set"], 2)
            nc.gpsimd.memset(q[:, :, :], 0.0).then_inc(s["fa_set"], 1)

        @block.tensor
        def _(pe):
            pe.wait_ge(s["fa_w"], 16 * 6)
            pe.sem_inc(s["fa_done"], 1)
            with pe.Fori(0, B) as it:
                pe.wait_ge(s["fa_done"], it + 1)
                for i in range(HALVES):
                    if i:
                        pe.wait_ge(s["fa_zn"], up("fa_zn", it, i - 1))
                    nc.tensor.matmul(ps[:, 0, :], c.mean_w[:, :], c.xnt[:, tokens(it * T + i * BLK, BLK)],
                                     start=True, stop=True).then_inc(s["fa_mean"], 1)
                    pe.wait_ge(s["fa_sq"], up("fa_sq", it, i))
                    nc.tensor.matmul(ps[:, 1, :], c.mean_w[:, :], tmp[:, 1, :],
                                     start=True, stop=True).then_inc(s["fa_var"], 1)
                pe.wait_ge(s["fa_zn"], up("fa_zn", it, 1))
                for n in range(4):
                    if n >= 2:
                        pe.wait_ge(s["fa_qk"], up("fa_qk", it, n - 2))
                    nc.tensor.matmul(ps[:, n % 2, :], wqk[:, n // 2, :], znt[:, n % 2 * BLK:(n % 2 + 1) * BLK],
                                     start=True, stop=True).then_inc(s["fa_qk_ps"], 1)
                for t in range(TILES):
                    if t >= 2:
                        pe.wait_ge(s["fa_v"], up("fa_v", it, t - 2))
                    nc.tensor.matmul(ps[:, 2 + t % 2, 0:P], znt[:, t * P:(t + 1) * P], wv[:, :],
                                     start=True, stop=True).then_inc(s["fa_v_ps"], 1)
                pe.wait_ge(s["fa_v"], up("fa_v", it, 7))
                pe.wait_ge(s["fa_rows"], (it + 1) * 288)

                def by_query(n):
                    h, t = n // TILES, n % TILES
                    if n >= 2:
                        pe.wait_ge(s["fa_max"], up("fa_max", it, n - 2))
                    for i in range(HALVES):
                        last = nc.tensor.matmul(ps[:, 2 * (n % 2) + i, :], q[0:72, h, t * P:(t + 1) * P],
                                                k[0:72, h, i * BLK:(i + 1) * BLK], start=True, stop=True)
                    last.then_inc(s["fa_s_ps"], 1)

                def turn_maxima(g, i):
                    pe.wait_ge(s["fa_max"], up("fa_max", it, (g + 1) * MU - 1))
                    if i:
                        pe.wait_ge(s["fa_m"], up("fa_m", it, 2 * g))
                    elif g:
                        pe.wait_ge(s["fa_ot"], up("fa_ot", it, 2 * g - 2))
                    for t in range(4):
                        last = nc.tensor.transpose(ps[0:GRP, 7, t * P:(t + 1) * P], mx[:, g % 2, 4 * i + t, :],
                                                   c.ident[:, :])
                    last.then_inc(s["fa_m_ps"], 1)

                def by_key(n):
                    g, i, j, t = n // EU, n // 32 % 2, n // 8 % 4, n % 8
                    if n >= 2:
                        pe.wait_ge(s["fa_exp"], up("fa_exp", it, n - 2))
                    if n % EU == 0:
                        pe.wait_ge(s["fa_m_in"], it * NG0 * PARTS * 16 + (g + 1) * PARTS * 16)
                    h = GRP * g + j
                    nc.tensor.matmul(ps[:, 4 + n % 2, :], k[0:KROWS, h, t * P:(t + 1) * P],
                                     q[0:KROWS, h, i * BLK:(i + 1) * BLK], start=True, stop=True).then_inc(s["fa_st"], 1)

                def values(n):
                    g, j, t, m = n // EU, n // 8 % 4, n % 8, n // 32
                    if n % 32 == 0 and m:
                        pe.wait_ge(s["fa_o"], up("fa_o", it, m - 1))
                    pe.wait_ge(s["fa_exp"], up("fa_exp", it, n))
                    nc.tensor.matmul(ps[32 * j:32 * j + 32, 6, :], v[:, t, GRP * g + j, :], pt[:, n % 3, :],
                                     start=(t == 0), stop=(t == TILES - 1),
                                     tile_position=(0, 32 * j)).then_inc(s["fa_av"], 1)

                def sums(m):
                    pe.wait_ge(s["fa_o"], up("fa_o", it, m))
                    if m:
                        pe.wait_ge(s["fa_ot"], up("fa_ot", it, m - 1))
                    pe.wait_ge(s["fa_m"], up("fa_m", it, min(2 * (m // 2 + m % 2) + 1, 7)))
                    nc.tensor.matmul(ps[:, 7, :], row8[:, :], os[:, :],
                                     start=True, stop=True).then_inc(s["fa_sum_ps"], 1)

                for n in range(MU):
                    by_query(n)
                for i in range(HALVES):
                    turn_maxima(0, i)
                for n in range(NG0 * EU + 2):
                    g = n // EU
                    if n < NG0 * EU:
                        if n % EU == 0 and n:
                            values(n - 2)
                            values(n - 1)
                            for i in range(HALVES):
                                turn_maxima(g, i)
                            sums(2 * g - 1)
                        by_key(n)
                        if n % 2 == 0 and g + 1 < NG0:
                            by_query((g + 1) * MU + n % EU // 2)
                    if n >= 2 and not (n < NG0 * EU and n % EU < 2):
                        values(n - 2)
                    if n < NG0 * EU and n % EU == 40:
                        sums(2 * g)
                sums(7)
                pe.wait_ge(s["fa_ot"], up("fa_ot", it, 7))
                for i in range(HALVES):
                    for g in range(NG0):
                        last = nc.tensor.matmul(ps[:, i, :], wp[:, g, :], ot[:, g, i * BLK:(i + 1) * BLK],
                                                start=(g == 0), stop=(g == NG0 - 1))
                    last.then_inc(s["fa_y_ps"], 1)

        @block.scalar
        def _(act):
            act.wait_ge(s["fa_w"], 16 * 6)
            with act.Fori(0, B) as it:
                for i in range(HALVES):
                    act.wait_ge(s["fa_xc"], up("fa_xc", it, i))
                    nc.scalar.activation(tmp[:, 1, :], tmp[:, 0, :], ACT.Square).then_inc(s["fa_sq"], 1)
                    act.wait_ge(s["fa_var"], up("fa_var", it, i))
                    nc.scalar.activation(tmp[:, 2, :], ps[:, 1, :], ACT.Sqrt,
                                         bias=c.eps5[:, 0:1]).then_inc(s["fa_sd"], 1)
                for n in range(4):
                    act.wait_ge(s["fa_qk_ps"], up("fa_qk_ps", it, n))
                    if n >= 2:
                        act.wait_ge(s["fa_split"], up("fa_split", it, n - 2))
                    nc.scalar.activation(qf[:, n % 2, :], ps[:, n % 2, :], ACT.Identity,
                                         bias=cols[:, 3 + n // 2:4 + n // 2]).then_inc(s["fa_qk"], 1)

                def copy_out(m):
                    act.wait_ge(s["fa_av"], up("fa_av", it, 32 * m + 31))
                    if m:
                        act.wait_ge(s["fa_ot"], up("fa_ot", it, m - 1))
                    nc.scalar.activation(os[:, :], ps[:, 6, :], ACT.Copy).then_inc(s["fa_o"], 1)

                for n in range(NG0 * EU):
                    if n % EU == 0 and n:
                        copy_out(n // 32 - 1)
                    act.wait_ge(s["fa_st"], up("fa_st", it, n))
                    if n >= 3:
                        act.wait_ge(s["fa_av"], up("fa_av", it, n - 3))
                    nc.scalar.activation(pt[:, n % 3, :], ps[:, 4 + n % 2, :], ACT.Exp,
                                         scale=scale).then_inc(s["fa_exp"], 1)
                    if n % EU == 33:
                        copy_out(n // 32 - 1)
                copy_out(7)

        @block.vector
        def _(dve):
            link = Chain(c, dve, "fa_dve", 2 * HALVES + 4 * 4 + 8 * 4 + 8 + HALVES)
            nc.vector.memset(k[:, :, :], 0.0).then_inc(s["fa_kset"], 1)
            dve.wait_ge(s["fa_kset"], 1)
            nc.vector.memset(k[MROW:P, :, :], 1.0).then_inc(s["fa_kset"], 1)
            dve.wait_ge(s["fa_w"], 16 * 6)
            dve.wait_ge(s["fa_set"], 3)
            with dve.Fori(0, B) as it:
                link.start(it)
                for i in range(HALVES):
                    dve.wait_ge(s["fa_mean"], up("fa_mean", it, i))
                    nc.vector.tensor_tensor(tmp[:, 0, :], c.xnt[:, tokens(it * T + i * BLK, BLK)], ps[:, 0, :],
                                            ALU.subtract).then_inc(s["fa_xc"], 1)
                    dve.wait_ge(s["fa_sd"], up("fa_sd", it, i))
                    link(nc.vector.reciprocal(tmp[:, 2, :], tmp[:, 2, :]))
                    link(nc.vector.tensor_tensor(tmp[:, 1, :], tmp[:, 0, :], tmp[:, 2, :], ALU.mult))
                    nc.vector.tensor_scalar(znt[:, i * BLK:(i + 1) * BLK], tmp[:, 1, :], cols[:, 0:1], cols[:, 1:2],
                                            ALU.mult, ALU.add).then_inc(s["fa_zn"], 1)
                for n in range(4):
                    half = slice(n % 2 * BLK, (n % 2 + 1) * BLK)
                    dve.wait_ge(s["fa_qk"], up("fa_qk", it, n))
                    if n:
                        dve.wait_ge(s["fa_split"], up("fa_split", it, n - 1))
                    split_parts(nc, link, qf[:, n % 2, :], tmp[:, 0, :],
                                [qp[:, n // 2, p, half] for p in range(PARTS)]).then_inc(s["fa_split"], 1)
                for t in range(TILES):
                    dve.wait_ge(s["fa_v_ps"], up("fa_v_ps", it, t))
                    nc.vector.tensor_tensor(v[:, t, :, 0:8],
                                            ps[:, 2 + t % 2, 0:P].rearrange("p (h e) -> p h e", e=8),
                                            bv[:, :].rearrange("p (h e) -> p h e", e=8),
                                            ALU.add).then_inc(s["fa_v"], 1)

                def maxima(n):
                    g, j, t = n // MU, n // TILES % GRP, n % TILES
                    dve.wait_ge(s["fa_s_ps"], up("fa_s_ps", it, n))
                    nc.vector.tensor_reduce(mx[:, g % 2, t, j:j + 1], ps[:, 2 * (n % 2):2 * (n % 2) + 2, :],
                                            mybir.AxisListType.XY, ALU.max, negate=True).then_inc(s["fa_max"], 1)

                def split_maxima(g):
                    for i in range(HALVES):
                        half = slice(i * BLK, (i + 1) * BLK)
                        dve.wait_ge(s["fa_m_ps"], up("fa_m_ps", it, 2 * g + i))
                        if i == 0 and g:
                            dve.wait_ge(s["fa_m_in"], it * NG0 * PARTS * 16 + g * PARTS * 16)
                        split_parts(nc, link, ps[0:GRP, 7, :], mf[:, :],
                                    [mp[:, p, half] for p in range(PARTS)]).then_inc(s["fa_m"], 1)
                        dve.wait_ge(s["fa_m"], up("fa_m", it, 2 * g + i))

                def normalise(m):
                    g, i = m // 2, m % 2
                    dve.wait_ge(s["fa_sum_ps"], up("fa_sum_ps", it, m))
                    link(nc.vector.reciprocal(rs[:, :], ps[:, 7, :]))
                    nc.vector.tensor_tensor(ot[:, g, i * BLK:(i + 1) * BLK], os[:, :], rs[:, :],
                                            ALU.mult).then_inc(s["fa_ot"], 1)
                    dve.wait_ge(s["fa_ot"], up("fa_ot", it, m))

                for n in range(MU):
                    maxima(n)
                split_maxima(0)
                for g in range(NG0):
                    if g + 1 < NG0:
                        for n in range(20):
                            maxima((g + 1) * MU + n)
                    normalise(2 * g)
                    if g + 1 < NG0:
                        for n in range(20, MU):
                            maxima((g + 1) * MU + n)
                        split_maxima(g + 1)
                    normalise(2 * g + 1)
                for i in range(HALVES):
                    here = tokens(it * T + i * BLK, BLK)
                    dve.wait_ge(s["fa_y_ps"], up("fa_y_ps", it, i))
                    link(nc.vector.scalar_tensor_tensor(tmp[:, i, :], ps[:, i, :], cols[:, 2:3],
                                                        c.xnt[:, here], ALU.add, ALU.add))
                    ins = nc.vector.tensor_tensor(c.xt[:, here], c.xt[:, here], tmp[:, i, :], ALU.add)
                    if i == HALVES - 1:
                        ins.then_inc(s["fa_done"], 1)
            link.close()


HD1, NPAIR = 64, 4
HID = 341
CHUNKS = [(0, 128), (128, 128), (256, HID - 256)]


def shifted_copy(nc, c, dst, start, link, last):
    link(nc.vector.tensor_scalar(dst[0:64, :], c.xnt[0:64, tokens(start, T)], 1.0, None, ALU.mult))
    nc.vector.tensor_scalar(dst[64:P, 1:T], c.xnt[64:P, tokens(start, T - 1)], 1.0, None, ALU.mult).then_inc(last, 1)


def window_phase(c, run):
    QK, U = 16, 2 * TILES
    s = c.signals(wa_w=1, wa_set=1, wa_h=1, wa_qk_ps=QK, wa_sq=QK, wa_ss=2, wa_sd=2, wa_r=1, wa_rot=QK, wa_raw=QK,
                  wa_b_ps=QK, wa_qk=QK,
                  wa_v_ps=TILES, wa_v=TILES, wa_s_ps=U, wa_sm=U, wa_nmx=U, wa_exp=U, wa_p=U, wa_t_ps=U, wa_t=U,
                  wa_o_ps=U, wa_o=U, wa_y_ps=TILES, wa_y=TILES,
                  wm_h=1, wm_mean=2, wm_xc=2, wm_sq=2, wm_var=2, wm_sd=2, wm_n=2, wm_ag=6, wm_gelu=6, wm_hg=6,
                  wm_y_ps=2, wm_y=2, wa_done=1)
    nc, d, up = c.nc, c.d, c.up
    ps = c.ps
    NW = 16
    with ExitStack() as ctx:
        name = lambda n: f"wa{run}_{n}"
        sb = lambda n, shape: c.sb(ctx, name(n), shape)
        wqk = sb("wqk", [P, 2, BLK])
        wsw = sb("wsw", [P, 2, BLK])
        wv = sb("wv", [P, BLK])
        wo = sb("wo", [P, NPAIR, P])
        w1 = sb("w1", [P, 2 * HID])
        w2 = sb("w2", [P, 3, P])
        qks = sb("qks", [P, 4])
        lnc = sb("lnc", [P, 3])
        b1 = sb("b1", [P, 3, 2])
        tab = sb("tab", [P, 4, T])
        band = sb("band", [P, 2, 2 * P])
        gather = sb("gather", [P, 8, 16])
        spread = sb("spread", [P, 8, P])
        length = sb("length", [P, T])
        h = sb("h", [P, T])
        sq = sb("sq", [P, 2, BLK])
        sd = sb("sd", [P, 2, BLK])
        rot = sb("rot", [P, 2, BLK])
        qt = sb("qt", [P, NPAIR, P + T])
        kt = sb("kt", [P, NPAIR, P + T])
        v = sb("v", [P, 1 + TILES, BLK])
        sm = sb("sm", [P, 3, 4, 2 * P])
        nmx = sb("nmx", [P, 3, 4])
        tot = sb("tot", [P, 3, 4])
        pt = sb("pt", [P, 2, 4, 2, P])
        ot = sb("ot", [P, 2, NPAIR, P])
        hg = sb("hg", [P, 3, BLK])
        block = ctx.enter_context(nc.Block())
        ITS = (run * B, (run + 1) * B)

        @block.sync
        def _(sp):
            loads = [(wqk[:, :, :], d["wa_wqk"][run]), (wsw[:, :, :], d["wa_wsw"][run]), (wv[:, :], d["wa_wv"][run]),
                     (wo[:, :, :], d["wa_wo"][run]), (w1[:, :], d["wa_w1"][run]), (w2[:, :, :], d["wa_w2"][run]),
                     (qks[:, :], d["wa_qks"][run]),
                     (lnc[:, :], d["wa_lnc"][run]), (b1[:, :, :], d["wa_b1"][run]),
                     (tab[:, :, :], d["c_tab"]),
                     (band[:, :, :], d["c_band"]), (gather[:, :, :], d["c_gather"]), (spread[:, :, :], d["c_spread"])]
            for dst, src in loads:
                sp.dma_start(dst, src).then_inc(s["wa_w"], 16)
            sp.wait_ge(s["wa_w"], 16 * 13 * (run + 1))

        @block.tensor
        def _(pe):
            pe.wait_ge(s["wa_w"], 16 * 13 * (run + 1))
            pe.wait_ge(s["wa_set"], 4 * (run + 1))
            with pe.Fori(*ITS) as it:
                pe.wait_ge(s["wa_h"], up("wa_h", it))

                def square_sums(n):
                    x, p, i = n // 8, n % 8 // 2, n % 2
                    pe.wait_ge(s["wa_sq"], up("wa_sq", it, n))
                    ins = nc.tensor.matmul(ps[0:16, 4 + i, :], gather[:, 4 * x + p, :], sq[:, n % 2, :],
                                           start=(n < 2), stop=(n >= QK - 2))
                    if n >= QK - 2:
                        ins.then_inc(s["wa_ss"], 1)

                for n in range(QK):
                    x, p, i = n // 8, n % 8 // 2, n % 2
                    if n >= 2:
                        pe.wait_ge(s["wa_rot"], up("wa_rot", it, n - 2))
                    nc.tensor.matmul(ps[:, n % 2, :], wqk[:, x, p * P:(p + 1) * P], h[:, i * BLK:(i + 1) * BLK],
                                     start=True, stop=True)
                    nc.tensor.matmul(ps[:, 2 + n % 2, :], wsw[:, x, p * P:(p + 1) * P], h[:, i * BLK:(i + 1) * BLK],
                                     start=True, stop=True).then_inc(s["wa_qk_ps"], 1)
                    if n:
                        square_sums(n - 1)
                square_sums(QK - 1)
                for t in range(TILES):
                    if t >= 2:
                        pe.wait_ge(s["wa_v"], up("wa_v", it, t - 2))
                    nc.tensor.matmul(ps[:, 6 + t % 2, :], h[:, t * P:(t + 1) * P], wv[:, :],
                                     start=True, stop=True).then_inc(s["wa_v_ps"], 1)
                pe.wait_ge(s["wa_raw"], up("wa_raw", it, QK - 1))
                pe.wait_ge(s["wa_r"], up("wa_r", it))
                for n in range(QK):
                    x, p, i = n // 8, n % 8 // 2, n % 2
                    if n >= 2:
                        pe.wait_ge(s["wa_qk"], up("wa_qk", it, n - 2))
                    nc.tensor.matmul(ps[:, n % 2, :], spread[:, 4 * x + p, :], length[:, i * BLK:(i + 1) * BLK],
                                     start=True, stop=True).then_inc(s["wa_b_ps"], 1)
                pe.wait_ge(s["wa_qk"], up("wa_qk", it, QK - 1))
                pe.wait_ge(s["wa_v"], up("wa_v", it, TILES - 1))

                def scores(u):
                    t, hh = u // 2, u % 2
                    if u >= 2:
                        pe.wait_ge(s["wa_sm"], up("wa_sm", it, u - 2))
                    for k in range(4):
                        p, j = 2 * hh + k % 2, k // 2
                        rows = slice(64 * j, 64 * j + 64)
                        last = nc.tensor.matmul(ps[:, 2 * (u % 2) + k // 2, (k % 2) * 2 * P:(k % 2 + 1) * 2 * P],
                                                qt[rows, p, t * P:(t + 1) * P], kt[rows, p, t * P:(t + 2) * P],
                                                start=True, stop=True, tile_position=(64 * j, 0))
                    last.then_inc(s["wa_s_ps"], 1)

                def turn(u):
                    if u:
                        pe.wait_ge(s["wa_t"], up("wa_t", it, u - 1))
                    pe.wait_ge(s["wa_p"], up("wa_p", it, u))
                    for k in range(8):
                        last = nc.tensor.transpose(ps[:, 4 + k // 4, (k % 4) * P:(k % 4 + 1) * P],
                                                   sm[:, u % 3, k // 2, (k % 2) * P:(k % 2 + 1) * P], c.ident[:, :])
                    last.then_inc(s["wa_t_ps"], 1)

                def values(u):
                    t, hh = u // 2, u % 2
                    if u:
                        pe.wait_ge(s["wa_o"], up("wa_o", it, u - 1))
                    pe.wait_ge(s["wa_t"], up("wa_t", it, u))
                    for k in range(4):
                        p, j = 2 * hh + k % 2, k // 2
                        head = 2 * p + j
                        for e in range(2):
                            last = nc.tensor.matmul(ps[64 * j:64 * j + 64, 6, (k % 2) * P:(k % 2 + 1) * P],
                                                    v[:, t + e, head * 64:head * 64 + 64], pt[:, u % 2, k, e, :],
                                                    start=(e == 0), stop=(e == 1), tile_position=(0, 64 * j))
                    last.then_inc(s["wa_o_ps"], 1)

                def project(t):
                    if t:
                        pe.wait_ge(s["wa_y"], up("wa_y", it, t - 1))
                    pe.wait_ge(s["wa_o"], up("wa_o", it, 2 * t + 1))
                    for p in range(NPAIR):
                        last = nc.tensor.matmul(ps[:, 7, 0:P], wo[:, p, :], ot[:, t % 2, p, :],
                                                start=(p == 0), stop=(p == NPAIR - 1))
                    last.then_inc(s["wa_y_ps"], 1)

                scores(0)
                scores(1)
                for u in range(U + 1):
                    if u < U:
                        turn(u)
                    if u + 2 < U:
                        scores(u + 2)
                    if u:
                        values(u - 1)
                    if u % 2 == 1 and u >= 3:
                        project(u // 2 - 1)
                project(TILES - 1)
                pe.wait_ge(s["wm_h"], up("wm_h", it))
                for i in range(HALVES):
                    if i:
                        pe.wait_ge(s["wm_n"], up("wm_n", it, i - 1))
                    nc.tensor.matmul(ps[:, 0, :], c.mean_w[:, :], h[:, i * BLK:(i + 1) * BLK],
                                     start=True, stop=True).then_inc(s["wm_mean"], 1)
                    pe.wait_ge(s["wm_sq"], up("wm_sq", it, i))
                    nc.tensor.matmul(ps[:, 1, :], c.mean_w[:, :], sq[:, 0, :],
                                     start=True, stop=True).then_inc(s["wm_var"], 1)
                    pe.wait_ge(s["wm_n"], up("wm_n", it, i))
                    for k, (r0, r) in enumerate(CHUNKS):
                        n = 3 * i + k
                        if n >= 2:
                            pe.wait_ge(s["wm_hg"], up("wm_hg", it, n - 2))
                        nc.tensor.matmul(ps[0:r, 2 + n % 2, :], w1[:, r0:r0 + r], rot[:, i, :],
                                         start=True, stop=True)
                        nc.tensor.matmul(ps[0:r, 4 + n % 2, :], w1[:, HID + r0:HID + r0 + r], rot[:, i, :],
                                         start=True, stop=True).then_inc(s["wm_ag"], 1)
                    for k, (r0, r) in enumerate(CHUNKS):
                        pe.wait_ge(s["wm_hg"], up("wm_hg", it, 3 * i + k))
                        last = nc.tensor.matmul(ps[:, 6 + i, :], w2[0:r, k, :], hg[0:r, k, :],
                                                start=(k == 0), stop=(k == 2))
                    last.then_inc(s["wm_y_ps"], 1)

        @block.scalar
        def _(act):
            act.wait_ge(s["wa_w"], 16 * 13 * (run + 1))
            with act.Fori(*ITS) as it:

                for n in range(QK):
                    act.wait_ge(s["wa_qk_ps"], up("wa_qk_ps", it, n))
                    nc.scalar.activation(sq[:, n % 2, :], ps[:, n % 2, :], ACT.Square).then_inc(s["wa_sq"], 1)
                for i in range(HALVES):
                    act.wait_ge(s["wa_ss"], up("wa_ss", it, i))
                    nc.scalar.activation(length[0:16, i * BLK:(i + 1) * BLK], ps[0:16, 4 + i, :],
                                         ACT.Sqrt).then_inc(s["wa_sd"], 1)
                for t in range(TILES):
                    act.wait_ge(s["wa_v_ps"], up("wa_v_ps", it, t))
                    nc.scalar.activation(v[:, 1 + t, :], ps[:, 6 + t % 2, :], ACT.Copy).then_inc(s["wa_v"], 1)
                def exps(u):
                    act.wait_ge(s["wa_nmx"], up("wa_nmx", it, u))
                    for k in range(4):
                        ins = nc.scalar.activation(sm[:, u % 3, k, :], sm[:, u % 3, k, :], ACT.Exp, scale=8.0,
                                                   bias=nmx[:, u % 3, k:k + 1], accum_out=tot[:, u % 3, k:k + 1])
                    ins.then_inc(s["wa_exp"], 1)

                def copy_out(u):
                    act.wait_ge(s["wa_o_ps"], up("wa_o_ps", it, u))
                    t, hh = u // 2, u % 2
                    if t >= 2:
                        act.wait_ge(s["wa_y_ps"], up("wa_y_ps", it, t - 2))
                    nc.scalar.activation(ot[:, t % 2, 2 * hh:2 * hh + 2, :],
                                         ps[:, 6, 0:2 * P].rearrange("p (a q) -> p a q", a=2),
                                         ACT.Copy).then_inc(s["wa_o"], 1)

                exps(0)
                for u in range(U):
                    if u + 1 < U:
                        exps(u + 1)
                    act.wait_ge(s["wa_t_ps"], up("wa_t_ps", it, u))
                    if u >= 2:
                        act.wait_ge(s["wa_o_ps"], up("wa_o_ps", it, u - 2))
                    nc.scalar.activation(pt[:, u % 2, :, :, :].rearrange("p a b q -> p (a b q)"),
                                         ps[:, 4:6, :].rearrange("p a q -> p (a q)"),
                                         ACT.Copy).then_inc(s["wa_t"], 1)
                    if u:
                        copy_out(u - 1)
                copy_out(U - 1)
                for i in range(HALVES):
                    act.wait_ge(s["wm_xc"], up("wm_xc", it, i))
                    nc.scalar.activation(sq[:, 0, :], sd[:, 1, :], ACT.Square).then_inc(s["wm_sq"], 1)
                    act.wait_ge(s["wm_var"], up("wm_var", it, i))
                    nc.scalar.activation(sd[:, 0, :], ps[:, 1, :], ACT.Sqrt,
                                         bias=c.eps5[:, 0:1]).then_inc(s["wm_sd"], 1)
                    for k, (r0, r) in enumerate(CHUNKS):
                        n = 3 * i + k
                        act.wait_ge(s["wm_ag"], up("wm_ag", it, n))
                        if n >= 3:
                            act.wait_ge(s["wm_y_ps"], up("wm_y_ps", it, n // 3 - 1))
                        nc.scalar.activation(hg[0:r, k, :], ps[0:r, 4 + n % 2, :], ACT.Gelu,
                                             bias=b1[0:r, k, 1:2]).then_inc(s["wm_gelu"], 1)

        @block.vector
        def _(dve):
            link = Chain(c, dve, "wa_dve", QK + 1 + 2 * U + 2 + HALVES * 3)
            dve.wait_ge(s["wa_w"], 16 * 13 * (run + 1))
            nc.vector.memset(length[:, :], 0.0).then_inc(s["wa_set"], 1)
            nc.vector.memset(h[64:P, 0:1], 0.0).then_inc(s["wa_set"], 1)
            nc.vector.memset(kt[:, :, 0:P], 0.0).then_inc(s["wa_set"], 1)
            nc.vector.memset(v[:, 0, :], 0.0).then_inc(s["wa_set"], 1)
            if run == 0:
                dve.sem_inc(s["wa_done"], 1)
            with dve.Fori(*ITS) as it:
                link.start(it)
                base = (it - run * B) * T
                dve.wait_ge(s["wa_done"], it + 1)
                shifted_copy(nc, c, h, base, link, s["wa_h"])
                def heads(n):
                    x, p, i = n // 8, n % 8 // 2, n % 2
                    off = (0, P)[x] + i * BLK
                    return (qt, kt)[x][:, p, off:off + BLK]

                for n in range(QK):
                    x, p, i = n // 8, n % 8 // 2, n % 2
                    half = slice(i * BLK, (i + 1) * BLK)
                    dve.wait_ge(s["wa_sq"], up("wa_sq", it, n))
                    link(nc.vector.scalar_tensor_tensor(rot[:, 0, :], ps[:, n % 2, :], qks[:, 2 * x:2 * x + 1],
                                                        tab[:, 2 * x, half], ALU.mult, ALU.mult))
                    nc.vector.scalar_tensor_tensor(rot[:, 1, :], ps[:, 2 + n % 2, :], qks[:, 2 * x + 1:2 * x + 2],
                                                   tab[:, 2 * x + 1, half], ALU.mult, ALU.mult).then_inc(s["wa_rot"], 1)
                    dve.wait_ge(s["wa_rot"], up("wa_rot", it, n))
                    nc.vector.tensor_tensor(heads(n), rot[:, 0, :], rot[:, 1, :], ALU.add).then_inc(s["wa_raw"], 1)
                    dve.wait_ge(s["wa_raw"], up("wa_raw", it, n))
                dve.wait_ge(s["wa_sd"], up("wa_sd", it, 1))
                link(nc.vector.tensor_scalar(length[0:16, :], length[0:16, :], 1e-12, None, ALU.max))
                nc.vector.reciprocal(length[0:16, :], length[0:16, :]).then_inc(s["wa_r"], 1)
                for n in range(QK):
                    dve.wait_ge(s["wa_b_ps"], up("wa_b_ps", it, n))
                    nc.vector.tensor_tensor(heads(n), heads(n), ps[:, n % 2, :], ALU.mult).then_inc(s["wa_qk"], 1)

                def mask(u):
                    dve.wait_ge(s["wa_s_ps"], up("wa_s_ps", it, u))
                    if u >= 3:
                        dve.wait_ge(s["wa_t_ps"], up("wa_t_ps", it, u - 3))
                    first = 0 if u < 2 else 1
                    nc.vector.tensor_tensor(sm[:, u % 3, :, :],
                                            ps[:, 2 * (u % 2):2 * (u % 2) + 2, :].rearrange("p a (b k) -> p (a b) k", b=2),
                                            band[:, first:first + 1, :].to_broadcast([P, 4, 2 * P]),
                                            ALU.add).then_inc(s["wa_sm"], 1)
                    dve.wait_ge(s["wa_sm"], up("wa_sm", it, u))
                    link(nc.vector.tensor_reduce(nmx[:, u % 3, :], sm[:, u % 3, :, :], AX, ALU.max, negate=True))
                    nc.vector.tensor_scalar(nmx[:, u % 3, :], nmx[:, u % 3, :], 8.0, None,
                                            ALU.mult).then_inc(s["wa_nmx"], 1)

                def out_tile(t):
                    here = tokens(base + t * P, P)
                    dve.wait_ge(s["wa_y_ps"], up("wa_y_ps", it, t))
                    nc.vector.tensor_tensor(c.xnt[:, here], c.xnt[:, here], ps[:, 7, 0:P],
                                            ALU.add).then_inc(s["wa_y"], 1)

                mask(0)
                mask(1)
                for u in range(U):
                    dve.wait_ge(s["wa_exp"], up("wa_exp", it, u))
                    link(nc.vector.reciprocal(tot[:, u % 3, :], tot[:, u % 3, :]))
                    nc.vector.tensor_tensor(sm[:, u % 3, :, :], sm[:, u % 3, :, :],
                                            tot[:, u % 3, :].unsqueeze(2).to_broadcast([P, 4, 2 * P]),
                                            ALU.mult).then_inc(s["wa_p"], 1)
                    if u + 2 < U:
                        mask(u + 2)
                    if u % 2 == 1 and u >= 5:
                        out_tile(u // 2 - 2)
                out_tile(TILES - 2)
                out_tile(TILES - 1)
                dve.wait_ge(s["wa_y"], up("wa_y", it, TILES - 1))
                shifted_copy(nc, c, h, base, link, s["wm_h"])
                for i in range(HALVES):
                    half = slice(i * BLK, (i + 1) * BLK)
                    here = tokens(base + i * BLK, BLK)
                    dve.wait_ge(s["wm_mean"], up("wm_mean", it, i))
                    nc.vector.tensor_tensor(sd[:, 1, :], h[:, half], ps[:, 0, :], ALU.subtract).then_inc(s["wm_xc"], 1)
                    dve.wait_ge(s["wm_sd"], up("wm_sd", it, i))
                    link(nc.vector.reciprocal(sd[:, 0, :], sd[:, 0, :]))
                    link(nc.vector.tensor_tensor(sq[:, 1, :], sd[:, 1, :], sd[:, 0, :], ALU.mult))
                    nc.vector.tensor_scalar(rot[:, i, :], sq[:, 1, :], lnc[:, 0:1], lnc[:, 1:2],
                                            ALU.mult, ALU.add).then_inc(s["wm_n"], 1)
                    for k, (r0, r) in enumerate(CHUNKS):
                        n = 3 * i + k
                        dve.wait_ge(s["wm_gelu"], up("wm_gelu", it, n))
                        nc.vector.scalar_tensor_tensor(hg[0:r, k, :], ps[0:r, 2 + n % 2, :], b1[0:r, k, 0:1],
                                                       hg[0:r, k, :], ALU.add, ALU.mult).then_inc(s["wm_hg"], 1)
                    dve.wait_ge(s["wm_y_ps"], up("wm_y_ps", it, i))
                    link(nc.vector.scalar_tensor_tensor(c.xnt[:, here], ps[:, 6 + i, :], lnc[:, 2:3],
                                                        c.xnt[:, here], ALU.add, ALU.add))
                    if run == 1:
                        last = nc.vector.tensor_tensor(c.xt[:, here], c.xt[:, here], c.xnt[:, here], ALU.add)
                if run == 1:
                    last.then_inc(s["wa_done"], 1)
                else:
                    dve.sem_inc(s["wa_done"], 1)
            link.close()


GQ, LAT = 4, 32


def grouped_attention_phase(c, run):
    units = []
    for t in range(TILES):
        for k in range(0 if run == 0 else max(t - 1, 0), t + 1):
            units += [(t, k, j, None if run == 0 and k < t else t - k) for j in range(4)]
    U = len(units)
    last_of = {t: max(n for n, x in enumerate(units) if x[0] == t) for t in range(TILES)}
    masked = [n for n, x in enumerate(units) if x[3] is not None]
    NQK = 4
    pre = f"ga{run}_"
    counts = dict(w=1, set=1, sq=2, ms=2, sd=2, h=2, lat_ps=2, lat=2, qk_ps=NQK, rot=NQK, qsq=NQK, qms=NQK, qsd=NQK,
                  qk=NQK, split=NQK, out=6 * 16, rows=18 * 16, v_ps=TILES, v=TILES, st=U, exp=U, mask=len(masked), av=U, o=TILES, sum_ps=TILES, ot=TILES,
                  y_ps=2, done=1)
    c.signals(**{pre + k: n for k, n in counts.items()})
    s = {k: c.sem[pre + k] for k in counts}
    up = lambda name, it, i=0: c.up(pre + name, it, i)
    nc, d, ps = c.nc, c.d, c.ps
    R = LAT if run == 0 else P
    NW = 10 if run == 0 else 9
    scratch = nc.dram_tensor(pre + "scratch", [2, PARTS, P, T], BF16, kind="Internal").ap()
    with ExitStack() as ctx:
        sb = lambda n, shape: c.sb(ctx, pre + "b_" + n, shape)
        wq = sb("wq", [P, 2, P])
        wk = sb("wk", [P, 2, P])
        wv = sb("wv", [P, 32])
        wd = sb("wd", [P, LAT])
        wo = sb("wo", [P, GQ, P])
        nw = sb("nw", [P, 1])
        tab = sb("tab", [P, 2, T])
        msk = sb("msk", [P, 2, P])
        row8 = sb("row8", [P, P])
        m8 = sb("m8", [P, P])
        h = sb("h", [P, T])
        lat = sb("lat", [P, T])
        sq = sb("sq", [P, 2, BLK])
        sd = sb("sd", [P, 2, BLK])
        rot = sb("rot", [P, 2, 2, BLK])
        part = c.sb(ctx, pre + "b_part", [P, 2, PARTS, T], BF16)
        q6 = c.sb(ctx, pre + "b_q6", [P, 16, T], BF16)
        k6 = c.sb(ctx, pre + "b_k6", [P, 4, T], BF16)
        v = sb("v", [P, TILES, 4, 32])
        pt = sb("pt", [P, 3, BLK])
        os = sb("os", [P, 2, BLK])
        rs = sb("rs", [P, 2, BLK])
        ot = sb("ot", [P, GQ, T])
        src = lat if run == 0 else h
        block = ctx.enter_context(nc.Block())

        @block.sync
        def _(sp):
            loads = [(wq[:, :, :], d[pre + "wq"]), (wk[0:R, :, :], d[pre + "wk"]), (wv[0:R, :], d[pre + "wv"]),
                     (wo[:, :, :], d[pre + "wo"]), (nw[:, :], d[pre + "nw"]), (tab[:, :, :], d["c_" + pre + "tab"]),
                     (msk[:, :, :], d["c_" + pre + "mask"]), (row8[:, :], d["c_row8"]), (m8[:, :], d["c_mean8"])]
            if run == 0:
                loads.append((wd[:, :], d["ga0_wd"]))
            for dst, x in loads:
                sp.dma_start(dst, x).then_inc(s["w"], 16)
            sp.wait_ge(s["w"], 16 * NW)
            with sp.Fori(0, B) as it:
                sp.wait_ge(s["split"], up("split", it, NQK - 1))
                for x in range(2):
                    r = (P, 32)[x]
                    for p in range(PARTS):
                        sp.dma_start(scratch[x, p, 0:r], part[0:r, x, p, :]).then_inc(s["out"], 16)
                sp.wait_ge(s["out"], (it + 1) * 96)
                for x, dst in ((0, q6), (1, k6)):
                    for r in range(9):
                        src_rows = scratch[x, r // 3 if x == 0 else r % 3, 0:(P, 32)[x]]
                        sp.dma_start(dst[8 * r:8 * r + 8, :, :],
                                     src_rows.rearrange("(h e) t -> e h t", e=8)).then_inc(s["rows"], 16)
            sp.wait_ge(s["rows"], B * 288)

        @block.tensor
        def _(pe):
            pe.wait_ge(s["w"], 16 * NW)
            pe.wait_ge(s["set"], 2)
            with pe.Fori(0, B) as it:
                for i in range(HALVES):
                    pe.wait_ge(s["sq"], up("sq", it, i))
                    nc.tensor.matmul(ps[:, i, :], c.mean_w[:, :], sq[:, i, :],
                                     start=True, stop=True).then_inc(s["ms"], 1)
                for i in range(HALVES):
                    pe.wait_ge(s["h"], up("h", it, i))
                    if run == 0:
                        nc.tensor.matmul(ps[0:LAT, 2 + i, :], wd[:, :], h[:, i * BLK:(i + 1) * BLK],
                                         start=True, stop=True).then_inc(s["lat_ps"], 1)
                if run == 0:
                    pe.wait_ge(s["lat"], up("lat", it, 1))

                def head_means(n):
                    pe.wait_ge(s["qsq"], up("qsq", it, n))
                    nc.tensor.matmul(ps[:, 4 + n % 2, :], m8[:, :], sq[:, n % 2, :],
                                     start=True, stop=True).then_inc(s["qms"], 1)

                for n in range(NQK):
                    half = slice(n % 2 * BLK, (n % 2 + 1) * BLK)
                    if n >= 2:
                        pe.wait_ge(s["rot"], up("rot", it, n - 2))
                    for x in range(2):
                        if n < 2:
                            last = nc.tensor.matmul(ps[:, 2 * x + n % 2, :], wq[:, x, :], h[:, half],
                                                    start=True, stop=True)
                        else:
                            last = nc.tensor.matmul(ps[:, 2 * x + n % 2, :], wk[0:R, x, :], src[0:R, half],
                                                    start=True, stop=True)
                    last.then_inc(s["qk_ps"], 1)
                    if n:
                        head_means(n - 1)
                head_means(NQK - 1)
                for t in range(TILES):
                    if t >= 2:
                        pe.wait_ge(s["v"], up("v", it, t - 2))
                    nc.tensor.matmul(ps[:, 6 + t % 2, 0:32], src[0:R, t * P:(t + 1) * P], wv[0:R, :],
                                     start=True, stop=True).then_inc(s["v_ps"], 1)
                pe.wait_ge(s["v"], up("v", it, TILES - 1))
                pe.wait_ge(s["rows"], (it + 1) * 288)

                def scores(n):
                    t, k, j, m = units[n]
                    if n >= 3:
                        pe.wait_ge(s["exp"], up("exp", it, n - 3))
                    nc.tensor.matmul(ps[:, n % 3, :].rearrange("p (g q) -> p g q", g=GQ),
                                     k6[0:72, j, k * P:(k + 1) * P], q6[0:72, GQ * j:GQ * (j + 1), t * P:(t + 1) * P],
                                     start=True, stop=True).then_inc(s["st"], 1)

                def values(n):
                    t, k, j, m = units[n]
                    if (n == 0 or units[n - 1][0] != t) and t >= 2:
                        pe.wait_ge(s["o"], up("o", it, t - 2))
                    if m is None:
                        pe.wait_ge(s["exp"], up("exp", it, n))
                    else:
                        pe.wait_ge(s["mask"], up("mask", it, masked.index(n)))
                    first = units[n][1] == (0 if run == 0 else max(t - 1, 0))
                    nc.tensor.matmul(ps[32 * j:32 * j + 32, 3 + t % 2, :], v[:, k, j, :], pt[:, n % 3, :],
                                     start=first, stop=(k == t), tile_position=(0, 32 * j)).then_inc(s["av"], 1)

                def sums(t):
                    pe.wait_ge(s["o"], up("o", it, t))
                    if t:
                        pe.wait_ge(s["ot"], up("ot", it, t - 1))
                    nc.tensor.matmul(ps[:, 5, :], row8[:, :], os[:, t % 2, :],
                                     start=True, stop=True).then_inc(s["sum_ps"], 1)

                for n in range(U + 2):
                    if n < U:
                        scores(n)
                    if n >= 2:
                        values(n - 2)
                        t = units[n - 2][0]
                        if t and n - 2 == last_of[t - 1] + 4:
                            sums(t - 1)
                sums(TILES - 1)
                pe.wait_ge(s["ot"], up("ot", it, TILES - 1))
                for i in range(HALVES):
                    for g in range(GQ):
                        last = nc.tensor.matmul(ps[:, 6 + i, :], wo[:, g, :], ot[:, g, i * BLK:(i + 1) * BLK],
                                                start=(g == 0), stop=(g == GQ - 1))
                    last.then_inc(s["y_ps"], 1)

        @block.scalar
        def _(act):
            with act.Fori(0, B) as it:
                for i in range(HALVES):
                    act.wait_ge(s["ms"], up("ms", it, i))
                    nc.scalar.activation(sd[:, i, :], ps[:, i, :], ACT.Sqrt, bias=c.eps6[:, 0:1]).then_inc(s["sd"], 1)
                if run == 0:
                    for i in range(HALVES):
                        act.wait_ge(s["lat_ps"], up("lat_ps", it, i))
                        nc.scalar.activation(lat[0:LAT, i * BLK:(i + 1) * BLK], ps[0:LAT, 2 + i, :],
                                             ACT.Copy).then_inc(s["lat"], 1)

                def root(n):
                    act.wait_ge(s["qms"], up("qms", it, n))
                    if n >= 2:
                        act.wait_ge(s["qk"], up("qk", it, n - 2))
                    nc.scalar.activation(sd[:, n % 2, :], ps[:, 4 + n % 2, :], ACT.Sqrt,
                                         bias=c.eps6[:, 0:1]).then_inc(s["qsd"], 1)

                for n in range(NQK):
                    act.wait_ge(s["rot"], up("rot", it, n))
                    nc.scalar.activation(sq[:, n % 2, :], rot[:, n % 2, 0, :], ACT.Square).then_inc(s["qsq"], 1)
                    if n:
                        root(n - 1)
                root(NQK - 1)
                for t in range(TILES):
                    act.wait_ge(s["v_ps"], up("v_ps", it, t))
                    nc.scalar.activation(v[:, t, :, 0:8], ps[:, 6 + t % 2, 0:32].rearrange("p (j e) -> p j e", e=8),
                                         ACT.Copy).then_inc(s["v"], 1)

                def copy_out(t):
                    act.wait_ge(s["av"], up("av", it, last_of[t]))
                    if t >= 2:
                        act.wait_ge(s["ot"], up("ot", it, t - 2))
                    nc.scalar.activation(os[:, t % 2, :], ps[:, 3 + t % 2, :], ACT.Copy).then_inc(s["o"], 1)

                for n in range(U):
                    act.wait_ge(s["st"], up("st", it, n))
                    if n >= 3:
                        act.wait_ge(s["av"], up("av", it, n - 3))
                    nc.scalar.activation(pt[:, n % 3, :], ps[:, n % 3, :], ACT.Exp,
                                         scale=float(8) ** -0.5).then_inc(s["exp"], 1)
                    t = units[n][0]
                    if t and n == last_of[t - 1] + 3:
                        copy_out(t - 1)
                copy_out(TILES - 1)

        @block.vector
        def _(dve):
            link = Chain(c, dve, pre + "dve", 7 * NQK + TILES + 2 * HALVES)
            dve.wait_ge(s["w"], 16 * NW)
            nc.vector.memset(v[:, :, :, :], 0.0).then_inc(s["set"], 1)
            dve.wait_ge(s["set"], 1)
            nc.vector.memset(v[:, :, :, 8:9], 1.0).then_inc(s["set"], 1)
            dve.sem_inc(s["done"], 1)
            with dve.Fori(0, B) as it:
                link.start(it)
                dve.wait_ge(s["done"], it + 1)
                for i in range(HALVES):
                    here = tokens(it * T + i * BLK, BLK)
                    nc.vector.tensor_tensor(sq[:, i, :], c.xnt[:, here], c.xnt[:, here], ALU.mult).then_inc(s["sq"], 1)
                for i in range(HALVES):
                    here = tokens(it * T + i * BLK, BLK)
                    dve.wait_ge(s["sd"], up("sd", it, i))
                    link(nc.vector.reciprocal(sd[:, i, :], sd[:, i, :]))
                    nc.vector.scalar_tensor_tensor(h[:, i * BLK:(i + 1) * BLK], c.xnt[:, here], nw[:, 0:1],
                                                   sd[:, i, :], ALU.mult, ALU.mult).then_inc(s["h"], 1)
                def to_length(n):
                    x, half = n // 2, slice(n % 2 * BLK, (n % 2 + 1) * BLK)
                    dve.wait_ge(s["qsd"], up("qsd", it, n))
                    link(nc.vector.reciprocal(sd[0:P, n % 2, :], sd[0:P, n % 2, :]))
                    nc.vector.tensor_tensor(rot[0:P, n % 2, 0, :], rot[0:P, n % 2, 0, :], sd[0:P, n % 2, :],
                                            ALU.mult).then_inc(s["qk"], 1)
                    dve.wait_ge(s["qk"], up("qk", it, n))
                    split_parts(nc, link, rot[0:P, n % 2, 0, :], sd[0:P, n % 2, :],
                                [part[0:P, x, p, half] for p in range(PARTS)]).then_inc(s["split"], 1)
                    dve.wait_ge(s["split"], up("split", it, n))

                for n in range(NQK):
                    half = slice(n % 2 * BLK, (n % 2 + 1) * BLK)
                    rn = rot[:, n % 2]
                    dve.wait_ge(s["qk_ps"], up("qk_ps", it, n))
                    link(nc.vector.tensor_tensor(rn[:, 0, :], tab[0:P, 0, half], ps[0:P, n % 2, :], ALU.mult))
                    link(nc.vector.tensor_tensor(rn[:, 1, :], tab[0:P, 1, half], ps[0:P, 2 + n % 2, :], ALU.mult))
                    nc.vector.tensor_tensor(rn[:, 0, :], rn[:, 0, :], rn[:, 1, :], ALU.add).then_inc(s["rot"], 1)
                    if n:
                        to_length(n - 1)
                to_length(NQK - 1)

                def normalise(t):
                    dve.wait_ge(s["sum_ps"], up("sum_ps", it, t))
                    link(nc.vector.reciprocal(rs[:, t % 2, :], ps[:, 5, :]))
                    nc.vector.tensor_tensor(ot[:, :, t * P:(t + 1) * P],
                                            os[:, t % 2, :].rearrange("p (g q) -> p g q", g=GQ),
                                            rs[:, t % 2, :].rearrange("p (g q) -> p g q", g=GQ),
                                            ALU.mult).then_inc(s["ot"], 1)

                for n in masked:
                    t, k, j, m = units[n]
                    dve.wait_ge(s["exp"], up("exp", it, n))
                    here = pt[:, n % 3, :].rearrange("p (g q) -> p g q", g=GQ)
                    nc.vector.tensor_tensor(here, here, msk[:, m:m + 1, :].to_broadcast([P, GQ, P]),
                                            ALU.mult).then_inc(s["mask"], 1)
                    if n == last_of[t] and t:
                        normalise(t - 1)
                normalise(TILES - 1)
                for i in range(HALVES):
                    here = tokens(it * T + i * BLK, BLK)
                    dve.wait_ge(s["y_ps"], up("y_ps", it, i))
                    link(nc.vector.tensor_tensor(c.xnt[:, here], c.xnt[:, here], ps[:, 6 + i, :], ALU.add))
                    if run == 1:
                        last = nc.vector.tensor_tensor(c.xt[:, here], c.xt[:, here], c.xnt[:, here], ALU.add)
                if run == 1:
                    last.then_inc(s["done"], 1)
                else:
                    dve.sem_inc(s["done"], 1)
            link.close()


NE, FF = 8, 256


def experts_phase(c, which):
    swiglu = which == 1
    E = NE + 1 if swiglu else NE
    U = 2 * E
    pre = f"moe{which}_"
    counts = dict(w=1, h=1, mean=1, xc=1, sq=1, var=1, sd=1, rn=1, lg_ps=1, lg=1, exp=1, wt_ps=1, gate=1, wt=1,
                  wb=NE, h_ps=U, act=U, hs=U, out=U, done=1)
    if swiglu:
        for k in ("mean", "xc", "sq", "var", "sd", "rn"):
            del counts[k]
    c.signals(**{pre + k: n for k, n in counts.items()})
    s = {k: c.sem[pre + k] for k in counts}
    up = lambda name, it, i=0: c.up(pre + name, it, i)
    nc, d, ps = c.nc, c.d, c.ps
    NW = 5 if not swiglu else 6
    with ExitStack() as ctx:
        sb = lambda n, shape, dt=F32: c.sb(ctx, pre + "b_" + n, shape, dt)
        w1 = sb("w1", [P, E, FF])
        w3 = sb("w3", [P, E, FF]) if swiglu else None
        w2 = sb("w2", [P, E, 2, P])
        wr = sb("wr", [P, NE])
        gcon = sb("gcon", [P, 2 + 4 * NE])
        sel = sb("sel", [NE, NE, P])
        order = sb("order", [P, 4, NE])
        h = sb("h", [P, BLK])
        rn = sb("rn", [P, BLK])
        tmp = sb("tmp", [P, 3, BLK])
        lg = sb("lg", [P, 4, NE])
        lr = sb("lr", [P, 4, NE])
        others = sb("others", [P, 4, NE])
        hot = sb("hot", [P, 4, NE])
        hot2 = sb("hot2", [P, 4, NE])
        g1 = sb("g1", [P, 4])
        wt = sb("wt", [NE, BLK])
        ga = sb("ga", [P, 2, BLK])
        hs = sb("hs", [P, 2, BLK])
        block = ctx.enter_context(nc.Block())

        @block.sync
        def _(sp):
            loads = [(w1[:, :, :], pre + "w1"), (w2[:, :, :, :], pre + "w2"), (wr[:, :], pre + "wr"),
                     (gcon[:, :], pre + "gcon"), (sel[:, :, :], "c_sel")]
            if swiglu:
                loads.append((w3[:, :, :], pre + "w3"))
            for dst, x in loads:
                sp.dma_start(dst, d[x]).then_inc(s["w"], 16)
            sp.dma_start(order[:, :, :], d["c_order"]).then_inc(s["w"], 16)
            sp.wait_ge(s["w"], 16 * (NW + 1))

        @block.tensor
        def _(pe):
            pe.wait_ge(s["w"], 16 * (NW + 1))
            with pe.Fori(0, NB) as it:
                pe.wait_ge(s["h"], up("h", it))
                if not swiglu:
                    nc.tensor.matmul(ps[:, 0, :], c.mean_w[:, :], h[:, :], start=True, stop=True).then_inc(s["mean"], 1)
                    pe.wait_ge(s["sq"], up("sq", it))
                    nc.tensor.matmul(ps[:, 1, :], c.mean_w[:, :], tmp[:, 1, :],
                                     start=True, stop=True).then_inc(s["var"], 1)
                    pe.wait_ge(s["rn"], up("rn", it))
                for t in range(4):
                    x = h if swiglu else rn
                    last = nc.tensor.matmul(ps[:, 0, t * NE:(t + 1) * NE], x[:, t * P:(t + 1) * P], wr[:, :],
                                            start=True, stop=True)
                last.then_inc(s["lg_ps"], 1)

                def first(n):
                    e, f = n // 2, slice(n % 2 * P, n % 2 * P + P)
                    if n >= 2:
                        pe.wait_ge(s["hs"], up("hs", it, n - 2))
                    last = nc.tensor.matmul(ps[:, 2 + n % 2, :], w1[:, e, f], h[:, :], start=True, stop=True)
                    if swiglu:
                        last = nc.tensor.matmul(ps[:, 4 + n % 2, :], w3[:, e, f], h[:, :], start=True, stop=True)
                    last.then_inc(s["h_ps"], 1)

                def spread(e):
                    if e >= 2:
                        pe.wait_ge(s["hs"], up("hs", it, 2 * e - 3))
                    nc.tensor.matmul(ps[:, e % 2, :], sel[:, e, :], wt[:, :],
                                     start=True, stop=True).then_inc(s["wb"], 1)

                def second(n):
                    pe.wait_ge(s["hs"], up("hs", it, n))
                    nc.tensor.matmul(ps[:, 6, :], w2[:, n // 2, n % 2, :], hs[:, n % 2, :],
                                     start=(n == 0), stop=(n == U - 1)).then_inc(s["out"], 1)

                first(0)
                first(1)
                pe.wait_ge(s["gate"], up("gate", it))
                for t in range(4):
                    last = nc.tensor.transpose(ps[0:NE, 7, t * P:(t + 1) * P], lr[:, t, :], c.ident[:, :])
                last.then_inc(s["wt_ps"], 1)
                pe.wait_ge(s["wt"], up("wt", it))
                spread(0)
                for n in range(U):
                    if n % 2 == 0 and n // 2 + 1 < NE:
                        spread(n // 2 + 1)
                    if n + 2 < U:
                        first(n + 2)
                    second(n)

        @block.scalar
        def _(act):
            with act.Fori(0, NB) as it:
                if not swiglu:
                    act.wait_ge(s["xc"], up("xc", it))
                    nc.scalar.activation(tmp[:, 1, :], tmp[:, 0, :], ACT.Square).then_inc(s["sq"], 1)
                    act.wait_ge(s["var"], up("var", it))
                    nc.scalar.activation(tmp[:, 2, :], ps[:, 1, :], ACT.Sqrt, bias=c.eps5[:, 0:1]).then_inc(s["sd"], 1)
                act.wait_ge(s["lg"], up("lg", it))
                nc.scalar.activation(lr[:, :, :], lr[:, :, :], ACT.Exp).then_inc(s["exp"], 1)
                act.wait_ge(s["wt_ps"], up("wt_ps", it))
                nc.scalar.activation(wt[:, :], ps[0:NE, 7, :], ACT.Copy).then_inc(s["wt"], 1)
                for n in range(U):
                    act.wait_ge(s["h_ps"], up("h_ps", it, n))
                    if n >= 2:
                        act.wait_ge(s["hs"], up("hs", it, n - 2))
                    if swiglu:
                        nc.scalar.activation(ga[:, n % 2, :], ps[:, 4 + n % 2, :], ACT.Silu).then_inc(s["act"], 1)
                    else:
                        nc.scalar.activation(ga[:, n % 2, :], ps[:, 2 + n % 2, :], ACT.Gelu).then_inc(s["act"], 1)

        @block.vector
        def _(dve):
            link = Chain(c, dve, pre + "dve", (20 + 2 * NE) if swiglu else 18)
            dve.wait_ge(s["w"], 16 * (NW + 1))
            dve.sem_inc(s["done"], 1)
            with dve.Fori(0, NB) as it:
                link.start(it)
                here = tokens(it * BLK, BLK)
                dve.wait_ge(s["done"], it + 1)
                nc.vector.tensor_scalar(h[:, :], c.xnt[:, here], 1.0, None, ALU.mult).then_inc(s["h"], 1)
                spread4 = lambda x: x.unsqueeze(2).to_broadcast([P, 4, NE])
                if not swiglu:
                    dve.wait_ge(s["mean"], up("mean", it))
                    nc.vector.tensor_tensor(tmp[:, 0, :], h[:, :], ps[:, 0, :], ALU.subtract).then_inc(s["xc"], 1)
                    dve.wait_ge(s["sd"], up("sd", it))
                    link(nc.vector.reciprocal(tmp[:, 2, :], tmp[:, 2, :]))
                    link(nc.vector.tensor_tensor(tmp[:, 1, :], tmp[:, 0, :], tmp[:, 2, :], ALU.mult))
                    nc.vector.tensor_scalar(rn[:, :], tmp[:, 1, :], gcon[:, 0:1], gcon[:, 1:2],
                                            ALU.mult, ALU.add).then_inc(s["rn"], 1)

                def best_two(x, others):
                    for k, dst in enumerate((hot, hot2)):
                        link(nc.vector.tensor_reduce(g1[:, :], x[:, :, :], AX, ALU.max))
                        link(nc.vector.tensor_tensor(dst[:, :, :], x[:, :, :], spread4(g1[:, :]), ALU.is_equal))
                        link(nc.vector.tensor_tensor(dst[:, :, :], dst[:, :, :], order[:, :, :], ALU.mult))
                        link(nc.vector.tensor_reduce(g1[:, :], dst[:, :, :], AX, ALU.max))
                        link(nc.vector.tensor_tensor(dst[:, :, :], dst[:, :, :], spread4(g1[:, :]), ALU.is_equal))
                        if k == 0:
                            link(nc.vector.scalar_tensor_tensor(others[:, :, :], hot[:, :, :], -1e30, x[:, :, :],
                                                                ALU.mult, ALU.add))
                            x = others
                    link(nc.vector.tensor_tensor(hot[:, :, :], hot[:, :, :], hot2[:, :, :], ALU.add))

                dve.wait_ge(s["lg_ps"], up("lg_ps", it))
                logits = ps[:, 0, 0:4 * NE].rearrange("p (t e) -> p t e", e=NE)
                if swiglu:
                    link(nc.vector.tensor_scalar(lg[:, :, :], logits, float(P) ** -0.5, None, ALU.mult))
                    link(nc.vector.tensor_tensor(lr[:, :, :], lg[:, :, :],
                                                 gcon[:, 2:].rearrange("p (t e) -> p t e", e=NE), ALU.add))
                    best_two(lr, others)
                    link(nc.vector.tensor_scalar(lr[:, :, :], hot[:, :, :], 1e30, -1e30, ALU.mult, ALU.add))
                    link(nc.vector.tensor_tensor(lg[:, :, :], lg[:, :, :], hot[:, :, :], ALU.mult))
                    link(nc.vector.tensor_tensor(lr[:, :, :], lr[:, :, :], lg[:, :, :], ALU.add))
                    src = lr
                else:
                    src = logits
                link(nc.vector.tensor_reduce(g1[:, :], src if src is logits else src[:, :, :], AX, ALU.max, negate=True))
                nc.vector.tensor_tensor(lr[:, :, :], src if src is logits else src[:, :, :], spread4(g1[:, :]),
                                        ALU.add).then_inc(s["lg"], 1)
                dve.wait_ge(s["exp"], up("exp", it))
                link(nc.vector.tensor_reduce(g1[:, :], lr[:, :, :], AX, ALU.add))
                link(nc.vector.reciprocal(g1[:, :], g1[:, :]))
                if swiglu:
                    nc.vector.tensor_tensor(lr[:, :, :], lr[:, :, :], spread4(g1[:, :]), ALU.mult).then_inc(s["gate"], 1)
                else:
                    link(nc.vector.tensor_tensor(lg[:, :, :], lr[:, :, :], spread4(g1[:, :]), ALU.mult))
                    best_two(lg, others)
                    nc.vector.tensor_tensor(lr[:, :, :], lg[:, :, :], hot[:, :, :], ALU.mult).then_inc(s["gate"], 1)

                for n in range(U):
                    e = n // 2
                    dve.wait_ge(s["act"], up("act", it, n))
                    if n >= 2:
                        dve.wait_ge(s["out"], up("out", it, n - 2))
                    if e < NE:
                        dve.wait_ge(s["wb"], up("wb", it, e))
                    if swiglu and e < NE:
                        link(nc.vector.tensor_tensor(ga[:, n % 2, :], ga[:, n % 2, :], ps[:, 2 + n % 2, :], ALU.mult))
                    other = ps[:, e % 2, :] if e < NE else ps[:, 2 + n % 2, :]
                    nc.vector.tensor_tensor(hs[:, n % 2, :], ga[:, n % 2, :], other, ALU.mult).then_inc(s["hs"], 1)
                dve.wait_ge(s["out"], up("out", it, U - 1))
                nc.vector.tensor_tensor(c.xt[:, here], c.xt[:, here], ps[:, 6, :], ALU.add).then_inc(s["done"], 1)
            link.close()


THRESH = 0.01


def threshold_attention_phase(c):
    s = c.signals(th_w=1, th_set=1, th_x=1, th_x_ps=1, th_v=1, th_s_ps=TILES, th_exp=TILES, th_p=TILES, th_t_ps=TILES,
                  th_t=TILES, th_y_ps=TILES, th_done=1)
    nc, d, up, ps = c.nc, c.d, c.up, c.ps
    with ExitStack() as ctx:
        w = c.sb(ctx, "th_wt", [P, P])
        ones = c.sb(ctx, "th_ones", [P, P])
        xb = c.sb(ctx, "th_xb", [P, T])
        v = c.sb(ctx, "th_vt", [P, TILES, P])
        e = c.sb(ctx, "th_e", [P, 2, T])
        keep = c.sb(ctx, "th_keep", [P, 2, T])
        low = c.sb(ctx, "th_low", [P, T])
        z = c.sb(ctx, "th_z", [P, 2, 4])
        vac = c.sb(ctx, "th_vac", [P, 2, P])
        pt = c.sb(ctx, "th_pt", [P, TILES + 1, P])
        block = ctx.enter_context(nc.Block())

        @block.sync
        def _(sp):
            sp.dma_start(w[:, :], d["th_w"]).then_inc(s["th_w"], 16)
            sp.wait_ge(s["th_w"], 16)

        @block.tensor
        def _(pe):
            pe.wait_ge(s["th_w"], 16)
            with pe.Fori(0, B) as it:
                pe.wait_ge(s["th_x"], up("th_x", it))
                for t in range(TILES):
                    last = nc.tensor.transpose(ps[:, 6 + t // 4, (t % 4) * P:(t % 4 + 1) * P],
                                               xb[:, t * P:(t + 1) * P], c.ident[:, :])
                last.then_inc(s["th_x_ps"], 1)
                pe.wait_ge(s["th_v"], up("th_v", it))

                def scores(t):
                    if t >= 2:
                        pe.wait_ge(s["th_exp"], up("th_exp", it, t - 2))
                    for i in range(HALVES):
                        last = nc.tensor.matmul(ps[:, 2 * (t % 2) + i, :], xb[:, t * P:(t + 1) * P],
                                                xb[:, i * BLK:(i + 1) * BLK], start=True, stop=True)
                    last.then_inc(s["th_s_ps"], 1)

                def turn(t):
                    if t:
                        pe.wait_ge(s["th_t"], up("th_t", it, t - 1))
                    pe.wait_ge(s["th_p"], up("th_p", it, t))
                    for k in range(TILES):
                        nc.tensor.transpose(ps[:, 4 + k // 4, (k % 4) * P:(k % 4 + 1) * P],
                                            keep[:, t % 2, k * P:(k + 1) * P], c.ident[:, :])
                    nc.tensor.transpose(ps[:, 6, 0:P], vac[:, t % 2, :], c.ident[:, :]).then_inc(s["th_t_ps"], 1)

                def values(t):
                    pe.wait_ge(s["th_t"], up("th_t", it, t))
                    if t:
                        pe.wait_ge(s["th_done"], it * TILES + t + 1)
                    for k in range(TILES):
                        nc.tensor.matmul(ps[:, 7, 0:P], v[:, k, :], pt[:, k, :], start=(k == 0), stop=False)
                    nc.tensor.matmul(ps[:, 7, 0:P], w[:, :], pt[:, TILES, :],
                                     start=False, stop=True).then_inc(s["th_y_ps"], 1)

                scores(0)
                for t in range(TILES):
                    if t + 1 < TILES:
                        scores(t + 1)
                    turn(t)
                    values(t)

        @block.scalar
        def _(act):
            with act.Fori(0, B) as it:
                act.wait_ge(s["th_x_ps"], up("th_x_ps", it))
                nc.scalar.activation(v[:, :, :].rearrange("p a q -> p (a q)"),
                                     ps[:, 6:8, :].rearrange("p a q -> p (a q)"), ACT.Copy).then_inc(s["th_v"], 1)
                for t in range(TILES):
                    act.wait_ge(s["th_s_ps"], up("th_s_ps", it, t))
                    if t >= 2:
                        act.wait_ge(s["th_p"], up("th_p", it, t - 2))
                    nc.scalar.activation(e[:, t % 2, :], ps[:, 2 * (t % 2):2 * (t % 2) + 2, :].rearrange("p a q -> p (a q)"),
                                         ACT.Exp, scale=float(P) ** -0.5,
                                         accum_out=z[:, t % 2, 0:1]).then_inc(s["th_exp"], 1)
                    act.wait_ge(s["th_t_ps"], up("th_t_ps", it, t))
                    if t:
                        act.wait_ge(s["th_y_ps"], up("th_y_ps", it, t - 1))
                    nc.scalar.activation(pt[:, 0:TILES, :].rearrange("p a q -> p (a q)"),
                                         ps[:, 4:6, :].rearrange("p a q -> p (a q)"), ACT.Copy)
                    nc.scalar.activation(pt[:, TILES, :], ps[:, 6, 0:P], ACT.Copy).then_inc(s["th_t"], 1)

        @block.vector
        def _(dve):
            link = Chain(c, dve, "th_dve", 7 * TILES)
            nc.vector.memset(ones[:, :], 1.0).then_inc(s["th_set"], 1)
            dve.wait_ge(s["th_set"], 1)
            dve.sem_inc(s["th_done"], 1)
            with dve.Fori(0, B) as it:
                link.start(it)
                dve.wait_ge(s["th_done"], it * TILES + 1)
                nc.vector.tensor_scalar(xb[:, :], c.xnt[:, tokens(it * T, T)], 1.0, None,
                                        ALU.mult).then_inc(s["th_x"], 1)
                for t in range(TILES):
                    m = t % 2
                    dve.wait_ge(s["th_exp"], up("th_exp", it, t))
                    if t >= 2:
                        dve.wait_ge(s["th_t_ps"], up("th_t_ps", it, t - 2))
                    link(nc.vector.reciprocal(z[:, m, 1:2], z[:, m, 0:1]))
                    link(nc.vector.tensor_scalar(e[:, m, :], e[:, m, :], z[:, m, 1:2], None, ALU.mult))
                    link(nc.vector.scalar_tensor_tensor(keep[:, m, :], e[:, m, :], THRESH, e[:, m, :],
                                                        ALU.is_ge, ALU.mult, accum_out=z[:, m, 2:3]))
                    link(nc.vector.scalar_tensor_tensor(low[:, :], e[:, m, :], THRESH, e[:, m, :],
                                                        ALU.is_lt, ALU.mult, accum_out=z[:, m, 3:4]))
                    link(nc.vector.tensor_scalar(z[:, m, 2:3], z[:, m, 2:3], 1e-9, None, ALU.add))
                    link(nc.vector.reciprocal(z[:, m, 2:3], z[:, m, 2:3]))
                    link(nc.vector.tensor_scalar(keep[:, m, :], keep[:, m, :], z[:, m, 2:3], None, ALU.mult))
                    nc.vector.tensor_scalar(vac[:, m, :], ones[:, :], z[:, m, 3:4], 0.01,
                                            ALU.mult, ALU.mult).then_inc(s["th_p"], 1)
                    here = tokens(it * T + t * P, P)
                    dve.wait_ge(s["th_y_ps"], up("th_y_ps", it, t))
                    nc.vector.tensor_tensor(c.xt[:, here], c.xt[:, here], ps[:, 7, 0:P], ALU.add).then_inc(s["th_done"], 1)
            link.close()


def quantise(c, link, x, q, sc, tmp, n):
    nc = c.nc
    g = 4 * n
    grp = lambda t: t.rearrange("p n (b e) -> p (n b) e", e=32)
    by = lambda t: t.unsqueeze(2).to_broadcast([P, g, 32])
    a, b, y = tmp[:, 0, 0:n, :], tmp[:, 1, 0:n, :], tmp[:, 2, 0:n, :]
    big = 1.5 * 2.0 ** 23
    link(nc.vector.tensor_reduce(sc[:, 0, 0:g], grp(x), AX, ALU.max, apply_absolute_value=True))
    link(nc.vector.tensor_scalar(sc[:, 0, 0:g], sc[:, 0, 0:g], 1 / 7.5, 1e-30, ALU.mult, ALU.max))
    link(nc.vector.reciprocal(sc[:, 1, 0:g], sc[:, 0, 0:g]))
    link(nc.vector.tensor_tensor(grp(y), grp(x), by(sc[:, 1, 0:g]), ALU.mult))
    link(nc.vector.scalar_tensor_tensor(a, y, -1.0, y, ALU.mult, ALU.max))
    link(nc.vector.tensor_scalar(b, a, 4.0, 2.0, ALU.is_lt, ALU.mult))
    link(nc.vector.tensor_scalar(a, a, 2.0, 4.0, ALU.is_lt, ALU.mult))
    link(nc.vector.scalar_tensor_tensor(q, b, 2.0, a, ALU.add, ALU.add))
    link(nc.vector.scalar_tensor_tensor(b, b, 4.0, a, ALU.mult, ALU.add))
    link(nc.vector.tensor_scalar(b, b, -1 / 32, 0.5, ALU.mult, ALU.add))
    link(nc.vector.tensor_tensor(y, y, q, ALU.mult))
    link(nc.vector.tensor_scalar(a, y, big, -big, ALU.add, ALU.add))
    link(nc.vector.tensor_tensor(y, a, y, ALU.subtract))
    link(nc.vector.scalar_tensor_tensor(a, y, 0.5, a, ALU.is_ge, ALU.subtract))
    link(nc.vector.scalar_tensor_tensor(a, a, -1.0, b, ALU.mult, ALU.mult))
    return nc.vector.tensor_tensor(grp(q), grp(a), by(sc[:, 0, 0:g]), ALU.mult)


def quantised_linear_phase(c):
    s = c.signals(ql_w=1, ql_wq=1, ql_w_ps=1, ql_x=1, ql_t_ps=1, ql_t=1, ql_q=1, ql_q_ps=1, ql_qt=1, ql_y_ps=1,
                  ql_done=1)
    nc, d, up, ps = c.nc, c.d, c.up, c.ps
    with ExitStack() as ctx:
        w = c.sb(ctx, "ql_wb", [P, 1, P])
        wt = c.sb(ctx, "ql_wt", [P, P])
        bias = c.sb(ctx, "ql_bias", [P, 1])
        xb = c.sb(ctx, "ql_xb", [P, BLK])
        x = c.sb(ctx, "ql_xr", [P, 4, P])
        q = c.sb(ctx, "ql_qb", [P, 4, P])
        qt = c.sb(ctx, "ql_qtb", [P, BLK])
        tmp = c.sb(ctx, "ql_tmp", [P, 3, 4, P])
        sc = c.sb(ctx, "ql_sc", [P, 2, 16])
        block = ctx.enter_context(nc.Block())

        @block.sync
        def _(sp):
            sp.dma_start(w[:, 0, :], d["ql_w"]).then_inc(s["ql_w"], 16)
            sp.dma_start(bias[:, :], d["ql_b"]).then_inc(s["ql_w"], 16)
            sp.wait_ge(s["ql_w"], 32)

        @block.tensor
        def _(pe):
            pe.wait_ge(s["ql_wq"], 1)
            nc.tensor.transpose(ps[:, 0, 0:P], q[:, 0, :], c.ident[:, :]).then_inc(s["ql_w_ps"], 1)
            with pe.Fori(0, NB) as it:
                pe.wait_ge(s["ql_x"], up("ql_x", it))
                for t in range(4):
                    last = nc.tensor.transpose(ps[:, 1, t * P:(t + 1) * P], xb[:, t * P:(t + 1) * P], c.ident[:, :])
                last.then_inc(s["ql_t_ps"], 1)
                pe.wait_ge(s["ql_q"], up("ql_q", it))
                for t in range(4):
                    last = nc.tensor.transpose(ps[:, 2, t * P:(t + 1) * P], q[:, t, :], c.ident[:, :])
                last.then_inc(s["ql_q_ps"], 1)
                pe.wait_ge(s["ql_qt"], up("ql_qt", it))
                nc.tensor.matmul(ps[:, 3, :], wt[:, :], qt[:, :], start=True, stop=True).then_inc(s["ql_y_ps"], 1)

        @block.scalar
        def _(act):
            with act.Fori(0, NB) as it:
                act.wait_ge(s["ql_t_ps"], up("ql_t_ps", it))
                nc.scalar.activation(x[:, :, :].rearrange("p a q -> p (a q)"), ps[:, 1, :], ACT.Copy).then_inc(s["ql_t"], 1)
                act.wait_ge(s["ql_q_ps"], up("ql_q_ps", it))
                nc.scalar.activation(qt[:, :], ps[:, 2, :], ACT.Copy).then_inc(s["ql_qt"], 1)

        @block.vector
        def _(dve):
            once = Chain(c, dve, "ql_once", 15)
            link = Chain(c, dve, "ql_dve", 15)
            dve.wait_ge(s["ql_w"], 32)
            once.start(0)
            quantise(c, once, w[:, :, :], q[:, 0:1, :], sc, tmp, 1).then_inc(s["ql_wq"], 1)
            once.close()
            dve.wait_ge(s["ql_w_ps"], 1)
            nc.vector.tensor_copy(wt[:, :], ps[:, 0, 0:P]).then_inc(s["ql_done"], 1)
            with dve.Fori(0, NB) as it:
                link.start(it)
                here = tokens(it * BLK, BLK)
                dve.wait_ge(s["ql_done"], it + 1)
                nc.vector.tensor_scalar(xb[:, :], c.xnt[:, here], 1.0, None, ALU.mult).then_inc(s["ql_x"], 1)
                dve.wait_ge(s["ql_t"], up("ql_t", it))
                quantise(c, link, x[:, :, :], q[:, :, :], sc, tmp, 4).then_inc(s["ql_q"], 1)
                dve.wait_ge(s["ql_y_ps"], up("ql_y_ps", it))
                nc.vector.scalar_tensor_tensor(c.xt[:, here], ps[:, 3, :], bias[:, 0:1], c.xt[:, here],
                                               ALU.add, ALU.add).then_inc(s["ql_done"], 1)
            link.close()


S = 32
NS = T // S


class LinearState:

    def __init__(self, c, ctx):
        self.u = c.sb(ctx, "li_u", [P, B, T])
        self.q = c.sb(ctx, "li_q", [P, B, T])
        self.z = c.sb(ctx, "li_z", [P, B, T])
        self.v = c.sb(ctx, "li_v", [P, B, TILES, P])
        self.wo = c.sb(ctx, "li_wo", [P, P])
        self.cols = c.sb(ctx, "li_cols", [P, 3])


def linear_project_phase(c, st):
    s = c.signals(lp_w=1, lp_x=1, lp_qk_ps=2, lp_k=2, lp_sq=2, lp_ms=2, lp_sd=2, lp_u=2, lp_s_ps=1, lp_s=1,
                  lp_v_ps=TILES, lp_v=TILES, lp_done=1)
    nc, d, up, ps = c.nc, c.d, c.up, c.ps
    with ExitStack() as ctx:
        w = c.sb(ctx, "lp_wb", [P, 3, P])
        bv = c.sb(ctx, "lp_bv", [P, P])
        ones = c.sb(ctx, "lp_ones", [P, 1])
        eps = c.eps6
        xb = c.sb(ctx, "lp_xb", [P, T])
        k = c.sb(ctx, "lp_kb", [P, T])
        kq = c.sb(ctx, "lp_kq", [P, T])
        sq = c.sb(ctx, "lp_sqb", [P, 2, BLK])
        sd = c.sb(ctx, "lp_sdb", [P, 2, BLK])
        sk = c.sb(ctx, "lp_sk", [P, TILES])
        vb = c.sb(ctx, "lp_vb", [P, P])
        block = ctx.enter_context(nc.Block())

        @block.sync
        def _(sp):
            for dst, x in [(w[:, :, :], "lp_w"), (bv[:, :], "lp_bv"), (st.wo[:, :], "li_wo"), (st.cols[:, :], "li_cols"),
                           (ones[:, :], "c_ones")]:
                sp.dma_start(dst, d[x]).then_inc(s["lp_w"], 16)
            sp.wait_ge(s["lp_w"], 80)

        @block.tensor
        def _(pe):
            pe.wait_ge(s["lp_w"], 80)
            with pe.Fori(0, B) as it:
                pe.wait_ge(s["lp_x"], up("lp_x", it))
                for i in range(HALVES):
                    for x in range(2):
                        last = nc.tensor.matmul(ps[:, 2 * x + i, :], w[:, x, :], xb[:, i * BLK:(i + 1) * BLK],
                                                start=True, stop=True)
                    last.then_inc(s["lp_qk_ps"], 1)
                for i in range(HALVES):
                    pe.wait_ge(s["lp_sq"], up("lp_sq", it, i))
                    nc.tensor.matmul(ps[:, 4 + i, :], c.mean_w[:, :], sq[:, i, :],
                                     start=True, stop=True).then_inc(s["lp_ms"], 1)
                pe.wait_ge(s["lp_u"], up("lp_u", it, 1))
                for t in range(TILES):
                    last = nc.tensor.matmul(ps[:, 0, t:t + 1], kq[:, t * P:(t + 1) * P], ones[:, :],
                                            start=True, stop=True)
                last.then_inc(s["lp_s_ps"], 1)
                for t in range(TILES):
                    if t >= 2:
                        pe.wait_ge(s["lp_v"], up("lp_v", it, t - 2))
                    nc.tensor.matmul(ps[:, 6 + t % 2, 0:P], xb[:, t * P:(t + 1) * P], w[:, 2, :],
                                     start=True, stop=True).then_inc(s["lp_v_ps"], 1)

        @block.scalar
        def _(act):
            with act.Fori(0, B) as it:
                for i in range(HALVES):
                    act.wait_ge(s["lp_k"], up("lp_k", it, i))
                    nc.scalar.activation(sq[:, i, :], k[:, i * BLK:(i + 1) * BLK], ACT.Square).then_inc(s["lp_sq"], 1)
                for i in range(HALVES):
                    act.wait_ge(s["lp_ms"], up("lp_ms", it, i))
                    nc.scalar.activation(sd[:, i, :], ps[:, 4 + i, :], ACT.Sqrt, scale=float(P)).then_inc(s["lp_sd"], 1)

        @block.vector
        def _(dve):
            link = Chain(c, dve, "lp_dve", 1 + HALVES + 3 * HALVES + TILES)
            dve.wait_ge(s["lp_w"], 80)
            dve.sem_inc(s["lp_done"], 1)
            with dve.Fori(0, B) as it:
                link.start(it)
                dve.wait_ge(s["lp_done"], it + 1)
                nc.vector.tensor_scalar(xb[:, :], c.xnt[:, tokens(it * T, T)], 1.0, None, ALU.mult).then_inc(s["lp_x"], 1)
                uu = st.u[:, :, :].rearrange("p b t -> p (b t)")
                qq = st.q[:, :, :].rearrange("p b t -> p (b t)")
                vv = st.v[:, :, :, :].rearrange("p b t e -> p (b t e)")
                for i in range(HALVES):
                    half = slice(i * BLK, (i + 1) * BLK)
                    here = tokens(it * T + i * BLK, BLK)
                    dve.wait_ge(s["lp_qk_ps"], up("lp_qk_ps", it, i))
                    link(nc.vector.tensor_scalar(qq[:, here], ps[:, i, :], st.cols[:, 0:1], None, ALU.add))
                    nc.vector.tensor_scalar(k[:, half], ps[:, 2 + i, :], st.cols[:, 1:2], None,
                                            ALU.add).then_inc(s["lp_k"], 1)
                for i in range(HALVES):
                    half = slice(i * BLK, (i + 1) * BLK)
                    here = tokens(it * T + i * BLK, BLK)
                    dve.wait_ge(s["lp_sd"], up("lp_sd", it, i))
                    link(nc.vector.tensor_tensor(kq[:, half], k[:, half], qq[:, here], ALU.mult))
                    link(nc.vector.tensor_scalar(sd[:, i, :], sd[:, i, :], 1e-6, None, ALU.add))
                    link(nc.vector.reciprocal(sd[:, i, :], sd[:, i, :]))
                    nc.vector.tensor_tensor(uu[:, here], k[:, half], sd[:, i, :], ALU.mult).then_inc(s["lp_u"], 1)
                dve.wait_ge(s["lp_s_ps"], up("lp_s_ps", it))
                link(nc.vector.tensor_scalar(sk[:, :], ps[:, 0, 0:TILES], 1.0, None, ALU.mult))
                for t in range(TILES):
                    dve.wait_ge(s["lp_v_ps"], up("lp_v_ps", it, t))
                    link(nc.vector.tensor_tensor(vb[:, :], bv[:, :], ps[:, 6 + t % 2, 0:P], ALU.add))
                    last = nc.vector.tensor_scalar(vv[:, tokens(it * T + t * P, P)], vb[:, :], sk[:, t:t + 1], None,
                                                   ALU.mult).then_inc(s["lp_v"], 1)
                    dve.wait_ge(s["lp_v"], up("lp_v", it, t))
                dve.sem_inc(s["lp_done"], 1)
            link.close()


def linear_scan_phase(c, st):
    s = c.signals(ls_w=1, ls_u=1, ls_v_ps=1, ls_v=1, ls_vt=1, ls_s_ps=1, ls_m=1, ls_w_ps=1, ls_wb=1, ls_zb=1,
                  ls_z_ps=1, ls_a_ps=1, ls_a=1)
    nc, d, up, ps = c.nc, c.d, c.up, c.ps
    with ExitStack() as ctx:
        eye = c.sb(ctx, "ls_eye", [P, S])
        below = c.sb(ctx, "ls_below", [P, S])
        diag = c.sb(ctx, "ls_diag", [P, B, S])
        a = c.sb(ctx, "ls_ab", [P, B, P])
        ub = c.sb(ctx, "ls_ub", [P, B, S])
        v = c.sb(ctx, "ls_vb", [P, P])
        vt = c.sb(ctx, "ls_vtb", [P, B, S])
        f = c.sb(ctx, "ls_f", [P, 2 * S])
        row = c.sb(ctx, "ls_row", [P, 2 * S])
        r = c.sb(ctx, "ls_r", [P, 2])
        dinv = c.sb(ctx, "ls_dinv", [P, 1])
        m = c.sb(ctx, "ls_mb", [P, 2, S])
        mt = c.sb(ctx, "ls_mtb", [P, 2, S])
        mz = c.sb(ctx, "ls_mz", [P, 2, B, S])
        w = c.sb(ctx, "ls_wbf", [P, P])
        z = c.sb(ctx, "ls_zbf", [P, P])
        block = ctx.enter_context(nc.Block())

        @block.sync
        def _(sp):
            sp.dma_start(eye[:, :], d["c_eye32"]).then_inc(s["ls_w"], 16)
            sp.dma_start(below[:, :], d["c_below"]).then_inc(s["ls_w"], 16)
            sp.dma_start(diag[:, :, :], d["c_diag"]).then_inc(s["ls_w"], 16)
            for b in range(B):
                sp.dma_start(a[:, b, :], c.ident[:, :]).then_inc(s["ls_w"], 16)
            sp.wait_ge(s["ls_w"], 112)

        @block.tensor
        def _(pe):
            pe.wait_ge(s["ls_w"], 112)
            with pe.Fori(0, NS) as it:
                pe.wait_ge(s["ls_u"], up("ls_u", it))
                for b in range(B):
                    last = nc.tensor.matmul(ps[:, 1, b * S:(b + 1) * S], a[:, b, :], ub[:, b, :], start=True, stop=True)
                for b in range(B):
                    last = nc.tensor.matmul(ps[b * S:(b + 1) * S, 0, 0:P], ub[:, b, :], a[:, b, :],
                                            start=True, stop=True, tile_position=(0, b * S))
                last.then_inc(s["ls_v_ps"], 1)
                pe.wait_ge(s["ls_vt"], up("ls_vt", it))
                for b in range(B):
                    last = nc.tensor.matmul(ps[b * S:(b + 1) * S, 2, 0:S], vt[:, b, :], ub[:, b, :],
                                            start=True, stop=True, tile_position=(0, b * S))
                last.then_inc(s["ls_s_ps"], 1)
                pe.wait_ge(s["ls_v"], up("ls_v", it))
                pe.wait_ge(s["ls_m"], up("ls_m", it))
                nc.tensor.matmul(ps[:, 0, 0:P], mz[:, 0, :, :].rearrange("p b i -> p (b i)"), v[:, :],
                                 start=True, stop=True).then_inc(s["ls_w_ps"], 1)
                nc.tensor.matmul(ps[:, 3, 0:P], v[:, :], mz[:, 1, :, :].rearrange("p b i -> p (b i)"),
                                 start=True, stop=True).then_inc(s["ls_z_ps"], 1)
                pe.wait_ge(s["ls_wb"], up("ls_wb", it))
                pe.wait_ge(s["ls_zb"], up("ls_zb", it))
                for b in range(B):
                    last = nc.tensor.matmul(ps[:, 4 + b, 0:P], w[b * S:(b + 1) * S, :], z[b * S:(b + 1) * S, :],
                                            start=True, stop=True, tile_position=(b * S, 0))
                last.then_inc(s["ls_a_ps"], 1)

        @block.scalar
        def _(act):
            with act.Fori(0, NS) as it:
                act.wait_ge(s["ls_v_ps"], up("ls_v_ps", it))
                nc.scalar.activation(v[:, :], ps[:, 0, 0:P], ACT.Copy).then_inc(s["ls_v"], 1)
                act.wait_ge(s["ls_w_ps"], up("ls_w_ps", it))
                nc.scalar.activation(w[:, :], ps[:, 0, 0:P], ACT.Copy).then_inc(s["ls_wb"], 1)
                act.wait_ge(s["ls_wb"], up("ls_wb", it))
                nc.scalar.activation(z[:, :], w[:, :], ACT.Copy, scale=dinv[:, 0:1]).then_inc(s["ls_zb"], 1)

        @block.vector
        def _(dve):
            link = LocalChain(c, dve, "ls_dve")
            dve.wait_ge(s["ls_w"], 112)
            dve.sem_inc(s["ls_a"], 1)
            with dve.Fori(0, NS) as it:
                dve.wait_ge(s["ls_a"], it + 1)
                link(nc.vector.tensor_scalar(f[:, S:2 * S], eye[:, :], 1.0, None, ALU.mult))
                nc.vector.tensor_scalar(ub[:, :, :], st.u[:, :, tokens(it * S, S)], 1.0, None,
                                        ALU.mult).then_inc(s["ls_u"], 1)
                dve.wait_ge(s["ls_v_ps"], up("ls_v_ps", it))
                nc.vector.tensor_scalar(vt[:, :, :].rearrange("p b e -> p (b e)"), ps[:, 1, 0:P], 1.0, None,
                                        ALU.mult).then_inc(s["ls_vt"], 1)
                dve.wait_ge(s["ls_s_ps"], up("ls_s_ps", it))
                link(nc.vector.tensor_tensor(f[:, 0:S], eye[:, :], ps[:, 2, 0:S], ALU.add))
                for t in range(S - 1):
                    n = 2 * S - t - (S - 1 - t)
                    here = slice(t, S + t + 1)
                    link(nc.vector.stream_shuffle(row[:, here], f[:, here], [t] * S))
                    link(nc.vector.reciprocal(r[:, 0:1], row[:, t:t + 1]))
                    link(nc.vector.scalar_tensor_tensor(r[:, 1:2], f[:, t:t + 1], r[:, 0:1], below[:, t:t + 1],
                                                        ALU.mult, ALU.mult))
                    link(nc.vector.scalar_tensor_tensor(f[:, here], row[:, here], r[:, 1:2], f[:, here],
                                                        ALU.mult, ALU.add))
                link(nc.vector.tensor_tensor(row[:, 0:S], f[:, 0:S], eye[:, :], ALU.mult))
                link(nc.vector.tensor_reduce(dinv[:, :], row[:, 0:S], AX, ALU.add))
                link(nc.vector.reciprocal(dinv[:, :], dinv[:, :]))
                link(nc.vector.tensor_scalar(m[:, 0, :], f[:, S:2 * S], 1.0, None, ALU.mult))
                link(nc.vector.tensor_scalar(m[:, 1, :], f[:, S:2 * S], dinv[:, 0:1], None, ALU.mult))
                link(nc.vector.transpose(mt[:, :, :].rearrange("p x i -> p (x i)"), m[:, :, :].rearrange("p x i -> p (x i)")))
                for x in range(2):
                    last = nc.vector.tensor_tensor(mz[:, x, :, :], mt[:, x:x + 1, :].to_broadcast([P, B, S]),
                                                   diag[:, :, :], ALU.mult)
                last.then_inc(s["ls_m"], 1)
                dve.wait_ge(s["ls_z_ps"], up("ls_z_ps", it))
                link(nc.vector.tensor_scalar(st.z[:, :, tokens(it * S, S)],
                                             ps[:, 3, 0:P].rearrange("p (b e) -> p b e", e=S), 1.0, None, ALU.mult))
                dve.wait_ge(s["ls_a_ps"], up("ls_a_ps", it))
                nc.vector.tensor_tensor(a[:, :, :], a[:, :, :], ps[:, 4:8, 0:P], ALU.subtract).then_inc(s["ls_a"], 1)
                link.clear()


def linear_output_phase(c, st):
    units = [(i, k) for i in range(HALVES) for k in range(4 * i + 4)]
    U = len(units)
    s = c.signals(lo_w=1, lo_in=1, lo_s_ps=U, lo_p=U, lo_av=U, lo_o=2, lo_y_ps=2, lo_done=1)
    nc, d, up, ps = c.nc, c.d, c.up, c.ps
    with ExitStack() as ctx:
        causal = c.sb(ctx, "lo_causal", [P, P])
        z = c.sb(ctx, "lo_z", [P, T])
        q = c.sb(ctx, "lo_q", [P, T])
        v = c.sb(ctx, "lo_v", [P, T])
        pt = c.sb(ctx, "lo_pt", [P, 3, BLK])
        o = c.sb(ctx, "lo_ob", [P, 2, BLK])
        block = ctx.enter_context(nc.Block())
        start = lambda i, k: max(k * P, i * BLK)

        @block.sync
        def _(sp):
            sp.dma_start(causal[:, :], d["c_causal"]).then_inc(s["lo_w"], 16)
            sp.wait_ge(s["lo_w"], 16)

        @block.tensor
        def _(pe):
            with pe.Fori(0, B) as it:
                pe.wait_ge(s["lo_in"], up("lo_in", it))

                def scores(n):
                    i, k = units[n]
                    q0, q1 = start(i, k), (i + 1) * BLK
                    if n >= 3:
                        pe.wait_ge(s["lo_p"], up("lo_p", it, n - 3))
                    nc.tensor.matmul(ps[:, n % 3, 0:q1 - q0], z[:, k * P:(k + 1) * P], q[:, q0:q1],
                                     start=True, stop=True).then_inc(s["lo_s_ps"], 1)

                def values(n):
                    i, k = units[n]
                    q0, q1 = start(i, k), (i + 1) * BLK
                    pe.wait_ge(s["lo_p"], up("lo_p", it, n))
                    nc.tensor.matmul(ps[:, 4 + i, q0 - i * BLK:BLK], v[:, k * P:(k + 1) * P], pt[:, n % 3, 0:q1 - q0],
                                     start=(k == 0), stop=(k == 4 * i + 3)).then_inc(s["lo_av"], 1)

                for n in range(U + 2):
                    if n < U:
                        scores(n)
                    if n >= 2:
                        values(n - 2)
                for i in range(HALVES):
                    pe.wait_ge(s["lo_o"], up("lo_o", it, i))
                    nc.tensor.matmul(ps[:, 6 + i, :], st.wo[:, :], o[:, i, :], start=True, stop=True).then_inc(s["lo_y_ps"], 1)

        @block.scalar
        def _(act):
            with act.Fori(0, B) as it:
                for i in range(HALVES):
                    act.wait_ge(s["lo_av"], up("lo_av", it, (3, U - 1)[i]))
                    nc.scalar.activation(o[:, i, :], ps[:, 4 + i, :], ACT.Copy).then_inc(s["lo_o"], 1)

        @block.vector
        def _(dve):
            link = Chain(c, dve, "lo_dve", 1)
            dve.wait_ge(s["lo_w"], 16)
            dve.sem_inc(s["lo_done"], 1)
            with dve.Fori(0, B) as it:
                link.start(it)
                dve.wait_ge(s["lo_done"], it + 1)
                here = tokens(it * T, T)
                for dst, src in ((z, st.z[:, :, :].rearrange("p b t -> p (b t)")),
                                 (q, st.q[:, :, :].rearrange("p b t -> p (b t)")),
                                 (v, st.v[:, :, :, :].rearrange("p b t e -> p (b t e)"))):
                    last = nc.vector.tensor_scalar(dst[:, :], src[:, here], 1.0, None, ALU.mult)
                last.then_inc(s["lo_in"], 1)
                for n, (i, k) in enumerate(units):
                    q0, q1 = start(i, k), (i + 1) * BLK
                    dve.wait_ge(s["lo_s_ps"], up("lo_s_ps", it, n))
                    if n >= 3:
                        dve.wait_ge(s["lo_av"], up("lo_av", it, n - 3))
                    off = P if k >= 4 * i else 0
                    if off:
                        last = nc.vector.tensor_tensor(pt[:, n % 3, 0:P], ps[:, n % 3, 0:P], causal[:, :], ALU.mult)
                    if q1 - q0 > off:
                        last = nc.vector.tensor_scalar(pt[:, n % 3, off:q1 - q0], ps[:, n % 3, off:q1 - q0], 1.0, None,
                                                       ALU.mult)
                    last.then_inc(s["lo_p"], 1)
                for i in range(HALVES):
                    here = tokens(it * T + i * BLK, BLK)
                    dve.wait_ge(s["lo_y_ps"], up("lo_y_ps", it, i))
                    ins = nc.vector.scalar_tensor_tensor(c.xt[:, here], ps[:, 6 + i, :], st.cols[:, 2:3], c.xt[:, here],
                                                         ALU.add, ALU.add)
                    if i == 0:
                        link(ins)
                ins.then_inc(s["lo_done"], 1)
            link.close()


def linear_attention(c):
    with ExitStack() as ctx:
        st = LinearState(c, ctx)
        linear_project_phase(c, st)
        linear_scan_phase(c, st)
        linear_output_phase(c, st)


def more_constants(np):
    f = np.float32
    o = {}
    gather = np.zeros((P, 8, 16), f)
    spread = np.zeros((P, 8, P), f)
    for n in range(8):
        for j in range(2):
            gather[64 * j:64 * j + 64, n, 2 * n + j] = 1
            spread[2 * n + j, n, 64 * j:64 * j + 64] = 1
    o["c_gather"], o["c_spread"] = gather, spread
    i, j = np.arange(P)[:, None], np.arange(2 * P)[None, :] - P
    ok = (i >= j) & (i <= j + 64)
    band = np.where(ok, 0, -1e30).astype(f)
    first = np.where(ok & (j >= 0), 0, -1e30).astype(f)
    o["c_band"] = np.stack([first, band], 1)
    half = np.arange(0, 64, 2, dtype=f)
    inv = (f(1.0) / f(10000.0) ** (half / f(64))).astype(f)
    t = np.arange(T, dtype=f)
    fr = (t[:, None] * inv[None, :]).astype(f)
    base = ((half + f(0.4 * 64)) / f(1.4 * 64)).astype(f)
    power = ((t - T // 2) / f(32)).astype(f)
    scale = (base[None, :] ** power[:, None]).astype(f)
    cos, sin = np.cos(fr), np.sin(fr)
    tabs = []
    for sc in (scale, 1 / scale):
        tabs.append(np.concatenate([cos * sc] * 4, 1).T)
        tabs.append(np.concatenate([-sin * sc, sin * sc] * 2, 1).T)
    o["c_tab"] = np.stack(tabs, 1).astype(f)
    head = np.arange(P) // 8
    o["c_mean8"] = (head[:, None] == head[None, :]).astype(f) / 8
    k, q = np.arange(P)[:, None], np.arange(P)[None, :]
    causal = (k <= q).astype(f)
    o["c_causal"] = causal
    o["c_ga0_mask"] = np.stack([causal, causal], 1)
    o["c_ga1_mask"] = np.stack([((q - k >= 0) & (q - k < 32)), (q + P - k < 32)], 1).astype(f)
    for n, theta in enumerate((1000000.0, 10000.0)):
        inv = (f(1.0) / f(theta) ** (np.arange(0, 8, 2, dtype=f) / f(8))).astype(f)
        fr = (t[:, None] * inv[None, :]).astype(f)
        tab = np.zeros((P, 2, T), f)
        for r in range(P):
            tab[r, 0] = np.cos(fr[:, r % 8 // 2])
            tab[r, 1] = np.sin(fr[:, r % 8 // 2]) * (1 if r % 2 else -1)
        o[f"c_ga{n}_tab"] = tab
    sel = np.zeros((8, 8, P), f)
    sel[np.arange(8), np.arange(8)] = 1
    o["c_sel"] = sel
    o["c_order"] = np.broadcast_to(np.arange(8, 0, -1, dtype=f), (P, 4, 8))
    i = np.arange(P)[:, None] % 32
    j = np.arange(32)[None, :]
    o["c_eye32"] = (i == j).astype(f)
    o["c_below"] = -(i > j).astype(f)
    o["c_diag"] = np.repeat((np.arange(P)[:, None] // 32 == np.arange(4)[None, :]).astype(f), 32, 1).reshape(P, 4, 32)
    o["c_ones"] = np.ones((P, 1), f)
    return o


def halves_swapped(np, w):
    w = w.reshape(w.shape[:-1] + (w.shape[-1] // 64, 2, 32))
    return w[..., ::-1, :].reshape(w.shape[:-3] + (-1,))


def more_layout(np, x):
    o = {}
    w = x["L0_ffn_wqkv"]
    qk = w[:, :, 0:1024].reshape(2, P, 2, 512)
    o["wa_wqk"], o["wa_wsw"], o["wa_wv"] = qk, halves_swapped(np, qk), w[:, :, 1024:]
    o["wa_wo"] = x["L0_ffn_wo"].reshape(2, 4, P, P).transpose(0, 2, 1, 3)
    o["wa_w1"] = x["L0_ffn_w1"]
    w2 = np.zeros((2, 3 * P, P), w.dtype)
    w2[:, :HID] = x["L0_ffn_w2"]
    o["wa_w2"] = w2.reshape(2, 3, P, P).transpose(0, 2, 1, 3)
    qs, ks = x["L0_ffn_q_scale"], x["L0_ffn_k_scale"]
    four = np.stack([qs, halves_swapped(np, qs), ks, halves_swapped(np, ks)], 2)
    o["wa_qks"] = np.concatenate([four, four], 1)
    o["wa_lnc"] = np.stack([x["L0_ffn_ln_g"], x["L0_ffn_ln_b"], x["L0_ffn_b2"]], 2)
    b1 = np.zeros((2, 2, 3 * P), w.dtype)
    b1[:, :, :HID] = x["L0_ffn_b1"].reshape(2, 2, HID)
    o["wa_b1"] = b1.reshape(2, 2, 3, P).transpose(0, 3, 2, 1)
    for n, p in enumerate(("g", "l")):
        wq = x[f"L1_attn_{p}_wq"]
        wk = x["L1_attn_g_k_up" if n == 0 else "L1_attn_l_wk"]
        exchanged = lambda w: w.reshape(w.shape[0], -1, 2)[..., ::-1].reshape(w.shape)
        o[f"ga{n}_wq"] = np.stack([wq, exchanged(wq)], 1)
        o[f"ga{n}_wk"] = np.zeros((wk.shape[0], 2, P), wk.dtype)
        o[f"ga{n}_wk"][:, :, :32] = np.stack([wk, exchanged(wk)], 1)
        o[f"ga{n}_wv"] = x["L1_attn_g_v_up" if n == 0 else "L1_attn_l_wv"]
        wo = np.zeros((4, 32, 4, P), wq.dtype)
        wo[:, :8] = x[f"L1_attn_{p}_wo"].reshape(4, 4, 8, P).transpose(0, 2, 1, 3)
        o[f"ga{n}_wo"] = wo.reshape(P, 4, P)
        o[f"ga{n}_nw"] = x[f"L1_attn_norm{n + 1}_w"].reshape(P, 1)
    o["ga0_wd"] = x["L1_attn_g_kv_down"]
    o["moe1_w1"] = np.concatenate([x["L1_ffn_W1"], x["L1_ffn_Ws1"][None]]).transpose(1, 0, 2)
    o["moe1_w3"] = np.concatenate([x["L1_ffn_W3"], x["L1_ffn_Ws3"][None]]).transpose(1, 0, 2)
    o["moe1_w2"] = np.concatenate([x["L1_ffn_W2"], x["L1_ffn_Ws2"][None]]).reshape(9, 2, P, P).transpose(2, 0, 1, 3)
    o["moe1_wr"] = x["L1_ffn_Wr"]
    gcon = np.zeros((P, 2 + 32), wo.dtype)
    gcon[:, 2:] = np.tile(x["L1_ffn_rb"], 4)
    o["moe1_gcon"] = gcon
    o["moe3_w1"] = x["L3_ffn_w1"].transpose(2, 0, 1)
    o["moe3_w2"] = x["L3_ffn_w2"].reshape(8, P, 2, P).transpose(3, 0, 2, 1)
    o["moe3_wr"] = x["L3_ffn_gate_w"].T
    gcon = np.zeros((P, 2 + 32), wo.dtype)
    gcon[:, 0], gcon[:, 1] = x["L3_ffn_ln_gamma"], x["L3_ffn_ln_beta"]
    o["moe3_gcon"] = gcon
    o["th_w"] = x["L2_attn_W"].T
    o["ql_w"] = x["L2_ffn_weight"]
    o["ql_b"] = x["L2_ffn_bias"].reshape(P, 1)
    o["lp_w"] = np.stack([x["L3_attn_Wq"].T, x["L3_attn_Wk"].T, x["L3_attn_Wv"].T], 1)
    o["lp_bv"] = np.broadcast_to(x["L3_attn_bv"], (P, P))
    o["li_wo"] = x["L3_attn_Wo"].T
    o["li_cols"] = np.stack([x["L3_attn_bq"], x["L3_attn_bk"], x["L3_attn_bo"]], 1)
    return o



def build(nc, d):
    with ExitStack() as ctx:
        c = Core(nc, ctx, d)
        load_phase(c)
        norm_phase(c, 0)
        full_attention_phase(c)
        window_phase(c, 0)
        window_phase(c, 1)
        c.retire("load_", "fa_", "wa_", "wm_")
        norm_phase(c, 1)
        experts_phase(c, 1)
        grouped_attention_phase(c, 0)
        grouped_attention_phase(c, 1)
        c.retire("moe1_", "ga0_", "ga1_")
        norm_phase(c, 2)
        threshold_attention_phase(c)
        quantised_linear_phase(c)
        norm_phase(c, 3)
        experts_phase(c, 3)
        linear_attention(c)
        store_phase(c)


def constants():
    import numpy as np
    f = np.float32
    out = {"c_ident": np.eye(P, dtype=f)}
    row8 = np.zeros((P, P), f)
    for j in range(4):
        row8[32 * j + 8, 32 * j:32 * j + 32] = 1
    out["c_row8"] = row8
    out.update(more_constants(np))
    return out


def heads_padded(np, w):
    w = w.reshape(w.shape[:-1] + (4, 4, 8))
    out = np.zeros(w.shape[:-1] + (32,), w.dtype)
    out[..., :8] = w
    return out.reshape(w.shape[:-3] + (4, P))


def laid_out(np, x):
    o = {"z": x["L0_attn_z"]}
    wqkv, bqkv = x["L0_attn_W_qkv"], x["L0_attn_b_qkv"]
    o["fa_wqk"] = wqkv[:, 0:2 * P].reshape(P, 2, P)
    o["fa_wv"] = wqkv[:, 2 * P:]
    o["fa_wp"] = heads_padded(np, x["L0_attn_W_proj"].T).transpose(2, 1, 0)
    o["fa_bv"] = np.broadcast_to(bqkv[2 * P:], (P, P))
    o["fa_cols"] = np.stack([x["L0_attn_ln_w"], x["L0_attn_ln_b"], x["L0_attn_b_proj"], bqkv[0:P], bqkv[P:2 * P]], 1)
    o.update(more_layout(np, x))
    return o


def kernel(**inputs):
    import numpy as np
    import concourse.bacc as bacc
    from concourse.bass_utils import run_bass_kernel_spmd

    nc = bacc.Bacc("TRN2", target_bir_lowering=False, num_devices=1)
    host = constants()
    host.update(laid_out(np, {k: np.asarray(a) for k, a in inputs.items()}))
    arrays, d = {}, {}
    for name, a in host.items():
        arrays[f"in_{name}"] = np.ascontiguousarray(a)
        d[name] = nc.dram_tensor(f"in_{name}", a.shape, mybir.dt.from_np(a.dtype), kind="ExternalInput").ap()
    d["out"] = nc.dram_tensor("out_x", (B, T, P), F32, kind="ExternalOutput").ap()
    build(nc, d)
    r = run_bass_kernel_spmd(nc, [arrays], core_ids=[0])
    return r.results[0]["out_x"]
```

```python
from contextlib import ExitStack

import concourse.bass as bass
from concourse import mybir

F32 = mybir.dt.float32
BF16 = mybir.dt.bfloat16
ALU = mybir.AluOpType
ACT = mybir.ActivationFunctionType
AX = mybir.AxisListType.X

P = 128
B, T = 4, 1024
NTOK = B * T
BLK = 512
NB = NTOK // BLK
HALVES = T // BLK
TILES = T // P


class Core:

    def __init__(self, nc, ctx, d):
        self.nc, self.ctx, self.d = nc, ctx, d
        self.sem, self.per = {}, {}
        self.xt = self.sb(ctx, "xt", [P, NTOK])
        self.xnt = self.sb(ctx, "xnt", [P, NTOK])
        self.ps = ctx.enter_context(nc.psum_tensor("ps", [P, 8, BLK], F32))
        self.mean_w = self.sb(ctx, "mean_w", [P, P])
        self.ident = self.sb(ctx, "ident", [P, P])
        self.eps5 = self.sb(ctx, "eps5", [P, 1])
        self.eps6 = self.sb(ctx, "eps6", [P, 1])

    def sb(self, ctx, name, shape, dt=F32):
        return ctx.enter_context(self.nc.sbuf_tensor(name, shape, dt))

    def signals(self, **per):
        for name, n in per.items():
            if name not in self.sem:
                self.sem[name] = self.nc.alloc_semaphore(name)
                self.per[name] = n
        return self.sem

    def retire(self, *prefixes):
        names = [n for n in self.sem if n.startswith(prefixes)]
        with self.nc.Block() as block:
            @block.gpsimd
            def _(pool):
                for n in names:
                    pool.sem_clear(self.sem[n])
        for n in names:
            self.nc.release_semaphore(self.sem.pop(n))
            del self.per[n]

    def up(self, name, it, i=0):
        return it * self.per[name] + (i + 1)


class Chain:

    def __init__(self, core, eng, name, per):
        core.signals(**{name: per})
        self.core, self.eng, self.name, self.n = core, eng, name, 0
        self.it = 0

    def start(self, it):
        self.it, self.n = it, 0

    def __call__(self, ins):
        ins.then_inc(self.core.sem[self.name], 1)
        self.eng.wait_ge(self.core.sem[self.name], self.core.up(self.name, self.it, self.n))
        self.n += 1

    def close(self):
        assert self.n == self.core.per[self.name], (self.name, self.n)


class LocalChain:

    def __init__(self, core, eng, name):
        core.signals(**{name: 1})
        self.sem, self.eng, self.n = core.sem[name], eng, 0

    def __call__(self, ins):
        self.n += 1
        ins.then_inc(self.sem, 1)
        self.eng.wait_ge(self.sem, self.n)

    def later(self, ins):
        self.n += 1
        ins.then_inc(self.sem, 1)

    def clear(self):
        self.n = 0
        self.eng.sem_clear(self.sem)


def tokens(start, n):
    return bass.ds(start, n)


def load_phase(c):
    s = c.signals(load_in0=1, load_in1=1, load_in2=1, load_in3=1, load_const=1, load_set=1, load_ps=32, load_xt=32)
    nc, d = c.nc, c.d
    with ExitStack() as ctx:
        raw = c.sb(ctx, "load_raw", [P, NTOK // P, P])
        block = ctx.enter_context(nc.Block())

        @block.sync
        def _(sp):
            sp.dma_start(c.ident[:, :], d["c_ident"]).then_inc(s["load_const"], 16)
            z = d["z"].rearrange("b (n p) d -> p (b n) d", p=P)
            for i in range(4):
                sp.dma_start(raw[:, 8 * i:8 * i + 8, :], z[:, 8 * i:8 * i + 8, :]).then_inc(s[f"load_in{i}"], 16)
            sp.wait_ge(s["load_const"], 16)
            for i in range(4):
                sp.wait_ge(s[f"load_in{i}"], 16)

        @block.vector
        def _(dve):
            nc.vector.memset(c.mean_w[:, :], 1.0 / P).then_inc(s["load_set"], 1)
            nc.vector.memset(c.eps5[:, :], 1e-5).then_inc(s["load_set"], 1)
            nc.vector.memset(c.eps6[:, :], 1e-6).then_inc(s["load_set"], 1)
            for n in range(8):
                dve.wait_ge(s["load_ps"], 4 * n + 4)
                nc.vector.tensor_copy(c.xt[:, n * BLK:(n + 1) * BLK], c.ps[:, n, :]).then_inc(s["load_xt"], 1)

        @block.tensor
        def _(pe):
            pe.wait_ge(s["load_const"], 16)
            for n in range(32):
                if n % 8 == 0:
                    pe.wait_ge(s[f"load_in{n // 8}"], 16)
                nc.tensor.transpose(c.ps[:, n // 4, (n % 4) * P:(n % 4 + 1) * P], raw[:, n, :],
                                    c.ident[:, :]).then_inc(s["load_ps"], 1)


def norm_phase(c, run):
    s = c.signals(ln_w=1, ln_set=1, ln_mean=NB, ln_xc=NB, ln_sq=NB, ln_var=NB, ln_sd=1, ln_inv=1, ln_b=NB, ln_out=NB)
    nc, up, ps = c.nc, c.up, c.ps
    of = lambda n: slice(n * BLK, (n + 1) * BLK)
    with ExitStack() as ctx:
        pick = c.sb(ctx, f"ln{run}_pick", [P, NB, NB])
        spread = c.sb(ctx, f"ln{run}_spread", [P, NB, P])
        sq = c.sb(ctx, f"ln{run}_sq", [P, 2, BLK])
        sd = c.sb(ctx, f"ln{run}_sd", [P, BLK])
        block = ctx.enter_context(nc.Block())

        @block.sync
        def _(sp):
            sp.dma_start(pick[:, :, :], c.d["c_pick"]).then_inc(s["ln_w"], 16)
            sp.dma_start(spread[:, :, :], c.d["c_spread_rows"]).then_inc(s["ln_w"], 16)
            sp.wait_ge(s["ln_w"], 32 * (run + 1))

        @block.tensor
        def _(pe):
            for n in range(NB + 1):
                if n < NB:
                    if n >= 4:
                        pe.wait_ge(s["ln_xc"], up("ln_xc", run, n - 4))
                    nc.tensor.matmul(ps[:, n % 4, :], c.mean_w[:, :], c.xt[:, of(n)],
                                     start=True, stop=True).then_inc(s["ln_mean"], 1)
                if n == 1:
                    pe.wait_ge(s["ln_w"], 32 * (run + 1))
                if n:
                    pe.wait_ge(s["ln_sq"], up("ln_sq", run, n - 1))
                    nc.tensor.matmul(ps[0:NB, 4, :], pick[:, n - 1, :], sq[:, (n - 1) % 2, :],
                                     start=(n == 1), stop=(n == NB)).then_inc(s["ln_var"], 1)
            pe.wait_ge(s["ln_inv"], run + 1)
            for n in range(NB):
                if n >= 4:
                    pe.wait_ge(s["ln_out"], up("ln_out", run, n - 4))
                nc.tensor.matmul(ps[:, n % 4, :], spread[:, n, :], sd[:, :],
                                 start=True, stop=True).then_inc(s["ln_b"], 1)

        @block.scalar
        def _(act):
            for n in range(NB):
                act.wait_ge(s["ln_xc"], up("ln_xc", run, n))
                if n >= 2:
                    act.wait_ge(s["ln_var"], up("ln_var", run, n - 2))
                nc.scalar.activation(sq[:, n % 2, :], c.xnt[:, of(n)], ACT.Square).then_inc(s["ln_sq"], 1)
            act.wait_ge(s["ln_set"], run + 1)
            act.wait_ge(s["ln_var"], up("ln_var", run, NB - 1))
            nc.scalar.activation(sd[0:NB, :], ps[0:NB, 4, :], ACT.Sqrt, bias=c.eps5[0:NB, 0:1]).then_inc(s["ln_sd"], 1)

        @block.vector
        def _(dve):
            nc.vector.memset(sd[:, :], 0.0).then_inc(s["ln_set"], 1)
            for n in range(NB):
                dve.wait_ge(s["ln_mean"], up("ln_mean", run, n))
                nc.vector.tensor_tensor(c.xnt[:, of(n)], c.xt[:, of(n)], ps[:, n % 4, :],
                                        ALU.subtract).then_inc(s["ln_xc"], 1)
            dve.wait_ge(s["ln_sd"], run + 1)
            nc.vector.reciprocal(sd[0:NB, :], sd[0:NB, :]).then_inc(s["ln_inv"], 1)
            for n in range(NB):
                dve.wait_ge(s["ln_b"], up("ln_b", run, n))
                nc.vector.tensor_tensor(c.xnt[:, of(n)], c.xnt[:, of(n)], ps[:, n % 4, :],
                                        ALU.mult).then_inc(s["ln_out"], 1)


def store_phase(c):
    s = c.signals(store_ps=8, store_sb=8, store_out=1)
    nc = c.nc
    with ExitStack() as ctx:
        rows = c.sb(ctx, "store_rows", [P, NTOK // P, P])
        block = ctx.enter_context(nc.Block())

        @block.tensor
        def _(pe):
            for n in range(8):
                for i in range(4):
                    t = 4 * n + i
                    last = nc.tensor.transpose(c.ps[:, n, i * P:(i + 1) * P], c.xt[:, t * P:(t + 1) * P],
                                               c.ident[:, :])
                last.then_inc(s["store_ps"], 1)

        @block.vector
        def _(dve):
            for n in range(8):
                dve.wait_ge(s["store_ps"], n + 1)
                nc.vector.tensor_copy(rows[:, 4 * n:4 * n + 4, :],
                                      c.ps[:, n, :].rearrange("p (i d) -> p i d", i=4)).then_inc(s["store_sb"], 1)

        @block.sync
        def _(sp):
            out = c.d["out"].rearrange("b (n p) d -> p (b n) d", p=P)
            for n in range(8):
                sp.wait_ge(s["store_sb"], n + 1)
                sp.dma_start(out[:, 4 * n:4 * n + 4, :], rows[:, 4 * n:4 * n + 4, :]).then_inc(s["store_out"], 16)
            sp.wait_ge(s["store_out"], 16 * 8)


NH0, HD0, GRP, NG0 = 16, 8, 4, 4
PARTS = 3
MROW = 96
KROWS = MROW + PARTS


def split_parts(nc, link, x, rest, parts):
    for k in range(PARTS - 1):
        link(nc.vector.tensor_scalar(parts[k], x, 1.0, None, ALU.mult))
        link(nc.vector.tensor_tensor(rest, x, parts[k], ALU.subtract))
        x = rest
    return nc.vector.tensor_scalar(parts[PARTS - 1], x, 1.0, None, ALU.mult)


def full_attention_phase(c):
    MU, EU = GRP * TILES, GRP * HALVES * TILES
    s = c.signals(fa_w=1, fa_set=1, fa_kset=1, fa_mean=2, fa_xc=2, fa_sq=2, fa_var=2, fa_sd=2, fa_zn=2,
                  fa_qk_ps=4, fa_qk=4, fa_split=4, fa_parted=1, fa_out=96, fa_rows=288, fa_v_ps=8, fa_v=8,
                  fa_s_ps=NG0 * MU, fa_max=NG0 * MU, fa_m_ps=8, fa_m=8, fa_m_in=NG0 * PARTS * 16,
                  fa_st=NG0 * EU, fa_exp=NG0 * EU, fa_av=NG0 * EU, fa_o=8, fa_sum_ps=8, fa_ot=8,
                  fa_y_ps=2, fa_done=1)
    nc, d, up = c.nc, c.d, c.up
    scale = float(HD0) ** -0.5
    steps = [(name, i) for i in range(HALVES) for name in ("mean", "centre", "square", "var", "root", "norm")]
    steps += [(name, n) for n in range(4) for name in ("project", "bias", "split")]
    LAST = (NG0 - 1) * EU
    due = {LAST + 2 + (EU - 4) * k // len(steps): step for k, step in enumerate(steps)}
    scratch = nc.dram_tensor("fa_scratch", [2, PARTS, P, T], BF16, kind="Internal").ap()
    with ExitStack() as ctx:
        wqk = c.sb(ctx, "fa_wqk", [P, 2, P])
        wv = c.sb(ctx, "fa_wv", [P, P])
        wp = c.sb(ctx, "fa_wp", [P, NG0, P])
        cols = c.sb(ctx, "fa_cols", [P, 5])
        bv = c.sb(ctx, "fa_bv", [P, P])
        row8 = c.sb(ctx, "fa_row8", [P, P])
        znt = c.sb(ctx, "fa_znt", [P, T])
        tmp = c.sb(ctx, "fa_tmp", [P, 3, BLK])
        qf = c.sb(ctx, "fa_qf", [P, 2, BLK])
        qp = c.sb(ctx, "fa_qp", [P, 2, PARTS, T], BF16)
        q = c.sb(ctx, "fa_q6", [P, NH0, T], BF16)
        k = c.sb(ctx, "fa_k6", [P, NH0, T], BF16)
        mx = c.sb(ctx, "fa_mx", [P, 2, TILES, GRP])
        mf = c.sb(ctx, "fa_mf", [GRP, BLK])
        mp = c.sb(ctx, "fa_mp", [GRP, PARTS, T], BF16)
        v = c.sb(ctx, "fa_vt", [P, TILES, NH0, 32])
        pt = c.sb(ctx, "fa_pt", [P, 3, BLK])
        rs = c.sb(ctx, "fa_rs", [P, BLK])
        ot = c.sb(ctx, "fa_otb", [P, NG0, T])
        block = ctx.enter_context(nc.Block())
        ps = c.ps

        @block.sync
        def _(sp):
            loads = [(wqk[:, :, :], "fa_wqk"), (wv[:, :], "fa_wv"), (wp[:, :, :], "fa_wp"), (bv[:, :], "fa_bv"),
                     (cols[:, :], "fa_cols"), (row8[:, :], "c_row8")]
            for dst, name in loads:
                sp.dma_start(dst, d[name]).then_inc(s["fa_w"], 16)
            sp.wait_ge(s["fa_w"], 16 * 6)
            sp.wait_ge(s["fa_set"], 3)
            sp.wait_ge(s["fa_kset"], 2)

            def parts_out(it):
                sp.wait_ge(s["fa_split"], up("fa_split", it, 3))
                for x in range(2):
                    for p in range(PARTS):
                        sp.dma_start(scratch[x, p], qp[:, x, p, :]).then_inc(s["fa_out"], 16)
                sp.wait_ge(s["fa_out"], (it + 1) * 96)
                sp.sem_inc(s["fa_parted"], 1)

            def rows_in(it):
                for x, dst in ((0, q), (1, k)):
                    for r in range(9):
                        part = r // 3 if x == 0 else r % 3
                        sp.dma_start(dst[8 * r:8 * r + 8, :, :],
                                     scratch[x, part].rearrange("(h e) t -> e h t", e=HD0)).then_inc(s["fa_rows"], 16)
                for g in range(NG0):
                    sp.wait_ge(s["fa_m"], up("fa_m", it, 2 * g + 1))
                    for p in range(PARTS):
                        sp.dma_start(q[MROW + p:MROW + p + 1, GRP * g:GRP * (g + 1), :],
                                     mp[:, p, :]).then_inc(s["fa_m_in"], 16)

            parts_out(0)
            rows_in(0)
            with sp.Fori(1, B) as it:
                parts_out(it)
                sp.wait_ge(s["fa_st"], it * NG0 * EU)
                rows_in(it)
            sp.wait_ge(s["fa_m_in"], B * NG0 * PARTS * 16)

        @block.gpsimd
        def _(pool):
            nc.gpsimd.memset(v[:, :, :, :], 0.0).then_inc(s["fa_set"], 1)
            pool.wait_ge(s["fa_set"], 1)
            nc.gpsimd.memset(v[:, :, :, 8:9], 1.0).then_inc(s["fa_set"], 1)
            pool.wait_ge(s["fa_set"], 2)
            nc.gpsimd.memset(q[:, :, :], 0.0).then_inc(s["fa_set"], 1)

        @block.tensor
        def _(pe):
            pe.wait_ge(s["fa_w"], 16 * 6)
            pe.sem_inc(s["fa_done"], 1)

            def prepare(it, step):
                name, n = step
                if name == "mean":
                    if n:
                        pe.wait_ge(s["fa_zn"], up("fa_zn", it, n - 1))
                    nc.tensor.matmul(ps[:, 0, :], c.mean_w[:, :], c.xnt[:, tokens(it * T + n * BLK, BLK)],
                                     start=True, stop=True).then_inc(s["fa_mean"], 1)
                elif name == "var":
                    pe.wait_ge(s["fa_sq"], up("fa_sq", it, n))
                    nc.tensor.matmul(ps[:, 1, :], c.mean_w[:, :], tmp[:, 1, :],
                                     start=True, stop=True).then_inc(s["fa_var"], 1)
                elif name == "project":
                    if n >= 2:
                        pe.wait_ge(s["fa_qk"], up("fa_qk", it, n - 2))
                    else:
                        pe.wait_ge(s["fa_zn"], up("fa_zn", it, 1))
                    nc.tensor.matmul(ps[:, n % 2, :], wqk[:, n // 2, :], znt[:, n % 2 * BLK:(n % 2 + 1) * BLK],
                                     start=True, stop=True).then_inc(s["fa_qk_ps"], 1)

            def attend(it, nxt):
                pe.wait_ge(s["fa_done"], it + 1)
                pe.wait_ge(s["fa_zn"], up("fa_zn", it, 1))
                for t in range(TILES):
                    if t >= 2:
                        pe.wait_ge(s["fa_v"], up("fa_v", it, t - 2))
                    nc.tensor.matmul(ps[:, 2 + t % 2, 0:P], znt[:, t * P:(t + 1) * P], wv[:, :],
                                     start=True, stop=True).then_inc(s["fa_v_ps"], 1)
                pe.wait_ge(s["fa_v"], up("fa_v", it, 7))
                pe.wait_ge(s["fa_rows"], (it + 1) * 288)

                def by_query(n):
                    h, t = n // TILES, n % TILES
                    if n >= 2:
                        pe.wait_ge(s["fa_max"], up("fa_max", it, n - 2))
                    for i in range(HALVES):
                        last = nc.tensor.matmul(ps[:, 2 * (n % 2) + i, :], q[0:72, h, t * P:(t + 1) * P],
                                                k[0:72, h, i * BLK:(i + 1) * BLK], start=True, stop=True)
                    last.then_inc(s["fa_s_ps"], 1)

                def turn_maxima(g, i):
                    pe.wait_ge(s["fa_max"], up("fa_max", it, (g + 1) * MU - 1))
                    if g or i:
                        pe.wait_ge(s["fa_m"], up("fa_m", it, 2 * g + i - 1))
                    for t in range(4):
                        last = nc.tensor.transpose(ps[0:GRP, 7, t * P:(t + 1) * P], mx[:, g % 2, 4 * i + t, :],
                                                   c.ident[:, :])
                    last.then_inc(s["fa_m_ps"], 1)

                def by_key(n):
                    g, i, j, t = n // EU, n // 32 % 2, n // 8 % 4, n % 8
                    if n >= 2:
                        pe.wait_ge(s["fa_exp"], up("fa_exp", it, n - 2))
                    if n % EU == 0:
                        pe.wait_ge(s["fa_m_in"], it * NG0 * PARTS * 16 + (g + 1) * PARTS * 16)
                    h = GRP * g + j
                    nc.tensor.matmul(ps[:, 4 + n % 2, :], k[0:KROWS, h, t * P:(t + 1) * P],
                                     q[0:KROWS, h, i * BLK:(i + 1) * BLK], start=True, stop=True).then_inc(s["fa_st"], 1)

                def values(n):
                    g, j, t, m = n // EU, n // 8 % 4, n % 8, n // 32
                    if n % 32 == 0 and m:
                        pe.wait_ge(s["fa_o"], up("fa_o", it, m - 1))
                    pe.wait_ge(s["fa_exp"], up("fa_exp", it, n))
                    nc.tensor.matmul(ps[32 * j:32 * j + 32, 6, :], v[:, t, GRP * g + j, :], pt[:, n % 3, :],
                                     start=(t == 0), stop=(t == TILES - 1),
                                     tile_position=(0, 32 * j)).then_inc(s["fa_av"], 1)

                def sums(m):
                    pe.wait_ge(s["fa_o"], up("fa_o", it, m))
                    if m:
                        pe.wait_ge(s["fa_ot"], up("fa_ot", it, m - 1))
                    else:
                        pe.wait_ge(s["fa_m"], up("fa_m", it, 2 * NG0 - 1))
                    nc.tensor.matmul(ps[:, 7, :], row8[:, :], ot[:, m // 2, m % 2 * BLK:(m % 2 + 1) * BLK],
                                     start=True, stop=True).then_inc(s["fa_sum_ps"], 1)

                for n in range(MU):
                    by_query(n)
                for i in range(HALVES):
                    turn_maxima(0, i)
                for n in range(NG0 * EU + 2):
                    g = n // EU
                    if n < NG0 * EU:
                        if n % EU == 0 and n:
                            values(n - 2)
                            values(n - 1)
                            for i in range(HALVES):
                                turn_maxima(g, i)
                        if nxt is not None and n in due:
                            prepare(nxt, due[n])
                        by_key(n)
                        if n % 2 == 0 and g + 1 < NG0:
                            by_query((g + 1) * MU + n % EU // 2)
                    if n >= 2 and not (n < NG0 * EU and n % EU < 2):
                        values(n - 2)
                    m = (n - (NG0 - 1) * EU) // 8 - 1
                    if n % 8 == 0 and 0 <= m < 2 * NG0 - 2:
                        sums(m)
                sums(2 * NG0 - 2)
                sums(2 * NG0 - 1)
                pe.wait_ge(s["fa_ot"], up("fa_ot", it, 7))
                if nxt is not None:
                    pe.wait_ge(s["fa_qk"], up("fa_qk", nxt, 3))
                for i in range(HALVES):
                    for g in range(NG0):
                        last = nc.tensor.matmul(ps[:, i, :], wp[:, g, :], ot[:, g, i * BLK:(i + 1) * BLK],
                                                start=(g == 0), stop=(g == NG0 - 1))
                    last.then_inc(s["fa_y_ps"], 1)

            for step in steps:
                prepare(0, step)
            with pe.Fori(0, B - 1) as it:
                attend(it, it + 1)
            attend(B - 1, None)

        @block.scalar
        def _(act):
            act.wait_ge(s["fa_w"], 16 * 6)

            def prepare(it, step):
                name, n = step
                if name == "square":
                    act.wait_ge(s["fa_xc"], up("fa_xc", it, n))
                    nc.scalar.activation(tmp[:, 1, :], tmp[:, 0, :], ACT.Square).then_inc(s["fa_sq"], 1)
                elif name == "root":
                    act.wait_ge(s["fa_var"], up("fa_var", it, n))
                    nc.scalar.activation(tmp[:, 2, :], ps[:, 1, :], ACT.Sqrt,
                                         bias=c.eps5[:, 0:1]).then_inc(s["fa_sd"], 1)
                elif name == "bias":
                    act.wait_ge(s["fa_qk_ps"], up("fa_qk_ps", it, n))
                    if n >= 2:
                        act.wait_ge(s["fa_split"], up("fa_split", it, n - 2))
                    nc.scalar.activation(qf[:, n % 2, :], ps[:, n % 2, :], ACT.Identity,
                                         bias=cols[:, 3 + n // 2:4 + n // 2]).then_inc(s["fa_qk"], 1)

            def attend(it, nxt):
                def copy_out(m):
                    act.wait_ge(s["fa_av"], up("fa_av", it, 32 * m + 31))
                    nc.scalar.activation(ot[:, m // 2, m % 2 * BLK:(m % 2 + 1) * BLK], ps[:, 6, :],
                                         ACT.Copy).then_inc(s["fa_o"], 1)

                for n in range(NG0 * EU):
                    if nxt is not None and n in due:
                        prepare(nxt, due[n])
                    if n % EU == 0 and n:
                        copy_out(n // 32 - 1)
                    act.wait_ge(s["fa_st"], up("fa_st", it, n))
                    if n >= 3:
                        act.wait_ge(s["fa_av"], up("fa_av", it, n - 3))
                    nc.scalar.activation(pt[:, n % 3, :], ps[:, 4 + n % 2, :], ACT.Exp,
                                         scale=scale).then_inc(s["fa_exp"], 1)
                    if n % EU == 33:
                        copy_out(n // 32 - 1)
                copy_out(7)

            for step in steps:
                prepare(0, step)
            with act.Fori(0, B - 1) as it:
                attend(it, it + 1)
            attend(B - 1, None)

        @block.vector
        def _(dve):
            link = Chain(c, dve, "fa_dve", 8 * 4 + 8 + HALVES)
            plink = Chain(c, dve, "fa_prep", 2 * HALVES + 4 * 4)
            nc.vector.memset(k[:, :, :], 0.0).then_inc(s["fa_kset"], 1)
            dve.wait_ge(s["fa_kset"], 1)
            nc.vector.memset(k[MROW:P, :, :], 1.0).then_inc(s["fa_kset"], 1)
            dve.wait_ge(s["fa_w"], 16 * 6)
            dve.wait_ge(s["fa_set"], 3)

            def prepare(it, step):
                name, n = step
                if name == "centre":
                    if n == 0:
                        plink.start(it)
                    dve.wait_ge(s["fa_mean"], up("fa_mean", it, n))
                    nc.vector.tensor_tensor(tmp[:, 0, :], c.xnt[:, tokens(it * T + n * BLK, BLK)], ps[:, 0, :],
                                            ALU.subtract).then_inc(s["fa_xc"], 1)
                elif name == "norm":
                    dve.wait_ge(s["fa_sd"], up("fa_sd", it, n))
                    plink(nc.vector.reciprocal(tmp[:, 2, :], tmp[:, 2, :]))
                    plink(nc.vector.tensor_tensor(tmp[:, 1, :], tmp[:, 0, :], tmp[:, 2, :], ALU.mult))
                    nc.vector.tensor_scalar(znt[:, n * BLK:(n + 1) * BLK], tmp[:, 1, :], cols[:, 0:1], cols[:, 1:2],
                                            ALU.mult, ALU.add).then_inc(s["fa_zn"], 1)
                elif name == "split":
                    half = slice(n % 2 * BLK, (n % 2 + 1) * BLK)
                    dve.wait_ge(s["fa_qk"], up("fa_qk", it, n))
                    if n:
                        dve.wait_ge(s["fa_split"], up("fa_split", it, n - 1))
                    split_parts(nc, plink, qf[:, n % 2, :], tmp[:, 0, :],
                                [qp[:, n // 2, p, half] for p in range(PARTS)]).then_inc(s["fa_split"], 1)
                    if n == 3:
                        dve.wait_ge(s["fa_split"], up("fa_split", it, n))

            def attend(it, nxt):
                link.start(it)
                for t in range(TILES):
                    dve.wait_ge(s["fa_v_ps"], up("fa_v_ps", it, t))
                    nc.vector.tensor_tensor(v[:, t, :, 0:8],
                                            ps[:, 2 + t % 2, 0:P].rearrange("p (h e) -> p h e", e=8),
                                            bv[:, :].rearrange("p (h e) -> p h e", e=8),
                                            ALU.add).then_inc(s["fa_v"], 1)

                def maxima(n):
                    g, j, t = n // MU, n // TILES % GRP, n % TILES
                    dve.wait_ge(s["fa_s_ps"], up("fa_s_ps", it, n))
                    nc.vector.tensor_reduce(mx[:, g % 2, t, j:j + 1], ps[:, 2 * (n % 2):2 * (n % 2) + 2, :],
                                            mybir.AxisListType.XY, ALU.max, negate=True).then_inc(s["fa_max"], 1)

                def split_maxima(g):
                    for i in range(HALVES):
                        half = slice(i * BLK, (i + 1) * BLK)
                        dve.wait_ge(s["fa_m_ps"], up("fa_m_ps", it, 2 * g + i))
                        if i == 0 and g:
                            dve.wait_ge(s["fa_m_in"], it * NG0 * PARTS * 16 + g * PARTS * 16)
                        split_parts(nc, link, ps[0:GRP, 7, :], mf[:, :],
                                    [mp[:, p, half] for p in range(PARTS)]).then_inc(s["fa_m"], 1)
                        dve.wait_ge(s["fa_m"], up("fa_m", it, 2 * g + i))

                def normalise(m):
                    g, i = m // 2, m % 2
                    dve.wait_ge(s["fa_sum_ps"], up("fa_sum_ps", it, m))
                    link(nc.vector.reciprocal(rs[:, :], ps[:, 7, :]))
                    here = ot[:, g, i * BLK:(i + 1) * BLK]
                    nc.vector.tensor_tensor(here, here, rs[:, :],
                                            ALU.mult).then_inc(s["fa_ot"], 1)
                    dve.wait_ge(s["fa_ot"], up("fa_ot", it, m))

                for n in range(MU):
                    maxima(n)
                split_maxima(0)
                for g in range(1, NG0):
                    for n in range(MU):
                        maxima(g * MU + n)
                    split_maxima(g)
                for n in range(LAST, LAST + EU):
                    if nxt is not None and n in due:
                        prepare(nxt, due[n])
                    m = (n - LAST) // 8 - 1
                    if (n - LAST) % 8 == 2 and 0 <= m < 2 * NG0 - 2:
                        normalise(m)
                normalise(2 * NG0 - 2)
                normalise(2 * NG0 - 1)
                for i in range(HALVES):
                    here = tokens(it * T + i * BLK, BLK)
                    dve.wait_ge(s["fa_y_ps"], up("fa_y_ps", it, i))
                    link(nc.vector.scalar_tensor_tensor(tmp[:, i, :], ps[:, i, :], cols[:, 2:3],
                                                        c.xnt[:, here], ALU.add, ALU.add))
                    ins = nc.vector.tensor_tensor(c.xt[:, here], c.xt[:, here], tmp[:, i, :], ALU.add)
                    if i == HALVES - 1:
                        ins.then_inc(s["fa_done"], 1)

            for step in steps:
                prepare(0, step)
            with dve.Fori(0, B - 1) as it:
                attend(it, it + 1)
            attend(B - 1, None)
            link.close()
            plink.close()


HD1, NPAIR = 64, 4
HID = 341
CHUNKS = [(0, 128), (128, 128), (256, HID - 256)]


def shifted_copy(nc, c, dst, start, link, last):
    link(nc.vector.tensor_scalar(dst[0:64, :], c.xnt[0:64, tokens(start, T)], 1.0, None, ALU.mult))
    nc.vector.tensor_scalar(dst[64:P, 1:T], c.xnt[64:P, tokens(start, T - 1)], 1.0, None, ALU.mult).then_inc(last, 1)


def window_phase(c, run):
    QK, U = 16, 2 * TILES
    s = c.signals(wa_w=1, wa_set=1, wa_h=1, wa_qk_ps=QK, wa_sq=QK, wa_ss=2, wa_sd=2, wa_r=1, wa_rot=QK, wa_raw=QK,
                  wa_b_ps=QK, wa_qk=QK,
                  wa_v_ps=TILES, wa_v=TILES, wa_s_ps=U, wa_sm=U, wa_nmx=U, wa_exp=U, wa_p=U, wa_t_ps=U, wa_t=U,
                  wa_o_ps=U, wa_o=U, wa_y_ps=TILES, wa_y=TILES,
                  wm_h=1, wm_mean=2, wm_xc=2, wm_sq=2, wm_var=1, wm_sd=1, wm_inv=1, wm_b=2, wm_n=2, wm_ag=6, wm_gelu=6, wm_hg=6,
                  wm_y_ps=2, wm_y=2, wa_done=1)
    nc, d, up = c.nc, c.d, c.up
    ps = c.ps
    with ExitStack() as ctx:
        name = lambda n: f"wa{run}_{n}"
        sb = lambda n, shape: c.sb(ctx, name(n), shape)
        wqk = sb("wqk", [P, 2, BLK])
        wsw = sb("wsw", [P, 2, BLK])
        wv = sb("wv", [P, BLK])
        wo = sb("wo", [P, NPAIR, P])
        w1 = sb("w1", [P, 2 * HID])
        w2 = sb("w2", [P, 3, P])
        qks = sb("qks", [P, 4])
        lnc = sb("lnc", [P, 3])
        b1 = sb("b1", [P, 3, 2])
        tab = sb("tab", [P, 4, T])
        band = sb("band", [P, 2, 2 * P])
        gather = sb("gather", [P, 8, 16])
        spread = sb("spread", [P, 8, P])
        pick = sb("pick", [P, NB, NB])
        rows = sb("rows", [P, HALVES, P])
        length = sb("length", [P, T])
        stat = sb("stat", [P, BLK])
        h = sb("h", [P, T])
        sq = sb("sq", [P, 2, BLK])
        xc = sb("xc", [P, HALVES, BLK])
        rot = sb("rot", [P, 2, BLK])
        qt = sb("qt", [P, NPAIR, P + T])
        kt = sb("kt", [P, NPAIR, P + T])
        v = sb("v", [P, 1 + TILES, BLK])
        sm = sb("sm", [P, 3, 4, 2 * P])
        nmx = sb("nmx", [P, 3, 4])
        tot = sb("tot", [P, 3, 4])
        pt = sb("pt", [P, 2, 4, 2, P])
        ot = sb("ot", [P, 2, NPAIR, P])
        hg = sb("hg", [P, 3, BLK])
        block = ctx.enter_context(nc.Block())
        ITS = (run * B, (run + 1) * B)

        @block.sync
        def _(sp):
            loads = [(wqk[:, :, :], d["wa_wqk"][run]), (wsw[:, :, :], d["wa_wsw"][run]), (wv[:, :], d["wa_wv"][run]),
                     (wo[:, :, :], d["wa_wo"][run]), (w1[:, :], d["wa_w1"][run]), (w2[:, :, :], d["wa_w2"][run]),
                     (qks[:, :], d["wa_qks"][run]),
                     (lnc[:, :], d["wa_lnc"][run]), (b1[:, :, :], d["wa_b1"][run]),
                     (tab[:, :, :], d["c_tab"]),
                     (band[:, :, :], d["c_band"]), (gather[:, :, :], d["c_gather"]), (spread[:, :, :], d["c_spread"]),
                     (pick[:, :, :], d["c_pick"]), (rows[:, :, :], d["c_spread_rows"][:, 0:HALVES])]
            for dst, src in loads:
                sp.dma_start(dst, src).then_inc(s["wa_w"], 16)
            sp.wait_ge(s["wa_w"], 16 * 15 * (run + 1))

        @block.tensor
        def _(pe):
            pe.wait_ge(s["wa_w"], 16 * 15 * (run + 1))
            pe.wait_ge(s["wa_set"], 5 * (run + 1))
            with pe.Fori(*ITS) as it:
                pe.wait_ge(s["wa_h"], up("wa_h", it))

                def square_sums(n):
                    x, p, i = n // 8, n % 8 // 2, n % 2
                    pe.wait_ge(s["wa_sq"], up("wa_sq", it, n))
                    ins = nc.tensor.matmul(ps[0:16, 4 + i, :], gather[:, 4 * x + p, :], sq[:, n % 2, :],
                                           start=(n < 2), stop=(n >= QK - 2))
                    if n >= QK - 2:
                        ins.then_inc(s["wa_ss"], 1)

                for n in range(QK):
                    x, p, i = n // 8, n % 8 // 2, n % 2
                    if n >= 2:
                        pe.wait_ge(s["wa_rot"], up("wa_rot", it, n - 2))
                    nc.tensor.matmul(ps[:, n % 2, :], wqk[:, x, p * P:(p + 1) * P], h[:, i * BLK:(i + 1) * BLK],
                                     start=True, stop=True)
                    nc.tensor.matmul(ps[:, 2 + n % 2, :], wsw[:, x, p * P:(p + 1) * P], h[:, i * BLK:(i + 1) * BLK],
                                     start=True, stop=True).then_inc(s["wa_qk_ps"], 1)
                    if n:
                        square_sums(n - 1)
                square_sums(QK - 1)
                for t in range(TILES):
                    if t >= 2:
                        pe.wait_ge(s["wa_v"], up("wa_v", it, t - 2))
                    nc.tensor.matmul(ps[:, 6 + t % 2, :], h[:, t * P:(t + 1) * P], wv[:, :],
                                     start=True, stop=True).then_inc(s["wa_v_ps"], 1)
                pe.wait_ge(s["wa_raw"], up("wa_raw", it, QK - 1))
                pe.wait_ge(s["wa_r"], up("wa_r", it))
                for n in range(QK):
                    x, p, i = n // 8, n % 8 // 2, n % 2
                    if n >= 2:
                        pe.wait_ge(s["wa_qk"], up("wa_qk", it, n - 2))
                    nc.tensor.matmul(ps[:, n % 2, :], spread[:, 4 * x + p, :], length[:, i * BLK:(i + 1) * BLK],
                                     start=True, stop=True).then_inc(s["wa_b_ps"], 1)
                pe.wait_ge(s["wa_qk"], up("wa_qk", it, QK - 1))
                pe.wait_ge(s["wa_v"], up("wa_v", it, TILES - 1))

                def scores(u):
                    t, hh = u // 2, u % 2
                    if u >= 2:
                        pe.wait_ge(s["wa_sm"], up("wa_sm", it, u - 2))
                    for k in range(4):
                        p, j = 2 * hh + k % 2, k // 2
                        rows = slice(64 * j, 64 * j + 64)
                        last = nc.tensor.matmul(ps[:, 2 * (u % 2) + k // 2, (k % 2) * 2 * P:(k % 2 + 1) * 2 * P],
                                                qt[rows, p, t * P:(t + 1) * P], kt[rows, p, t * P:(t + 2) * P],
                                                start=True, stop=True, tile_position=(64 * j, 0))
                    last.then_inc(s["wa_s_ps"], 1)

                def turn(u):
                    if u:
                        pe.wait_ge(s["wa_t"], up("wa_t", it, u - 1))
                    pe.wait_ge(s["wa_p"], up("wa_p", it, u))
                    for k in range(8):
                        last = nc.tensor.transpose(ps[:, 4 + k // 4, (k % 4) * P:(k % 4 + 1) * P],
                                                   sm[:, u % 3, k // 2, (k % 2) * P:(k % 2 + 1) * P], c.ident[:, :])
                    last.then_inc(s["wa_t_ps"], 1)

                def values(u):
                    t, hh = u // 2, u % 2
                    if u:
                        pe.wait_ge(s["wa_o"], up("wa_o", it, u - 1))
                    pe.wait_ge(s["wa_t"], up("wa_t", it, u))
                    for k in range(4):
                        p, j = 2 * hh + k % 2, k // 2
                        head = 2 * p + j
                        for e in range(2):
                            last = nc.tensor.matmul(ps[64 * j:64 * j + 64, 6, (k % 2) * P:(k % 2 + 1) * P],
                                                    v[:, t + e, head * 64:head * 64 + 64], pt[:, u % 2, k, e, :],
                                                    start=(e == 0), stop=(e == 1), tile_position=(0, 64 * j))
                    last.then_inc(s["wa_o_ps"], 1)

                def project(t):
                    if t:
                        pe.wait_ge(s["wa_y"], up("wa_y", it, t - 1))
                    pe.wait_ge(s["wa_o"], up("wa_o", it, 2 * t + 1))
                    for p in range(NPAIR):
                        last = nc.tensor.matmul(ps[:, 7, 0:P], wo[:, p, :], ot[:, t % 2, p, :],
                                                start=(p == 0), stop=(p == NPAIR - 1))
                    last.then_inc(s["wa_y_ps"], 1)

                scores(0)
                scores(1)
                for u in range(U + 1):
                    if u < U:
                        turn(u)
                    if u + 2 < U:
                        scores(u + 2)
                    if u:
                        values(u - 1)
                    if u % 2 == 1 and u >= 3:
                        project(u // 2 - 1)
                project(TILES - 1)
                pe.wait_ge(s["wm_h"], up("wm_h", it))
                for i in range(HALVES):
                    nc.tensor.matmul(ps[:, i, :], c.mean_w[:, :], h[:, i * BLK:(i + 1) * BLK],
                                     start=True, stop=True).then_inc(s["wm_mean"], 1)
                for i in range(HALVES):
                    pe.wait_ge(s["wm_sq"], up("wm_sq", it, i))
                    last = nc.tensor.matmul(ps[0:NB, 2, :], pick[:, i, :], sq[:, i, :],
                                            start=(i == 0), stop=(i == HALVES - 1))
                last.then_inc(s["wm_var"], 1)
                pe.wait_ge(s["wm_inv"], up("wm_inv", it))
                for i in range(HALVES):
                    nc.tensor.matmul(ps[:, i, :], rows[:, i, :], stat[:, :], start=True, stop=True).then_inc(s["wm_b"], 1)
                for i in range(HALVES):
                    pe.wait_ge(s["wm_n"], up("wm_n", it, i))
                    for k, (r0, r) in enumerate(CHUNKS):
                        n = 3 * i + k
                        if n >= 2:
                            pe.wait_ge(s["wm_hg"], up("wm_hg", it, n - 2))
                        nc.tensor.matmul(ps[0:r, 2 + n % 2, :], w1[:, r0:r0 + r], rot[:, i, :],
                                         start=True, stop=True)
                        nc.tensor.matmul(ps[0:r, 4 + n % 2, :], w1[:, HID + r0:HID + r0 + r], rot[:, i, :],
                                         start=True, stop=True).then_inc(s["wm_ag"], 1)
                    for k, (r0, r) in enumerate(CHUNKS):
                        pe.wait_ge(s["wm_hg"], up("wm_hg", it, 3 * i + k))
                        last = nc.tensor.matmul(ps[:, 6 + i, :], w2[0:r, k, :], hg[0:r, k, :],
                                                start=(k == 0), stop=(k == 2))
                    last.then_inc(s["wm_y_ps"], 1)

        @block.scalar
        def _(act):
            act.wait_ge(s["wa_w"], 16 * 15 * (run + 1))
            with act.Fori(*ITS) as it:

                for n in range(QK):
                    act.wait_ge(s["wa_qk_ps"], up("wa_qk_ps", it, n))
                    nc.scalar.activation(sq[:, n % 2, :], ps[:, n % 2, :], ACT.Square).then_inc(s["wa_sq"], 1)
                for i in range(HALVES):
                    act.wait_ge(s["wa_ss"], up("wa_ss", it, i))
                    nc.scalar.activation(length[0:16, i * BLK:(i + 1) * BLK], ps[0:16, 4 + i, :],
                                         ACT.Sqrt).then_inc(s["wa_sd"], 1)
                for t in range(TILES):
                    act.wait_ge(s["wa_v_ps"], up("wa_v_ps", it, t))
                    nc.scalar.activation(v[:, 1 + t, :], ps[:, 6 + t % 2, :], ACT.Copy).then_inc(s["wa_v"], 1)
                def exps(u):
                    act.wait_ge(s["wa_nmx"], up("wa_nmx", it, u))
                    for k in range(4):
                        ins = nc.scalar.activation(sm[:, u % 3, k, :], sm[:, u % 3, k, :], ACT.Exp, scale=8.0,
                                                   bias=nmx[:, u % 3, k:k + 1], accum_out=tot[:, u % 3, k:k + 1])
                    ins.then_inc(s["wa_exp"], 1)

                def copy_out(u):
                    act.wait_ge(s["wa_o_ps"], up("wa_o_ps", it, u))
                    t, hh = u // 2, u % 2
                    if t >= 2:
                        act.wait_ge(s["wa_y_ps"], up("wa_y_ps", it, t - 2))
                    nc.scalar.activation(ot[:, t % 2, 2 * hh:2 * hh + 2, :],
                                         ps[:, 6, 0:2 * P].rearrange("p (a q) -> p a q", a=2),
                                         ACT.Copy).then_inc(s["wa_o"], 1)

                exps(0)
                for u in range(U):
                    if u + 1 < U:
                        exps(u + 1)
                    act.wait_ge(s["wa_t_ps"], up("wa_t_ps", it, u))
                    if u >= 2:
                        act.wait_ge(s["wa_o_ps"], up("wa_o_ps", it, u - 2))
                    nc.scalar.activation(pt[:, u % 2, :, :, :].rearrange("p a b q -> p (a b q)"),
                                         ps[:, 4:6, :].rearrange("p a q -> p (a q)"),
                                         ACT.Copy).then_inc(s["wa_t"], 1)
                    if u:
                        copy_out(u - 1)
                copy_out(U - 1)
                for i in range(HALVES):
                    act.wait_ge(s["wm_xc"], up("wm_xc", it, i))
                    nc.scalar.activation(sq[:, i, :], xc[:, i, :], ACT.Square).then_inc(s["wm_sq"], 1)
                act.wait_ge(s["wm_var"], up("wm_var", it))
                nc.scalar.activation(stat[0:NB, :], ps[0:NB, 2, :], ACT.Sqrt,
                                     bias=c.eps5[0:NB, 0:1]).then_inc(s["wm_sd"], 1)
                for i in range(HALVES):
                    for k, (r0, r) in enumerate(CHUNKS):
                        n = 3 * i + k
                        act.wait_ge(s["wm_ag"], up("wm_ag", it, n))
                        if n >= 3:
                            act.wait_ge(s["wm_y_ps"], up("wm_y_ps", it, n // 3 - 1))
                        nc.scalar.activation(hg[0:r, k, :], ps[0:r, 4 + n % 2, :], ACT.Gelu,
                                             bias=b1[0:r, k, 1:2]).then_inc(s["wm_gelu"], 1)

        @block.vector
        def _(dve):
            link = Chain(c, dve, "wa_dve", QK + 1 + 2 * U + 2 + HALVES * 2)
            dve.wait_ge(s["wa_w"], 16 * 15 * (run + 1))
            nc.vector.memset(length[:, :], 0.0).then_inc(s["wa_set"], 1)
            nc.vector.memset(stat[:, :], 0.0).then_inc(s["wa_set"], 1)
            nc.vector.memset(h[64:P, 0:1], 0.0).then_inc(s["wa_set"], 1)
            nc.vector.memset(kt[:, :, 0:P], 0.0).then_inc(s["wa_set"], 1)
            nc.vector.memset(v[:, 0, :], 0.0).then_inc(s["wa_set"], 1)
            if run == 0:
                dve.sem_inc(s["wa_done"], 1)
            with dve.Fori(*ITS) as it:
                link.start(it)
                base = (it - run * B) * T
                dve.wait_ge(s["wa_done"], it + 1)
                shifted_copy(nc, c, h, base, link, s["wa_h"])
                def heads(n):
                    x, p, i = n // 8, n % 8 // 2, n % 2
                    off = (0, P)[x] + i * BLK
                    return (qt, kt)[x][:, p, off:off + BLK]

                for n in range(QK):
                    x, p, i = n // 8, n % 8 // 2, n % 2
                    half = slice(i * BLK, (i + 1) * BLK)
                    dve.wait_ge(s["wa_sq"], up("wa_sq", it, n))
                    link(nc.vector.scalar_tensor_tensor(rot[:, 0, :], ps[:, n % 2, :], qks[:, 2 * x:2 * x + 1],
                                                        tab[:, 2 * x, half], ALU.mult, ALU.mult))
                    nc.vector.scalar_tensor_tensor(rot[:, 1, :], ps[:, 2 + n % 2, :], qks[:, 2 * x + 1:2 * x + 2],
                                                   tab[:, 2 * x + 1, half], ALU.mult, ALU.mult).then_inc(s["wa_rot"], 1)
                    dve.wait_ge(s["wa_rot"], up("wa_rot", it, n))
                    nc.vector.tensor_tensor(heads(n), rot[:, 0, :], rot[:, 1, :], ALU.add).then_inc(s["wa_raw"], 1)
                    dve.wait_ge(s["wa_raw"], up("wa_raw", it, n))
                dve.wait_ge(s["wa_sd"], up("wa_sd", it, 1))
                link(nc.vector.tensor_scalar(length[0:16, :], length[0:16, :], 1e-12, None, ALU.max))
                nc.vector.reciprocal(length[0:16, :], length[0:16, :]).then_inc(s["wa_r"], 1)
                for n in range(QK):
                    dve.wait_ge(s["wa_b_ps"], up("wa_b_ps", it, n))
                    nc.vector.tensor_tensor(heads(n), heads(n), ps[:, n % 2, :], ALU.mult).then_inc(s["wa_qk"], 1)

                def mask(u):
                    dve.wait_ge(s["wa_s_ps"], up("wa_s_ps", it, u))
                    if u >= 3:
                        dve.wait_ge(s["wa_t_ps"], up("wa_t_ps", it, u - 3))
                    first = 0 if u < 2 else 1
                    nc.vector.tensor_tensor(sm[:, u % 3, :, :],
                                            ps[:, 2 * (u % 2):2 * (u % 2) + 2, :].rearrange("p a (b k) -> p (a b) k", b=2),
                                            band[:, first:first + 1, :].to_broadcast([P, 4, 2 * P]),
                                            ALU.add).then_inc(s["wa_sm"], 1)
                    dve.wait_ge(s["wa_sm"], up("wa_sm", it, u))
                    link(nc.vector.tensor_reduce(nmx[:, u % 3, :], sm[:, u % 3, :, :], AX, ALU.max, negate=True))
                    nc.vector.tensor_scalar(nmx[:, u % 3, :], nmx[:, u % 3, :], 8.0, None,
                                            ALU.mult).then_inc(s["wa_nmx"], 1)

                def out_tile(t):
                    here = tokens(base + t * P, P)
                    dve.wait_ge(s["wa_y_ps"], up("wa_y_ps", it, t))
                    nc.vector.tensor_tensor(c.xnt[:, here], c.xnt[:, here], ps[:, 7, 0:P],
                                            ALU.add).then_inc(s["wa_y"], 1)

                mask(0)
                mask(1)
                for u in range(U):
                    dve.wait_ge(s["wa_exp"], up("wa_exp", it, u))
                    link(nc.vector.reciprocal(tot[:, u % 3, :], tot[:, u % 3, :]))
                    nc.vector.tensor_tensor(sm[:, u % 3, :, :], sm[:, u % 3, :, :],
                                            tot[:, u % 3, :].unsqueeze(2).to_broadcast([P, 4, 2 * P]),
                                            ALU.mult).then_inc(s["wa_p"], 1)
                    if u + 2 < U:
                        mask(u + 2)
                    if u % 2 == 1 and u >= 5:
                        out_tile(u // 2 - 2)
                out_tile(TILES - 2)
                out_tile(TILES - 1)
                dve.wait_ge(s["wa_y"], up("wa_y", it, TILES - 1))
                shifted_copy(nc, c, h, base, link, s["wm_h"])
                for i in range(HALVES):
                    half = slice(i * BLK, (i + 1) * BLK)
                    dve.wait_ge(s["wm_mean"], up("wm_mean", it, i))
                    nc.vector.tensor_tensor(xc[:, i, :], h[:, half], ps[:, i, :], ALU.subtract).then_inc(s["wm_xc"], 1)
                dve.wait_ge(s["wm_sd"], up("wm_sd", it))
                nc.vector.reciprocal(stat[0:NB, :], stat[0:NB, :]).then_inc(s["wm_inv"], 1)
                for i in range(HALVES):
                    dve.wait_ge(s["wm_b"], up("wm_b", it, i))
                    link(nc.vector.tensor_tensor(xc[:, i, :], xc[:, i, :], ps[:, i, :], ALU.mult))
                    nc.vector.tensor_scalar(rot[:, i, :], xc[:, i, :], lnc[:, 0:1], lnc[:, 1:2],
                                            ALU.mult, ALU.add).then_inc(s["wm_n"], 1)
                for i in range(HALVES):
                    here = tokens(base + i * BLK, BLK)
                    for k, (r0, r) in enumerate(CHUNKS):
                        n = 3 * i + k
                        dve.wait_ge(s["wm_gelu"], up("wm_gelu", it, n))
                        nc.vector.scalar_tensor_tensor(hg[0:r, k, :], ps[0:r, 2 + n % 2, :], b1[0:r, k, 0:1],
                                                       hg[0:r, k, :], ALU.add, ALU.mult).then_inc(s["wm_hg"], 1)
                    dve.wait_ge(s["wm_y_ps"], up("wm_y_ps", it, i))
                    link(nc.vector.scalar_tensor_tensor(c.xnt[:, here], ps[:, 6 + i, :], lnc[:, 2:3],
                                                        c.xnt[:, here], ALU.add, ALU.add))
                    if run == 1:
                        last = nc.vector.tensor_tensor(c.xt[:, here], c.xt[:, here], c.xnt[:, here], ALU.add)
                if run == 1:
                    last.then_inc(s["wa_done"], 1)
                else:
                    dve.sem_inc(s["wa_done"], 1)
            link.close()


GQ, LAT = 4, 32
NQK = 4
FAR = -30000.0


def grouped_attention_phase(c, run):
    units = []
    for t in range(TILES):
        for k in range(0 if run == 0 else max(t - 1, 0), t + 1):
            units += [(t, k, j, None if run == 0 and k < t else t - k) for j in range(4)]
    U = len(units)
    last_of = {t: max(n for n, x in enumerate(units) if x[0] == t) for t in range(TILES)}
    steps = [("square", 0), ("mean", 0), ("root", 0), ("norm", 0)]
    if run == 0:
        steps += [("latent", 0), ("keep_latent", 0)]
    for n in range(NQK):
        steps += [("project", n), ("rotate", n), ("head_square", n)]
    steps += [("head_means", 0), ("head_root", 0), ("head_inverse", 0)]
    for n in range(NQK):
        steps += [("spread", n), ("split", n)]
    length_of = dict(square=3, mean=4, root=7, norm=17, latent=4, keep_latent=2, project=4, rotate=5, head_square=2,
                     head_means=3, head_root=6, head_inverse=8, spread=2, split=7)
    total = sum(length_of[name] for name, _ in steps)
    due, before = {}, 0
    for name, n in steps:
        unit = 2 + before * (U - 2) // total
        while unit in due:
            unit += 1
        due[unit] = (name, n)
        before += length_of[name]
    pre = f"ga{run}_"
    counts = dict(w=1, set=1, con=1, sq=1, ms=1, sd=1, h=1, lat_ps=1, lat=1, qk_ps=NQK, rot=NQK, qsq=NQK, qms=1,
                  qsd=1, inv=1, qb_ps=NQK, qk=NQK, split=NQK, out=6 * 16, parted=1, rows=18 * 16, v_ps=1, v=1, st=U, exp=U,
                  av=U, o=TILES, sum_ps=TILES, ot=TILES, y_ps=2, done=1)
    c.signals(**{pre + k: n for k, n in counts.items()})
    s = {k: c.sem[pre + k] for k in counts}
    up = lambda name, it, i=0: c.up(pre + name, it, i)
    nc, d, ps = c.nc, c.d, c.ps
    R = LAT if run == 0 else P
    NW = 11 if run == 0 else 10
    scratch = nc.dram_tensor(pre + "scratch", [2, PARTS, P, T], BF16, kind="Internal").ap()
    halves = [slice(i * BLK, (i + 1) * BLK) for i in range(HALVES)]
    with ExitStack() as ctx:
        sb = lambda n, shape: c.sb(ctx, pre + "b_" + n, shape)
        wq = sb("wq", [P, 2, P])
        wk = sb("wk", [P, 2, P])
        wv = sb("wv", [P, 32])
        wd = sb("wd", [P, LAT])
        wo = sb("wo", [P, GQ, P])
        nw = sb("nw", [P, 1])
        tab = sb("tab", [P, 2, T])
        msk = sb("msk", [P, 2, P])
        row8 = sb("row8", [P, P])
        gather = sb("gather", [P, NQK, 16 * NQK])
        spread = sb("spread", [P, NQK, P])
        eye16 = c.sb(ctx, pre + "b_eye16", [P, P], BF16)
        far = c.sb(ctx, pre + "b_far", [P, 2, GQ, P], BF16)
        h = sb("h", [P, T])
        lat = sb("lat", [P, T])
        sq = sb("sq", [P, NQK, BLK])
        sd = sb("sd", [P, 2, BLK])
        length = sb("length", [P, BLK])
        rot = sb("rot", [P, NQK, BLK])
        rot2 = sb("rot2", [P, BLK])
        part = c.sb(ctx, pre + "b_part", [P, 2, PARTS, T], BF16)
        q6 = c.sb(ctx, pre + "b_q6", [P, 16, T], BF16)
        k6 = c.sb(ctx, pre + "b_k6", [P, 4, T], BF16)
        v = sb("v", [P, TILES, 4, 32])
        pt = sb("pt", [P, 3, BLK])
        os = sb("os", [P, 2, BLK])
        rs = sb("rs", [P, 2, BLK])
        ot = sb("ot", [P, GQ, T])
        src = lat if run == 0 else h
        block = ctx.enter_context(nc.Block())

        @block.sync
        def _(sp):
            loads = [(wq[:, :, :], d[pre + "wq"]), (wk[0:R, :, :], d[pre + "wk"]), (wv[0:R, :], d[pre + "wv"]),
                     (wo[:, :, :], d[pre + "wo"]), (nw[:, :], d[pre + "nw"]), (tab[:, :, :], d["c_" + pre + "tab"]),
                     (msk[:, :, :], d["c_" + pre + "mask"]), (row8[:, :], d["c_row8"]),
                     (gather[:, :, :], d["c_gather8"]), (spread[:, :, :], d["c_spread8"])]
            if run == 0:
                loads.append((wd[:, :], d["ga0_wd"]))
            for dst, x in loads:
                sp.dma_start(dst, x).then_inc(s["w"], 16)
            sp.wait_ge(s["w"], 16 * NW)

            def parts_out(it):
                sp.wait_ge(s["split"], up("split", it, NQK - 1))
                for x in range(2):
                    r = (P, 32)[x]
                    for p in range(PARTS):
                        sp.dma_start(scratch[x, p, 0:r], part[0:r, x, p, :]).then_inc(s["out"], 16)
                sp.wait_ge(s["out"], (it + 1) * 96)
                sp.sem_inc(s["parted"], 1)

            def rows_in(it):
                for r in range(9):
                    sp.dma_start(k6[8 * r:8 * r + 8, :, :],
                                 scratch[1, r % 3, 0:32].rearrange("(h e) t -> e h t", e=8)).then_inc(s["rows"], 16)
                    sp.dma_start(q6[8 * r:8 * r + 8, :, :],
                                 scratch[0, r // 3].rearrange("(h e) t -> e h t", e=8)).then_inc(s["rows"], 16)

            parts_out(0)
            rows_in(0)
            with sp.Fori(1, B) as it:
                parts_out(it)
                sp.wait_ge(s["st"], it * U)
                rows_in(it)
            sp.wait_ge(s["rows"], B * 288)

        @block.tensor
        def _(pe):
            pe.wait_ge(s["w"], 16 * NW)
            pe.wait_ge(s["con"], 2)

            def prepare(it, step):
                name, n = step
                if name == "mean":
                    pe.wait_ge(s["sq"], up("sq", it))
                    for i in range(HALVES):
                        last = nc.tensor.matmul(ps[:, 6 + i, :], c.mean_w[:, :], sq[:, i, :], start=True, stop=True)
                    last.then_inc(s["ms"], 1)
                elif name == "latent":
                    pe.wait_ge(s["h"], up("h", it))
                    for i in range(HALVES):
                        last = nc.tensor.matmul(ps[0:LAT, 6 + i, :], wd[:, :], h[:, halves[i]], start=True, stop=True)
                    last.then_inc(s["lat_ps"], 1)
                elif name == "project":
                    if n:
                        pe.wait_ge(s["rot"], up("rot", it, n - 1))
                    elif run == 0:
                        pe.wait_ge(s["lat"], up("lat", it))
                    else:
                        pe.wait_ge(s["h"], up("h", it))
                    for x in range(2):
                        if n < 2:
                            last = nc.tensor.matmul(ps[:, 6 + x, :], wq[:, x, :], h[:, halves[n % 2]],
                                                    start=True, stop=True)
                        else:
                            last = nc.tensor.matmul(ps[:, 6 + x, :], wk[0:R, x, :], src[0:R, halves[n % 2]],
                                                    start=True, stop=True)
                    last.then_inc(s["qk_ps"], 1)
                elif name == "head_means":
                    pe.wait_ge(s["qsq"], up("qsq", it, NQK - 1))
                    for m in range(NQK):
                        last = nc.tensor.matmul(ps[0:16 * NQK, 6, :], gather[:, m, :], sq[:, m, :],
                                                start=(m == 0), stop=(m == NQK - 1))
                    last.then_inc(s["qms"], 1)
                elif name == "spread":
                    if n == 0:
                        pe.wait_ge(s["inv"], up("inv", it))
                    if n >= 2:
                        pe.wait_ge(s["qk"], up("qk", it, n - 2))
                    nc.tensor.matmul(ps[:, 6 + n % 2, :], spread[:, n, :], length[:, :],
                                     start=True, stop=True).then_inc(s["qb_ps"], 1)

            def attend(it, nxt):
                pe.wait_ge(s["done"], it + 1)
                pe.wait_ge(s["qk"], up("qk", it, NQK - 1))
                for t in range(TILES):
                    last = nc.tensor.matmul(ps[:, 6, t * 32:(t + 1) * 32], src[0:R, t * P:(t + 1) * P], wv[0:R, :],
                                            start=True, stop=True)
                last.then_inc(s["v_ps"], 1)
                pe.wait_ge(s["v"], up("v", it))
                pe.wait_ge(s["rows"], (it + 1) * 288)

                def scores(n):
                    t, k, j, m = units[n]
                    if n >= 3:
                        pe.wait_ge(s["exp"], up("exp", it, n - 3))
                    if m is not None:
                        nc.tensor.matmul(ps[:, n % 3, :], eye16[:, :], far[:, m, :, :].rearrange("p g q -> p (g q)"),
                                         start=True, stop=False)
                    nc.tensor.matmul(ps[:, n % 3, :].rearrange("p (g q) -> p g q", g=GQ),
                                     k6[0:72, j, k * P:(k + 1) * P], q6[0:72, GQ * j:GQ * (j + 1), t * P:(t + 1) * P],
                                     start=(m is None), stop=True).then_inc(s["st"], 1)

                def values(n):
                    t, k, j, m = units[n]
                    if (n == 0 or units[n - 1][0] != t) and t >= 2:
                        pe.wait_ge(s["o"], up("o", it, t - 2))
                    pe.wait_ge(s["exp"], up("exp", it, n))
                    first = k == (0 if run == 0 else max(t - 1, 0))
                    nc.tensor.matmul(ps[32 * j:32 * j + 32, 3 + t % 2, :], v[:, k, j, :], pt[:, n % 3, :],
                                     start=first, stop=(k == t), tile_position=(0, 32 * j)).then_inc(s["av"], 1)

                def sums(t):
                    pe.wait_ge(s["o"], up("o", it, t))
                    if t:
                        pe.wait_ge(s["ot"], up("ot", it, t - 1))
                    nc.tensor.matmul(ps[:, 5, :], row8[:, :], os[:, t % 2, :],
                                     start=True, stop=True).then_inc(s["sum_ps"], 1)

                for n in range(U + 2):
                    if nxt is not None and n in due:
                        prepare(nxt, due[n])
                    if n < U:
                        scores(n)
                    if n >= 2:
                        values(n - 2)
                        t = units[n - 2][0]
                        if t and n - 2 == last_of[t - 1] + 4:
                            sums(t - 1)
                sums(TILES - 1)
                if nxt is not None:
                    pe.wait_ge(s["qk"], up("qk", nxt, NQK - 1))
                pe.wait_ge(s["ot"], up("ot", it, TILES - 1))
                for i in range(HALVES):
                    for g in range(GQ):
                        last = nc.tensor.matmul(ps[:, 6 + i, :], wo[:, g, :], ot[:, g, halves[i]],
                                                start=(g == 0), stop=(g == GQ - 1))
                    last.then_inc(s["y_ps"], 1)

            for step in steps:
                prepare(0, step)
            with pe.Fori(0, B - 1) as it:
                attend(it, it + 1)
            attend(B - 1, None)

        @block.scalar
        def _(act):
            act.wait_ge(s["con"], 2)

            def prepare(it, step):
                name, n = step
                if name == "root":
                    act.wait_ge(s["ms"], up("ms", it))
                    nc.scalar.activation(sd[:, :, :], ps[:, 6:8, :], ACT.Sqrt, bias=c.eps6[:, 0:1]).then_inc(s["sd"], 1)
                elif name == "keep_latent":
                    act.wait_ge(s["lat_ps"], up("lat_ps", it))
                    nc.scalar.activation(lat[0:LAT, :].rearrange("p (i t) -> p i t", i=HALVES), ps[0:LAT, 6:8, :],
                                         ACT.Copy).then_inc(s["lat"], 1)
                elif name == "head_square":
                    act.wait_ge(s["rot"], up("rot", it, n))
                    nc.scalar.activation(sq[:, n, :], rot[:, n, :], ACT.Square).then_inc(s["qsq"], 1)
                elif name == "head_root":
                    act.wait_ge(s["qms"], up("qms", it))
                    nc.scalar.activation(length[0:16 * NQK, :], ps[0:16 * NQK, 6, :], ACT.Sqrt,
                                         bias=c.eps6[0:16 * NQK, 0:1]).then_inc(s["qsd"], 1)

            def attend(it, nxt):
                act.wait_ge(s["v_ps"], up("v_ps", it))
                nc.scalar.activation(v[:, :, :, 0:8], ps[:, 6, 0:32 * TILES].rearrange("p (t j e) -> p t j e", e=8, j=4),
                                     ACT.Copy).then_inc(s["v"], 1)

                def copy_out(t):
                    act.wait_ge(s["av"], up("av", it, last_of[t]))
                    if t >= 2:
                        act.wait_ge(s["ot"], up("ot", it, t - 2))
                    nc.scalar.activation(os[:, t % 2, :], ps[:, 3 + t % 2, :], ACT.Copy).then_inc(s["o"], 1)

                for n in range(U):
                    if nxt is not None and n in due:
                        prepare(nxt, due[n])
                    act.wait_ge(s["st"], up("st", it, n))
                    if n >= 3:
                        act.wait_ge(s["av"], up("av", it, n - 3))
                    nc.scalar.activation(pt[:, n % 3, :], ps[:, n % 3, :], ACT.Exp,
                                         scale=float(8) ** -0.5).then_inc(s["exp"], 1)
                    t = units[n][0]
                    if t and n == last_of[t - 1] + 3:
                        copy_out(t - 1)
                copy_out(TILES - 1)

            for step in steps:
                prepare(0, step)
            with act.Fori(0, B - 1) as it:
                attend(it, it + 1)
            attend(B - 1, None)

        @block.vector
        def _(dve):
            link = Chain(c, dve, pre + "dve", TILES + HALVES)
            plink = Chain(c, dve, pre + "prep", 1 + NQK * (2 + 2 * (PARTS - 1)))
            dve.wait_ge(s["w"], 16 * NW)
            nc.vector.memset(length[:, :], 0.0).then_inc(s["set"], 1)
            nc.vector.memset(v[:, :, :, :], 0.0).then_inc(s["set"], 1)
            dve.wait_ge(s["set"], 2)
            nc.vector.memset(v[:, :, :, 8:9], 1.0).then_inc(s["set"], 1)
            dve.wait_ge(s["set"], 3)
            for g in range(GQ):
                last = nc.vector.tensor_scalar(far[:, :, g, :], msk[:, :, :], -1.0, -FAR, ALU.add, ALU.mult)
            last.then_inc(s["con"], 1)
            nc.vector.tensor_scalar(eye16[:, :], c.ident[:, :], 1.0, None, ALU.mult).then_inc(s["con"], 1)
            dve.sem_inc(s["done"], 1)

            def prepare(it, step):
                name, n = step
                whole = tokens(it * T, T)
                if name == "square":
                    plink.start(it)
                    nc.vector.tensor_tensor(sq[:, 0:2, :].rearrange("p i t -> p (i t)"), c.xnt[:, whole],
                                            c.xnt[:, whole], ALU.mult).then_inc(s["sq"], 1)
                elif name == "norm":
                    dve.wait_ge(s["sd"], up("sd", it))
                    plink(nc.vector.reciprocal(sd[:, :, :], sd[:, :, :]))
                    nc.vector.scalar_tensor_tensor(h[:, :], c.xnt[:, whole], nw[:, 0:1],
                                                   sd[:, :, :].rearrange("p i t -> p (i t)"),
                                                   ALU.mult, ALU.mult).then_inc(s["h"], 1)
                elif name == "rotate":
                    half = halves[n % 2]
                    dve.wait_ge(s["qk_ps"], up("qk_ps", it, n))
                    plink(nc.vector.tensor_tensor(rot[:, n, :], tab[:, 0, half], ps[:, 6, :], ALU.mult))
                    plink(nc.vector.tensor_tensor(rot2[:, :], tab[:, 1, half], ps[:, 7, :], ALU.mult))
                    nc.vector.tensor_tensor(rot[:, n, :], rot[:, n, :], rot2[:, :], ALU.add).then_inc(s["rot"], 1)
                    dve.wait_ge(s["rot"], up("rot", it, n))
                elif name == "head_inverse":
                    dve.wait_ge(s["qsd"], up("qsd", it))
                    nc.vector.reciprocal(length[0:16 * NQK, :], length[0:16 * NQK, :]).then_inc(s["inv"], 1)
                elif name == "split":
                    x, half = n // 2, halves[n % 2]
                    dve.wait_ge(s["qb_ps"], up("qb_ps", it, n))
                    nc.vector.tensor_tensor(rot[:, n, :], rot[:, n, :], ps[:, 6 + n % 2, :],
                                            ALU.mult).then_inc(s["qk"], 1)
                    dve.wait_ge(s["qk"], up("qk", it, n))
                    split_parts(nc, plink, rot[:, n, :], rot2[:, :],
                                [part[:, x, p, half] for p in range(PARTS)]).then_inc(s["split"], 1)
                    dve.wait_ge(s["split"], up("split", it, n))

            def attend(it, nxt):
                link.start(it)

                def normalise(t):
                    dve.wait_ge(s["sum_ps"], up("sum_ps", it, t))
                    link(nc.vector.reciprocal(rs[:, t % 2, :], ps[:, 5, :]))
                    nc.vector.tensor_tensor(ot[:, :, t * P:(t + 1) * P],
                                            os[:, t % 2, :].rearrange("p (g q) -> p g q", g=GQ),
                                            rs[:, t % 2, :].rearrange("p (g q) -> p g q", g=GQ),
                                            ALU.mult).then_inc(s["ot"], 1)

                normal = {last_of[t] + 7: t for t in range(TILES - 1)}
                for n in range(U):
                    if nxt is not None and n in due:
                        prepare(nxt, due[n])
                    if n in normal:
                        normalise(normal[n])
                normalise(TILES - 1)
                for i in range(HALVES):
                    here = tokens(it * T + i * BLK, BLK)
                    dve.wait_ge(s["y_ps"], up("y_ps", it, i))
                    link(nc.vector.tensor_tensor(c.xnt[:, here], c.xnt[:, here], ps[:, 6 + i, :], ALU.add))
                    if run == 1:
                        last = nc.vector.tensor_tensor(c.xt[:, here], c.xt[:, here], c.xnt[:, here], ALU.add)
                if run == 1:
                    last.then_inc(s["done"], 1)
                else:
                    dve.sem_inc(s["done"], 1)

            for step in steps:
                prepare(0, step)
            with dve.Fori(0, B - 1) as it:
                attend(it, it + 1)
            attend(B - 1, None)
            link.close()
            plink.close()


NE, FF = 8, 256


def experts_phase(c):
    E = NE + 1
    U = 2 * E
    pre = "moe1_"
    counts = dict(w=1, h=1, lg_ps=1, lg=1, exp=1, wt_ps=1, gate=1, wt=1,
                  wb=NE, h_ps=U, act=U, hs=U, out=U, done=1)
    c.signals(**{pre + k: n for k, n in counts.items()})
    s = {k: c.sem[pre + k] for k in counts}
    up = lambda name, it, i=0: c.up(pre + name, it, i)
    nc, d, ps = c.nc, c.d, c.ps
    with ExitStack() as ctx:
        sb = lambda n, shape, dt=F32: c.sb(ctx, pre + "b_" + n, shape, dt)
        w1 = sb("w1", [P, E, FF])
        w3 = sb("w3", [P, E, FF])
        w2 = sb("w2", [P, E, 2, P])
        wr = sb("wr", [P, NE])
        gcon = sb("gcon", [P, 2 + 4 * NE])
        sel = sb("sel", [NE, NE, P])
        order = sb("order", [P, 4, NE])
        h = sb("h", [P, BLK])
        lg = sb("lg", [P, 4, NE])
        lr = sb("lr", [P, 4, NE])
        others = sb("others", [P, 4, NE])
        hot = sb("hot", [P, 4, NE])
        hot2 = sb("hot2", [P, 4, NE])
        g1 = sb("g1", [P, 4])
        wt = sb("wt", [NE, BLK])
        ga = sb("ga", [P, 2, BLK])
        hs = sb("hs", [P, 2, BLK])
        block = ctx.enter_context(nc.Block())

        @block.sync
        def _(sp):
            loads = [(w1[:, :, :], pre + "w1"), (w2[:, :, :, :], pre + "w2"), (wr[:, :], pre + "wr"),
                     (gcon[:, :], pre + "gcon"), (sel[:, :, :], "c_sel"), (w3[:, :, :], pre + "w3"),
                     (order[:, :, :], "c_order")]
            for dst, x in loads:
                sp.dma_start(dst, d[x]).then_inc(s["w"], 16)
            sp.wait_ge(s["w"], 16 * 7)

        @block.tensor
        def _(pe):
            pe.wait_ge(s["w"], 16 * 7)
            with pe.Fori(0, NB) as it:
                pe.wait_ge(s["h"], up("h", it))
                for t in range(4):
                    last = nc.tensor.matmul(ps[:, 0, t * NE:(t + 1) * NE], h[:, t * P:(t + 1) * P], wr[:, :],
                                            start=True, stop=True)
                last.then_inc(s["lg_ps"], 1)

                def first(n):
                    e, f = n // 2, slice(n % 2 * P, n % 2 * P + P)
                    if n >= 2:
                        pe.wait_ge(s["hs"], up("hs", it, n - 2))
                    nc.tensor.matmul(ps[:, 2 + n % 2, :], w1[:, e, f], h[:, :], start=True, stop=True)
                    nc.tensor.matmul(ps[:, 4 + n % 2, :], w3[:, e, f], h[:, :],
                                     start=True, stop=True).then_inc(s["h_ps"], 1)

                def spread(e):
                    if e >= 2:
                        pe.wait_ge(s["hs"], up("hs", it, 2 * e - 3))
                    nc.tensor.matmul(ps[:, e % 2, :], sel[:, e, :], wt[:, :],
                                     start=True, stop=True).then_inc(s["wb"], 1)

                def second(n):
                    pe.wait_ge(s["hs"], up("hs", it, n))
                    nc.tensor.matmul(ps[:, 6, :], w2[:, n // 2, n % 2, :], hs[:, n % 2, :],
                                     start=(n == 0), stop=(n == U - 1)).then_inc(s["out"], 1)

                first(0)
                first(1)
                pe.wait_ge(s["gate"], up("gate", it))
                for t in range(4):
                    last = nc.tensor.transpose(ps[0:NE, 7, t * P:(t + 1) * P], lr[:, t, :], c.ident[:, :])
                last.then_inc(s["wt_ps"], 1)
                pe.wait_ge(s["wt"], up("wt", it))
                spread(0)
                for n in range(U):
                    if n % 2 == 0 and n // 2 + 1 < NE:
                        spread(n // 2 + 1)
                    if n + 2 < U:
                        first(n + 2)
                    second(n)

        @block.scalar
        def _(act):
            with act.Fori(0, NB) as it:
                act.wait_ge(s["lg"], up("lg", it))
                nc.scalar.activation(lr[:, :, :], lr[:, :, :], ACT.Exp).then_inc(s["exp"], 1)
                act.wait_ge(s["wt_ps"], up("wt_ps", it))
                nc.scalar.activation(wt[:, :], ps[0:NE, 7, :], ACT.Copy).then_inc(s["wt"], 1)
                for n in range(U):
                    act.wait_ge(s["h_ps"], up("h_ps", it, n))
                    if n >= 2:
                        act.wait_ge(s["hs"], up("hs", it, n - 2))
                    nc.scalar.activation(ga[:, n % 2, :], ps[:, 4 + n % 2, :], ACT.Silu).then_inc(s["act"], 1)

        @block.vector
        def _(dve):
            link = Chain(c, dve, pre + "dve", 20 + 2 * NE)
            dve.wait_ge(s["w"], 16 * 7)
            dve.sem_inc(s["done"], 1)
            with dve.Fori(0, NB) as it:
                link.start(it)
                here = tokens(it * BLK, BLK)
                dve.wait_ge(s["done"], it + 1)
                nc.vector.tensor_scalar(h[:, :], c.xnt[:, here], 1.0, None, ALU.mult).then_inc(s["h"], 1)
                spread4 = lambda x: x.unsqueeze(2).to_broadcast([P, 4, NE])

                def best_two(x, others):
                    for k, dst in enumerate((hot, hot2)):
                        link(nc.vector.tensor_reduce(g1[:, :], x[:, :, :], AX, ALU.max))
                        link(nc.vector.tensor_tensor(dst[:, :, :], x[:, :, :], spread4(g1[:, :]), ALU.is_equal))
                        link(nc.vector.tensor_tensor(dst[:, :, :], dst[:, :, :], order[:, :, :], ALU.mult))
                        link(nc.vector.tensor_reduce(g1[:, :], dst[:, :, :], AX, ALU.max))
                        link(nc.vector.tensor_tensor(dst[:, :, :], dst[:, :, :], spread4(g1[:, :]), ALU.is_equal))
                        if k == 0:
                            link(nc.vector.scalar_tensor_tensor(others[:, :, :], hot[:, :, :], -1e30, x[:, :, :],
                                                                ALU.mult, ALU.add))
                            x = others
                    link(nc.vector.tensor_tensor(hot[:, :, :], hot[:, :, :], hot2[:, :, :], ALU.add))

                dve.wait_ge(s["lg_ps"], up("lg_ps", it))
                logits = ps[:, 0, 0:4 * NE].rearrange("p (t e) -> p t e", e=NE)
                link(nc.vector.tensor_scalar(lg[:, :, :], logits, float(P) ** -0.5, None, ALU.mult))
                link(nc.vector.tensor_tensor(lr[:, :, :], lg[:, :, :],
                                             gcon[:, 2:].rearrange("p (t e) -> p t e", e=NE), ALU.add))
                best_two(lr, others)
                link(nc.vector.tensor_scalar(lr[:, :, :], hot[:, :, :], 1e30, -1e30, ALU.mult, ALU.add))
                link(nc.vector.tensor_tensor(lg[:, :, :], lg[:, :, :], hot[:, :, :], ALU.mult))
                link(nc.vector.tensor_tensor(lr[:, :, :], lr[:, :, :], lg[:, :, :], ALU.add))
                link(nc.vector.tensor_reduce(g1[:, :], lr[:, :, :], AX, ALU.max, negate=True))
                nc.vector.tensor_tensor(lr[:, :, :], lr[:, :, :], spread4(g1[:, :]), ALU.add).then_inc(s["lg"], 1)
                dve.wait_ge(s["exp"], up("exp", it))
                link(nc.vector.tensor_reduce(g1[:, :], lr[:, :, :], AX, ALU.add))
                link(nc.vector.reciprocal(g1[:, :], g1[:, :]))
                nc.vector.tensor_tensor(lr[:, :, :], lr[:, :, :], spread4(g1[:, :]), ALU.mult).then_inc(s["gate"], 1)

                for n in range(U):
                    e = n // 2
                    dve.wait_ge(s["act"], up("act", it, n))
                    if n >= 2:
                        dve.wait_ge(s["out"], up("out", it, n - 2))
                    if e < NE:
                        dve.wait_ge(s["wb"], up("wb", it, e))
                    if e < NE:
                        link(nc.vector.tensor_tensor(ga[:, n % 2, :], ga[:, n % 2, :], ps[:, 2 + n % 2, :], ALU.mult))
                    other = ps[:, e % 2, :] if e < NE else ps[:, 2 + n % 2, :]
                    nc.vector.tensor_tensor(hs[:, n % 2, :], ga[:, n % 2, :], other, ALU.mult).then_inc(s["hs"], 1)
                dve.wait_ge(s["out"], up("out", it, U - 1))
                nc.vector.tensor_tensor(c.xt[:, here], c.xt[:, here], ps[:, 6, :], ALU.add).then_inc(s["done"], 1)
            link.close()


THRESH = 0.01


def threshold_attention_phase(c):
    s = c.signals(th_w=1, th_set=1, th_x=1, th_x_ps=1, th_v=1, th_s_ps=TILES, th_exp=TILES, th_p=TILES, th_t_ps=TILES,
                  th_t=TILES, th_y_ps=TILES, th_done=1)
    nc, d, up, ps = c.nc, c.d, c.up, c.ps
    with ExitStack() as ctx:
        w = c.sb(ctx, "th_wt", [P, P])
        ones = c.sb(ctx, "th_ones", [P, P])
        xb = c.sb(ctx, "th_xb", [P, T])
        v = c.sb(ctx, "th_vt", [P, TILES, P])
        e = c.sb(ctx, "th_e", [P, 2, T])
        keep = c.sb(ctx, "th_keep", [P, 2, T])
        low = c.sb(ctx, "th_low", [P, T])
        z = c.sb(ctx, "th_z", [P, 2, 4])
        vac = c.sb(ctx, "th_vac", [P, 2, P])
        pt = c.sb(ctx, "th_pt", [P, TILES + 1, P])
        block = ctx.enter_context(nc.Block())

        @block.sync
        def _(sp):
            sp.dma_start(w[:, :], d["th_w"]).then_inc(s["th_w"], 16)
            sp.wait_ge(s["th_w"], 16)

        @block.tensor
        def _(pe):
            pe.wait_ge(s["th_w"], 16)
            with pe.Fori(0, B) as it:
                pe.wait_ge(s["th_x"], up("th_x", it))
                for t in range(TILES):
                    last = nc.tensor.transpose(ps[:, 6 + t // 4, (t % 4) * P:(t % 4 + 1) * P],
                                               xb[:, t * P:(t + 1) * P], c.ident[:, :])
                last.then_inc(s["th_x_ps"], 1)
                pe.wait_ge(s["th_v"], up("th_v", it))

                def scores(t):
                    if t >= 2:
                        pe.wait_ge(s["th_exp"], up("th_exp", it, t - 2))
                    for i in range(HALVES):
                        last = nc.tensor.matmul(ps[:, 2 * (t % 2) + i, :], xb[:, t * P:(t + 1) * P],
                                                xb[:, i * BLK:(i + 1) * BLK], start=True, stop=True)
                    last.then_inc(s["th_s_ps"], 1)

                def turn(t):
                    if t:
                        pe.wait_ge(s["th_t"], up("th_t", it, t - 1))
                    pe.wait_ge(s["th_p"], up("th_p", it, t))
                    for k in range(TILES):
                        nc.tensor.transpose(ps[:, 4 + k // 4, (k % 4) * P:(k % 4 + 1) * P],
                                            keep[:, t % 2, k * P:(k + 1) * P], c.ident[:, :])
                    nc.tensor.transpose(ps[:, 6, 0:P], vac[:, t % 2, :], c.ident[:, :]).then_inc(s["th_t_ps"], 1)

                def values(t):
                    pe.wait_ge(s["th_t"], up("th_t", it, t))
                    if t:
                        pe.wait_ge(s["th_done"], it * TILES + t + 1)
                    for k in range(TILES):
                        nc.tensor.matmul(ps[:, 7, 0:P], v[:, k, :], pt[:, k, :], start=(k == 0), stop=False)
                    nc.tensor.matmul(ps[:, 7, 0:P], w[:, :], pt[:, TILES, :],
                                     start=False, stop=True).then_inc(s["th_y_ps"], 1)

                scores(0)
                scores(1)
                for t in range(TILES):
                    turn(t)
                    if t + 2 < TILES:
                        scores(t + 2)
                    values(t)

        @block.scalar
        def _(act):
            with act.Fori(0, B) as it:
                act.wait_ge(s["th_x_ps"], up("th_x_ps", it))
                nc.scalar.activation(v[:, :, :].rearrange("p a q -> p (a q)"),
                                     ps[:, 6:8, :].rearrange("p a q -> p (a q)"), ACT.Copy).then_inc(s["th_v"], 1)

                def exps(t):
                    act.wait_ge(s["th_s_ps"], up("th_s_ps", it, t))
                    if t >= 2:
                        act.wait_ge(s["th_p"], up("th_p", it, t - 2))
                    nc.scalar.activation(e[:, t % 2, :], ps[:, 2 * (t % 2):2 * (t % 2) + 2, :].rearrange("p a q -> p (a q)"),
                                         ACT.Exp, scale=float(P) ** -0.5,
                                         accum_out=z[:, t % 2, 0:1]).then_inc(s["th_exp"], 1)

                exps(0)
                for t in range(TILES):
                    if t + 1 < TILES:
                        exps(t + 1)
                    act.wait_ge(s["th_t_ps"], up("th_t_ps", it, t))
                    if t:
                        act.wait_ge(s["th_y_ps"], up("th_y_ps", it, t - 1))
                    nc.scalar.activation(pt[:, 0:TILES, :].rearrange("p a q -> p (a q)"),
                                         ps[:, 4:6, :].rearrange("p a q -> p (a q)"), ACT.Copy)
                    nc.scalar.activation(pt[:, TILES, :], ps[:, 6, 0:P], ACT.Copy).then_inc(s["th_t"], 1)

        @block.vector
        def _(dve):
            link = Chain(c, dve, "th_dve", 7 * TILES)
            nc.vector.memset(ones[:, :], 1.0).then_inc(s["th_set"], 1)
            dve.wait_ge(s["th_set"], 1)
            dve.sem_inc(s["th_done"], 1)
            with dve.Fori(0, B) as it:
                link.start(it)
                dve.wait_ge(s["th_done"], it * TILES + 1)
                nc.vector.tensor_scalar(xb[:, :], c.xnt[:, tokens(it * T, T)], 1.0, None,
                                        ALU.mult).then_inc(s["th_x"], 1)

                def probabilities(t):
                    m = t % 2
                    dve.wait_ge(s["th_exp"], up("th_exp", it, t))
                    if t >= 2:
                        dve.wait_ge(s["th_t_ps"], up("th_t_ps", it, t - 2))
                    link(nc.vector.reciprocal(z[:, m, 1:2], z[:, m, 0:1]))
                    link(nc.vector.tensor_scalar(e[:, m, :], e[:, m, :], z[:, m, 1:2], None, ALU.mult))
                    link(nc.vector.scalar_tensor_tensor(keep[:, m, :], e[:, m, :], THRESH, e[:, m, :],
                                                        ALU.is_ge, ALU.mult, accum_out=z[:, m, 2:3]))
                    link(nc.vector.scalar_tensor_tensor(low[:, :], e[:, m, :], THRESH, e[:, m, :],
                                                        ALU.is_lt, ALU.mult, accum_out=z[:, m, 3:4]))
                    link(nc.vector.tensor_scalar(z[:, m, 2:3], z[:, m, 2:3], 1e-9, None, ALU.add))
                    link(nc.vector.reciprocal(z[:, m, 2:3], z[:, m, 2:3]))
                    link(nc.vector.tensor_scalar(keep[:, m, :], keep[:, m, :], z[:, m, 2:3], None, ALU.mult))
                    nc.vector.tensor_scalar(vac[:, m, :], ones[:, :], z[:, m, 3:4], 0.01,
                                            ALU.mult, ALU.mult).then_inc(s["th_p"], 1)

                def add_out(t):
                    here = tokens(it * T + t * P, P)
                    dve.wait_ge(s["th_y_ps"], up("th_y_ps", it, t))
                    nc.vector.tensor_tensor(c.xt[:, here], c.xt[:, here], ps[:, 7, 0:P], ALU.add).then_inc(s["th_done"], 1)

                probabilities(0)
                for t in range(TILES):
                    if t + 1 < TILES:
                        probabilities(t + 1)
                    add_out(t)
            link.close()


def quantise(c, link, x, q, sc, tmp, n):
    nc = c.nc
    g = 4 * n
    grp = lambda t: t.rearrange("p n (b e) -> p (n b) e", e=32)
    by = lambda t: t.unsqueeze(2).to_broadcast([P, g, 32])
    a, b, y = tmp[:, 0, 0:n, :], tmp[:, 1, 0:n, :], tmp[:, 2, 0:n, :]
    big = 1.5 * 2.0 ** 23
    link(nc.vector.tensor_reduce(sc[:, 0, 0:g], grp(x), AX, ALU.max, apply_absolute_value=True))
    link(nc.vector.tensor_scalar(sc[:, 0, 0:g], sc[:, 0, 0:g], 1 / 7.5, 1e-30, ALU.mult, ALU.max))
    link(nc.vector.reciprocal(sc[:, 1, 0:g], sc[:, 0, 0:g]))
    link(nc.vector.tensor_tensor(grp(y), grp(x), by(sc[:, 1, 0:g]), ALU.mult))
    link(nc.vector.scalar_tensor_tensor(a, y, -1.0, y, ALU.mult, ALU.max))
    link(nc.vector.tensor_scalar(b, a, 4.0, 2.0, ALU.is_lt, ALU.mult))
    link(nc.vector.tensor_scalar(a, a, 2.0, 4.0, ALU.is_lt, ALU.mult))
    link(nc.vector.scalar_tensor_tensor(q, b, 2.0, a, ALU.add, ALU.add))
    link(nc.vector.scalar_tensor_tensor(b, b, 4.0, a, ALU.mult, ALU.add))
    link(nc.vector.tensor_scalar(b, b, -1 / 32, 0.5, ALU.mult, ALU.add))
    link(nc.vector.tensor_tensor(y, y, q, ALU.mult))
    link(nc.vector.tensor_scalar(a, y, big, -big, ALU.add, ALU.add))
    link(nc.vector.tensor_tensor(y, a, y, ALU.subtract))
    link(nc.vector.scalar_tensor_tensor(a, y, 0.5, a, ALU.is_ge, ALU.subtract))
    link(nc.vector.scalar_tensor_tensor(a, a, -1.0, b, ALU.mult, ALU.mult))
    return nc.vector.tensor_tensor(grp(q), grp(a), by(sc[:, 0, 0:g]), ALU.mult)


QL = 4


def quantised_linear_phase(c):
    s = c.signals(ql_w=1, ql_wq=1, ql_w_ps=1, ql_x=QL, ql_t_ps=QL, ql_t=QL, ql_q=QL, ql_q_ps=QL, ql_qt=QL, ql_y_ps=QL,
                  ql_done=1)
    nc, d, up, ps = c.nc, c.d, c.up, c.ps
    with ExitStack() as ctx:
        w = c.sb(ctx, "ql_wb", [P, 1, P])
        wt = c.sb(ctx, "ql_wt", [P, P])
        bias = c.sb(ctx, "ql_bias", [P, 1])
        xb = c.sb(ctx, "ql_xb", [P, QL, BLK])
        x = c.sb(ctx, "ql_xr", [P, QL, 4, P])
        q = c.sb(ctx, "ql_qb", [P, QL, 4, P])
        qt = c.sb(ctx, "ql_qtb", [P, 2, BLK])
        tmp = c.sb(ctx, "ql_tmp", [P, 3, 4, P])
        sc = c.sb(ctx, "ql_sc", [P, 2, 16])
        block = ctx.enter_context(nc.Block())

        @block.sync
        def _(sp):
            sp.dma_start(w[:, 0, :], d["ql_w"]).then_inc(s["ql_w"], 16)
            sp.dma_start(bias[:, :], d["ql_b"]).then_inc(s["ql_w"], 16)
            sp.wait_ge(s["ql_w"], 32)

        @block.tensor
        def _(pe):
            pe.wait_ge(s["ql_wq"], 1)
            nc.tensor.transpose(ps[:, 4, 0:P], q[:, 0, 0, :], c.ident[:, :]).then_inc(s["ql_w_ps"], 1)
            with pe.Fori(0, NB // QL) as it:
                for n in range(QL):
                    pe.wait_ge(s["ql_x"], up("ql_x", it, n))
                    for t in range(4):
                        last = nc.tensor.transpose(ps[:, n, t * P:(t + 1) * P], xb[:, n, t * P:(t + 1) * P],
                                                   c.ident[:, :])
                    last.then_inc(s["ql_t_ps"], 1)
                for n in range(QL):
                    pe.wait_ge(s["ql_q"], up("ql_q", it, n))
                    for t in range(4):
                        last = nc.tensor.transpose(ps[:, 4 + n % 2, t * P:(t + 1) * P], q[:, n, t, :], c.ident[:, :])
                    last.then_inc(s["ql_q_ps"], 1)
                    pe.wait_ge(s["ql_qt"], up("ql_qt", it, n))
                    nc.tensor.matmul(ps[:, n, :], wt[:, :], qt[:, n % 2, :],
                                     start=True, stop=True).then_inc(s["ql_y_ps"], 1)

        @block.scalar
        def _(act):
            with act.Fori(0, NB // QL) as it:
                for n in range(QL):
                    act.wait_ge(s["ql_t_ps"], up("ql_t_ps", it, n))
                    nc.scalar.activation(x[:, n, :, :].rearrange("p a q -> p (a q)"), ps[:, n, :],
                                         ACT.Copy).then_inc(s["ql_t"], 1)
                for n in range(QL):
                    act.wait_ge(s["ql_q_ps"], up("ql_q_ps", it, n))
                    if n >= 2:
                        act.wait_ge(s["ql_y_ps"], up("ql_y_ps", it, n - 2))
                    nc.scalar.activation(qt[:, n % 2, :], ps[:, 4 + n % 2, :], ACT.Copy).then_inc(s["ql_qt"], 1)

        @block.vector
        def _(dve):
            once = Chain(c, dve, "ql_once", 15)
            link = Chain(c, dve, "ql_dve", 15 * QL)
            dve.wait_ge(s["ql_w"], 32)
            once.start(0)
            quantise(c, once, w[:, :, :], q[:, 0, 0:1, :], sc, tmp, 1).then_inc(s["ql_wq"], 1)
            once.close()
            dve.wait_ge(s["ql_w_ps"], 1)
            nc.vector.tensor_copy(wt[:, :], ps[:, 4, 0:P]).then_inc(s["ql_done"], 1)
            with dve.Fori(0, NB // QL) as it:
                link.start(it)
                dve.wait_ge(s["ql_done"], it + 1)
                for n in range(QL):
                    nc.vector.tensor_scalar(xb[:, n, :], c.xnt[:, tokens((it * QL + n) * BLK, BLK)], 1.0, None,
                                            ALU.mult).then_inc(s["ql_x"], 1)

                def add_out(n):
                    here = tokens((it * QL + n) * BLK, BLK)
                    dve.wait_ge(s["ql_y_ps"], up("ql_y_ps", it, n))
                    return nc.vector.scalar_tensor_tensor(c.xt[:, here], ps[:, n, :], bias[:, 0:1], c.xt[:, here],
                                                          ALU.add, ALU.add)

                for n in range(QL):
                    dve.wait_ge(s["ql_t"], up("ql_t", it, n))
                    quantise(c, link, x[:, n, :, :], q[:, n, :, :], sc, tmp, 4).then_inc(s["ql_q"], 1)
                    dve.wait_ge(s["ql_q"], up("ql_q", it, n))
                    if n:
                        add_out(n - 1)
                add_out(QL - 1).then_inc(s["ql_done"], 1)
            link.close()


S = 32
NS = T // S


class LinearState:

    def __init__(self, c, ctx):
        self.u = c.sb(ctx, "li_u", [P, B, T])
        self.q = c.sb(ctx, "li_q", [P, B, T])
        self.z = c.sb(ctx, "li_z", [P, B, T])
        self.v = c.sb(ctx, "li_v", [P, B, TILES, P])
        self.wo = c.sb(ctx, "li_wo", [P, P])
        self.cols = c.sb(ctx, "li_cols", [P, 3])


def linear_project_phase(c, st):
    s = c.signals(lp_w=1, lp_x=1, lp_qk_ps=2, lp_k=2, lp_sq=2, lp_ms=2, lp_sd=2, lp_u=2, lp_s_ps=1, lp_s=1,
                  lp_v_ps=TILES, lp_v=TILES, lp_done=1)
    nc, d, up, ps = c.nc, c.d, c.up, c.ps
    with ExitStack() as ctx:
        w = c.sb(ctx, "lp_wb", [P, 3, P])
        bv = c.sb(ctx, "lp_bv", [P, P])
        ones = c.sb(ctx, "lp_ones", [P, 1])
        xb = c.sb(ctx, "lp_xb", [P, T])
        k = c.sb(ctx, "lp_kb", [P, T])
        kq = c.sb(ctx, "lp_kq", [P, T])
        sq = c.sb(ctx, "lp_sqb", [P, 2, BLK])
        sd = c.sb(ctx, "lp_sdb", [P, 2, BLK])
        sk = c.sb(ctx, "lp_sk", [P, TILES])
        vb = c.sb(ctx, "lp_vb", [P, P])
        block = ctx.enter_context(nc.Block())

        @block.sync
        def _(sp):
            for dst, x in [(w[:, :, :], "lp_w"), (bv[:, :], "lp_bv"), (st.wo[:, :], "li_wo"), (st.cols[:, :], "li_cols"),
                           (ones[:, :], "c_ones")]:
                sp.dma_start(dst, d[x]).then_inc(s["lp_w"], 16)
            sp.wait_ge(s["lp_w"], 80)

        @block.tensor
        def _(pe):
            pe.wait_ge(s["lp_w"], 80)
            with pe.Fori(0, B) as it:
                pe.wait_ge(s["lp_x"], up("lp_x", it))
                for i in range(HALVES):
                    for x in range(2):
                        last = nc.tensor.matmul(ps[:, 2 * x + i, :], w[:, x, :], xb[:, i * BLK:(i + 1) * BLK],
                                                start=True, stop=True)
                    last.then_inc(s["lp_qk_ps"], 1)
                for i in range(HALVES):
                    pe.wait_ge(s["lp_sq"], up("lp_sq", it, i))
                    nc.tensor.matmul(ps[:, 4 + i, :], c.mean_w[:, :], sq[:, i, :],
                                     start=True, stop=True).then_inc(s["lp_ms"], 1)
                pe.wait_ge(s["lp_u"], up("lp_u", it, 1))
                for t in range(TILES):
                    last = nc.tensor.matmul(ps[:, 0, t:t + 1], kq[:, t * P:(t + 1) * P], ones[:, :],
                                            start=True, stop=True)
                last.then_inc(s["lp_s_ps"], 1)
                for t in range(TILES):
                    if t >= 2:
                        pe.wait_ge(s["lp_v"], up("lp_v", it, t - 2))
                    nc.tensor.matmul(ps[:, 6 + t % 2, 0:P], xb[:, t * P:(t + 1) * P], w[:, 2, :],
                                     start=True, stop=True).then_inc(s["lp_v_ps"], 1)

        @block.scalar
        def _(act):
            with act.Fori(0, B) as it:
                for i in range(HALVES):
                    act.wait_ge(s["lp_k"], up("lp_k", it, i))
                    nc.scalar.activation(sq[:, i, :], k[:, i * BLK:(i + 1) * BLK], ACT.Square).then_inc(s["lp_sq"], 1)
                for i in range(HALVES):
                    act.wait_ge(s["lp_ms"], up("lp_ms", it, i))
                    nc.scalar.activation(sd[:, i, :], ps[:, 4 + i, :], ACT.Sqrt, scale=float(P)).then_inc(s["lp_sd"], 1)

        @block.vector
        def _(dve):
            link = Chain(c, dve, "lp_dve", 1 + HALVES + 3 * HALVES + TILES)
            dve.wait_ge(s["lp_w"], 80)
            dve.sem_inc(s["lp_done"], 1)
            with dve.Fori(0, B) as it:
                link.start(it)
                dve.wait_ge(s["lp_done"], it + 1)
                nc.vector.tensor_scalar(xb[:, :], c.xnt[:, tokens(it * T, T)], 1.0, None, ALU.mult).then_inc(s["lp_x"], 1)
                uu = st.u[:, :, :].rearrange("p b t -> p (b t)")
                qq = st.q[:, :, :].rearrange("p b t -> p (b t)")
                vv = st.v[:, :, :, :].rearrange("p b t e -> p (b t e)")
                for i in range(HALVES):
                    half = slice(i * BLK, (i + 1) * BLK)
                    here = tokens(it * T + i * BLK, BLK)
                    dve.wait_ge(s["lp_qk_ps"], up("lp_qk_ps", it, i))
                    link(nc.vector.tensor_scalar(qq[:, here], ps[:, i, :], st.cols[:, 0:1], None, ALU.add))
                    nc.vector.tensor_scalar(k[:, half], ps[:, 2 + i, :], st.cols[:, 1:2], None,
                                            ALU.add).then_inc(s["lp_k"], 1)
                for i in range(HALVES):
                    half = slice(i * BLK, (i + 1) * BLK)
                    here = tokens(it * T + i * BLK, BLK)
                    dve.wait_ge(s["lp_sd"], up("lp_sd", it, i))
                    link(nc.vector.tensor_tensor(kq[:, half], k[:, half], qq[:, here], ALU.mult))
                    link(nc.vector.tensor_scalar(sd[:, i, :], sd[:, i, :], 1e-6, None, ALU.add))
                    link(nc.vector.reciprocal(sd[:, i, :], sd[:, i, :]))
                    nc.vector.tensor_tensor(uu[:, here], k[:, half], sd[:, i, :], ALU.mult).then_inc(s["lp_u"], 1)
                dve.wait_ge(s["lp_s_ps"], up("lp_s_ps", it))
                link(nc.vector.tensor_scalar(sk[:, :], ps[:, 0, 0:TILES], 1.0, None, ALU.mult))
                for t in range(TILES):
                    dve.wait_ge(s["lp_v_ps"], up("lp_v_ps", it, t))
                    link(nc.vector.tensor_tensor(vb[:, :], bv[:, :], ps[:, 6 + t % 2, 0:P], ALU.add))
                    last = nc.vector.tensor_scalar(vv[:, tokens(it * T + t * P, P)], vb[:, :], sk[:, t:t + 1], None,
                                                   ALU.mult).then_inc(s["lp_v"], 1)
                    dve.wait_ge(s["lp_v"], up("lp_v", it, t))
                dve.sem_inc(s["lp_done"], 1)
            link.close()


SUBS = NS // NB
ROUTER = 18


def expert_steps():
    steps = [("D", "load", 0), ("P", "mean", 0), ("D", "centre", 0), ("A", "square", 0), ("P", "var", 0),
             ("A", "root", 0), ("D", "inverse", 0), ("D", "scale", 0), ("D", "affine", 0), ("P", "logits", 0),
             ("D", "router", 0), ("D", "router", 1), ("A", "exp", 0)]
    steps += [("D", "router", r) for r in range(2, ROUTER)]
    steps += [("P", "first", 0), ("A", "gelu", 0), ("P", "first", 1), ("A", "gelu", 1), ("P", "turn", 0),
              ("A", "weights", 0), ("P", "spread", 0), ("P", "spread", 1)]
    for n in range(2 * NE):
        steps += [("D", "weigh", n), ("P", "second", n)]
        if n + 2 < 2 * NE:
            steps += [("P", "first", n + 2), ("A", "gelu", n + 2)]
        if n % 2 and n // 2 + 2 < NE:
            steps.append(("P", "spread", n // 2 + 2))
    return steps + [("D", "add", 0)]


def linear_scan_phase(c, st):
    per = dict(ls_w=1, ls_u=SUBS, ls_v_ps=SUBS, ls_v=SUBS, ls_vt=SUBS, ls_s_ps=SUBS, ls_m=SUBS, ls_dm=SUBS, ls_w_ps=SUBS,
               ls_wb=SUBS, ls_zb=SUBS, ls_z_ps=SUBS, ls_a_ps=SUBS, ls_a=SUBS, ls_step=1)
    per.update(me_h=1, me_mean=1, me_xc=1, me_sq=1, me_var=1, me_sd=1, me_norm=3, me_lg_ps=1, me_router=ROUTER,
               me_exp=1, me_wt_ps=1, me_wt=1, me_wb=NE, me_h_ps=2 * NE, me_act=2 * NE, me_hs=2 * NE, me_out=2 * NE,
               me_done=1)
    s = c.signals(**per)
    nc, d, up, ps = c.nc, c.d, c.up, c.ps
    steps = expert_steps()
    pivots, mine = SUBS * (S - 1), sum(e == "D" for e, _, _ in steps)
    place, seen = {}, 0
    for e, name, n in steps:
        place.setdefault((max(seen - 1, 0) if e != "D" else seen) * (pivots - 2) // mine, []).append((e, name, n))
        seen += e == "D"

    def steps_of(engine, sub):
        return [(name, n) for t in range(S - 1) for e, name, n in place.get(sub * (S - 1) + t, []) if e == engine]

    with ExitStack() as ctx:
        eye = c.sb(ctx, "ls_eye", [P, S])
        below = c.sb(ctx, "ls_below", [P, S])
        diag = c.sb(ctx, "ls_diag", [P, B, S])
        a = c.sb(ctx, "ls_ab", [P, B, P])
        ub = c.sb(ctx, "ls_ub", [P, B, S])
        v = c.sb(ctx, "ls_vb", [P, P])
        vt = c.sb(ctx, "ls_vtb", [P, B, S])
        f = c.sb(ctx, "ls_f", [P, 2 * S])
        row = c.sb(ctx, "ls_row", [P, 2 * S])
        step = c.sb(ctx, "ls_stepb", [P, 2 * S])
        r = c.sb(ctx, "ls_r", [P, 1])
        dinv = c.sb(ctx, "ls_dinv", [P, 1])
        dd = c.sb(ctx, "ls_dd", [P, B])
        m = c.sb(ctx, "ls_mb", [P, S])
        mt = c.sb(ctx, "ls_mtb", [P, 2, S])
        mz = c.sb(ctx, "ls_mz", [P, 2, B, S])
        w = c.sb(ctx, "ls_wbf", [P, P])
        z = c.sb(ctx, "ls_zbf", [P, B, P])
        w1 = c.sb(ctx, "me_w1", [P, NE, FF])
        w2 = c.sb(ctx, "me_w2", [P, NE, 2, P])
        wr = c.sb(ctx, "me_wr", [P, NE])
        gcon = c.sb(ctx, "me_gcon", [P, 2 + 4 * NE])
        sel = c.sb(ctx, "me_sel", [NE, NE, P])
        order = c.sb(ctx, "me_order", [P, 4, NE])
        h = c.sb(ctx, "me_hb", [P, BLK])
        rn = c.sb(ctx, "me_rn", [P, BLK])
        tmp = c.sb(ctx, "me_tmp", [P, 3, BLK])
        lg = c.sb(ctx, "me_lg", [P, 4, NE])
        lr = c.sb(ctx, "me_lr", [P, 4, NE])
        others = c.sb(ctx, "me_others", [P, 4, NE])
        hot = c.sb(ctx, "me_hot", [P, 2, 4, NE])
        g1 = c.sb(ctx, "me_g1", [P, 4])
        wt = c.sb(ctx, "me_wtb", [NE, BLK])
        ga = c.sb(ctx, "me_ga", [P, 2, BLK])
        hs = c.sb(ctx, "me_hsb", [P, 2, BLK])
        block = ctx.enter_context(nc.Block())
        LOADS = 9 + B

        @block.sync
        def _(sp):
            loads = [(eye[:, :], "c_eye32"), (below[:, :], "c_below"), (diag[:, :, :], "c_diag"),
                     (w1[:, :, :], "moe3_w1"), (w2[:, :, :, :], "moe3_w2"), (wr[:, :], "moe3_wr"),
                     (gcon[:, :], "moe3_gcon"), (sel[:, :, :], "c_sel"), (order[:, :, :], "c_order")]
            for dst, x in loads:
                sp.dma_start(dst, d[x]).then_inc(s["ls_w"], 16)
            for b in range(B):
                sp.dma_start(a[:, b, :], c.ident[:, :]).then_inc(s["ls_w"], 16)
            sp.wait_ge(s["ls_w"], 16 * LOADS)

        @block.tensor
        def _(pe):
            pe.wait_ge(s["ls_w"], 16 * LOADS)

            def expert(it, name, n):
                if name == "mean":
                    pe.wait_ge(s["me_h"], up("me_h", it))
                    nc.tensor.matmul(ps[:, 5, :], c.mean_w[:, :], h[:, :], start=True, stop=True).then_inc(s["me_mean"], 1)
                elif name == "var":
                    pe.wait_ge(s["me_sq"], up("me_sq", it))
                    nc.tensor.matmul(ps[:, 6, :], c.mean_w[:, :], tmp[:, 1, :],
                                     start=True, stop=True).then_inc(s["me_var"], 1)
                elif name == "logits":
                    pe.wait_ge(s["me_norm"], up("me_norm", it, 2))
                    for t in range(4):
                        last = nc.tensor.matmul(ps[:, 5, t * NE:(t + 1) * NE], rn[:, t * P:(t + 1) * P], wr[:, :],
                                                start=True, stop=True)
                    last.then_inc(s["me_lg_ps"], 1)
                elif name == "first":
                    if n >= 2:
                        pe.wait_ge(s["me_hs"], up("me_hs", it, n - 2))
                    nc.tensor.matmul(ps[:, 3 + n % 2, :], w1[:, n // 2, n % 2 * P:n % 2 * P + P], h[:, :],
                                     start=True, stop=True).then_inc(s["me_h_ps"], 1)
                elif name == "turn":
                    pe.wait_ge(s["me_router"], up("me_router", it, ROUTER - 1))
                    for t in range(4):
                        last = nc.tensor.transpose(ps[0:NE, 6, t * P:(t + 1) * P], lr[:, t, :], c.ident[:, :])
                    last.then_inc(s["me_wt_ps"], 1)
                elif name == "spread":
                    if n == 0:
                        pe.wait_ge(s["me_wt"], up("me_wt", it))
                    if n >= 2:
                        pe.wait_ge(s["me_hs"], up("me_hs", it, 2 * n - 3))
                    nc.tensor.matmul(ps[:, 5 + n % 2, :], sel[:, n, :], wt[:, :],
                                     start=True, stop=True).then_inc(s["me_wb"], 1)
                elif name == "second":
                    pe.wait_ge(s["me_hs"], up("me_hs", it, n))
                    nc.tensor.matmul(ps[:, 7, :], w2[:, n // 2, n % 2, :], hs[:, n % 2, :],
                                     start=(n == 0), stop=(n == 2 * NE - 1)).then_inc(s["me_out"], 1)

            with pe.Fori(0, NB) as it:
                for sub in range(SUBS):
                    pe.wait_ge(s["ls_u"], up("ls_u", it, sub))
                    for b in range(B):
                        last = nc.tensor.matmul(ps[:, 1, b * S:(b + 1) * S], a[:, b, :], ub[:, b, :],
                                                start=True, stop=True)
                    for b in range(B):
                        last = nc.tensor.matmul(ps[b * S:(b + 1) * S, 0, 0:P], ub[:, b, :], a[:, b, :],
                                                start=True, stop=True, tile_position=(0, b * S))
                    last.then_inc(s["ls_v_ps"], 1)
                    pe.wait_ge(s["ls_vt"], up("ls_vt", it, sub))
                    for b in range(B):
                        last = nc.tensor.matmul(ps[b * S:(b + 1) * S, 2, 0:S], vt[:, b, :], ub[:, b, :],
                                                start=True, stop=True, tile_position=(0, b * S))
                    last.then_inc(s["ls_s_ps"], 1)
                    for name, n in steps_of("P", sub):
                        expert(it, name, n)
                    pe.wait_ge(s["ls_v"], up("ls_v", it, sub))
                    pe.wait_ge(s["ls_m"], up("ls_m", it, sub))
                    nc.tensor.matmul(ps[:, 0, 0:P], mz[:, 0, :, :].rearrange("p b i -> p (b i)"), v[:, :],
                                     start=True, stop=True).then_inc(s["ls_w_ps"], 1)
                    pe.wait_ge(s["ls_zb"], up("ls_zb", it, sub))
                    nc.tensor.matmul(ps[:, 2, :], w[:, :], z[:, :, :].rearrange("p b e -> p (b e)"),
                                     start=True, stop=True).then_inc(s["ls_a_ps"], 1)
                    pe.wait_ge(s["ls_dm"], up("ls_dm", it, sub))
                    nc.tensor.matmul(ps[:, 1, 0:P], v[:, :], mz[:, 1, :, :].rearrange("p b i -> p (b i)"),
                                     start=True, stop=True).then_inc(s["ls_z_ps"], 1)

        @block.scalar
        def _(act):
            def expert(it, name, n):
                if name == "square":
                    act.wait_ge(s["me_xc"], up("me_xc", it))
                    nc.scalar.activation(tmp[:, 1, :], tmp[:, 0, :], ACT.Square).then_inc(s["me_sq"], 1)
                elif name == "root":
                    act.wait_ge(s["me_var"], up("me_var", it))
                    nc.scalar.activation(tmp[:, 2, :], ps[:, 6, :], ACT.Sqrt,
                                         bias=c.eps5[:, 0:1]).then_inc(s["me_sd"], 1)
                elif name == "exp":
                    act.wait_ge(s["me_router"], up("me_router", it, 1))
                    nc.scalar.activation(lr[:, :, :], lr[:, :, :], ACT.Exp).then_inc(s["me_exp"], 1)
                elif name == "weights":
                    act.wait_ge(s["me_wt_ps"], up("me_wt_ps", it))
                    nc.scalar.activation(wt[:, :], ps[0:NE, 6, :], ACT.Copy).then_inc(s["me_wt"], 1)
                elif name == "gelu":
                    act.wait_ge(s["me_h_ps"], up("me_h_ps", it, n))
                    if n >= 2:
                        act.wait_ge(s["me_hs"], up("me_hs", it, n - 2))
                    nc.scalar.activation(ga[:, n % 2, :], ps[:, 3 + n % 2, :], ACT.Gelu).then_inc(s["me_act"], 1)

            with act.Fori(0, NB) as it:
                for sub in range(SUBS):
                    act.wait_ge(s["ls_v_ps"], up("ls_v_ps", it, sub))
                    nc.scalar.activation(v[:, :], ps[:, 0, 0:P], ACT.Copy).then_inc(s["ls_v"], 1)
                    for name, n in steps_of("A", sub):
                        expert(it, name, n)
                    act.wait_ge(s["ls_w_ps"], up("ls_w_ps", it, sub))
                    nc.scalar.activation(w[:, :], ps[:, 0, 0:P], ACT.Copy).then_inc(s["ls_wb"], 1)

        @block.vector
        def _(dve):
            link = LocalChain(c, dve, "ls_dve")
            dve.wait_ge(s["ls_w"], 16 * LOADS)
            dve.sem_inc(s["ls_a"], 1)
            dve.sem_inc(s["me_done"], 1)
            wide = lambda x: x.unsqueeze(2).to_broadcast([P, 4, NE])
            logits = ps[:, 5, 0:4 * NE].rearrange("p (t e) -> p t e", e=NE)

            def router(r, it):
                if r == 0:
                    dve.wait_ge(s["me_lg_ps"], up("me_lg_ps", it))
                else:
                    dve.wait_ge(s["me_router"], up("me_router", it, r - 1))
                if r == 0:
                    return nc.vector.tensor_reduce(g1[:, :], logits, AX, ALU.max, negate=True)
                if r == 1:
                    return nc.vector.tensor_tensor(lr[:, :, :], logits, wide(g1[:, :]), ALU.add)
                if r == 2:
                    dve.wait_ge(s["me_exp"], up("me_exp", it))
                    return nc.vector.tensor_reduce(g1[:, :], lr[:, :, :], AX, ALU.add)
                if r == 3:
                    return nc.vector.reciprocal(g1[:, :], g1[:, :])
                if r == 4:
                    return nc.vector.tensor_tensor(lg[:, :, :], lr[:, :, :], wide(g1[:, :]), ALU.mult)
                if r == ROUTER - 2:
                    return nc.vector.tensor_tensor(hot[:, 0, :, :], hot[:, 0, :, :], hot[:, 1, :, :], ALU.add)
                if r == ROUTER - 1:
                    return nc.vector.tensor_tensor(lr[:, :, :], lg[:, :, :], hot[:, 0, :, :], ALU.mult)
                k = (r - 5) // 6
                x, dst = (lg, others)[k], hot[:, k, :, :]
                part = (r - 5) % 6
                if part == 0:
                    return nc.vector.tensor_reduce(g1[:, :], x[:, :, :], AX, ALU.max)
                if part == 1:
                    return nc.vector.tensor_tensor(dst, x[:, :, :], wide(g1[:, :]), ALU.is_equal)
                if part == 2:
                    return nc.vector.tensor_tensor(dst, dst, order[:, :, :], ALU.mult)
                if part == 3:
                    return nc.vector.tensor_reduce(g1[:, :], dst, AX, ALU.max)
                if part == 4:
                    return nc.vector.tensor_tensor(dst, dst, wide(g1[:, :]), ALU.is_equal)
                return nc.vector.scalar_tensor_tensor(others[:, :, :], dst, -1e30, x[:, :, :], ALU.mult, ALU.add)

            def expert(it, name, n):
                here = tokens(it * BLK, BLK)
                if name == "load":
                    dve.wait_ge(s["me_done"], it + 1)
                    nc.vector.tensor_scalar(h[:, :], c.xnt[:, here], 1.0, None, ALU.mult).then_inc(s["me_h"], 1)
                elif name == "centre":
                    dve.wait_ge(s["me_mean"], up("me_mean", it))
                    nc.vector.tensor_tensor(tmp[:, 0, :], h[:, :], ps[:, 5, :], ALU.subtract).then_inc(s["me_xc"], 1)
                elif name == "inverse":
                    dve.wait_ge(s["me_sd"], up("me_sd", it))
                    nc.vector.reciprocal(tmp[:, 2, :], tmp[:, 2, :]).then_inc(s["me_norm"], 1)
                elif name == "scale":
                    dve.wait_ge(s["me_norm"], up("me_norm", it, 0))
                    nc.vector.tensor_tensor(tmp[:, 1, :], tmp[:, 0, :], tmp[:, 2, :],
                                            ALU.mult).then_inc(s["me_norm"], 1)
                elif name == "affine":
                    dve.wait_ge(s["me_norm"], up("me_norm", it, 1))
                    nc.vector.tensor_scalar(rn[:, :], tmp[:, 1, :], gcon[:, 0:1], gcon[:, 1:2],
                                            ALU.mult, ALU.add).then_inc(s["me_norm"], 1)
                elif name == "router":
                    router(n, it).then_inc(s["me_router"], 1)
                elif name == "weigh":
                    dve.wait_ge(s["me_act"], up("me_act", it, n))
                    dve.wait_ge(s["me_wb"], up("me_wb", it, n // 2))
                    if n >= 2:
                        dve.wait_ge(s["me_out"], up("me_out", it, n - 2))
                    nc.vector.tensor_tensor(hs[:, n % 2, :], ga[:, n % 2, :], ps[:, 5 + n // 2 % 2, :],
                                            ALU.mult).then_inc(s["me_hs"], 1)
                elif name == "add":
                    dve.wait_ge(s["me_out"], up("me_out", it, 2 * NE - 1))
                    nc.vector.tensor_tensor(c.xt[:, here], c.xt[:, here], ps[:, 7, :], ALU.add).then_inc(s["me_done"], 1)

            with dve.Fori(0, NB) as it:
                for sub in range(SUBS):
                    here = tokens(it * (SUBS * S) + sub * S, S)
                    dve.wait_ge(s["ls_a"], up("ls_a", it, sub))
                    link.later(nc.vector.tensor_scalar(f[:, S:2 * S], eye[:, :], 1.0, None, ALU.mult))
                    nc.vector.tensor_scalar(ub[:, :, :], st.u[:, :, here], 1.0, None, ALU.mult).then_inc(s["ls_u"], 1)
                    dve.wait_ge(s["ls_v_ps"], up("ls_v_ps", it, sub))
                    nc.vector.tensor_scalar(vt[:, :, :].rearrange("p b e -> p (b e)"), ps[:, 1, 0:P], 1.0, None,
                                            ALU.mult).then_inc(s["ls_vt"], 1)
                    dve.wait_ge(s["ls_s_ps"], up("ls_s_ps", it, sub))
                    link(nc.vector.tensor_tensor(f[:, 0:S], eye[:, :], ps[:, 2, 0:S], ALU.add))
                    for t in range(S - 1):
                        cols = slice(t, S + t + 1)
                        shuffled = nc.vector.stream_shuffle(row[:, cols], f[:, cols], [t] * S)
                        shuffled.then_inc(s["ls_step"], 1)
                        for e, name, n in place.get(sub * (S - 1) + t, []):
                            if e == "D":
                                expert(it, name, n)
                        dve.wait_ge(s["ls_step"], 2 * (sub * (S - 1) + t) + 1)
                        nc.vector.tensor_scalar(step[:, cols], row[:, cols], f[:, t:t + 1], below[:, t:t + 1],
                                                ALU.mult, ALU.mult).then_inc(s["ls_step"], 1)
                        link(nc.vector.reciprocal(r[:, :], row[:, t:t + 1]))
                        dve.wait_ge(s["ls_step"], 2 * (sub * (S - 1) + t) + 2)
                        link(nc.vector.scalar_tensor_tensor(f[:, cols], step[:, cols], r[:, :], f[:, cols],
                                                            ALU.mult, ALU.add))
                    link(nc.vector.transpose(mt[:, 0, :], f[:, S:2 * S]))
                    nc.vector.tensor_tensor(mz[:, 0, :, :], mt[:, 0:1, :].to_broadcast([P, B, S]), diag[:, :, :],
                                            ALU.mult).then_inc(s["ls_m"], 1)
                    link(nc.vector.tensor_tensor(row[:, 0:S], f[:, 0:S], eye[:, :], ALU.mult))
                    link(nc.vector.tensor_reduce(dinv[:, :], row[:, 0:S], AX, ALU.add))
                    link(nc.vector.reciprocal(dinv[:, :], dinv[:, :]))
                    link.later(nc.vector.tensor_scalar(m[:, :], f[:, S:2 * S], dinv[:, 0:1], None, ALU.mult))
                    link(nc.vector.tensor_scalar(dd[:, :], diag[:, :, 0], dinv[:, 0:1], None, ALU.mult))
                    dve.wait_ge(s["ls_wb"], up("ls_wb", it, sub))
                    nc.vector.tensor_tensor(z[:, :, :], w[:, :].unsqueeze(1).to_broadcast([P, B, P]),
                                            dd[:, :].unsqueeze(2).to_broadcast([P, B, P]),
                                            ALU.mult).then_inc(s["ls_zb"], 1)
                    link(nc.vector.transpose(mt[:, 1, :], m[:, :]))
                    nc.vector.tensor_tensor(mz[:, 1, :, :], mt[:, 1:2, :].to_broadcast([P, B, S]), diag[:, :, :],
                                            ALU.mult).then_inc(s["ls_dm"], 1)
                    dve.wait_ge(s["ls_a_ps"], up("ls_a_ps", it, sub))
                    nc.vector.tensor_tensor(a[:, :, :], a[:, :, :], ps[:, 2, :].rearrange("p (b e) -> p b e", b=B),
                                            ALU.subtract).then_inc(s["ls_a"], 1)
                    dve.wait_ge(s["ls_z_ps"], up("ls_z_ps", it, sub))
                    link(nc.vector.tensor_scalar(st.z[:, :, here], ps[:, 1, 0:P].rearrange("p (b e) -> p b e", e=S),
                                                 1.0, None, ALU.mult))
                dve.sem_clear(s["ls_step"])
                link.clear()


def linear_output_phase(c, st):
    units = [(i, k) for i in range(HALVES) for k in range(4 * i + 4)]
    U = len(units)
    s = c.signals(lo_w=1, lo_in=1, lo_s_ps=U, lo_p=U, lo_av=U, lo_o=2, lo_y_ps=2, lo_done=1)
    nc, d, up, ps = c.nc, c.d, c.up, c.ps
    with ExitStack() as ctx:
        causal = c.sb(ctx, "lo_causal", [P, P])
        z = c.sb(ctx, "lo_z", [P, T])
        q = c.sb(ctx, "lo_q", [P, T])
        v = c.sb(ctx, "lo_v", [P, T])
        pt = c.sb(ctx, "lo_pt", [P, 3, BLK])
        o = c.sb(ctx, "lo_ob", [P, 2, BLK])
        block = ctx.enter_context(nc.Block())
        start = lambda i, k: max(k * P, i * BLK)

        @block.sync
        def _(sp):
            sp.dma_start(causal[:, :], d["c_causal"]).then_inc(s["lo_w"], 16)
            sp.wait_ge(s["lo_w"], 16)

        @block.tensor
        def _(pe):
            with pe.Fori(0, B) as it:
                pe.wait_ge(s["lo_in"], up("lo_in", it))

                def scores(n):
                    i, k = units[n]
                    q0, q1 = start(i, k), (i + 1) * BLK
                    if n >= 3:
                        pe.wait_ge(s["lo_p"], up("lo_p", it, n - 3))
                    nc.tensor.matmul(ps[:, n % 3, 0:q1 - q0], z[:, k * P:(k + 1) * P], q[:, q0:q1],
                                     start=True, stop=True).then_inc(s["lo_s_ps"], 1)

                def values(n):
                    i, k = units[n]
                    q0, q1 = start(i, k), (i + 1) * BLK
                    pe.wait_ge(s["lo_p"], up("lo_p", it, n))
                    nc.tensor.matmul(ps[:, 4 + i, q0 - i * BLK:BLK], v[:, k * P:(k + 1) * P], pt[:, n % 3, 0:q1 - q0],
                                     start=(k == 0), stop=(k == 4 * i + 3)).then_inc(s["lo_av"], 1)

                for n in range(U + 2):
                    if n < U:
                        scores(n)
                    if n >= 2:
                        values(n - 2)
                for i in range(HALVES):
                    pe.wait_ge(s["lo_o"], up("lo_o", it, i))
                    nc.tensor.matmul(ps[:, 6 + i, :], st.wo[:, :], o[:, i, :], start=True, stop=True).then_inc(s["lo_y_ps"], 1)

        @block.scalar
        def _(act):
            with act.Fori(0, B) as it:
                for i in range(HALVES):
                    act.wait_ge(s["lo_av"], up("lo_av", it, (3, U - 1)[i]))
                    nc.scalar.activation(o[:, i, :], ps[:, 4 + i, :], ACT.Copy).then_inc(s["lo_o"], 1)

        @block.vector
        def _(dve):
            link = Chain(c, dve, "lo_dve", 1)
            dve.wait_ge(s["lo_w"], 16)
            dve.sem_inc(s["lo_done"], 1)
            with dve.Fori(0, B) as it:
                link.start(it)
                dve.wait_ge(s["lo_done"], it + 1)
                here = tokens(it * T, T)
                for dst, src in ((z, st.z[:, :, :].rearrange("p b t -> p (b t)")),
                                 (q, st.q[:, :, :].rearrange("p b t -> p (b t)")),
                                 (v, st.v[:, :, :, :].rearrange("p b t e -> p (b t e)"))):
                    last = nc.vector.tensor_scalar(dst[:, :], src[:, here], 1.0, None, ALU.mult)
                last.then_inc(s["lo_in"], 1)
                for n, (i, k) in enumerate(units):
                    q0, q1 = start(i, k), (i + 1) * BLK
                    dve.wait_ge(s["lo_s_ps"], up("lo_s_ps", it, n))
                    if n >= 3:
                        dve.wait_ge(s["lo_av"], up("lo_av", it, n - 3))
                    off = P if k >= 4 * i else 0
                    if off:
                        last = nc.vector.tensor_tensor(pt[:, n % 3, 0:P], ps[:, n % 3, 0:P], causal[:, :], ALU.mult)
                    if q1 - q0 > off:
                        last = nc.vector.tensor_scalar(pt[:, n % 3, off:q1 - q0], ps[:, n % 3, off:q1 - q0], 1.0, None,
                                                       ALU.mult)
                    last.then_inc(s["lo_p"], 1)
                for i in range(HALVES):
                    here = tokens(it * T + i * BLK, BLK)
                    dve.wait_ge(s["lo_y_ps"], up("lo_y_ps", it, i))
                    ins = nc.vector.scalar_tensor_tensor(c.xt[:, here], ps[:, 6 + i, :], st.cols[:, 2:3], c.xt[:, here],
                                                         ALU.add, ALU.add)
                    if i == 0:
                        link(ins)
                ins.then_inc(s["lo_done"], 1)
            link.close()


def linear_attention(c):
    with ExitStack() as ctx:
        st = LinearState(c, ctx)
        linear_project_phase(c, st)
        linear_scan_phase(c, st)
        linear_output_phase(c, st)


def more_constants(np):
    f = np.float32
    o = {}
    gather = np.zeros((P, 8, 16), f)
    spread = np.zeros((P, 8, P), f)
    for n in range(8):
        for j in range(2):
            gather[64 * j:64 * j + 64, n, 2 * n + j] = 1
            spread[2 * n + j, n, 64 * j:64 * j + 64] = 1
    o["c_gather"], o["c_spread"] = gather, spread
    o["c_pick"], o["c_spread_rows"] = np.zeros((P, 8, 8), f), np.zeros((P, 8, P), f)
    for n in range(8):
        o["c_pick"][:, n, n] = 1 / P
        o["c_spread_rows"][n, n] = 1
    gather8, spread8 = np.zeros((P, 4, 64), f), np.zeros((P, 4, P), f)
    for n in range(4):
        for h in range(16):
            gather8[8 * h:8 * h + 8, n, 16 * n + h] = 1 / 8
            spread8[16 * n + h, n, 8 * h:8 * h + 8] = 1
    o["c_gather8"], o["c_spread8"] = gather8, spread8
    i, j = np.arange(P)[:, None], np.arange(2 * P)[None, :] - P
    ok = (i >= j) & (i <= j + 64)
    band = np.where(ok, 0, -1e30).astype(f)
    first = np.where(ok & (j >= 0), 0, -1e30).astype(f)
    o["c_band"] = np.stack([first, band], 1)
    half = np.arange(0, 64, 2, dtype=f)
    inv = (f(1.0) / f(10000.0) ** (half / f(64))).astype(f)
    t = np.arange(T, dtype=f)
    fr = (t[:, None] * inv[None, :]).astype(f)
    base = ((half + f(0.4 * 64)) / f(1.4 * 64)).astype(f)
    power = ((t - T // 2) / f(32)).astype(f)
    scale = (base[None, :] ** power[:, None]).astype(f)
    cos, sin = np.cos(fr), np.sin(fr)
    tabs = []
    for sc in (scale, 1 / scale):
        tabs.append(np.concatenate([cos * sc] * 4, 1).T)
        tabs.append(np.concatenate([-sin * sc, sin * sc] * 2, 1).T)
    o["c_tab"] = np.stack(tabs, 1).astype(f)
    k, q = np.arange(P)[:, None], np.arange(P)[None, :]
    causal = (k <= q).astype(f)
    o["c_causal"] = causal
    o["c_ga0_mask"] = np.stack([causal, causal], 1)
    o["c_ga1_mask"] = np.stack([((q - k >= 0) & (q - k < 32)), (q + P - k < 32)], 1).astype(f)
    for n, theta in enumerate((1000000.0, 10000.0)):
        inv = (f(1.0) / f(theta) ** (np.arange(0, 8, 2, dtype=f) / f(8))).astype(f)
        fr = (t[:, None] * inv[None, :]).astype(f)
        tab = np.zeros((P, 2, T), f)
        for r in range(P):
            tab[r, 0] = np.cos(fr[:, r % 8 // 2])
            tab[r, 1] = np.sin(fr[:, r % 8 // 2]) * (1 if r % 2 else -1)
        o[f"c_ga{n}_tab"] = tab
    sel = np.zeros((8, 8, P), f)
    sel[np.arange(8), np.arange(8)] = 1
    o["c_sel"] = sel
    o["c_order"] = np.broadcast_to(np.arange(8, 0, -1, dtype=f), (P, 4, 8))
    i = np.arange(P)[:, None] % 32
    j = np.arange(32)[None, :]
    o["c_eye32"] = (i == j).astype(f)
    o["c_below"] = -(i > j).astype(f)
    o["c_diag"] = np.repeat((np.arange(P)[:, None] // 32 == np.arange(4)[None, :]).astype(f), 32, 1).reshape(P, 4, 32)
    o["c_ones"] = np.ones((P, 1), f)
    return o


def halves_swapped(np, w):
    w = w.reshape(w.shape[:-1] + (w.shape[-1] // 64, 2, 32))
    return w[..., ::-1, :].reshape(w.shape[:-3] + (-1,))


def more_layout(np, x):
    o = {}
    w = x["L0_ffn_wqkv"]
    qk = w[:, :, 0:1024].reshape(2, P, 2, 512)
    o["wa_wqk"], o["wa_wsw"], o["wa_wv"] = qk, halves_swapped(np, qk), w[:, :, 1024:]
    o["wa_wo"] = x["L0_ffn_wo"].reshape(2, 4, P, P).transpose(0, 2, 1, 3)
    o["wa_w1"] = x["L0_ffn_w1"]
    w2 = np.zeros((2, 3 * P, P), w.dtype)
    w2[:, :HID] = x["L0_ffn_w2"]
    o["wa_w2"] = w2.reshape(2, 3, P, P).transpose(0, 2, 1, 3)
    qs, ks = x["L0_ffn_q_scale"], x["L0_ffn_k_scale"]
    four = np.stack([qs, halves_swapped(np, qs), ks, halves_swapped(np, ks)], 2)
    o["wa_qks"] = np.concatenate([four, four], 1)
    o["wa_lnc"] = np.stack([x["L0_ffn_ln_g"], x["L0_ffn_ln_b"], x["L0_ffn_b2"]], 2)
    b1 = np.zeros((2, 2, 3 * P), w.dtype)
    b1[:, :, :HID] = x["L0_ffn_b1"].reshape(2, 2, HID)
    o["wa_b1"] = b1.reshape(2, 2, 3, P).transpose(0, 3, 2, 1)
    for n, p in enumerate(("g", "l")):
        wq = x[f"L1_attn_{p}_wq"]
        wk = x["L1_attn_g_k_up" if n == 0 else "L1_attn_l_wk"]
        exchanged = lambda w: w.reshape(w.shape[0], -1, 2)[..., ::-1].reshape(w.shape)
        o[f"ga{n}_wq"] = np.stack([wq, exchanged(wq)], 1)
        o[f"ga{n}_wk"] = np.zeros((wk.shape[0], 2, P), wk.dtype)
        o[f"ga{n}_wk"][:, :, :32] = np.stack([wk, exchanged(wk)], 1)
        o[f"ga{n}_wv"] = x["L1_attn_g_v_up" if n == 0 else "L1_attn_l_wv"]
        wo = np.zeros((4, 32, 4, P), wq.dtype)
        wo[:, :8] = x[f"L1_attn_{p}_wo"].reshape(4, 4, 8, P).transpose(0, 2, 1, 3)
        o[f"ga{n}_wo"] = wo.reshape(P, 4, P)
        o[f"ga{n}_nw"] = x[f"L1_attn_norm{n + 1}_w"].reshape(P, 1)
    o["ga0_wd"] = x["L1_attn_g_kv_down"]
    o["moe1_w1"] = np.concatenate([x["L1_ffn_W1"], x["L1_ffn_Ws1"][None]]).transpose(1, 0, 2)
    o["moe1_w3"] = np.concatenate([x["L1_ffn_W3"], x["L1_ffn_Ws3"][None]]).transpose(1, 0, 2)
    o["moe1_w2"] = np.concatenate([x["L1_ffn_W2"], x["L1_ffn_Ws2"][None]]).reshape(9, 2, P, P).transpose(2, 0, 1, 3)
    o["moe1_wr"] = x["L1_ffn_Wr"]
    gcon = np.zeros((P, 2 + 32), wo.dtype)
    gcon[:, 2:] = np.tile(x["L1_ffn_rb"], 4)
    o["moe1_gcon"] = gcon
    o["moe3_w1"] = x["L3_ffn_w1"].transpose(2, 0, 1)
    o["moe3_w2"] = x["L3_ffn_w2"].reshape(8, P, 2, P).transpose(3, 0, 2, 1)
    o["moe3_wr"] = x["L3_ffn_gate_w"].T
    gcon = np.zeros((P, 2 + 32), wo.dtype)
    gcon[:, 0], gcon[:, 1] = x["L3_ffn_ln_gamma"], x["L3_ffn_ln_beta"]
    o["moe3_gcon"] = gcon
    o["th_w"] = x["L2_attn_W"].T
    o["ql_w"] = x["L2_ffn_weight"]
    o["ql_b"] = x["L2_ffn_bias"].reshape(P, 1)
    o["lp_w"] = np.stack([x["L3_attn_Wq"].T, x["L3_attn_Wk"].T, x["L3_attn_Wv"].T], 1)
    o["lp_bv"] = np.broadcast_to(x["L3_attn_bv"], (P, P))
    o["li_wo"] = x["L3_attn_Wo"].T
    o["li_cols"] = np.stack([x["L3_attn_bq"], x["L3_attn_bk"], x["L3_attn_bo"]], 1)
    return o



def build(nc, d):
    with ExitStack() as ctx:
        c = Core(nc, ctx, d)
        load_phase(c)
        norm_phase(c, 0)
        full_attention_phase(c)
        window_phase(c, 0)
        window_phase(c, 1)
        c.retire("load_", "fa_", "wa_", "wm_")
        norm_phase(c, 1)
        experts_phase(c)
        grouped_attention_phase(c, 0)
        grouped_attention_phase(c, 1)
        c.retire("moe1_", "ga0_", "ga1_")
        norm_phase(c, 2)
        threshold_attention_phase(c)
        quantised_linear_phase(c)
        norm_phase(c, 3)
        linear_attention(c)
        store_phase(c)


def constants():
    import numpy as np
    f = np.float32
    out = {"c_ident": np.eye(P, dtype=f)}
    row8 = np.zeros((P, P), f)
    for j in range(4):
        row8[32 * j + 8, 32 * j:32 * j + 32] = 1
    out["c_row8"] = row8
    out.update(more_constants(np))
    return out


def heads_padded(np, w):
    w = w.reshape(w.shape[:-1] + (4, 4, 8))
    out = np.zeros(w.shape[:-1] + (32,), w.dtype)
    out[..., :8] = w
    return out.reshape(w.shape[:-3] + (4, P))


def laid_out(np, x):
    o = {"z": x["L0_attn_z"]}
    wqkv, bqkv = x["L0_attn_W_qkv"], x["L0_attn_b_qkv"]
    o["fa_wqk"] = wqkv[:, 0:2 * P].reshape(P, 2, P)
    o["fa_wv"] = wqkv[:, 2 * P:]
    o["fa_wp"] = heads_padded(np, x["L0_attn_W_proj"].T).transpose(2, 1, 0)
    o["fa_bv"] = np.broadcast_to(bqkv[2 * P:], (P, P))
    o["fa_cols"] = np.stack([x["L0_attn_ln_w"], x["L0_attn_ln_b"], x["L0_attn_b_proj"], bqkv[0:P], bqkv[P:2 * P]], 1)
    o.update(more_layout(np, x))
    return o


def kernel(**inputs):
    import numpy as np
    import concourse.bacc as bacc
    from concourse.bass_utils import run_bass_kernel_spmd

    nc = bacc.Bacc("TRN2", target_bir_lowering=False, num_devices=1)
    host = constants()
    host.update(laid_out(np, {k: np.asarray(a) for k, a in inputs.items()}))
    arrays, d = {}, {}
    for name, a in host.items():
        arrays[f"in_{name}"] = np.ascontiguousarray(a)
        d[name] = nc.dram_tensor(f"in_{name}", a.shape, mybir.dt.from_np(a.dtype), kind="ExternalInput").ap()
    d["out"] = nc.dram_tensor("out_x", (B, T, P), F32, kind="ExternalOutput").ap()
    build(nc, d)
    r = run_bass_kernel_spmd(nc, [arrays], core_ids=[0])
    return r.results[0]["out_x"]
```
